# Optimizing a Trainium2 kernel written in Bass

```python
import numpy as np
import jax
import jax.numpy as jnp

def _softmax(x, axis=-1):
    return jax.nn.softmax(x, axis=axis)

def _gelu(x):
    return jax.nn.gelu(x, approximate=True)

def _silu(x):
    return jax.nn.silu(x)

def _sigmoid(x):
    return jax.nn.sigmoid(x)

def _layernorm(x, axis=-1, eps=1e-05):
    m = jnp.mean(x, axis=axis, keepdims=True)
    v = jnp.var(x, axis=axis, keepdims=True)
    return (x - m) / jnp.sqrt(v + eps)

def _scatter_add(tgt, idx, src, axis=0):
    return tgt.at[idx].add(src)

def _segment_sum(src, seg, n):
    return jax.ops.segment_sum(src, seg, n)
kernel_name = 'mk_xattn_ffn_d4_seqx_r4_6cd319'

def setup_inputs(seed: int=0):
    np.random.seed(seed)
    _w = jnp.asarray

    def _rec_inputs():
        import jax
        import jax.numpy as jnp
        _rk = jax.random.key(seed)
        x = -0.0002928 + 1 * jax.random.normal(jax.random.fold_in(_rk, 1), (2, 1024, 256), jnp.float32)
        _lenS = 1024 - jax.random.randint(jax.random.fold_in(_rk, 7), (2,), 0, max(1, 1024 // 4) + 1, jnp.int32)
        _lenS2 = 77 - jax.random.randint(jax.random.fold_in(_rk, 8), (2,), 0, max(1, 77 // 4) + 1, jnp.int32)
        _ctx_768P = jax.random.normal(jax.random.fold_in(_rk, 11), (2, 16, 192), jnp.float32)
        _ctx_768c = jax.random.dirichlet(jax.random.fold_in(_rk, 511), 0.3 * jnp.ones((16,), jnp.float32), (2, 77))
        _ctx_768t = jnp.einsum('bsk,bkd->bsd', _ctx_768c, _ctx_768P)
        _ctx_768t = _ctx_768t * jax.lax.rsqrt(jnp.mean(jnp.square(_ctx_768t)) + 1e-12) * 0.953939
        ctx_768 = -0.00055796 + 0.999787 * (_ctx_768t + 0.3 * jax.random.normal(jax.random.fold_in(_rk, 611), (2, 77, 192), jnp.float32))
        _validS = jnp.arange(1024)[None, :] < _lenS[:, None]
        _validS2 = jnp.arange(77)[None, :] < _lenS2[:, None]
        _causal = jnp.tril(jnp.ones((1024, 1024), dtype=bool))
        mask_BxS_bf1 = jnp.ones((2, 1024), dtype=bool)
        mask_BxS2_bf1 = jnp.ones((2, 77), dtype=bool)
        return (x, ctx_768, mask_BxS_bf1, mask_BxS2_bf1)
    x, ctx_768, mask_BxS_bf1, mask_BxS2_bf1 = _rec_inputs()

    def _L0_xattn_setup():
        import jax, jax.numpy as jnp
        import numpy as np
        HEADS = 16
        DIM_HEAD = 64
        key = jax.random.key(seed)
        ks = jax.random.split(key, 7)
        b, n, m = (2, 512, 256)
        query_dim, context_dim = (256, 192)
        inner = HEADS * DIM_HEAD
        s_q = 1.0 / np.sqrt(query_dim)
        s_c = 1.0 / np.sqrt(context_dim)
        s_i = 1.0 / np.sqrt(inner)
        return {'x': jax.random.normal(ks[0], (b, n, query_dim), jnp.float32), 'context': jax.random.normal(ks[1], (b, m, context_dim), jnp.float32), 'Wq': jax.random.normal(ks[2], (query_dim, inner), jnp.float32) * s_q, 'Wk': jax.random.normal(ks[3], (context_dim, inner), jnp.float32) * s_c, 'Wv': jax.random.normal(ks[4], (context_dim, inner), jnp.float32) * s_c, 'Wo': jax.random.normal(ks[5], (inner, query_dim), jnp.float32) * s_i, 'bo': jax.random.normal(ks[6], (query_dim,), jnp.float32) * 0.01}
    _L0_xattn_all = _L0_xattn_setup()
    _L0_xattn_in = {k: v for k, v in _L0_xattn_all.items() if k in ('Wq', 'Wk', 'Wv', 'Wo', 'bo')}
    del _L0_xattn_all

    def _L0_ffn_setup():
        import jax, jax.numpy as jnp
        import numpy as np
        B, S, D, E, F = (2, 256, 256, 14, 512)
        key = jax.random.key(seed)
        k0, k1, k2, k3 = jax.random.split(key, 4)
        h = jax.random.normal(k0, (B, S, D), jnp.float32)
        gate_w = jax.random.normal(k1, (E, D), jnp.float32) * 0.02
        w1 = jax.random.normal(k2, (E, D, F), jnp.float32) * (1.0 / np.sqrt(D).astype(np.float32))
        b1 = jnp.zeros((E, F), jnp.float32)
        w2 = jax.random.normal(k3, (E, F, D), jnp.float32) * (1.0 / np.sqrt(F).astype(np.float32))
        b2 = jnp.zeros((E, D), jnp.float32)
        return {'h': h, 'gate_w': gate_w, 'w1': w1, 'b1': b1, 'w2': w2, 'b2': b2}
    _L0_ffn_all = _L0_ffn_setup()
    _L0_ffn_in = {k: v for k, v in _L0_ffn_all.items() if k in ('gate_w', 'w1', 'b1', 'w2', 'b2')}
    del _L0_ffn_all

    def _L1_xattn_setup():
        import jax, jax.numpy as jnp
        import numpy as np
        B, T, DT, G, DV = (16, 128, 256, 144, 192)
        H, DH = (4, 32)
        INNER = H * DH
        HID = 4 * DT
        N_STATE = 64
        K_TOP = 32

        def layernorm(x, g, b, eps=1e-05):
            m = x.mean(-1, keepdims=True)
            v = x.var(-1, keepdims=True)
            return (x - m) * jax.lax.rsqrt(v + eps) * g + b

        def s4d(x, log_dt, A_re, A_im, C_re, C_im, D_skip):
            Bb, L, D = x.shape
            dt = jnp.exp(log_dt)
            A = A_re + 1j * A_im
            C = C_re + 1j * C_im
            dtA = dt[:, None] * A
            dC = C * (jnp.exp(dtA) - 1.0) / A
            powers = jnp.exp(dtA[:, :, None] * jnp.arange(L))
            K = 2.0 * jnp.einsum('dn,dnl->dl', dC, powers).real
            n = 2 * L
            Kf = jnp.fft.rfft(K, n=n, axis=-1)
            xf = jnp.fft.rfft(x, n=n, axis=1)
            y = jnp.fft.irfft(xf * Kf.T[None], n=n, axis=1)[:, :L]
            return y + x * D_skip
        key = jax.random.key(seed)
        ks = jax.random.split(key, 16)
        s = 0.02
        inp = {'x_text': jax.random.normal(ks[0], (B, T, DT), jnp.float32), 'x_vision': jax.random.normal(ks[1], (B, G, DV), jnp.float32), 'text_mask': jnp.ones((B, T), bool), 'vision_mask': jnp.ones((B, G), bool), 'Wq': jax.random.normal(ks[2], (DT, INNER), jnp.float32) * s, 'Wk': jax.random.normal(ks[3], (DV, INNER), jnp.float32) * s, 'Wv': jax.random.normal(ks[4], (DV, DT), jnp.float32) * s, 'W_film_in': jax.random.normal(ks[5], (DT, 2 * DT), jnp.float32) * s, 'b_film_in': jnp.zeros((2 * DT,), jnp.float32), 'W_film_out': jax.random.normal(ks[6], (DT, 2 * DT), jnp.float32) * s, 'b_film_out': jnp.zeros((2 * DT,), jnp.float32), 'g_norm_in': jnp.ones((DT,), jnp.float32), 'b_norm_in': jnp.zeros((DT,), jnp.float32), 'g_norm_out': jnp.ones((DT,), jnp.float32), 'b_norm_out': jnp.zeros((DT,), jnp.float32), 'g_ffn': jnp.ones((DT,), jnp.float32), 'b_ffn': jnp.zeros((DT,), jnp.float32), 'W1': jax.random.normal(ks[7], (DT, HID), jnp.float32) * s, 'b1': jnp.zeros((HID,), jnp.float32), 'W2': jax.random.normal(ks[8], (HID, DT), jnp.float32) * s, 'b2': jnp.zeros((DT,), jnp.float32), 'log_dt': jnp.log(0.001) + jax.random.uniform(ks[9], (DT,), jnp.float32) * (jnp.log(0.1) - jnp.log(0.001)), 'A_re': -0.5 * jnp.ones((DT, N_STATE), jnp.float32), 'A_im': jnp.tile(jnp.pi * jnp.arange(N_STATE, dtype=jnp.float32), (DT, 1)), 'C_re': jax.random.normal(ks[10], (DT, N_STATE), jnp.float32) * 0.5 ** 0.5, 'C_im': jax.random.normal(ks[11], (DT, N_STATE), jnp.float32) * 0.5 ** 0.5, 'D_skip': jax.random.normal(ks[12], (DT,), jnp.float32), 'mod_gate': jnp.array(0.5, jnp.float32)}
        return inp
    _L1_xattn_all = _L1_xattn_setup()
    _L1_xattn_in = {k: v for k, v in _L1_xattn_all.items() if k in ('Wq', 'Wk', 'Wv', 'W_film_in', 'b_film_in', 'W_film_out', 'b_film_out', 'g_norm_in', 'b_norm_in', 'g_norm_out', 'b_norm_out', 'g_ffn', 'b_ffn', 'W1', 'b1', 'W2', 'b2', 'log_dt', 'A_re', 'A_im', 'C_re', 'C_im', 'D_skip', 'mod_gate')}
    del _L1_xattn_all

    def _L1_ffn_setup():
        import jax, jax.numpy as jnp
        import numpy as np
        B, S, H = (8, 1024, 256)
        NAV = 128
        E = 8
        F = 2 * H
        key = jax.random.key(seed)
        ks = jax.random.split(key, 12)

        def w(k, shape, fan_in):
            return jax.random.normal(k, shape, dtype=jnp.float32) / np.sqrt(fan_in)
        return {'hidden_states': jax.random.normal(ks[0], (B, S, H), dtype=jnp.float32), 'Wp1': w(ks[1], (H, NAV), H), 'bp1': jnp.zeros((NAV,), jnp.float32), 'Wp2': w(ks[2], (NAV, E), NAV), 'bp2': jnp.zeros((E,), jnp.float32), 'W1': w(ks[3], (E, H, F), H), 'b1': jnp.zeros((E, F), jnp.float32), 'W2': w(ks[4], (E, F, H), F), 'b2': jnp.zeros((E, H), jnp.float32), 'Wo': w(ks[5], (H, H), H), 'bo': jnp.zeros((H,), jnp.float32)}
    _L1_ffn_all = _L1_ffn_setup()
    _L1_ffn_in = {k: v for k, v in _L1_ffn_all.items() if k in ('Wp1', 'bp1', 'Wp2', 'bp2', 'W1', 'b1', 'W2', 'b2', 'Wo', 'bo')}
    del _L1_ffn_all

    def _L2_xattn_setup():
        import jax, jax.numpy as jnp
        import numpy as np
        N_HEADS = 16
        D_HEAD = 64
        key = jax.random.key(seed)
        ks = jax.random.split(key, 7)
        B, SQ, SKV = (2, 512, 512)
        D_MODEL, D_COND, D_ATTN = (256, 192, N_HEADS * D_HEAD)
        return {'x': jax.random.normal(ks[0], (B, SQ, D_MODEL), jnp.float32), 'cond': jax.random.normal(ks[1], (B, SKV, D_COND), jnp.float32), 'w_q': jax.random.normal(ks[2], (D_MODEL, D_ATTN), jnp.float32) * D_MODEL ** (-0.5), 'w_k': jax.random.normal(ks[3], (D_COND, D_ATTN), jnp.float32) * D_COND ** (-0.5), 'w_v': jax.random.normal(ks[4], (D_COND, D_ATTN), jnp.float32) * D_COND ** (-0.5), 'w_out': jax.random.normal(ks[5], (D_ATTN, D_MODEL), jnp.float32) * D_ATTN ** (-0.5), 'b_out': jnp.zeros((D_MODEL,), jnp.float32)}
    _L2_xattn_all = _L2_xattn_setup()
    _L2_xattn_in = {k: v for k, v in _L2_xattn_all.items() if k in ('w_q', 'w_k', 'w_v', 'w_out', 'b_out')}
    del _L2_xattn_all

    def _L2_ffn_setup():
        import jax, jax.numpy as jnp
        import numpy as np
        key = jax.random.key(seed)
        ks = jax.random.split(key, 5)
        B, T, D, E = (4, 512, 256, 8)
        inputs = jax.random.normal(ks[0], (B, T, D), dtype=jnp.float32)
        Wr = jax.random.normal(ks[1], (D, E), dtype=jnp.float32) * 0.02
        br = jnp.zeros((E,), dtype=jnp.float32)
        W1 = jax.random.normal(ks[2], (E, D, D), dtype=jnp.float32) * 0.02
        b1 = jnp.zeros((E, D), dtype=jnp.float32)
        W2 = jax.random.normal(ks[3], (E, D, D), dtype=jnp.float32) * 0.02
        b2 = jnp.zeros((E, D), dtype=jnp.float32)
        return {'inputs': inputs, 'Wr': Wr, 'br': br, 'W1': W1, 'b1': b1, 'W2': W2, 'b2': b2}
    _L2_ffn_all = _L2_ffn_setup()
    _L2_ffn_in = {k: v for k, v in _L2_ffn_all.items() if k in ('Wr', 'br', 'W1', 'b1', 'W2', 'b2')}
    del _L2_ffn_all

    def _L3_xattn_setup():
        import jax, jax.numpy as jnp
        import numpy as np
        IMAGE_DIM = 256
        TEXT_DIM = 192
        NUM_HEADS = 16
        HEAD_DIM = IMAGE_DIM // NUM_HEADS
        key = jax.random.key(seed)
        ks = jax.random.split(key, 14)
        B, N, M = (4, 1024, 128)
        s_img = 1.0 / np.sqrt(IMAGE_DIM)
        s_txt = 1.0 / np.sqrt(TEXT_DIM)
        s_ff = 1.0 / np.sqrt(2 * IMAGE_DIM)
        return {'x': jax.random.normal(ks[0], (B, N, IMAGE_DIM), jnp.float32), 'y': jax.random.normal(ks[1], (B, M, TEXT_DIM), jnp.float32), 'Wq': jax.random.normal(ks[2], (IMAGE_DIM, IMAGE_DIM), jnp.float32) * s_img, 'bq': jax.random.normal(ks[3], (IMAGE_DIM,), jnp.float32) * s_img, 'Wk': jax.random.normal(ks[4], (TEXT_DIM, IMAGE_DIM), jnp.float32) * s_txt, 'bk': jax.random.normal(ks[5], (IMAGE_DIM,), jnp.float32) * s_txt, 'Wv': jax.random.normal(ks[6], (TEXT_DIM, IMAGE_DIM), jnp.float32) * s_txt, 'bv': jax.random.normal(ks[7], (IMAGE_DIM,), jnp.float32) * s_txt, 'W1': jax.random.normal(ks[8], (IMAGE_DIM, 2 * IMAGE_DIM), jnp.float32) * s_img, 'b1': jax.random.normal(ks[9], (2 * IMAGE_DIM,), jnp.float32) * s_img, 'W2': jax.random.normal(ks[10], (2 * IMAGE_DIM, IMAGE_DIM), jnp.float32) * s_ff, 'b2': jax.random.normal(ks[11], (IMAGE_DIM,), jnp.float32) * s_ff}
    _L3_xattn_all = _L3_xattn_setup()
    _L3_xattn_in = {k: v for k, v in _L3_xattn_all.items() if k in ('Wq', 'bq', 'Wk', 'bk', 'Wv', 'bv', 'W1', 'b1', 'W2', 'b2')}
    del _L3_xattn_all

    def _L3_ffn_setup():
        import math
        import jax, jax.numpy as jnp
        import numpy as np
        B, T, D, H, E, K, S = (4, 1024, 256, 512, 16, 2, 2)
        ROUTE_SCALE = 1.0

        def _swiglu(x, w1, w3, w2):
            return jax.nn.silu(x @ w1) * (x @ w3) @ w2
        key = jax.random.key(seed)
        ks = jax.random.split(key, 9)
        s = 0.02
        return {'x': jax.random.normal(ks[0], (B, T, D), jnp.float32), 'gate_w': jax.random.normal(ks[1], (D, E), jnp.float32) * s, 'gate_b': jnp.zeros((E,), jnp.float32), 'ew1': jax.random.normal(ks[2], (E, D, H), jnp.float32) * s, 'ew3': jax.random.normal(ks[3], (E, D, H), jnp.float32) * s, 'ew2': jax.random.normal(ks[4], (E, H, D), jnp.float32) * s, 'sw1': jax.random.normal(ks[5], (S, D, H), jnp.float32) * s, 'sw3': jax.random.normal(ks[6], (S, D, H), jnp.float32) * s, 'sw2': jax.random.normal(ks[7], (S, H, D), jnp.float32) * s}
    _L3_ffn_all = _L3_ffn_setup()
    _L3_ffn_in = {k: v for k, v in _L3_ffn_all.items() if k in ('gate_w', 'gate_b', 'ew1', 'ew3', 'ew2', 'sw1', 'sw3', 'sw2')}
    del _L3_ffn_all
    return {'x': x, 'ctx_768': ctx_768, 'mask_BxS_bf1': mask_BxS_bf1, 'mask_BxS2_bf1': mask_BxS2_bf1, 'L0_xattn_Wq': _L0_xattn_in['Wq'], 'L0_xattn_Wk': _L0_xattn_in['Wk'], 'L0_xattn_Wv': _L0_xattn_in['Wv'], 'L0_xattn_Wo': _L0_xattn_in['Wo'], 'L0_xattn_bo': _L0_xattn_in['bo'], 'L0_ffn_gate_w': _L0_ffn_in['gate_w'], 'L0_ffn_w1': _L0_ffn_in['w1'], 'L0_ffn_b1': _L0_ffn_in['b1'], 'L0_ffn_w2': _L0_ffn_in['w2'], 'L0_ffn_b2': _L0_ffn_in['b2'], 'L1_xattn_Wq': _L1_xattn_in['Wq'], 'L1_xattn_Wk': _L1_xattn_in['Wk'], 'L1_xattn_Wv': _L1_xattn_in['Wv'], 'L1_xattn_W_film_in': _L1_xattn_in['W_film_in'], 'L1_xattn_b_film_in': _L1_xattn_in['b_film_in'], 'L1_xattn_W_film_out': _L1_xattn_in['W_film_out'], 'L1_xattn_b_film_out': _L1_xattn_in['b_film_out'], 'L1_xattn_g_norm_in': _L1_xattn_in['g_norm_in'], 'L1_xattn_b_norm_in': _L1_xattn_in['b_norm_in'], 'L1_xattn_g_norm_out': _L1_xattn_in['g_norm_out'], 'L1_xattn_b_norm_out': _L1_xattn_in['b_norm_out'], 'L1_xattn_g_ffn': _L1_xattn_in['g_ffn'], 'L1_xattn_b_ffn': _L1_xattn_in['b_ffn'], 'L1_xattn_W1': _L1_xattn_in['W1'], 'L1_xattn_b1': _L1_xattn_in['b1'], 'L1_xattn_W2': _L1_xattn_in['W2'], 'L1_xattn_b2': _L1_xattn_in['b2'], 'L1_xattn_log_dt': _L1_xattn_in['log_dt'], 'L1_xattn_A_re': _L1_xattn_in['A_re'], 'L1_xattn_A_im': _L1_xattn_in['A_im'], 'L1_xattn_C_re': _L1_xattn_in['C_re'], 'L1_xattn_C_im': _L1_xattn_in['C_im'], 'L1_xattn_D_skip': _L1_xattn_in['D_skip'], 'L1_xattn_mod_gate': _L1_xattn_in['mod_gate'], 'L1_ffn_Wp1': _L1_ffn_in['Wp1'], 'L1_ffn_bp1': _L1_ffn_in['bp1'], 'L1_ffn_Wp2': _L1_ffn_in['Wp2'], 'L1_ffn_bp2': _L1_ffn_in['bp2'], 'L1_ffn_W1': _L1_ffn_in['W1'], 'L1_ffn_b1': _L1_ffn_in['b1'], 'L1_ffn_W2': _L1_ffn_in['W2'], 'L1_ffn_b2': _L1_ffn_in['b2'], 'L1_ffn_Wo': _L1_ffn_in['Wo'], 'L1_ffn_bo': _L1_ffn_in['bo'], 'L2_xattn_w_q': _L2_xattn_in['w_q'], 'L2_xattn_w_k': _L2_xattn_in['w_k'], 'L2_xattn_w_v': _L2_xattn_in['w_v'], 'L2_xattn_w_out': _L2_xattn_in['w_out'], 'L2_xattn_b_out': _L2_xattn_in['b_out'], 'L2_ffn_Wr': _L2_ffn_in['Wr'], 'L2_ffn_br': _L2_ffn_in['br'], 'L2_ffn_W1': _L2_ffn_in['W1'], 'L2_ffn_b1': _L2_ffn_in['b1'], 'L2_ffn_W2': _L2_ffn_in['W2'], 'L2_ffn_b2': _L2_ffn_in['b2'], 'L3_xattn_Wq': _L3_xattn_in['Wq'], 'L3_xattn_bq': _L3_xattn_in['bq'], 'L3_xattn_Wk': _L3_xattn_in['Wk'], 'L3_xattn_bk': _L3_xattn_in['bk'], 'L3_xattn_Wv': _L3_xattn_in['Wv'], 'L3_xattn_bv': _L3_xattn_in['bv'], 'L3_xattn_W1': _L3_xattn_in['W1'], 'L3_xattn_b1': _L3_xattn_in['b1'], 'L3_xattn_W2': _L3_xattn_in['W2'], 'L3_xattn_b2': _L3_xattn_in['b2'], 'L3_ffn_gate_w': _L3_ffn_in['gate_w'], 'L3_ffn_gate_b': _L3_ffn_in['gate_b'], 'L3_ffn_ew1': _L3_ffn_in['ew1'], 'L3_ffn_ew3': _L3_ffn_in['ew3'], 'L3_ffn_ew2': _L3_ffn_in['ew2'], 'L3_ffn_sw1': _L3_ffn_in['sw1'], 'L3_ffn_sw3': _L3_ffn_in['sw3'], 'L3_ffn_sw2': _L3_ffn_in['sw2']}

def reference(x, ctx_768, mask_BxS_bf1, mask_BxS2_bf1, L0_xattn_Wq, L0_xattn_Wk, L0_xattn_Wv, L0_xattn_Wo, L0_xattn_bo, L0_ffn_gate_w, L0_ffn_w1, L0_ffn_b1, L0_ffn_w2, L0_ffn_b2, L1_xattn_Wq, L1_xattn_Wk, L1_xattn_Wv, L1_xattn_W_film_in, L1_xattn_b_film_in, L1_xattn_W_film_out, L1_xattn_b_film_out, L1_xattn_g_norm_in, L1_xattn_b_norm_in, L1_xattn_g_norm_out, L1_xattn_b_norm_out, L1_xattn_g_ffn, L1_xattn_b_ffn, L1_xattn_W1, L1_xattn_b1, L1_xattn_W2, L1_xattn_b2, L1_xattn_log_dt, L1_xattn_A_re, L1_xattn_A_im, L1_xattn_C_re, L1_xattn_C_im, L1_xattn_D_skip, L1_xattn_mod_gate, L1_ffn_Wp1, L1_ffn_bp1, L1_ffn_Wp2, L1_ffn_bp2, L1_ffn_W1, L1_ffn_b1, L1_ffn_W2, L1_ffn_b2, L1_ffn_Wo, L1_ffn_bo, L2_xattn_w_q, L2_xattn_w_k, L2_xattn_w_v, L2_xattn_w_out, L2_xattn_b_out, L2_ffn_Wr, L2_ffn_br, L2_ffn_W1, L2_ffn_b1, L2_ffn_W2, L2_ffn_b2, L3_xattn_Wq, L3_xattn_bq, L3_xattn_Wk, L3_xattn_bk, L3_xattn_Wv, L3_xattn_bv, L3_xattn_W1, L3_xattn_b1, L3_xattn_W2, L3_xattn_b2, L3_ffn_gate_w, L3_ffn_gate_b, L3_ffn_ew1, L3_ffn_ew3, L3_ffn_ew2, L3_ffn_sw1, L3_ffn_sw3, L3_ffn_sw2):
    import jax
    import jax.numpy as jnp

    def _L0_xattn_ref(x, context, Wq, Wk, Wv, Wo, bo):
        import jax, jax.numpy as jnp
        import numpy as np
        HEADS = 16
        DIM_HEAD = 64
        b, n, _ = x.shape
        h, d = (HEADS, DIM_HEAD)
        scale = d ** (-0.5)
        q = (x @ Wq).reshape(b, n, h, d).transpose(0, 2, 1, 3)
        k = (context @ Wk).reshape(b, -1, h, d).transpose(0, 2, 1, 3)
        v = (context @ Wv).reshape(b, -1, h, d).transpose(0, 2, 1, 3)
        sim = jnp.einsum('bhid,bhjd->bhij', q, k) * scale
        attn = jax.nn.softmax(sim, axis=-1)
        out = jnp.einsum('bhij,bhjd->bhid', attn, v)
        out = out.transpose(0, 2, 1, 3).reshape(b, n, h * d)
        return out @ Wo + bo

    def _L0_ffn_ref(h, gate_w, w1, b1, w2, b2):
        import jax, jax.numpy as jnp
        import numpy as np
        B, S, D, E, F = (2, 256, 256, 14, 512)
        Bb, Ss, Dd = h.shape
        x = h.reshape(Bb * Ss, Dd)
        logits = x @ gate_w.T
        probs = jax.nn.softmax(logits, axis=-1)
        top2_p, top2_i = jax.lax.top_k(probs, 2)
        w = top2_p / jnp.maximum(top2_p.sum(-1, keepdims=True), 1e-10)
        hh = jnp.einsum('nd,edf->nef', x, w1) + b1
        hh = jax.nn.gelu(hh, approximate=False)
        all_out = jnp.einsum('nef,efd->ned', hh, w2) + b2
        n = jnp.arange(x.shape[0])
        out0 = all_out[n, top2_i[:, 0]]
        out1 = all_out[n, top2_i[:, 1]]
        moe_out = w[:, 0:1] * out0 + w[:, 1:2] * out1
        result = jnp.clip(x + moe_out, -100.0, 100.0).reshape(Bb, Ss, Dd)
        return result

    def _L1_xattn_ref(x_text, x_vision, text_mask, vision_mask, Wq, Wk, Wv, W_film_in, b_film_in, W_film_out, b_film_out, g_norm_in, b_norm_in, g_norm_out, b_norm_out, g_ffn, b_ffn, W1, b1, W2, b2, log_dt, A_re, A_im, C_re, C_im, D_skip, mod_gate):
        import jax, jax.numpy as jnp
        import numpy as np
        B, T, DT, G, DV = (16, 128, 256, 144, 192)
        H, DH = (4, 32)
        INNER = H * DH
        HID = 4 * DT
        N_STATE = 64
        K_TOP = 32

        def layernorm(x, g, b, eps=1e-05):
            m = x.mean(-1, keepdims=True)
            v = x.var(-1, keepdims=True)
            return (x - m) * jax.lax.rsqrt(v + eps) * g + b

        def s4d(x, log_dt, A_re, A_im, C_re, C_im, D_skip):
            Bb, L, D = x.shape
            dt = jnp.exp(log_dt)
            A = A_re + 1j * A_im
            C = C_re + 1j * C_im
            dtA = dt[:, None] * A
            dC = C * (jnp.exp(dtA) - 1.0) / A
            powers = jnp.exp(dtA[:, :, None] * jnp.arange(L))
            K = 2.0 * jnp.einsum('dn,dnl->dl', dC, powers).real
            n = 2 * L
            Kf = jnp.fft.rfft(K, n=n, axis=-1)
            xf = jnp.fft.rfft(x, n=n, axis=1)
            y = jnp.fft.irfft(xf * Kf.T[None], n=n, axis=1)[:, :L]
            return y + x * D_skip
        Bb, Tt, D = x_text.shape
        Gg = x_vision.shape[1]
        Q = (x_text @ Wq).reshape(Bb, Tt, H, DH)
        K = (x_vision @ Wk).reshape(Bb, Gg, H, DH)
        scores = jnp.einsum('bthd,bghd->bhtg', Q, K) / np.sqrt(DH).astype(np.float32)
        scores = jnp.where(vision_mask[:, None, None, :], scores, -jnp.inf)
        topv, topi = jax.lax.top_k(scores, K_TOP)
        probs = jax.nn.softmax(topv, axis=-1)
        bi = jnp.arange(Bb)[:, None, None, None]
        hi = jnp.arange(H)[None, :, None, None]
        ti = jnp.arange(Tt)[None, None, :, None]
        attn = jnp.zeros_like(scores).at[bi, hi, ti, topi].set(probs)
        attn_mean = attn.mean(axis=1)
        V = x_vision @ Wv
        c_t = jnp.einsum('btg,bgd->btd', attn_mean, V)
        c_t = c_t * text_mask[..., None]
        x = layernorm(x_text, g_norm_in, b_norm_in)
        scale_in, shift_in = jnp.split(c_t @ W_film_in + b_film_in, 2, axis=-1)
        x = x * (1.0 + mod_gate * scale_in) + mod_gate * shift_in
        y = s4d(x, log_dt, A_re, A_im, C_re, C_im, D_skip)
        scale_out, shift_out = jnp.split(c_t @ W_film_out + b_film_out, 2, axis=-1)
        y = y * (1.0 + mod_gate * scale_out) + mod_gate * shift_out
        xt = x_text + y
        h = layernorm(xt, g_ffn, b_ffn)
        h = jax.nn.gelu(h @ W1 + b1, approximate=False) @ W2 + b2
        xt = xt + h
        return layernorm(xt, g_norm_out, b_norm_out)

    def _L1_ffn_ref(hidden_states, Wp1, bp1, Wp2, bp2, W1, b1, W2, b2, Wo, bo):
        import jax, jax.numpy as jnp
        import numpy as np
        B, S, H = (8, 1024, 256)
        NAV = 128
        E = 8
        F = 2 * H
        last = hidden_states[:, -1, :]
        logits = jax.nn.gelu(last @ Wp1 + bp1, approximate=False) @ Wp2 + bp2
        action_probs = jax.nn.softmax(logits, axis=-1)
        sel = jnp.argmax(action_probs, axis=-1)
        w1 = W1[sel]
        w2 = W2[sel]
        h = jax.nn.gelu(jnp.einsum('bsh,bhf->bsf', hidden_states, w1) + b1[sel][:, None, :], approximate=False)
        reasoned = jnp.einsum('bsf,bfh->bsh', h, w2) + b2[sel][:, None, :]
        out = reasoned @ Wo + bo
        return hidden_states + 0.3 * out

    def _L2_xattn_ref(x, cond, w_q, w_k, w_v, w_out, b_out):
        import jax, jax.numpy as jnp
        import numpy as np
        N_HEADS = 16
        D_HEAD = 64
        B, SQ, _ = x.shape
        SKV = cond.shape[1]
        scale = D_HEAD ** (-0.5)
        q = (x @ w_q).reshape(B, SQ, N_HEADS, D_HEAD)
        k = (cond @ w_k).reshape(B, SKV, N_HEADS, D_HEAD)
        v = (cond @ w_v).reshape(B, SKV, N_HEADS, D_HEAD)
        attn = jnp.einsum('bqhd,bkhd->bhqk', q, k) * scale
        attn = jax.nn.softmax(attn, axis=-1)
        out = jnp.einsum('bhqk,bkhd->bqhd', attn, v).reshape(B, SQ, N_HEADS * D_HEAD)
        return out @ w_out + b_out

    def _L2_ffn_ref(inputs, Wr, br, W1, b1, W2, b2):
        import jax, jax.numpy as jnp
        import numpy as np
        B, T, D = inputs.shape
        E = Wr.shape[1]
        x = inputs.reshape(B * T, D)
        N = x.shape[0]
        C = N // E
        logits = x @ Wr + br
        probs = jax.nn.softmax(logits, axis=-1)
        gate = jnp.max(probs, axis=-1, keepdims=True)
        idx = jnp.argmax(probs, axis=-1)
        mask = jax.nn.one_hot(idx, E, dtype=jnp.float32)
        pos = (jnp.cumsum(mask, axis=0) * mask).astype(jnp.int32)
        mask = mask * (pos < C).astype(jnp.float32)
        mask_flat = jnp.sum(mask, axis=-1, keepdims=True)
        gate = gate * mask_flat
        combine = (gate * mask_flat * jax.nn.one_hot(idx, E, dtype=jnp.float32))[..., None] * jax.nn.one_hot(pos, C, dtype=jnp.float32)
        dispatch = combine
        expert_in = jnp.einsum('nd,nec->ecd', x, dispatch)
        h = jax.nn.relu(jnp.einsum('ecd,edf->ecf', expert_in, W1) + b1[:, None, :])
        eo = jnp.einsum('ecf,efd->ecd', h, W2) + b2[:, None, :]
        out = jnp.einsum('ecd,nec->nd', eo, combine)
        return out.reshape(B, T, D)

    def _L3_xattn_ref(x, y, Wq, bq, Wk, bk, Wv, bv, W1, b1, W2, b2):
        import jax, jax.numpy as jnp
        import numpy as np
        IMAGE_DIM = 256
        TEXT_DIM = 192
        NUM_HEADS = 16
        HEAD_DIM = IMAGE_DIM // NUM_HEADS
        B, N, _ = x.shape
        M = y.shape[1]
        q = (x @ Wq + bq).reshape(B, N, NUM_HEADS, HEAD_DIM)
        k = (y @ Wk + bk).reshape(B, M, NUM_HEADS, HEAD_DIM)
        v = (y @ Wv + bv).reshape(B, M, NUM_HEADS, HEAD_DIM)
        scale = 1.0 / np.sqrt(HEAD_DIM)
        scores = jnp.einsum('bnhd,bmhd->bhnm', q, k) * scale
        attn = jax.nn.softmax(scores, axis=-1)
        out = jnp.einsum('bhnm,bmhd->bnhd', attn, v).reshape(B, N, IMAGE_DIM)
        h = jax.nn.relu(out @ W1 + b1)
        return h @ W2 + b2

    def _L3_ffn_ref(x, gate_w, gate_b, ew1, ew3, ew2, sw1, sw3, sw2):
        import math
        import jax, jax.numpy as jnp
        import numpy as np
        B, T, D, H, E, K, S = (4, 1024, 256, 512, 16, 2, 2)
        ROUTE_SCALE = 1.0

        def _swiglu(x, w1, w3, w2):
            return jax.nn.silu(x @ w1) * (x @ w3) @ w2
        Bx, Tx, Dx = x.shape
        flat = x.reshape(-1, Dx)
        N = flat.shape[0]
        n_experts = gate_w.shape[1]
        logits = flat @ gate_w
        scores = jax.nn.softmax(logits.astype(jnp.float32), -1) + gate_b
        _, topi = jax.lax.top_k(scores, K)
        weights = jnp.take_along_axis(logits, topi, axis=-1) * ROUTE_SCALE
        weights = weights.astype(flat.dtype)
        capacity = math.ceil(N * K / n_experts * 1.25)

        def per_expert(gid, w1, w3, w2):
            match = topi == gid
            assigned = match.any(-1)
            w_tok = jnp.sum(jnp.where(match, weights, 0.0), -1)
            wm = jnp.where(assigned, w_tok, -jnp.inf)
            vals, idx = jax.lax.top_k(wm, capacity)
            valid = assigned[idx]
            xs = flat[idx]
            y = _swiglu(xs, w1, w3, w2) * jnp.where(valid, vals, 0.0)[:, None]
            return (idx, y)
        idxs, ys = jax.vmap(per_expert)(jnp.arange(n_experts), ew1, ew3, ew2)
        out = jnp.zeros_like(flat).at[idxs.reshape(-1)].add(ys.reshape(-1, Dx))
        shared = jax.vmap(lambda w1, w3, w2: _swiglu(flat, w1, w3, w2))(sw1, sw3, sw2)
        out = out + shared.mean(0)
        return out.reshape(Bx, Tx, Dx)
    x = x + _L0_xattn_ref(_layernorm(x, axis=-1), ctx_768, L0_xattn_Wq, L0_xattn_Wk, L0_xattn_Wv, L0_xattn_Wo, L0_xattn_bo)
    x = x + _L0_ffn_ref(_layernorm(x, axis=-1), L0_ffn_gate_w, L0_ffn_w1, L0_ffn_b1, L0_ffn_w2, L0_ffn_b2)
    x = x + _L1_xattn_ref(_layernorm(x, axis=-1), ctx_768, mask_BxS_bf1, mask_BxS2_bf1, L1_xattn_Wq, L1_xattn_Wk, L1_xattn_Wv, L1_xattn_W_film_in, L1_xattn_b_film_in, L1_xattn_W_film_out, L1_xattn_b_film_out, L1_xattn_g_norm_in, L1_xattn_b_norm_in, L1_xattn_g_norm_out, L1_xattn_b_norm_out, L1_xattn_g_ffn, L1_xattn_b_ffn, L1_xattn_W1, L1_xattn_b1, L1_xattn_W2, L1_xattn_b2, L1_xattn_log_dt, L1_xattn_A_re, L1_xattn_A_im, L1_xattn_C_re, L1_xattn_C_im, L1_xattn_D_skip, L1_xattn_mod_gate)
    x = x + _L1_ffn_ref(_layernorm(x, axis=-1), L1_ffn_Wp1, L1_ffn_bp1, L1_ffn_Wp2, L1_ffn_bp2, L1_ffn_W1, L1_ffn_b1, L1_ffn_W2, L1_ffn_b2, L1_ffn_Wo, L1_ffn_bo)
    x = x + _L2_xattn_ref(_layernorm(x, axis=-1), ctx_768, L2_xattn_w_q, L2_xattn_w_k, L2_xattn_w_v, L2_xattn_w_out, L2_xattn_b_out)
    x = x + _L2_ffn_ref(_layernorm(x, axis=-1), L2_ffn_Wr, L2_ffn_br, L2_ffn_W1, L2_ffn_b1, L2_ffn_W2, L2_ffn_b2)
    x = x + _L3_xattn_ref(_layernorm(x, axis=-1), ctx_768, L3_xattn_Wq, L3_xattn_bq, L3_xattn_Wk, L3_xattn_bk, L3_xattn_Wv, L3_xattn_bv, L3_xattn_W1, L3_xattn_b1, L3_xattn_W2, L3_xattn_b2)
    x = x + _L3_ffn_ref(_layernorm(x, axis=-1), L3_ffn_gate_w, L3_ffn_gate_b, L3_ffn_ew1, L3_ffn_ew3, L3_ffn_ew2, L3_ffn_sw1, L3_ffn_sw3, L3_ffn_sw2)
    return x

_drawn_inputs = setup_inputs


def setup_inputs(seed=0):
    import zlib

    import numpy as np

    out = dict(_drawn_inputs(seed))
    spreads = {'L0_ffn_b1': (0.0, 0.394),
     'L0_ffn_b2': (0.0, 0.1),
     'L1_xattn_b_film_in': (0.0, 0.351),
     'L1_xattn_b_film_out': (0.0, 0.519),
     'L1_xattn_g_norm_in': (1.0, 0.2),
     'L1_xattn_b_norm_in': (0.0, 0.1),
     'L1_xattn_g_norm_out': (1.0, 0.2),
     'L1_xattn_b_norm_out': (0.0, 0.1),
     'L1_xattn_g_ffn': (1.0, 0.6),
     'L1_xattn_b_ffn': (0.0, 0.8),
     'L1_xattn_b1': (0.0, 0.8),
     'L1_xattn_b2': (0.0, 0.487),
     'L1_xattn_A_re': (-0.5, 0.2),
     'L1_ffn_bp1': (0.0, 0.1),
     'L1_ffn_bp2': (0.0, 0.1),
     'L1_ffn_b1': (0.0, 0.8),
     'L1_ffn_b2': (0.0, 0.8),
     'L1_ffn_bo': (0.0, 0.8),
     'L2_xattn_b_out': (0.0, 0.306),
     'L2_ffn_br': (0.0, 0.8),
     'L2_ffn_b1': (0.0, 0.8),
     'L2_ffn_b2': (0.0, 0.8),
     'L3_ffn_gate_b': (0.0, 0.8)}
    factors = {'L1_xattn_Wq': 8.0,
     'L1_xattn_Wk': 8.0,
     'L1_xattn_Wv': 4.576,
     'L1_xattn_W_film_in': 5.621,
     'L1_xattn_W_film_out': 8.0,
     'L1_xattn_W1': 3.145,
     'L1_xattn_W2': 2.893,
     'L2_ffn_Wr': 8.0,
     'L2_ffn_W1': 8.0,
     'L2_ffn_W2': 8.0,
     'L3_xattn_bq': 8.0,
     'L3_xattn_bk': 8.0,
     'L3_xattn_bv': 4.887,
     'L3_xattn_b1': 5.466,
     'L3_xattn_b2': 5.315,
     'L3_ffn_gate_w': 8.0,
     'L3_ffn_ew1': 8.0,
     'L3_ffn_ew3': 8.0,
     'L3_ffn_ew2': 8.0,
     'L3_ffn_sw1': 8.0,
     'L3_ffn_sw3': 8.0,
     'L3_ffn_sw2': 8.0}
    for name, (base, spread) in spreads.items():
        noise = np.random.default_rng([zlib.crc32(name.encode()), seed]).standard_normal(out[name].shape)
        drawn = base * np.exp(spread * noise) if base else spread * noise
        out[name] = jnp.asarray(drawn.astype(out[name].dtype))
    for name, factor in factors.items():
        out[name] = (out[name] * factor).astype(out[name].dtype)
    return out
```

```python
from contextlib import ExitStack

import numpy as np

import concourse.bass as bass
from concourse import mybir

F32 = mybir.dt.float32
U32 = mybir.dt.uint32
U8 = mybir.dt.uint8
ALU = mybir.AluOpType
ACT = mybir.ActivationFunctionType
AX = mybir.AxisListType

P = 128
B, SEQ, D = 2, 1024, 256
NT = B * SEQ // P
TPB = NT // B
KD = D // P
J, DC = 77, 192
KC = DC // 2
BJ = B * J
CH = 512
NCH = B * SEQ // CH
TPC = CH // P
LN_EPS = 1e-5


class Signal:

    def __init__(self, handle):
        self.handle, self.base = handle, 0

    def at(self, n):
        return n + self.base


class Chain:

    def __init__(self, eng, signal, start=0):
        self.eng, self.counted, self.count = eng, signal, start

    def __call__(self, instruction):
        self.count = self.count + 1
        instruction.then_inc(self.counted.handle, 1)
        self.eng.wait_ge(self.counted.handle, self.counted.at(self.count))


class Core:

    def __init__(self, nc, ctx):
        self.nc, self.ctx = nc, ctx
        self.semaphores, self.names = {}, {}

    def sig(self, name):
        if name not in self.semaphores:
            self.semaphores[name] = Signal(self.ctx.enter_context(self.nc.semaphore(name)))
        return self.semaphores[name]

    def unique(self, name):
        self.names[name] = self.names.get(name, 0) + 1
        return f"{name}_{self.names[name]}"

    def sb(self, ctx, name, shape, dt=F32):
        return ctx.enter_context(self.nc.sbuf_tensor(self.unique(name), shape, dt))

    def ps(self, ctx, name, shape, dt=F32):
        return ctx.enter_context(self.nc.psum_tensor(self.unique(name), shape, dt))


def row(v, n):
    return v.rearrange("(o n) -> o n", o=1).to_broadcast([n, v.shape[0]])


def column(v):
    return v.rearrange("(t p) -> p t", p=P)


def bc(ap, shape):
    return ap.to_broadcast(shape)


def setup(c, x, ctx_in, mask_tok, mask_ctx):
    nc = c.nc
    c.x = c.sb(c.ctx, "x", [P, NT, D])
    c.xn = c.sb(c.ctx, "xn", [P, NT, D])
    c.ident = c.sb(c.ctx, "ident", [P, P])
    c.ones = c.sb(c.ctx, "ones", [1, P])
    c.ctxT = c.sb(c.ctx, "ctxT", [KC, 2, BJ])
    c.rstd = c.sb(c.ctx, "rstd", [P, NT])
    c.nmr = c.sb(c.ctx, "nmr", [P, NT])
    loaded, ident_ready = c.sig("setup_loaded"), c.sig("ident_ready")
    transposed, copied = c.sig("setup_transposed"), c.sig("setup_copied")
    with ExitStack() as st:
        ctx_rows = c.sb(st, "ctx_rows", [J, B, DC])
        psT = c.ps(st, "setup_psT", [KC, 4 * J])
        block = st.enter_context(nc.Block())

        @block.sync
        def _(sp):
            sp.dma_start(ctx_rows[:, :, :], ctx_in.rearrange("b j d -> j b d")).then_inc(loaded.handle, 16)
            sp.dma_start(c.x[:, :, :], x.rearrange("b (t p) d -> p (b t) d", p=P)).then_inc(loaded.handle, 16)
            sp.wait_ge(loaded.handle, 32)

        @block.gpsimd
        def _(pool):
            nc.gpsimd.memset(c.ident[:, :], 0.0).then_inc(ident_ready.handle, 1)
            pool.wait_ge(ident_ready.handle, 1)
            nc.gpsimd.affine_select(out=c.ident[:, :], in_=c.ident[:, :], compare_op=ALU.not_equal, fill=1.0,
                                    base=0, pattern=[[-1, P]], channel_multiplier=1).then_inc(ident_ready.handle, 1)
            nc.gpsimd.memset(c.ones[:, :], 1.0).then_inc(ident_ready.handle, 1)

        @block.tensor
        def _(pe):
            pe.wait_ge(ident_ready.handle, 3)
            pe.wait_ge(loaded.handle, 16)
            pe.wait_ge(loaded.handle, 32)
            for b in range(B):
                for k in range(2):
                    last = nc.tensor.transpose(psT[:, (k * B + b) * J:(k * B + b + 1) * J],
                                               ctx_rows[:, b, k * KC:(k + 1) * KC], c.ident[0:J, 0:J])
            last.then_inc(transposed.handle, 1)

        @block.vector
        def _(dve):
            dve.wait_ge(transposed.handle, 1)
            nc.vector.tensor_copy(c.ctxT[:, :, :], psT[:, :].rearrange("p (k n) -> p k n", k=2)).then_inc(copied.handle, 1)
            dve.wait_ge(copied.handle, 1)


def ln_stats(c, src):
    nc = c.nc
    stats_done, var_ready, std_ready, step = c.sig("ln_stats"), c.sig("ln_var"), c.sig("ln_std"), c.sig("ln_step")
    with ExitStack() as st:
        bn = c.sb(st, "ln_bn", [P, NT, 6])
        msum = c.sb(st, "ln_msum", [P, NT])
        diff = c.sb(st, "ln_diff", [P, NT])
        var = c.sb(st, "ln_var", [P, NT])
        std = c.sb(st, "ln_std", [P, NT])
        tmp = c.sb(st, "ln_tmp", [P, NT])
        block = st.enter_context(nc.Block())

        @block.vector
        def _(dve):
            with dve.Fori(0, NT) as t:
                nc.vector.bn_stats(bn[:, t, :], src[:, t, :]).then_inc(stats_done.handle, 1)
            dve.wait_ge(stats_done.handle, stats_done.at(NT))
            link = Chain(dve, step)
            nc.vector.tensor_tensor(msum[:, :], bn[:, :, 1], bn[:, :, 4], ALU.add).then_inc(stats_done.handle, 1)
            link(nc.vector.tensor_tensor(diff[:, :], bn[:, :, 1], bn[:, :, 4], ALU.subtract))
            nc.vector.tensor_tensor(var[:, :], bn[:, :, 2], bn[:, :, 5], ALU.add).then_inc(stats_done.handle, 1)
            link(nc.vector.tensor_tensor(diff[:, :], diff[:, :], diff[:, :], ALU.mult))
            dve.wait_ge(stats_done.handle, stats_done.at(NT + 2))
            link(nc.vector.tensor_scalar(var[:, :], var[:, :], 1.0 / D, LN_EPS, ALU.mult, ALU.add))
            nc.vector.scalar_tensor_tensor(var[:, :], diff[:, :], 0.25, var[:, :], ALU.mult, ALU.add)\
                .then_inc(var_ready.handle, 1)
            dve.wait_ge(std_ready.handle, std_ready.at(1))
            link(nc.vector.reciprocal(c.rstd[:, :], std[:, :]))
            link(nc.vector.tensor_tensor(tmp[:, :], c.rstd[:, :], c.rstd[:, :], ALU.mult))
            link(nc.vector.tensor_tensor(tmp[:, :], tmp[:, :], var[:, :], ALU.mult))
            link(nc.vector.tensor_scalar(tmp[:, :], tmp[:, :], -0.5, 1.5, ALU.mult, ALU.add))
            link(nc.vector.tensor_tensor(c.rstd[:, :], c.rstd[:, :], tmp[:, :], ALU.mult))
            link(nc.vector.scalar_tensor_tensor(c.nmr[:, :], msum[:, :], -0.5, c.rstd[:, :], ALU.mult, ALU.mult))

        @block.scalar
        def _(act):
            act.wait_ge(var_ready.handle, var_ready.at(1))
            nc.scalar.activation(std[:, :], var[:, :], ACT.Sqrt).then_inc(std_ready.handle, 1)
    stats_done.base += NT + 2
    var_ready.base += 1
    std_ready.base += 1
    step.base += 9


HEADS = 16
HJ = HEADS * J
HJC = (HJ + P - 1) // P
INNER = 1024
NI = INNER // P
SCORE_CUTS = [(0, 512), (512, 1024), (1024, HJ)]


def wide_attention(c, wq, wk, wv, wo, bo, scratch):
    nc = c.nc
    with ExitStack() as st:
        M = c.sb(st, "att_M", [P, KD, B, HJ])
        N = c.sb(st, "att_N", [P, B, HJC, D])
        wide_fold(c, wq, wk, wv, wo, scratch, M, N)
        attention(c, M, None, N, bo, None)


def wide_fold(c, wq, wk, wv, wo, scratch, M, N):
    nc = c.nc
    loaded, filled, mm, ev = c.sig("fold_loaded"), c.sig("fold_filled"), c.sig("fold_mm"), c.sig("fold_ev")
    stored = c.sig("fold_stored")
    TRIPLES = [range(g + odd, min(g + 6, HEADS), 2) for g in range(0, HEADS, 6) for odd in range(2)]
    PAIRS = [range(g + odd, g + 4, 2) for g in range(0, HEADS, 4) for odd in range(2)]
    with ExitStack() as st:
        Wq = c.sb(st, "fold_Wq", [P, KD, INNER])
        Wk = c.sb(st, "fold_Wk", [KC, 2, INNER])
        Wv = c.sb(st, "fold_Wv", [KC, 2, INNER])
        Wo = c.sb(st, "fold_Wo", [P, NI, D])
        KT = c.sb(st, "fold_KT", [P, NI, BJ])
        VT = c.sb(st, "fold_VT", [P, NI, BJ])
        WqT = c.sb(st, "fold_WqT", [P, NI, D])
        rows = c.sb(st, "fold_rows", [J, HEADS, D])
        ps = c.ps(st, "fold_ps", [P, 4, 512])
        block = st.enter_context(nc.Block())
        steps = [("K", m) for m in range(NI)] + [("V", m) for m in range(NI)] + [("Q", m) for m in range(0, NI, 2)]
        steps += [("M", (k, g)) for k in range(KD) for g in TRIPLES]
        steps += [("N", (b, g)) for b in range(B) for g in PAIRS]
        n_kvq = 2 * NI + NI // 2
        n_m = KD * len(TRIPLES)
        n_nb = HEADS // 2

        @block.sync
        def _(sp):
            sp.dma_start(Wk[:, :, :], wk.rearrange("(k p) n -> p k n", p=KC)).then_inc(loaded.handle, 16)
            sp.dma_start(Wv[:, :, :], wv.rearrange("(k p) n -> p k n", p=KC)).then_inc(loaded.handle, 16)
            sp.dma_start(Wq[:, :, :], wq.rearrange("(k p) n -> p k n", p=P)).then_inc(loaded.handle, 16)
            sp.dma_start(Wo[:, :, :], wo.rearrange("(k p) n -> p k n", p=P)).then_inc(loaded.handle, 16)
            for b in range(B):
                sp.wait_ge(ev.handle, ev.at(n_kvq + n_m + (b + 1) * n_nb))
                sp.dma_start(scratch[b, 0:HJ, :].rearrange("(h j) d -> j h d", j=J), rows[:, :, :])\
                    .then_inc(stored.handle, 16)
                sp.wait_ge(stored.handle, stored.at(16 * (3 * b + 1)))
                if b == 0:
                    sp.wait_ge(filled.handle, filled.at(1))
                full = HJ // P
                sp.dma_start(N[:, b, 0:full, :], scratch[b, 0:full * P, :].rearrange("(c p) d -> p c d", p=P))\
                    .then_inc(stored.handle, 16)
                sp.dma_start(N[0:HJ - full * P, b, full, :], scratch[b, full * P:HJ, :]).then_inc(stored.handle, 16)
                sp.wait_ge(stored.handle, stored.at(16 * (3 * b + 3)))

        @block.gpsimd
        def _(pool):
            nc.gpsimd.memset(N[:, :, HJC - 1, :], 0.0).then_inc(filled.handle, 1)

        @block.tensor
        def _(pe):
            pe.wait_ge(loaded.handle, loaded.at(64))
            for n, (kind, at) in enumerate(steps):
                bank = ps[:, n % 4, :]
                if n >= 4:
                    pe.wait_ge(ev.handle, ev.at(n - 3))
                if n == n_kvq:
                    pe.wait_ge(ev.handle, ev.at(n_kvq))
                if kind in "KV":
                    W = Wk if kind == "K" else Wv
                    for k in range(2):
                        last = nc.tensor.matmul(bank[:, 0:BJ], W[:, k, at * P:(at + 1) * P], c.ctxT[:, k, :],
                                                start=(k == 0), stop=(k == 1))
                elif kind == "Q":
                    for m in (at, at + 1):
                        for k in range(KD):
                            o = (m - at) * D + k * P
                            last = nc.tensor.transpose(bank[:, o:o + P], Wq[:, k, m * P:(m + 1) * P], c.ident[:, :])
                elif kind == "M":
                    k, g = at
                    for i, h in enumerate(g):
                        o = 64 * (h % 2)
                        last = nc.tensor.matmul(bank[:, i * BJ:(i + 1) * BJ], WqT[o:o + 64, h // 2, k * P:(k + 1) * P],
                                                KT[o:o + 64, h // 2, :], start=True, stop=True)
                else:
                    b, g = at
                    for i, h in enumerate(g):
                        o = 64 * (h % 2)
                        last = nc.tensor.matmul(bank[0:J, i * D:(i + 1) * D],
                                                VT[o:o + 64, h // 2, b * J:(b + 1) * J], Wo[o:o + 64, h // 2, :],
                                                start=True, stop=True)
                last.then_inc(mm.handle, 1)

        @block.vector
        def _(dve):
            for n, (kind, at) in enumerate(steps):
                bank = ps[:, n % 4, :]
                dve.wait_ge(mm.handle, mm.at(n + 1))
                if kind == "K":
                    last = nc.vector.tensor_scalar(KT[:, at, :], bank[:, 0:BJ], 64 ** -0.5, None, ALU.mult)
                elif kind == "V":
                    last = nc.vector.tensor_copy(VT[:, at, :], bank[:, 0:BJ])
                elif kind == "Q":
                    last = nc.vector.tensor_copy(WqT[:, at:at + 2, :], bank[:, :].rearrange("p (m d) -> p m d", m=2))
                elif kind == "M":
                    k, g = at
                    last = nc.vector.tensor_copy(
                        M[:, k, :, :].rearrange("p b (h j) -> p h b j", j=J)[:, g[0]:g[-1] + 1:2, :, :],
                        bank[:, 0:len(g) * BJ].rearrange("p (h b j) -> p h b j", h=len(g), b=B))
                else:
                    b, g = at
                    if b == 1 and g[0] == 0:
                        dve.wait_ge(stored.handle, stored.at(16))
                    last = nc.vector.tensor_copy(rows[:, g[0]:g[-1] + 1:2, :],
                                                 bank[0:J, :].rearrange("p (h d) -> p h d", h=2))
                last.then_inc(ev.handle, 1)
    loaded.base += 64
    filled.base += 1
    mm.base += len(steps)
    ev.base += len(steps)
    stored.base += 96


def attention(c, M, score_bias, N, bo, oT):
    nc = c.nc
    names = "norm xT_mm xT_ev scores shifted exped probs x_bo PT_mm PT_ev out_mm out_ev".split()
    s = {n: c.sig("att_" + n) for n in names}
    step = c.sig("att_step")
    loaded, bo_loaded = c.sig("att_padded"), c.sig("att_bo_loaded")
    with ExitStack() as st:
        xn = c.sb(st, "att_xn", [P, 2, D])
        xT = c.sb(st, "att_xT", [P, 2, KD, P])
        pr = c.sb(st, "att_probs", [P, 2, HJC * P])
        PT = c.sb(st, "att_PT", [P, 2, HJC, P])
        mx = c.sb(st, "att_mx", [P, 2, HEADS])
        rs = c.sb(st, "att_rs", [P, 2, HEADS])
        bo_row = c.sb(st, "att_bo", [P, D])
        ps_xT = c.ps(st, "att_ps_xT", [P, 512])
        ps_S = c.ps(st, "att_ps_S", [P, 3 * 512])
        ps_PT = c.ps(st, "att_ps_PT", [P, 3 * 512])
        ps_O = c.ps(st, "att_ps_O", [P, 512])
        pad = HJC * P - HJ
        block = st.enter_context(nc.Block())

        def heads(ap):
            return ap.rearrange("p (h j) -> p h j", j=J)

        if bo is not None:
            @block.sync
            def _(sp):
                sp.dma_start(bo_row[:, :], row(bo, P)).then_inc(bo_loaded.handle, 16)

        @block.tensor
        def _(pe):
            def front(n, j, b):
                pe.wait_ge(s["norm"].handle, s["norm"].at(n + 1))
                for k in range(KD):
                    last = nc.tensor.transpose(ps_xT[:, k * P:(k + 1) * P], xn[:, j, k * P:(k + 1) * P], c.ident[:, :])
                last.then_inc(s["xT_mm"].handle, 1)
                pe.wait_ge(s["xT_ev"].handle, s["xT_ev"].at(n + 1))
                pe.wait_ge(s["shifted"].handle, s["shifted"].at(n + 1))
                for lo, hi in SCORE_CUTS:
                    for k in range(KD):
                        last = nc.tensor.matmul(ps_S[:, lo:hi], xT[:, j, k, :], M[:, k, b, lo:hi], start=(k == 0),
                                                stop=(k == KD - 1 and score_bias is None))
                    if score_bias is not None:
                        last = nc.tensor.matmul(ps_S[:, lo:hi], c.ones[0:1, :], score_bias[0:1, b, lo:hi],
                                                start=False, stop=True)
                last.then_inc(s["scores"].handle, 1)

            def back(n, j, b):
                pe.wait_ge(s["probs"].handle, s["probs"].at(n + 1))
                for k in range(HJC):
                    last = nc.tensor.transpose(ps_PT[:, k * P:(k + 1) * P], pr[:, j, k * P:(k + 1) * P], c.ident[:, :])
                last.then_inc(s["PT_mm"].handle, 1)
                pe.wait_ge(s["PT_ev"].handle, s["PT_ev"].at(n + 1))
                pe.wait_ge(s["out_ev"].handle, s["out_ev"].at(n + 1))
                if oT is None:
                    for k in range(HJC):
                        last = nc.tensor.matmul(ps_O[:, 0:D], PT[:, j, k, :], N[:, b, k, :],
                                                start=(k == 0), stop=(k == HJC - 1))
                else:
                    for half in range(KD):
                        ks = range(half * HJ // 2 // P, ((half + 1) * HJ // 2 + P - 1) // P)
                        for k in ks:
                            last = nc.tensor.matmul(ps_O[:, half * P:(half + 1) * P],
                                                    N[:, b, k, half * P:(half + 1) * P], PT[:, j, k, :],
                                                    start=(k == ks[0]), stop=(k == ks[-1]))
                last.then_inc(s["out_mm"].handle, 1)

            pe.wait_ge(loaded.handle, loaded.at(1))
            front(0, 0, 0)
            for b in range(B):
                with pe.Fori(0, TPB // 2 - 1) as i:
                    for j in range(2):
                        front(i * 2 + (b * TPB + j + 1), 1 - j, b)
                        back(i * 2 + (b * TPB + j), j, b)
                front(b * TPB + TPB - 1, 1, b)
                back(b * TPB + TPB - 2, 0, b)
                if b + 1 < B:
                    front(b * TPB + TPB, 0, b + 1)
                back(b * TPB + TPB - 1, 1, b)

        @block.vector
        def _(dve):
            link = Chain(dve, step)

            def norm(n, j):
                nc.vector.tensor_scalar(xn[:, j, :], c.x[:, n, :], c.rstd[:, bass.ts(n, 1)], c.nmr[:, bass.ts(n, 1)],
                                        ALU.mult, ALU.add).then_inc(s["norm"].handle, 1)

            def softmax(n, j, ahead):
                dve.wait_ge(s["scores"].handle, s["scores"].at(n + 1))
                link(nc.vector.tensor_reduce(mx[:, j, :], heads(ps_S[:, 0:HJ]), AX.X, ALU.max))
                nc.vector.tensor_tensor(heads(pr[:, j, 0:HJ]), heads(ps_S[:, 0:HJ]),
                                        bc(mx[:, j, :].unsqueeze(2), [P, HEADS, J]), ALU.subtract)\
                    .then_inc(s["shifted"].handle, 1)
                if ahead:
                    norm(n + 2, j)
                dve.wait_ge(s["exped"].handle, s["exped"].at(n + 1))
                link(nc.vector.tensor_reduce(rs[:, j, :], heads(pr[:, j, 0:HJ]), AX.X, ALU.add))
                link(nc.vector.reciprocal(rs[:, j, :], rs[:, j, :]))
                nc.vector.tensor_tensor(heads(pr[:, j, 0:HJ]), heads(pr[:, j, 0:HJ]),
                                        bc(rs[:, j, :].unsqueeze(2), [P, HEADS, J]), ALU.mult)\
                    .then_inc(s["probs"].handle, 1)

            def take(n):
                dve.wait_ge(s["out_mm"].handle, s["out_mm"].at(n + 1))
                if oT is None:
                    dve.wait_ge(s["x_bo"].handle, s["x_bo"].at(n + 1))
                    nc.vector.tensor_tensor(c.x[:, n, :], c.x[:, n, :], ps_O[:, 0:D], ALU.add)\
                        .then_inc(s["out_ev"].handle, 1)
                else:
                    nc.vector.tensor_copy(oT[:, :, bass.ts(n, P)], ps_O[:, 0:D].rearrange("p (k n) -> p k n", k=KD))\
                        .then_inc(s["out_ev"].handle, 1)

            dve.sem_inc(s["shifted"].handle, 1)
            dve.sem_inc(s["out_ev"].handle, 1)
            norm(0, 0)
            norm(1, 1)
            softmax(0, 0, True)
            last_rolled = NT - 4
            with dve.Fori(0, last_rolled // 2) as i:
                link.count = i * 6 + 3
                for j in (1, 0):
                    n = i * 2 + (2 - j)
                    softmax(n, j, True)
                    take(n - 1)
            link.count = 3 + 3 * last_rolled
            for n in range(last_rolled + 1, NT):
                softmax(n, n % 2, n + 2 < NT)
                take(n - 1)
            take(NT - 1)
            dve.wait_ge(s["out_ev"].handle, s["out_ev"].at(NT + 1))

        if bo is not None:
            @block.gpsimd
            def _(pool):
                nc.gpsimd.memset(pr[:, :, HJ:], 0.0).then_inc(loaded.handle, 1)
                pool.wait_ge(bo_loaded.handle, bo_loaded.at(16))
                with pool.Fori(0, NT) as n:
                    pool.wait_ge(s["norm"].handle, s["norm"].at(n + 1))
                    nc.gpsimd.tensor_tensor(c.x[:, n, :], c.x[:, n, :], bo_row[:, :], ALU.add)\
                        .then_inc(s["x_bo"].handle, 1)
        else:
            @block.gpsimd
            def _(pool):
                nc.gpsimd.memset(pr[:, :, HJ:], 0.0).then_inc(loaded.handle, 1)

        @block.scalar
        def _(act):
            def copy_xT(n, j):
                act.wait_ge(s["xT_mm"].handle, s["xT_mm"].at(n + 1))
                nc.scalar.copy(xT[:, j, :, :], ps_xT[:, 0:D].rearrange("p (k n) -> p k n", k=KD))\
                    .then_inc(s["xT_ev"].handle, 1)

            def exp_and_copy(n, j, ahead):
                act.wait_ge(s["shifted"].handle, s["shifted"].at(n + 2))
                nc.scalar.activation(pr[:, j, 0:HJ], pr[:, j, 0:HJ], ACT.Exp).then_inc(s["exped"].handle, 1)
                if ahead:
                    copy_xT(n + 1, 1 - j)
                act.wait_ge(s["PT_mm"].handle, s["PT_mm"].at(n + 1))
                nc.scalar.copy(PT[:, j, :, :], ps_PT[:, 0:HJC * P].rearrange("p (k n) -> p k n", k=HJC))\
                    .then_inc(s["PT_ev"].handle, 1)

            copy_xT(0, 0)
            with act.Fori(0, NT // 2 - 1) as i:
                for j in range(2):
                    exp_and_copy(i * 2 + j, j, True)
            exp_and_copy(NT - 2, 0, True)
            exp_and_copy(NT - 1, 1, False)
    for name, one in s.items():
        one.base += NT
    if bo is None:
        s["x_bo"].base -= NT
    s["shifted"].base += 1
    s["out_ev"].base += 1
    step.base += 3 * NT
    loaded.base += 1
    bo_loaded.base += 16 if bo is not None else 0


def ring(eng, signal, n):
    eng.sem_inc(signal.handle, n)


def normalise(c, src, xn_out=None, xT_out=None, affine=None, router=None, resident=None):
    nc = c.nc
    names = "loaded rows T_mm T_ev L_mm L_ev step".split()
    s = {n: c.sig("norm_" + n) for n in names}
    with ExitStack() as st:
        xb = c.sb(st, "norm_xb", [P, 2, D])
        xTb = c.sb(st, "norm_xTb", [P, 2, KD, P])
        gb = c.sb(st, "norm_gb", [P, 2, D])
        ps_T = c.ps(st, "norm_ps_T", [P, 2, 512])
        ps_L = c.ps(st, "norm_ps_L", [P, 2, 512])
        n_loads = 0
        if router is not None:
            w, n_r, logits = router
            wr = c.sb(st, "norm_wr", [P, KD, n_r]) if resident is None else None
        block = st.enter_context(nc.Block())
        transposing = xT_out is not None or router is not None
        per_pair = 4 if affine is not None else 0
        if affine is not None:
            n_loads += 2
        if router is not None and resident is None:
            n_loads += KD

        @block.sync
        def _(sp):
            if affine is not None:
                for i in range(2):
                    sp.dma_start(gb[:, i, :], row(affine[i], P)).then_inc(s["loaded"].handle, 16)
            if router is not None and resident is None:
                for k in range(KD):
                    sp.dma_start(wr[:, k, :], w[k * P:(k + 1) * P, :], allow_slow_non_contiguous=True)\
                        .then_inc(s["loaded"].handle, 16)
            if n_loads:
                sp.wait_ge(s["loaded"].handle, s["loaded"].at(16 * n_loads))

        @block.vector
        def _(dve):
            link = Chain(dve, s["step"])
            if affine is not None:
                dve.wait_ge(s["loaded"].handle, s["loaded"].at(16 * n_loads))

            def tile_pair(i, b):
                link.count = i * per_pair + b * (TPB // 2) * per_pair
                for j in range(2):
                    n = i * 2 + (b * TPB + j)
                    kept = None
                    if xn_out is not None:
                        kept = xn_out(n, b, i * 2 + j) if callable(xn_out) else xn_out[:, n, :]
                    rows = xb[:, j, :]
                    if transposing:
                        dve.wait_ge(s["T_mm"].handle, s["T_mm"].at(n + 1))
                    if affine is not None:
                        link(nc.vector.tensor_scalar(rows, src[:, n, :], c.rstd[:, bass.ts(n, 1)],
                                                     c.nmr[:, bass.ts(n, 1)], ALU.mult, ALU.add))
                        link(nc.vector.tensor_tensor(rows, rows, gb[:, 0, :], ALU.mult))
                        if kept is not None:
                            nc.vector.tensor_tensor(kept, rows, gb[:, 1, :], ALU.add)\
                                .then_inc(s["rows"].handle, 1)
                        if transposing:
                            nc.vector.tensor_tensor(rows, rows, gb[:, 1, :], ALU.add).then_inc(s["rows"].handle, 1)
                    else:
                        for out in ([kept] if kept is not None else []) + ([rows] if transposing else []):
                            nc.vector.tensor_scalar(out, src[:, n, :], c.rstd[:, bass.ts(n, 1)],
                                                    c.nmr[:, bass.ts(n, 1)], ALU.mult, ALU.add)\
                                .then_inc(s["rows"].handle, 1)

            for b in range(B):
                with dve.Fori(0, TPB // 2) as i:
                    tile_pair(i, b)
        per_tile = (1 if xn_out is not None else 0) + (1 if transposing else 0)

        if transposing:
            @block.tensor
            def _(pe):
                ring(pe, s["T_mm"], 2)
                ring(pe, s["L_mm"], 2)
                if router is not None and n_loads:
                    pe.wait_ge(s["loaded"].handle, s["loaded"].at(16 * n_loads))

                def route(n, j, b):
                    pe.wait_ge(s["T_ev"].handle, s["T_ev"].at(n + 3))
                    pe.wait_ge(s["L_ev"].handle, s["L_ev"].at(n + 1))
                    for k in range(KD):
                        right = wr[:, k, :] if resident is None else resident[0][:, k, b, :]
                        last = nc.tensor.matmul(ps_L[:, j, 0:n_r], xTb[:, j, k, :], right,
                                                start=(k == 0), stop=(k == KD - 1 and resident is None))
                    if resident is not None:
                        last = nc.tensor.matmul(ps_L[:, j, 0:n_r], c.ones[0:1, :], resident[1][0:1, b, :],
                                                start=False, stop=True)
                    last.then_inc(s["L_mm"].handle, 1)

                def tile_pair(i, b):
                    for j in range(2):
                        n = i * 2 + (b * TPB + j)
                        pe.wait_ge(s["rows"].handle, s["rows"].at((n + 1) * per_tile))
                        pe.wait_ge(s["T_ev"].handle, s["T_ev"].at(n + 1))
                        for k in range(KD):
                            last = nc.tensor.transpose(ps_T[:, j, k * P:(k + 1) * P], xb[:, j, k * P:(k + 1) * P],
                                                       c.ident[:, :])
                        last.then_inc(s["T_mm"].handle, 1)
                    if router is not None:
                        for j in range(2):
                            route(i * 2 + (b * TPB + j), j, b)

                for b in range(B):
                    with pe.Fori(0, TPB // 2) as i:
                        tile_pair(i, b)

            @block.scalar
            def _(act):
                ring(act, s["T_ev"], 2)
                ring(act, s["L_ev"], 2)
                with act.Fori(0, NT // 2) as i:
                    for j in range(2):
                        n = i * 2 + j
                        act.wait_ge(s["T_mm"].handle, s["T_mm"].at(n + 3))
                        tile = ps_T[:, j, 0:D].rearrange("p (k n) -> p k n", k=KD)
                        if xT_out is not None:
                            one = nc.scalar.copy(xT_out[:, :, bass.ts(n, P)], tile)
                        if router is not None:
                            act.wait_ge(s["L_mm"].handle, s["L_mm"].at(n + 1))
                            one = nc.scalar.copy(xTb[:, j, :, :], tile)
                        one.then_inc(s["T_ev"].handle, 1)
                    if router is not None:
                        for j in range(2):
                            n = i * 2 + j
                            act.wait_ge(s["L_mm"].handle, s["L_mm"].at(n + 3))
                            nc.scalar.copy(logits[:, n, :], ps_L[:, j, 0:n_r]).then_inc(s["L_ev"].handle, 1)
    s["loaded"].base += 16 * n_loads
    s["rows"].base += per_tile * NT
    if transposing:
        for n in ("T_mm", "T_ev"):
            s[n].base += NT + 2
        for n in ("L_mm", "L_ev"):
            s[n].base += 2 + (NT if router is not None else 0)
    if affine is not None:
        s["step"].base += 2 * NT


def each_expert(eng, n_exp, body):
    if n_exp == 1:
        body(0, 0, 1)
        return
    with eng.Fori(0, n_exp // 2) as i:
        for s in range(2):
            body(i * 2 + s, s, i + 1)


def experts(c, xT, n_exp, F, w1, w3, w2, b1, func, gate, acc, chunks=range(NCH), resident=None):
    nc = c.nc
    FT = F // P
    swiglu = w3 is not None
    names = "exp_H_mm exp_sil exp_H_ev exp_O_mm exp_O_ev exp_slot0 exp_slot1".split()
    H_mm, sil_done, H_ev, O_mm, O_ev, *slot = [c.sig(n) for n in names]
    n_w = 0 if resident else 2 + (w3 is not None) + (b1 is not None)
    n_ch = len(chunks)
    per_expert = n_ch * TPC
    n_slots = min(n_exp, 2)
    with ExitStack() as st:
        if resident:
            W1, W2, b1c = resident
        else:
            W1 = c.sb(st, "exp_W1", [P, n_slots, KD, F])
            W2 = c.sb(st, "exp_W2", [P, n_slots, FT, D])
            b1c = c.sb(st, "exp_b1c", [P, n_slots, FT]) if b1 is not None else None
        W3 = c.sb(st, "exp_W3", [P, n_slots, KD, F]) if swiglu else None
        hT = c.sb(st, "exp_hT", [P, 2, FT, CH])
        sil = c.sb(st, "exp_sil", [P, 2, CH]) if swiglu else None
        ps_H = c.ps(st, "exp_ps_H", [P, 2, 2 if swiglu else 1, CH])
        ps_O = c.ps(st, "exp_ps_O", [P, 2, 512])
        block = st.enter_context(nc.Block())

        if not resident:
            @block.sync
            def _(sp):
                def load(e, s, use):
                    if n_exp > 1:
                        sp.wait_ge(O_mm.handle, O_mm.at((e + 1) * per_expert))
                    sp.dma_start(W1[:, s, :, :], w1[e, :, :].rearrange("(k p) f -> p k f", p=P)).then_inc(slot[s].handle, 16)
                    if swiglu:
                        sp.dma_start(W3[:, s, :, :], w3[e, :, :].rearrange("(k p) f -> p k f", p=P))\
                            .then_inc(slot[s].handle, 16)
                    sp.dma_start(W2[:, s, :, :], w2[e, :, :].rearrange("(k p) f -> p k f", p=P)).then_inc(slot[s].handle, 16)
                    if b1 is not None:
                        sp.dma_start(b1c[:, s, :], b1[e, :].rearrange("(f p) -> p f", p=P),
                                     allow_slow_non_contiguous=True).then_inc(slot[s].handle, 16)

                each_expert(sp, n_exp, load)
                for s in range(n_slots):
                    sp.wait_ge(slot[s].handle, slot[s].at(16 * n_w * n_exp // n_slots))

        @block.tensor
        def _(pe):
            ring(pe, O_mm, 2 * per_expert)

            def up(e, s, i):
                g = e * n_ch + i
                at = chunks[i] * CH
                for f in range(FT):
                    pe.wait_ge(H_ev.handle, H_ev.at(g * FT + (f + 1)))
                    for m, W in enumerate([W1, W3] if swiglu else [W1]):
                        for k in range(KD):
                            last = nc.tensor.matmul(ps_H[:, f % 2, m, :], W[:, s, k, f * P:(f + 1) * P],
                                                    xT[:, k, at:at + CH], start=(k == 0), stop=(k == KD - 1))
                    last.then_inc(H_mm.handle, 1)

            def down(e, s, i):
                g = e * n_ch + i
                pe.wait_ge(H_ev.handle, H_ev.at((g + 1) * FT + 2))
                for j in range(TPC):
                    pe.wait_ge(O_ev.handle, O_ev.at(g * TPC + (j + 1)))
                    for f in range(FT):
                        last = nc.tensor.matmul(ps_O[:, j % 2, 0:D], hT[:, i % 2, f, j * P:(j + 1) * P], W2[:, s, f, :],
                                                start=(f == 0), stop=(f == FT - 1))
                    last.then_inc(O_mm.handle, 1)

            def one(e, s, use):
                if n_w:
                    pe.wait_ge(slot[s].handle, slot[s].at(use * (16 * n_w)))
                up(e, s, 0)
                for i in range(1, n_ch):
                    up(e, s, i)
                    down(e, s, i - 1)
                down(e, s, n_ch - 1)

            each_expert(pe, n_exp, one)

        @block.scalar
        def _(act):
            if not swiglu:
                ring(act, H_ev, 2)

            def one(e, s, use):
                if b1 is not None and n_w:
                    act.wait_ge(slot[s].handle, slot[s].at(use * (16 * n_w)))
                for i in range(n_ch):
                    for f in range(FT):
                        act.wait_ge(H_mm.handle, H_mm.at((e * n_ch + i) * FT + (f + 1)))
                        if swiglu:
                            nc.scalar.activation(sil[:, f % 2, :], ps_H[:, f % 2, 0, :], func).then_inc(sil_done.handle, 1)
                        else:
                            nc.scalar.activation(hT[:, i % 2, f, :], ps_H[:, f % 2, 0, :], func, bias=b1c[:, s, f:f + 1])\
                                .then_inc(H_ev.handle, 1)

            each_expert(act, n_exp, one)

        @block.vector
        def _(dve):
            if swiglu:
                ring(dve, H_ev, 2)
            ring(dve, O_ev, 2)

            def product(e, i):
                for f in range(FT):
                    dve.wait_ge(sil_done.handle, sil_done.at((e * n_ch + i) * FT + (f + 1)))
                    nc.vector.tensor_tensor(hT[:, i % 2, f, :], sil[:, f % 2, :], ps_H[:, f % 2, 1, :], ALU.mult)\
                        .then_inc(H_ev.handle, 1)

            def take(e, i):
                for j in range(TPC):
                    t = chunks[i] * TPC + j
                    dve.wait_ge(O_mm.handle, O_mm.at((e * n_ch + i) * TPC + (2 * per_expert + j + 1)))
                    nc.vector.scalar_tensor_tensor(acc[:, t, :], ps_O[:, j % 2, 0:D], gate(t, e), acc[:, t, :],
                                                   ALU.mult, ALU.add).then_inc(O_ev.handle, 1)

            def one(e, s, use):
                if swiglu:
                    product(e, 0)
                for i in range(n_ch):
                    if swiglu and i + 1 < n_ch:
                        product(e, i + 1)
                    take(e, i)

            each_expert(dve, n_exp, one)
            dve.wait_ge(O_ev.handle, O_ev.at(n_exp * n_ch * TPC + 2))
    for one, n in ((H_mm, FT), (H_ev, FT), (O_mm, TPC), (O_ev, TPC)):
        one.base += n * n_exp * n_ch
    sil_done.base += FT * n_exp * n_ch if swiglu else 0
    H_ev.base += 2
    O_ev.base += 2
    O_mm.base += 2 * per_expert
    for one in slot[:n_slots]:
        one.base += 16 * n_w * n_exp // n_slots


def gated_bias(c, gates, n_exp, b2, acc):
    nc = c.nc
    names = "gb_loaded gb_staged gb_T_mm gb_T_ev gb_O_mm gb_O_ev".split()
    loaded, staged, T_mm, T_ev, O_mm, O_ev = [c.sig(n) for n in names]
    with ExitStack() as st:
        bias = c.sb(st, "gb_bias", [n_exp, D])
        gb = c.sb(st, "gb_gates", [P, 2, n_exp])
        gT = c.sb(st, "gb_gT", [n_exp, 2, P])
        ps_T = c.ps(st, "gb_ps_T", [n_exp, 2, 512])
        ps_O = c.ps(st, "gb_ps_O", [P, 2, 512])
        block = st.enter_context(nc.Block())

        @block.sync
        def _(sp):
            sp.dma_start(bias[:, :], b2).then_inc(loaded.handle, 16)

        @block.gpsimd
        def _(pool):
            with pool.Fori(0, NT // 2) as i:
                for j in range(2):
                    n = i * 2 + j
                    pool.wait_ge(T_mm.handle, T_mm.at(n + 1))
                    nc.gpsimd.tensor_copy(gb[:, j, :], gates[:, n, :]).then_inc(staged.handle, 1)

        @block.tensor
        def _(pe):
            ring(pe, T_mm, 2)
            pe.wait_ge(loaded.handle, loaded.at(16))
            with pe.Fori(0, NT // 2) as i:
                for j in range(2):
                    n = i * 2 + j
                    pe.wait_ge(staged.handle, staged.at(n + 1))
                    pe.wait_ge(T_ev.handle, T_ev.at(n + 1))
                    nc.tensor.transpose(ps_T[:, j, 0:P], gb[:, j, :], c.ident[:, :]).then_inc(T_mm.handle, 1)
                for j in range(2):
                    n = i * 2 + j
                    pe.wait_ge(T_ev.handle, T_ev.at(n + 3))
                    pe.wait_ge(O_ev.handle, O_ev.at(n + 1))
                    nc.tensor.matmul(ps_O[:, j, 0:D], gT[:, j, :], bias[:, :], start=True, stop=True)\
                        .then_inc(O_mm.handle, 1)

        @block.scalar
        def _(act):
            ring(act, T_ev, 2)
            with act.Fori(0, NT // 2) as i:
                for j in range(2):
                    n = i * 2 + j
                    act.wait_ge(T_mm.handle, T_mm.at(n + 3))
                    nc.scalar.copy(gT[:, j, :], ps_T[:, j, 0:P]).then_inc(T_ev.handle, 1)

        @block.vector
        def _(dve):
            ring(dve, O_ev, 2)
            with dve.Fori(0, NT // 2) as i:
                for j in range(2):
                    n = i * 2 + j
                    dve.wait_ge(O_mm.handle, O_mm.at(n + 1))
                    nc.vector.tensor_tensor(acc[:, n, :], acc[:, n, :], ps_O[:, j, 0:D], ALU.add)\
                        .then_inc(O_ev.handle, 1)
    loaded.base += 16
    for one, n in ((staged, 0), (T_mm, 2), (T_ev, 2), (O_mm, 0), (O_ev, 2)):
        one.base += NT + n


class Router:

    def __init__(self, c, st, n_exp, dve_signal):
        self.c, self.nc, self.E = c, c.nc, n_exp
        self.iota = c.sb(st, "rt_iota", [P, NT, n_exp])
        self.cand = c.sb(st, "rt_cand", [P, NT, n_exp])

    def wide(self, small):
        return bc(small.unsqueeze(2), [P, NT, self.E])

    def first_max(self, link, scores, value, onehot, index):
        v = self.nc.vector
        link(v.tensor_reduce(value, scores, AX.X, ALU.max))
        link(v.tensor_tensor(self.cand[:, :, :], scores, self.wide(value), ALU.is_equal))
        link(v.scalar_tensor_tensor(self.cand[:, :, :], self.cand[:, :, :], -64.0, self.iota[:, :, :], ALU.mult, ALU.add))
        link(v.tensor_reduce(index, self.cand[:, :, :], AX.X, ALU.min))
        link(v.tensor_tensor(onehot, self.cand[:, :, :], self.wide(index), ALU.is_equal))

    def softmax_shift(self, link, scores, value):
        v = self.nc.vector
        link(v.tensor_reduce(value, scores, AX.X, ALU.max))
        link(v.tensor_tensor(scores, scores, self.wide(value), ALU.subtract))

    def softmax_divide(self, link, scores, value):
        v = self.nc.vector
        link(v.tensor_reduce(value, scores, AX.X, ALU.add))
        link(v.reciprocal(value, value))
        link(v.tensor_tensor(scores, scores, self.wide(value), ALU.mult))


def route_softmax_top(c, logits, n_exp, mode, gates, extra=None):
    nc = c.nc
    E = n_exp
    capacity1 = B * SEQ // E
    capacity2 = -(-(B * SEQ * 2 * 5) // (E * 4))
    FAR, TAKEN = -1.0e30, -3.0e38
    loaded, iota, ready, exped, step = [c.sig("rt_" + n) for n in ("loaded", "iota", "ready", "exped", "step")]
    mm, back = c.sig("rt_mm"), c.sig("rt_back")
    with ExitStack() as st:
        r = Router(c, st, E, step)
        probs = c.sb(st, "rt_probs", [P, NT, E])
        oh1 = c.sb(st, "rt_oh1", [P, NT, E])
        oh2 = c.sb(st, "rt_oh2", [P, NT, E])
        v1, v2, idx, tot = [c.sb(st, "rt_" + n, [P, NT]) for n in ("v1", "v2", "idx", "tot")]
        bias_row = c.sb(st, "rt_bias", [P, E])
        tri = c.sb(st, "rt_tri", [P, 2, P])
        eight = c.sb(st, "rt_eight", [E, 2, 8])
        wT = c.sb(st, "rt_wT", [E, 2, B * SEQ]) if mode == "capacity" else None
        ps = c.ps(st, "rt_ps", [P, 4, 512])
        ps_g = c.ps(st, "rt_ps_g", [P, 512])
        block = st.enter_context(nc.Block())
        bias = extra[0] if mode == "top1" else extra

        @block.sync
        def _(sp):
            if mode != "top2":
                sp.dma_start(bias_row[:, :], row(bias, P)).then_inc(loaded.handle, 16)

        @block.gpsimd
        def _(pool):
            nc.gpsimd.iota(r.iota[:, :, :], pattern=[[0, NT], [1, E]], base=0, channel_multiplier=0,
                           allow_small_or_imprecise_dtypes=True).then_inc(iota.handle, 1)
            nc.gpsimd.memset(tri[:, :, :], 1.0).then_inc(iota.handle, 1)
            pool.wait_ge(iota.handle, iota.at(2))
            nc.gpsimd.affine_select(out=tri[:, 0, :], in_=tri[:, 0, :], compare_op=ALU.is_ge, fill=0.0,
                                    base=0, pattern=[[1, P]], channel_multiplier=-1).then_inc(iota.handle, 1)

        @block.scalar
        def _(act):
            act.wait_ge(ready.handle, ready.at(1))
            nc.scalar.activation(probs[:, :, :], probs[:, :, :], ACT.Exp).then_inc(exped.handle, 1)

        @block.tensor
        def _(pe):
            if mode == "top1":
                pe.wait_ge(iota.handle, iota.at(3))
                pe.wait_ge(back.handle, back.at(1))
                nc.tensor.matmul(ps[:, 0, 0:NT * E], tri[:, 0, :], oh1[:, :, :], start=True, stop=False)
                for t in range(1, NT):
                    last = nc.tensor.matmul(ps[:, 0, t * E:NT * E], tri[:, 1, :], oh1[:, 0:NT - t, :],
                                            start=False, stop=(t == NT - 1))
                last.then_inc(mm.handle, 1)
            elif mode == "capacity":
                pe.wait_ge(back.handle, back.at(1))
                for t in range(NT):
                    last = nc.tensor.transpose(ps[0:E, t // 4, (t % 4) * P:(t % 4 + 1) * P], probs[:, t, :], c.ident[:, :])
                last.then_inc(mm.handle, 1)
                pe.wait_ge(back.handle, back.at(2))
                for t in range(NT):
                    last = nc.tensor.transpose(ps_g[:, t * E:(t + 1) * E], wT[:, 1, t * P:(t + 1) * P], c.ident[0:E, 0:E])
                last.then_inc(mm.handle, 1)

        @block.vector
        def _(dve):
            link = Chain(dve, step)
            v = nc.vector
            dve.wait_ge(iota.handle, iota.at(1))
            if mode != "top2":
                dve.wait_ge(loaded.handle, loaded.at(16))
            if mode == "top1":
                link(v.tensor_tensor(logits[:, :, :], logits[:, :, :], bc(bias_row[:, :].unsqueeze(1), [P, NT, E]), ALU.add))
            link(v.tensor_copy(probs[:, :, :], logits[:, :, :]))
            link(v.tensor_reduce(v1[:, :], probs[:, :, :], AX.X, ALU.max))
            v.tensor_tensor(probs[:, :, :], probs[:, :, :], r.wide(v1[:, :]), ALU.subtract).then_inc(ready.handle, 1)
            dve.wait_ge(exped.handle, exped.at(1))
            r.softmax_divide(link, probs[:, :, :], v1[:, :])
            if mode == "capacity":
                link(v.tensor_tensor(probs[:, :, :], probs[:, :, :], bc(bias_row[:, :].unsqueeze(1), [P, NT, E]), ALU.add))
            r.first_max(link, probs[:, :, :], v1[:, :], oh1[:, :, :], idx[:, :])
            if mode == "top1":
                v.tensor_copy(extra[1], v1[:, :]).then_inc(back.handle, 1)
                dve.wait_ge(mm.handle, mm.at(1))
                link(v.tensor_scalar(gates[:, :, :], ps[:, 0, 0:NT * E].rearrange("p (t e) -> p t e", e=E),
                                     float(capacity1), None, ALU.is_lt))
                link(v.tensor_tensor(gates[:, :, :], gates[:, :, :], oh1[:, :, :], ALU.mult))
                link(v.tensor_tensor(gates[:, :, :], gates[:, :, :], r.wide(v1[:, :]), ALU.mult))
            else:
                link(v.scalar_tensor_tensor(probs[:, :, :], oh1[:, :, :], FAR, probs[:, :, :], ALU.mult, ALU.add))
                r.first_max(link, probs[:, :, :], v2[:, :], oh2[:, :, :], idx[:, :])
            if mode == "top2":
                link(v.tensor_tensor(tot[:, :], v1[:, :], v2[:, :], ALU.add))
                link(v.tensor_scalar(tot[:, :], tot[:, :], 1e-10, None, ALU.max))
                link(v.reciprocal(tot[:, :], tot[:, :]))
                link(v.tensor_tensor(v1[:, :], v1[:, :], tot[:, :], ALU.mult))
                link(v.tensor_tensor(v2[:, :], v2[:, :], tot[:, :], ALU.mult))
                link(v.tensor_tensor(gates[:, :, :], oh1[:, :, :], r.wide(v1[:, :]), ALU.mult))
                link(v.tensor_tensor(oh2[:, :, :], oh2[:, :, :], r.wide(v2[:, :]), ALU.mult))
                link(v.tensor_tensor(gates[:, :, :], gates[:, :, :], oh2[:, :, :], ALU.add))
            if mode == "capacity":
                link(v.tensor_tensor(oh1[:, :, :], oh1[:, :, :], oh2[:, :, :], ALU.add))
                link(v.tensor_tensor(probs[:, :, :], logits[:, :, :], oh1[:, :, :], ALU.mult))
                link(v.tensor_scalar(oh2[:, :, :], oh1[:, :, :], 1.0, -FAR, ALU.subtract, ALU.mult))
                v.tensor_tensor(probs[:, :, :], probs[:, :, :], oh2[:, :, :], ALU.add).then_inc(back.handle, 1)
                dve.wait_ge(mm.handle, mm.at(1))
                link(v.tensor_copy(wT[:, 0, :], ps[0:E, :, :].rearrange("e a n -> e (a n)")))
                link(v.tensor_copy(wT[:, 1, :], ps[0:E, :, :].rearrange("e a n -> e (a n)")))
                for _ in range(capacity2 // 8):
                    link(v.max(eight[:, 0, :], wT[:, 1, :]))
                    link(v.match_replace(wT[:, 1, :], eight[:, 0, :], wT[:, 1, :], TAKEN))
                link(v.tensor_scalar(wT[:, 1, :], wT[:, 1, :], 2 * FAR, None, ALU.is_lt))
                v.tensor_tensor(wT[:, 1, :], wT[:, 1, :], wT[:, 0, :], ALU.mult).then_inc(back.handle, 1)
                dve.wait_ge(mm.handle, mm.at(2))
                link(v.tensor_tensor(gates[:, :, :], ps_g[:, 0:NT * E].rearrange("p (t e) -> p t e", e=E),
                                     oh1[:, :, :], ALU.mult))
            r.steps = link.count
    loaded.base += 16 if mode != "top2" else 0
    iota.base += 3
    ready.base += 1
    exped.base += 1
    step.base += r.steps
    mm.base += {"top2": 0, "top1": 1, "capacity": 2}[mode]
    back.base += {"top2": 0, "top1": 1, "capacity": 2}[mode]


def clip_add(c):
    nc = c.nc
    clipped = c.sig("clipped")
    with nc.Block() as block:
        @block.vector
        def _(dve):
            with dve.Fori(0, NT) as t:
                nc.vector.tensor_scalar(c.xn[:, t, :], c.xn[:, t, :], -100.0, 100.0, ALU.max, ALU.min)\
                    .then_inc(clipped.handle, 1)
                dve.wait_ge(clipped.handle, clipped.at(t * 2 + 1))
                nc.vector.tensor_tensor(c.x[:, t, :], c.x[:, t, :], c.xn[:, t, :], ALU.add).then_inc(clipped.handle, 1)
            dve.wait_ge(clipped.handle, clipped.at(2 * NT))
    clipped.base += 2 * NT


def L0_ffn(c, w, xT):
    E = 14
    with ExitStack() as st:
        logits = c.sb(st, "L0_logits", [P, NT, E])
        gates = c.sb(st, "L0_gates", [P, NT, E])
        normalise(c, c.x, xn_out=c.xn, xT_out=xT, router=(w["gate_w"].rearrange("e d -> d e"), E, logits))
        route_softmax_top(c, logits, E, "top2", gates)
        gated_bias(c, gates, E, w["b2"], c.xn)
        experts(c, xT, E, 512, w["w1"], None, w["w2"], w["b1"], ACT.Gelu,
                lambda t, e: gates[:, t, bass.ts(e, 1)], c.xn)
        clip_add(c)


def L2_ffn(c, w, xT):
    E = 8
    nc = c.nc
    with ExitStack() as st:
        logits = c.sb(st, "L2_logits", [P, NT, E])
        gates = c.sb(st, "L2_gates", [P, NT, E])
        top = c.sb(st, "L2_top", [P, NT])
        normalise(c, c.x, router=(w["Wr"], E, logits))
        route_softmax_top(c, logits, E, "top1", gates, (w["br"], top[:, :]))
        scaled = c.sig("L2_scaled")
        with nc.Block() as block:
            @block.vector
            def _(dve):
                nc.vector.tensor_tensor(c.rstd[:, :], c.rstd[:, :], top[:, :], ALU.mult).then_inc(scaled.handle, 1)
                nc.vector.tensor_tensor(c.nmr[:, :], c.nmr[:, :], top[:, :], ALU.mult).then_inc(scaled.handle, 1)
                dve.wait_ge(scaled.handle, scaled.at(2))
        scaled.base += 2
        normalise(c, c.x, xT_out=xT)
        gated_bias(c, gates, E, w["b2"], c.x)
        experts(c, xT, E, 256, w["W1"], None, w["W2"], w["b1"], ACT.Relu,
                lambda t, e: gates[:, t, bass.ts(e, 1)], c.x)


def L3_ffn(c, w, xT):
    E = 16
    with ExitStack() as st:
        logits = c.sb(st, "L3_logits", [P, NT, E])
        gates = c.sb(st, "L3_gates", [P, NT, E])
        normalise(c, c.x, xT_out=xT, router=(w["gate_w"], E, logits))
        route_softmax_top(c, logits, E, "capacity", gates, w["gate_b"])
        experts(c, xT, 2, 512, w["sw1"], w["sw3"], w["sw2"], None, ACT.Silu, lambda t, e: 0.5, c.x)
        experts(c, xT, E, 512, w["ew1"], w["ew3"], w["ew2"], None, ACT.Silu,
                lambda t, e: gates[:, t, bass.ts(e, 1)], c.x)


def add_row(c, acc, v, tiles=range(NT)):
    nc = c.nc
    loaded, added = c.sig("row_loaded"), c.sig("row_added")
    with ExitStack() as st:
        r = c.sb(st, "row", [P, D])
        block = st.enter_context(nc.Block())

        @block.sync
        def _(sp):
            sp.dma_start(r[:, :], row(v, P)).then_inc(loaded.handle, 16)

        @block.vector
        def _(dve):
            dve.wait_ge(loaded.handle, loaded.at(16))
            nc.vector.tensor_tensor(acc[:, :, :], acc[:, :, :], bc(r[:, :].unsqueeze(1), [P, NT, D]), ALU.add)\
                .then_inc(added.handle, 1)
            dve.wait_ge(added.handle, added.at(1))
    loaded.base += 16
    added.base += 1


DH3 = D // HEADS
HPT = P // DH3
HPTJ = HPT * J


def narrow_fold(c, w, scratch, M, bias, N):
    nc = c.nc
    loaded, made, mm, ev, stored = [c.sig("nf_" + n) for n in ("loaded", "made", "mm", "ev", "stored")]
    with ExitStack() as st:
        Wq = c.sb(st, "nf_Wq", [P, KD, D])
        Wk = c.sb(st, "nf_Wk", [KC, 2, D])
        Wv = c.sb(st, "nf_Wv", [KC, 2, D])
        bq = c.sb(st, "nf_bq", [P, KD])
        bk = c.sb(st, "nf_bk", [P, KD])
        bv = c.sb(st, "nf_bv", [J, D])
        WqT = c.sb(st, "nf_WqT", [P, KD, D])
        KT = c.sb(st, "nf_KT", [P, KD, BJ])
        Kd = c.sb(st, "nf_Kd", [P, KD, B, HPTJ])
        V = c.sb(st, "nf_V", [J, B, D])
        own = c.sb(st, "nf_own", [P, HPT])
        zeros = c.sb(st, "nf_zeros", [P, HJC * D])
        ps = c.ps(st, "nf_ps", [P, 4, 512])
        block = st.enter_context(nc.Block())
        half = HPTJ // 2
        first = [("K", m) for m in range(KD)] + [("V", b) for b in range(B)] + [("Q", m) for m in range(KD)]
        halves = [(m, b, q) for m in range(KD) for b in range(B) for q in range(2)]
        steps = first + [("M", (k, *x)) for k in range(KD) for x in halves] + [("B", x) for x in halves]
        n_kd = KD * B

        @block.sync
        def _(sp):
            for out, a in ((Wk[:, :, :], w["Wk"].rearrange("(k p) n -> p k n", p=KC)),
                           (Wv[:, :, :], w["Wv"].rearrange("(k p) n -> p k n", p=KC)),
                           (Wq[:, :, :], w["Wq"].rearrange("(k p) n -> p k n", p=P)),
                           (bq[:, :], column(w["bq"])), (bk[:, :], column(w["bk"])), (bv[:, :], row(w["bv"], J))):
                sp.dma_start(out, a, allow_slow_non_contiguous=True).then_inc(loaded.handle, 16)
            sp.wait_ge(made.handle, made.at(4))
            for b in range(B):
                sp.dma_start(scratch[b, :, :].rearrange("(c p) d -> p c d", p=P),
                             zeros[:, :].rearrange("p (c d) -> p c d", d=D)).then_inc(stored.handle, 16)
            sp.wait_ge(stored.handle, stored.at(16 * B))
            sp.wait_ge(ev.handle, ev.at(KD + B))
            with sp.Fori(0, HEADS) as h:
                sp.dma_start(scratch[:, bass.ts(h, J), bass.ts(h, DH3)].rearrange("b j c -> j b c"),
                             V[:, :, bass.ts(h, DH3)]).then_inc(stored.handle, 16)
            sp.wait_ge(stored.handle, stored.at(16 * (B + HEADS)))
            for b in range(B):
                sp.dma_start(N[:, b, :, :], scratch[b, :, :].rearrange("(c p) d -> p c d", p=P)).then_inc(stored.handle, 16)
            sp.wait_ge(stored.handle, stored.at(16 * (2 * B + HEADS)))

        @block.gpsimd
        def _(pool):
            nc.gpsimd.memset(own[:, :], 1.0).then_inc(made.handle, 1)
            pool.wait_ge(made.handle, made.at(1))
            nc.gpsimd.affine_select(out=own[:, :], in_=own[:, :], compare_op=ALU.is_ge, fill=0.0, base=0,
                                    pattern=[[-DH3, HPT]], channel_multiplier=1).then_inc(made.handle, 1)
            pool.wait_ge(made.handle, made.at(2))
            nc.gpsimd.affine_select(out=own[:, :], in_=own[:, :], compare_op=ALU.is_ge, fill=0.0, base=DH3 - 1,
                                    pattern=[[DH3, HPT]], channel_multiplier=-1).then_inc(made.handle, 1)
            nc.gpsimd.memset(zeros[:, :], 0.0).then_inc(made.handle, 1)

        @block.tensor
        def _(pe):
            pe.wait_ge(loaded.handle, loaded.at(96))
            for n, (kind, at) in enumerate(steps):
                bank = ps[:, n % 4, :]
                if n == len(first):
                    pe.wait_ge(ev.handle, ev.at(len(first) + n_kd))
                elif n >= 4:
                    pe.wait_ge(ev.handle, ev.at(n - 3 + (n_kd if n > len(first) else 0)))
                if kind == "K":
                    for k in range(2):
                        last = nc.tensor.matmul(bank[:, 0:BJ], Wk[:, k, at * P:(at + 1) * P], c.ctxT[:, k, :],
                                                start=(k == 0), stop=(k == 1))
                elif kind == "V":
                    for k in range(2):
                        last = nc.tensor.matmul(bank[0:J, 0:D], c.ctxT[:, k, at * J:(at + 1) * J], Wv[:, k, :],
                                                start=(k == 0), stop=(k == 1))
                elif kind == "Q":
                    for k in range(KD):
                        last = nc.tensor.transpose(bank[:, k * P:(k + 1) * P], Wq[:, k, at * P:(at + 1) * P], c.ident[:, :])
                elif kind == "M":
                    k, m, b, q = at
                    last = nc.tensor.matmul(bank[:, 0:half], WqT[:, m, k * P:(k + 1) * P],
                                            Kd[:, m, b, q * half:(q + 1) * half], start=True, stop=True)
                else:
                    m, b, q = at
                    last = nc.tensor.matmul(bank[0:1, 0:half], bq[:, m:m + 1], Kd[:, m, b, q * half:(q + 1) * half],
                                            start=True, stop=True)
                last.then_inc(mm.handle, 1)

        @block.vector
        def _(dve):
            dve.wait_ge(loaded.handle, loaded.at(96))
            for n, (kind, at) in enumerate(steps):
                bank = ps[:, n % 4, :]
                if n == len(first):
                    dve.wait_ge(made.handle, made.at(3))
                    dve.wait_ge(ev.handle, ev.at(len(first)))
                    for m in range(KD):
                        for b in range(B):
                            nc.vector.tensor_tensor(Kd[:, m, b, :].rearrange("p (h j) -> p h j", j=J),
                                                    bc(KT[:, m, b * J:(b + 1) * J].unsqueeze(1), [P, HPT, J]),
                                                    bc(own[:, :].unsqueeze(2), [P, HPT, J]), ALU.mult).then_inc(ev.handle, 1)
                dve.wait_ge(mm.handle, mm.at(n + 1))
                if kind == "K":
                    last = nc.vector.tensor_scalar(KT[:, at, :], bank[:, 0:BJ], bk[:, at:at + 1], DH3 ** -0.5,
                                                   ALU.add, ALU.mult)
                elif kind == "V":
                    last = nc.vector.tensor_tensor(V[:, at, :], bank[0:J, 0:D], bv[:, :], ALU.add)
                elif kind == "Q":
                    last = nc.vector.tensor_copy(WqT[:, at, :], bank[:, 0:D])
                else:
                    m, b, q = at[-3:]
                    lo = m * HPTJ + q * half
                    if kind == "M":
                        last = nc.vector.tensor_copy(M[:, at[0], b, lo:lo + half], bank[:, 0:half])
                    else:
                        last = nc.vector.tensor_copy(bias[0:1, b, lo:lo + half], bank[0:1, 0:half])
                last.then_inc(ev.handle, 1)
            dve.wait_ge(ev.handle, ev.at(len(steps) + n_kd))
    loaded.base += 96
    made.base += 4
    mm.base += len(steps)
    ev.base += len(steps) + n_kd
    stored.base += 16 * (2 * B + HEADS)


def L3_xattn(c, w, scratch, xT):
    with ExitStack() as st:
        M = c.sb(st, "l3_M", [P, KD, B, HJ])
        N = c.sb(st, "l3_N", [P, B, HJC, D])
        bias = c.sb(st, "l3_bias", [1, B, HJ])
        narrow_fold(c, w, scratch, M, bias, N)
        attention(c, M, bias, N, None, xT)
    one = {n: w[n].unsqueeze(0) for n in ("W1", "W2", "b1")}
    experts(c, xT, 1, 512, one["W1"], None, one["W2"], one["b1"], ACT.Relu, lambda t, e: 1.0, c.x)
    add_row(c, c.x, w["b2"])


def L1_ffn(c, w, xT):
    nc = c.nc
    E, F = 8, 512
    FT = F // P
    names = "loaded mm act top weights T_ev step".split()
    s = {n: c.sig("l1f_" + n) for n in names}
    normalise(c, c.x, xn_out=c.xn, xT_out=xT)
    with ExitStack() as st:
        W1 = c.sb(st, "l1f_W1", [P, B, KD, F])
        W2o = c.sb(st, "l1f_W2o", [P, B, FT, D])
        b1 = c.sb(st, "l1f_b1", [P, B, FT])
        with ExitStack() as pre:
            Wp1 = c.sb(pre, "l1f_Wp1", [P, KD, P])
            bp1 = c.sb(pre, "l1f_bp1", [P, 1])
            Wp2 = c.sb(pre, "l1f_Wp2", [P, E])
            bp2 = c.sb(pre, "l1f_bp2", [1, E])
            Wo = c.sb(pre, "l1f_Wo", [P, KD, D])
            bo = c.sb(pre, "l1f_bo", [P, D])
            W2 = c.sb(pre, "l1f_W2", [P, B, FT, D])
            W2T = c.sb(pre, "l1f_W2T", [P, B, KD, F])
            b2 = c.sb(pre, "l1f_b2", [P, B, KD])
            b2w = c.sb(pre, "l1f_b2w", [P, B, KD, P])
            ends = c.sb(pre, "l1f_ends", [P, KD, B])
            nav = c.sb(pre, "l1f_nav", [P, B])
            lg = c.sb(pre, "l1f_lg", [1, B, E])
            v1 = c.sb(pre, "l1f_v1", [1, B])
            eight = c.sb(pre, "l1f_eight", [1, B, 8])
            idx = c.sb(pre, "l1f_idx", [1, B, 8], U32)
            rowb = c.sb(pre, "l1f_rowb", [P, B, D])
            ps = c.ps(pre, "l1f_ps", [P, 4, 512])
            block = pre.enter_context(nc.Block())

            @block.sync
            def _(sp):
                for out, a in ((Wp1[:, :, :], w["Wp1"].rearrange("(k p) n -> p k n", p=P)), (bp1[:, :], column(w["bp1"])),
                               (Wp2[:, :], w["Wp2"]), (bp2[:, :], row(w["bp2"], 1)),
                               (Wo[:, :, :], w["Wo"].rearrange("(k p) n -> p k n", p=P)), (bo[:, :], row(w["bo"], P))):
                    sp.dma_start(out, a, allow_slow_non_contiguous=True).then_inc(s["loaded"].handle, 16)
                sp.wait_ge(s["top"].handle, s["top"].at(1))
                for b in range(B):
                    e = sp.value_load(idx[0:1, b, 0:1], min_val=0, max_val=E - 1)
                    sp.dma_start(W2[:, b, :, :], w["W2"][e, :, :].rearrange("(k p) f -> p k f", p=P))\
                        .then_inc(s["weights"].handle, 16)
                    sp.dma_start(W1[:, b, :, :], w["W1"][e, :, :].rearrange("(k p) f -> p k f", p=P))\
                        .then_inc(s["weights"].handle, 16)
                    sp.dma_start(b1[:, b, :], w["b1"][e, :].rearrange("(f p) -> p f", p=P), allow_slow_non_contiguous=True)\
                        .then_inc(s["weights"].handle, 16)
                    sp.dma_start(b2[:, b, :], w["b2"][e, :].rearrange("(f p) -> p f", p=P), allow_slow_non_contiguous=True)\
                        .then_inc(s["weights"].handle, 16)
                sp.wait_ge(s["weights"].handle, s["weights"].at(128))

            @block.tensor
            def _(pe):
                pe.wait_ge(s["loaded"].handle, s["loaded"].at(96))
                pe.wait_ge(s["act"].handle, s["act"].at(1))
                for k in range(KD):
                    last = nc.tensor.matmul(ps[:, 0, 0:B], Wp1[:, k, :], ends[:, k, :], start=(k == 0), stop=(k == KD - 1))
                last.then_inc(s["mm"].handle, 1)
                pe.wait_ge(s["act"].handle, s["act"].at(2))
                for b in range(B):
                    last = nc.tensor.matmul(ps[0:1, 1, b * E:(b + 1) * E], nav[:, b:b + 1], Wp2[:, :], start=True, stop=True)
                last.then_inc(s["mm"].handle, 1)
                pe.wait_ge(s["weights"].handle, s["weights"].at(128))
                for b in range(B):
                    for k in range(KD):
                        if b:
                            pe.wait_ge(s["T_ev"].handle, s["T_ev"].at((b - 1) * KD + k + 1))
                        for f in range(FT):
                            last = nc.tensor.transpose(ps[:, 2 + k, f * P:(f + 1) * P], W2[:, b, f, k * P:(k + 1) * P],
                                                       c.ident[:, :])
                        last.then_inc(s["mm"].handle, 1)
                pe.wait_ge(s["T_ev"].handle, s["T_ev"].at(B * KD))
                pe.wait_ge(s["step"].handle, s["step"].at(8))
                for b in range(B):
                    for f in range(0, FT, 2):
                        n = b * FT // 2 + f // 2
                        if n:
                            pe.wait_ge(s["T_ev"].handle, s["T_ev"].at(B * KD + n))
                        for q in range(2):
                            for k in range(KD):
                                last = nc.tensor.matmul(ps[:, 0, q * D:(q + 1) * D],
                                                        W2T[:, b, k, (f + q) * P:(f + q + 1) * P], Wo[:, k, :],
                                                        start=(k == 0), stop=(k == KD - 1))
                        last.then_inc(s["mm"].handle, 1)
                for b in range(B):
                    for k in range(KD):
                        last = nc.tensor.matmul(ps[:, 1, b * D:(b + 1) * D], b2w[:, b, k, :], Wo[:, k, :],
                                                start=(k == 0), stop=(k == KD - 1))
                last.then_inc(s["mm"].handle, 1)

            @block.scalar
            def _(act):
                for b in range(B):
                    last = nc.scalar.copy(ends[:, :, b], xT[:, :, (b + 1) * SEQ - 1])
                last.then_inc(s["act"].handle, 1)
                act.wait_ge(s["mm"].handle, s["mm"].at(1))
                nc.scalar.activation(nav[:, :], ps[:, 0, 0:B], ACT.Gelu, bias=bp1[:, 0:1]).then_inc(s["act"].handle, 1)
                act.wait_ge(s["step"].handle, s["step"].at(3))
                nc.scalar.activation(lg[:, :, :], lg[:, :, :], ACT.Exp).then_inc(s["act"].handle, 1)

            @block.vector
            def _(dve):
                v = nc.vector
                link = Chain(dve, s["step"])
                wide = bc(v1[:, :].unsqueeze(2), [1, B, E])
                dve.wait_ge(s["mm"].handle, s["mm"].at(2))
                link(v.tensor_tensor(lg[:, :, :], ps[0:1, 1, 0:B * E].rearrange("p (b e) -> p b e", e=E),
                                     bc(bp2[:, :].unsqueeze(1), [1, B, E]), ALU.add))
                link(v.tensor_reduce(v1[:, :], lg[:, :, :], AX.X, ALU.max))
                link(v.tensor_tensor(lg[:, :, :], lg[:, :, :], wide, ALU.subtract))
                dve.wait_ge(s["act"].handle, s["act"].at(3))
                link(v.tensor_reduce(v1[:, :], lg[:, :, :], AX.X, ALU.add))
                link(v.reciprocal(v1[:, :], v1[:, :]))
                link(v.tensor_tensor(lg[:, :, :], lg[:, :, :], wide, ALU.mult))
                v.max(eight[:, 0, :], lg[:, 0, :])
                link(v.max(eight[:, 1, :], lg[:, 1, :]))
                v.max_index(idx[:, 0, :], eight[:, 0, :], lg[:, 0, :])
                v.max_index(idx[:, 1, :], eight[:, 1, :], lg[:, 1, :]).then_inc(s["top"].handle, 1)
                dve.wait_ge(s["weights"].handle, s["weights"].at(128))
                for b in range(B):
                    for k in range(KD):
                        dve.wait_ge(s["mm"].handle, s["mm"].at(3 + b * KD + k))
                        v.tensor_copy(W2T[:, b, k, :], ps[:, 2 + k, :]).then_inc(s["T_ev"].handle, 1)
                link(v.tensor_copy(b2w[:, :, :, :], bc(b2[:, :, :].unsqueeze(3), [P, B, KD, P])))
                for b in range(B):
                    for f in range(0, FT, 2):
                        dve.wait_ge(s["mm"].handle, s["mm"].at(7 + b * FT // 2 + f // 2))
                        v.tensor_copy(W2o[:, b, f:f + 2, :], ps[:, 0, :].rearrange("p (f d) -> p f d", d=D))\
                            .then_inc(s["T_ev"].handle, 1)
                dve.wait_ge(s["mm"].handle, s["mm"].at(7 + B * FT // 2))
                link(v.tensor_tensor(rowb[:, :, :], ps[:, 1, :].rearrange("p (b d) -> p b d", d=D),
                                     bc(bo[:, :].unsqueeze(1), [P, B, D]), ALU.add))
                for b in range(B):
                    tiles = slice(b * TPB, (b + 1) * TPB)
                    link(v.scalar_tensor_tensor(c.x[:, tiles, :], bc(rowb[:, b, :].unsqueeze(1), [P, TPB, D]), 0.3,
                                                c.x[:, tiles, :], ALU.mult, ALU.add))
                link(v.tensor_tensor(c.x[:, :, :], c.x[:, :, :], c.xn[:, :, :], ALU.add))
        s["loaded"].base += 96
        for n, k in (("mm", 12), ("act", 3), ("top", 1), ("weights", 128), ("T_ev", 8), ("step", 12)):
            s[n].base += k
        for b in range(B):
            experts(c, xT, 1, F, None, None, None, True, ACT.Gelu, lambda t, e: 0.3, c.x,
                    chunks=range(b * NCH // B, (b + 1) * NCH // B),
                    resident=(W1[:, b:b + 1, :, :], W2o[:, b:b + 1, :, :], b1[:, b:b + 1, :]))


H1, DH1 = 4, 32
HJ1 = H1 * J
JE = J + 1
TOP = 32
NS = 64
MASKED, TAKEN1 = -1.0e30, -3.0e38
NF1, NF2 = 5, 256
MAGIC = 1.5 * 2 ** 23
TWO_PI = 6.2831845
R2 = 0.5 ** 0.5


def constants():
    n = 2 * SEQ
    f1, j2, f2 = np.arange(NF1)[:, None, None], np.arange(NF2)[None, :, None], np.arange(NF2)[None, None, :]
    turn = 2 * np.pi * ((j2 * (f1 + 8 * f2)) % n) / n
    fwd = np.stack([np.cos(turn), np.sin(turn), -np.sin(turn)], axis=1)
    scale = np.array([1, 2, 2, 2, 1]).reshape(NF1, 1, 1, 1) / n
    inv = np.swapaxes(fwd, 2, 3) * scale
    return {"dft_fwd": fwd.astype(np.float32), "dft_inv": inv.astype(np.float32)}


def L1_fold(c, w, mask_tok, mask_ctx, M, mask_row, VF, tok_factor):
    nc = c.nc
    s = {n: c.sig("l1_" + n) for n in "loaded mm ev step bias".split()}
    with ExitStack() as st:
        Wq = c.sb(st, "l1_Wq", [P, KD, P])
        Wk = c.sb(st, "l1_Wk", [KC, 2, P])
        Wv = c.sb(st, "l1_Wv", [KC, 2, D])
        Wf = c.sb(st, "l1_Wf", [P, 2, KD, 2 * D])
        bf = c.sb(st, "l1_bf", [1, 2, 2 * D])
        KT = c.sb(st, "l1_KT", [P, BJ])
        VT = c.sb(st, "l1_VT", [P, KD, BJ])
        WqT = c.sb(st, "l1_WqT", [P, D])
        gate = c.sb(st, "l1_gate", [P, 1])
        mt8 = c.sb(st, "l1_mt8", [P, NT], U8)
        mc8 = c.sb(st, "l1_mc8", [1, B, J], U8)
        mcf = c.sb(st, "l1_mcf", [1, B, J])
        ps = c.ps(st, "l1_ps", [P, 4, 512])
        block = st.enter_context(nc.Block())
        steps = [("K", 0), ("V", 0), ("V", 1), ("Q", 0)] + [("M", h) for h in range(H1)]
        steps += [("F", (b, o)) for b in range(B) for o in range(2)]
        loads = 10

        @block.sync
        def _(sp):
            for out, a in ((Wk[:, :, :], w["Wk"].rearrange("(k p) n -> p k n", p=KC)),
                           (Wv[:, :, :], w["Wv"].rearrange("(k p) n -> p k n", p=KC)),
                           (Wq[:, :, :], w["Wq"].rearrange("(k p) n -> p k n", p=P)),
                           (Wf[:, 0, :, :], w["W_film_in"].rearrange("(k p) n -> p k n", p=P)),
                           (Wf[:, 1, :, :], w["W_film_out"].rearrange("(k p) n -> p k n", p=P)),
                           (bf[:, 0, :], row(w["b_film_in"], 1)), (bf[:, 1, :], row(w["b_film_out"], 1)),
                           (gate[:, :], row(w["mod_gate"], P)),
                           (mt8[:, :], mask_tok.rearrange("b (t p) -> p (b t)", p=P)),
                           (mc8[:, :, :], mask_ctx.unsqueeze(0))):
                sp.dma_start(out, a, allow_slow_non_contiguous=True).then_inc(s["loaded"].handle, 16)
            sp.wait_ge(s["step"].handle, s["step"].at(2))
            for b in range(B):
                sp.dma_start(VF[J:JE, b, :, :], bf[:, :, :]).then_inc(s["bias"].handle, 16)
            sp.wait_ge(s["bias"].handle, s["bias"].at(32))

        @block.tensor
        def _(pe):
            pe.wait_ge(s["loaded"].handle, s["loaded"].at(16 * loads))
            for n, (kind, at) in enumerate(steps):
                bank = ps[:, n % 4, :]
                if n >= 4:
                    pe.wait_ge(s["ev"].handle, s["ev"].at(max(n - 3, 4)))
                if kind == "K":
                    for k in range(2):
                        last = nc.tensor.matmul(bank[:, 0:BJ], Wk[:, k, :], c.ctxT[:, k, :], start=(k == 0), stop=(k == 1))
                elif kind == "V":
                    for k in range(2):
                        last = nc.tensor.matmul(bank[:, 0:BJ], Wv[:, k, at * P:(at + 1) * P], c.ctxT[:, k, :],
                                                start=(k == 0), stop=(k == 1))
                elif kind == "Q":
                    for k in range(KD):
                        last = nc.tensor.transpose(bank[:, k * P:(k + 1) * P], Wq[:, k, :], c.ident[:, :])
                elif kind == "M":
                    lo = at * DH1
                    for k in range(KD):
                        last = nc.tensor.matmul(bank[:, k * BJ:(k + 1) * BJ], WqT[lo:lo + DH1, k * P:(k + 1) * P],
                                                KT[lo:lo + DH1, :], start=True, stop=True)
                else:
                    b, o = at
                    for k in range(KD):
                        last = nc.tensor.matmul(bank[0:J, :], VT[:, k, b * J:(b + 1) * J], Wf[:, o, k, :],
                                                start=(k == 0), stop=(k == KD - 1))
                last.then_inc(s["mm"].handle, 1)

        @block.vector
        def _(dve):
            v = nc.vector
            link = Chain(dve, s["step"])
            dve.wait_ge(s["loaded"].handle, s["loaded"].at(16 * loads))
            link(v.tensor_scalar(bf[:, :, :], bf[:, :, :], gate[0:1, 0:1], None, ALU.mult))
            link(v.tensor_scalar(bf[:, :, 0:D], bf[:, :, 0:D], 1.0, None, ALU.add))
            link(v.tensor_copy(tok_factor, mt8[:, :]))
            link(v.tensor_scalar(tok_factor, tok_factor, 1.0 / H1, None, ALU.mult))
            link(v.tensor_copy(mcf[:, :, :], mc8[:, :, :]))
            link(v.tensor_scalar(mcf[:, :, :], mcf[:, :, :], 1.0, -MASKED, ALU.subtract, ALU.mult))
            for h in range(H1):
                link(v.tensor_copy(mask_row[:, :, h * J:(h + 1) * J], mcf[:, :, :]))
            for n, (kind, at) in enumerate(steps):
                bank = ps[:, n % 4, :]
                dve.wait_ge(s["mm"].handle, s["mm"].at(n + 1))
                if kind == "K":
                    last = v.tensor_scalar(KT[:, :], bank[:, 0:BJ], DH1 ** -0.5, None, ALU.mult)
                elif kind == "V":
                    last = v.tensor_copy(VT[:, at, :], bank[:, 0:BJ])
                elif kind == "Q":
                    last = v.tensor_copy(WqT[:, :], bank[:, 0:D])
                elif kind == "M":
                    last = v.tensor_copy(M[:, :, :, at * J:(at + 1) * J],
                                         bank[:, 0:KD * BJ].rearrange("p (k b j) -> p k b j", k=KD, b=B))
                else:
                    b, o = at
                    last = v.tensor_scalar(VF[0:J, b, o, :], bank[0:J, :], gate[0:J, 0:1], None, ALU.mult)
                last.then_inc(s["ev"].handle, 1)
            dve.wait_ge(s["ev"].handle, s["ev"].at(len(steps)))
    s["loaded"].base += 16 * loads
    s["mm"].base += len(steps)
    s["ev"].base += len(steps)
    s["step"].base += 6 + H1
    s["bias"].base += 32


def L1_modulate(c, scores, tok_factor, VF, UK, film_out):
    nc = c.nc
    s = {n: c.sig("l1m_" + n) for n in "step fence shifted exped mean T_mm T_ev F_mm F_ev kept".split()}
    rounds = TOP // 8
    with ExitStack() as st:
        sc = c.sb(st, "l1m_sc", [P, 2, H1, J])
        work = c.sb(st, "l1m_work", [P, H1, J])
        eight = c.sb(st, "l1m_eight", [P, H1, 8])
        mx = c.sb(st, "l1m_mx", [P, H1])
        rs = c.sb(st, "l1m_rs", [P, H1])
        am = c.sb(st, "l1m_am", [P, 2, JE])
        amT = c.sb(st, "l1m_amT", [JE, 2, P])
        ps_T = c.ps(st, "l1m_ps_T", [JE, 2, 512])
        ps_F = c.ps(st, "l1m_ps_F", [P, 2, 2, 512])
        block = st.enter_context(nc.Block())

        @block.vector
        def _(dve):
            v = nc.vector
            link = Chain(dve, s["step"])
            ring(dve, s["F_ev"], 2)
            link(v.memset(am[:, :, :], 1.0))

            def fence():
                dve.sem_inc(s["fence"].handle, 1)

            def select(n, j):
                link(v.tensor_copy(work[:, :, :], scores[:, n, :].rearrange("p (h j) -> p h j", j=J)))
                fence()
                for r in range(rounds):
                    for h in range(H1):
                        last = v.max(eight[:, h, :], work[:, h, :])
                    link(last)
                    fence()
                    if r == 0:
                        v.tensor_tensor(sc[:, j, :, :], scores[:, n, :].rearrange("p (h j) -> p h j", j=J),
                                        bc(eight[:, :, 0:1], [P, H1, J]), ALU.subtract).then_inc(s["shifted"].handle, 1)
                    for h in range(H1):
                        last = v.match_replace(work[:, h, :], eight[:, h, :], work[:, h, :], TAKEN1)
                    link(last)
                    fence()
                dve.wait_ge(s["exped"].handle, s["exped"].at(n + 1))
                link(v.scalar_tensor_tensor(sc[:, j, :, :], work[:, :, :], 10 * MASKED, sc[:, j, :, :], ALU.is_lt, ALU.mult))
                link(v.tensor_reduce(rs[:, :], sc[:, j, :, :], AX.X, ALU.add))
                link(v.reciprocal(rs[:, :], rs[:, :]))
                link(v.tensor_scalar(rs[:, :], rs[:, :], tok_factor[:, bass.ts(n, 1)], None, ALU.mult))
                link(v.tensor_tensor(sc[:, j, :, :], sc[:, j, :, :], bc(rs[:, :].unsqueeze(2), [P, H1, J]), ALU.mult))
                dve.wait_ge(s["T_mm"].handle, s["T_mm"].at(n + 1))
                v.tensor_reduce(am[:, j, 0:J], sc[:, j, :, :].rearrange("p h j -> p j h"), AX.X, ALU.add)\
                    .then_inc(s["mean"].handle, 1)

            def apply(n, t, b, j):
                dve.wait_ge(s["F_mm"].handle, s["F_mm"].at(n + 1))
                u = UK[:, t, b, :]
                link(v.tensor_tensor(u, u, ps_F[:, j, 0, 0:D], ALU.mult))
                link(v.tensor_tensor(u, u, ps_F[:, j, 0, D:2 * D], ALU.add))
                dve.wait_ge(s["kept"].handle, s["kept"].at(n + 1))
                dve.sem_inc(s["F_ev"].handle, 1)

            per_tile = 2 * rounds + 1 + 5 + 2
            for b in range(B):
                with dve.Fori(0, TPB // 2) as i:
                    link.count = i * (2 * per_tile) + (1 + b * TPB * per_tile)
                    for j in range(2):
                        select(i * 2 + (b * TPB + j), j)
                    for j in range(2):
                        apply(i * 2 + (b * TPB + j), i * 2 + j, b, j)

        @block.scalar
        def _(act):
            ring(act, s["T_ev"], 2)
            with act.Fori(0, NT // 2) as i:
                for j in range(2):
                    n = i * 2 + j
                    act.wait_ge(s["shifted"].handle, s["shifted"].at(n + 1))
                    nc.scalar.activation(sc[:, j, :, :], sc[:, j, :, :], ACT.Exp).then_inc(s["exped"].handle, 1)
                for j in range(2):
                    n = i * 2 + j
                    act.wait_ge(s["T_mm"].handle, s["T_mm"].at(n + 3))
                    nc.scalar.copy(amT[:, j, :], ps_T[:, j, 0:P]).then_inc(s["T_ev"].handle, 1)
                for j in range(2):
                    n = i * 2 + j
                    act.wait_ge(s["F_mm"].handle, s["F_mm"].at(n + 1))
                    nc.scalar.copy(film_out[:, n, :], ps_F[:, j, 1, :]).then_inc(s["kept"].handle, 1)

        @block.tensor
        def _(pe):
            ring(pe, s["T_mm"], 2)
            for b in range(B):
                with pe.Fori(0, TPB // 2) as i:
                    for j in range(2):
                        n = i * 2 + (b * TPB + j)
                        pe.wait_ge(s["mean"].handle, s["mean"].at(n + 1))
                        pe.wait_ge(s["T_ev"].handle, s["T_ev"].at(n + 1))
                        nc.tensor.transpose(ps_T[:, j, 0:P], am[:, j, :], c.ident[:, :]).then_inc(s["T_mm"].handle, 1)
                    for j in range(2):
                        n = i * 2 + (b * TPB + j)
                        pe.wait_ge(s["T_ev"].handle, s["T_ev"].at(n + 3))
                        pe.wait_ge(s["F_ev"].handle, s["F_ev"].at(n + 1))
                        for o in range(2):
                            last = nc.tensor.matmul(ps_F[:, j, o, :], amT[:, j, :], VF[:, b, o, :], start=True, stop=True)
                        last.then_inc(s["F_mm"].handle, 1)
    s["step"].base += 1 + NT * (2 * rounds + 1 + 5 + 2)
    s["fence"].base += NT * (2 * rounds + 1)
    for n in ("shifted", "exped", "mean", "F_mm", "kept"):
        s[n].base += NT
    for n in ("T_mm", "T_ev", "F_ev"):
        s[n].base += NT + 2


DB = 32
NDB = D // DB


def L1_kernel(c, w, UK):
    nc = c.nc
    s = {n: c.sig("ker_" + n) for n in "loaded made T_mm step act arg earg sined exped fine mm ev".split()}
    ARE, AIM, CRE, CIM = range(4)
    with ExitStack() as st:
        raw = c.sb(st, "ker_raw", [P, 4, KD, 2, NS])
        par = c.sb(st, "ker_par", [P, 4, D])
        dt = c.sb(st, "ker_dt", [P, D])
        a = c.sb(st, "ker_a", [P, D])
        r0 = c.sb(st, "ker_r0", [P, D])
        arg = c.sb(st, "ker_arg", [P, 3, D])
        ea = c.sb(st, "ker_ea", [P, 2, D])
        tmp = c.sb(st, "ker_tmp", [P, 8, D])
        P12 = c.sb(st, "ker_P12", [P, 2, D])
        cols = c.sb(st, "ker_cols", [P, 5])
        iota_p = c.sb(st, "ker_iota", [P, P])
        big = c.sb(st, "ker_big", [P, 3, SEQ // P, D])
        coarse = c.sb(st, "ker_coarse", [P, SEQ // P, D])
        NI8 = SEQ // P
        ps_T = c.ps(st, "ker_ps_T", [P, 2, 512])
        ps_K = c.ps(st, "ker_ps_K", [P, 2, 512])
        fine = c.sb(st, "ker_fine", [P, 2, DB, P])
        t = c.sb(st, "ker_t", [P, DB, P])
        e = c.sb(st, "ker_e", [P, DB, P])
        block = st.enter_context(nc.Block())
        m = big[:, 0:2, :, :].rearrange("p a i d -> p (a i d)").rearrange("p (q n) -> p q n", n=P)

        @block.sync
        def _(sp):
            for q, name in enumerate(("A_re", "A_im", "C_re", "C_im")):
                for twice in range(2):
                    sp.dma_start(raw[:, q, :, twice, :], w[name].rearrange("(t p) n -> p t n", p=P))\
                        .then_inc(s["loaded"].handle, 16)
            sp.dma_start(dt[:, :], row(w["log_dt"], P)).then_inc(s["loaded"].handle, 16)

        @block.gpsimd
        def _(pool):
            g = nc.gpsimd
            for q, (upper, lower) in enumerate(((2.0, 0.0), (0.0, -2.0), (-2.0, 0.0), (0.25, 0.0), (0.25 * TWO_PI, 0.0))):
                g.memset(cols[0:NS, q:q + 1], upper).then_inc(s["made"].handle, 1)
                pool.wait_ge(s["made"].handle, 2 * q + 1)
                g.memset(cols[NS:P, q:q + 1], lower).then_inc(s["made"].handle, 1)
                pool.wait_ge(s["made"].handle, 2 * q + 2)
            g.iota(iota_p[:, :], pattern=[[1, P]], base=0, channel_multiplier=0,
                   allow_small_or_imprecise_dtypes=True).then_inc(s["made"].handle, 1)
            pool.wait_ge(s["made"].handle, s["made"].at(11))
            pool.wait_ge(s["step"].handle, s["step"].at(1))
            with pool.Fori(0, NDB) as blk:
                pool.wait_ge(s["fine"].handle, s["fine"].at(blk + 1))
                g.tensor_tensor(e[:, :, :], bc(a[:, bass.ts(blk, DB)].unsqueeze(2), [P, DB, P]),
                                bc(iota_p[:, :].unsqueeze(1), [P, DB, P]), ALU.mult).then_inc(s["earg"].handle, 1)

        @block.tensor
        def _(pe):
            pe.wait_ge(s["loaded"].handle, s["loaded"].at(16 * 9))
            for q in range(4):
                for k in range(KD):
                    o = (q % 2) * D + k * P
                    last = nc.tensor.transpose(ps_T[:, q // 2, o:o + P], raw[:, q, k, :, :].rearrange("p a n -> p (a n)"),
                                               c.ident[:, :])
            last.then_inc(s["T_mm"].handle, 1)
            pe.wait_ge(s["act"].handle, s["act"].at(8))
            with pe.Fori(0, NDB // 2) as i:
                for j in range(2):
                    blk = i * 2 + j
                    pe.wait_ge(s["fine"].handle, s["fine"].at(blk + 2))
                    pe.wait_ge(s["ev"].handle, s["ev"].at(blk + 1))
                    for d in range(DB):
                        last = nc.tensor.matmul(ps_K[:, j, d * NI8:(d + 1) * NI8], fine[:, j, d, :],
                                                coarse[:, :, bass.ds(blk * DB + d, 1)].rearrange("p i o -> p (i o)"),
                                                start=True, stop=True)
                    last.then_inc(s["mm"].handle, 1)

        @block.scalar
        def _(act):
            A = s["act"]
            act.wait_ge(s["loaded"].handle, s["loaded"].at(16 * 9))
            nc.scalar.activation(dt[:, :], dt[:, :], ACT.Exp).then_inc(A.handle, 1)
            act.wait_ge(s["step"].handle, s["step"].at(8))
            nc.scalar.activation(ea[:, 0, :], a[:, :], ACT.Exp).then_inc(A.handle, 1)
            nc.scalar.activation(ea[:, 1, :], a[:, :], ACT.Tanh, scale=0.5).then_inc(A.handle, 1)
            nc.scalar.activation(arg[:, :, :], arg[:, :, :], ACT.Sin, scale=TWO_PI).then_inc(A.handle, 1)
            act.wait_ge(s["step"].handle, s["step"].at(STEP_COARSE))
            for q in range(2):
                nc.scalar.activation(big[:, q, :, :], big[:, q, :, :], ACT.Sin, scale=TWO_PI).then_inc(A.handle, 1)
            nc.scalar.activation(big[:, 2, :, :], big[:, 2, :, :], ACT.Exp).then_inc(A.handle, 1)
            act.wait_ge(s["step"].handle, s["step"].at(STEP_FINE))
            act.sem_inc(A.handle, 1)
            with act.Fori(0, NDB) as blk:
                act.wait_ge(s["earg"].handle, s["earg"].at(blk + 1))
                nc.scalar.activation(e[:, :, :], e[:, :, :], ACT.Exp).then_inc(s["exped"].handle, 1)
                act.wait_ge(s["arg"].handle, s["arg"].at(blk + 1))
                nc.scalar.activation(t[:, :, :], t[:, :, :], ACT.Sin, scale=TWO_PI).then_inc(s["sined"].handle, 1)

        @block.vector
        def _(dve):
            v = nc.vector
            link = Chain(dve, s["step"])
            x = tmp
            dve.wait_ge(s["T_mm"].handle, s["T_mm"].at(1))
            dve.wait_ge(s["act"].handle, s["act"].at(1))
            v.tensor_copy(par[:, :, :].rearrange("p (a q) d -> p a (q d)", a=2), ps_T[:, :, :]).then_inc(s["ev"].handle, 1)
            dve.wait_ge(s["ev"].handle, s["ev"].at(1))
            dve.wait_ge(s["made"].handle, s["made"].at(11))
            link(v.tensor_tensor(a[:, :], par[:, ARE, :], dt[:, :], ALU.mult))

            def turns(out, cycles, work, more=0.0):
                link(v.tensor_scalar(out, cycles, more, None, ALU.add))
                link(v.tensor_scalar(work, out, MAGIC, MAGIC, ALU.add, ALU.subtract))
                link(v.tensor_tensor(out, out, work, ALU.subtract))

            link(v.tensor_tensor(r0[:, :], par[:, AIM, :], dt[:, :], ALU.mult))
            link(v.tensor_scalar(r0[:, :], r0[:, :], 0.5 / np.pi, None, ALU.mult))
            link(v.tensor_scalar(x[:, 0, :], r0[:, :], MAGIC, MAGIC, ALU.add, ALU.subtract))
            link(v.tensor_tensor(r0[:, :], r0[:, :], x[:, 0, :], ALU.subtract))
            v.tensor_copy(arg[:, 0, :], r0[:, :])
            v.tensor_scalar(arg[:, 2, :], r0[:, :], 0.5, None, ALU.mult)
            turns(arg[:, 1, :], r0[:, :], x[:, 0, :], 0.25)
            dve.wait_ge(s["act"].handle, s["act"].at(4))
            sn, cs, sh, e1, th = arg[:, 0, :], arg[:, 1, :], arg[:, 2, :], ea[:, 0, :], ea[:, 1, :]
            are, aim, cre, cim = [par[:, q, :] for q in range(4)]

            def mul(out, p, q):
                link(v.tensor_tensor(out, p, q, ALU.mult))

            er, ei, tr, ti, q, u1, u2 = [x[:, n, :] for n in range(7)]
            link(v.tensor_scalar(u1, e1, 1.0, None, ALU.add))
            mul(er, th, u1)
            mul(er, er, cs)
            mul(u2, sh, sh)
            link(v.scalar_tensor_tensor(er, u2, -2.0, er, ALU.mult, ALU.add))
            mul(ei, e1, sn)
            mul(u1, er, are)
            mul(u2, ei, aim)
            link(v.tensor_tensor(tr, u1, u2, ALU.add))
            mul(u1, ei, are)
            mul(u2, er, aim)
            link(v.tensor_tensor(ti, u1, u2, ALU.subtract))
            mul(u1, are, are)
            mul(u2, aim, aim)
            link(v.tensor_tensor(q, u1, u2, ALU.add))
            link(v.reciprocal(q, q))
            mul(tr, tr, q)
            mul(ti, ti, q)
            mul(u1, cre, tr)
            mul(u2, cim, ti)
            link(v.tensor_tensor(er, u1, u2, ALU.subtract))
            mul(u1, cre, ti)
            mul(u2, cim, tr)
            link(v.tensor_tensor(ei, u1, u2, ALU.add))
            link(v.tensor_scalar(u1, ei, cols[:, 1:2], None, ALU.mult))
            link(v.scalar_tensor_tensor(P12[:, 0, :], er, cols[:, 0:1], u1, ALU.mult, ALU.add))
            link(v.tensor_scalar(u1, ei, cols[:, 2:3], None, ALU.mult))
            link(v.scalar_tensor_tensor(P12[:, 1, :], er, cols[:, 1:2], u1, ALU.mult, ALU.add))
            for i in range(NI8):
                v.tensor_scalar(big[:, 0, i, :], r0[:, :], float(i * P), None, ALU.mult)
                link(v.tensor_scalar(big[:, 2, i, :], a[:, :], float(i * P), None, ALU.mult))
            link(v.tensor_scalar(coarse[:, :, :], big[:, 0, :, :], MAGIC, MAGIC, ALU.add, ALU.subtract))
            link(v.tensor_tensor(big[:, 0, :, :], big[:, 0, :, :], coarse[:, :, :], ALU.subtract))
            turns(big[:, 1, :, :], big[:, 0, :, :], coarse[:, :, :], 0.25)
            check(link.count, STEP_COARSE)
            dve.wait_ge(s["act"].handle, s["act"].at(7))
            for q in range(2):
                mul(big[:, 1 - q, :, :], big[:, 1 - q, :, :], bc(P12[:, q, :].unsqueeze(1), [P, NI8, D]))
            link(v.tensor_tensor(big[:, 0, :, :], big[:, 0, :, :], big[:, 1, :, :], ALU.add))
            mul(coarse[:, :, :], big[:, 0, :, :], big[:, 2, :, :])
            check(link.count, STEP_FINE)
            ring(dve, s["fine"], 1)

            def take(blk, j):
                dve.wait_ge(s["mm"].handle, s["mm"].at(blk + 1))
                v.tensor_copy(UK[:, :, 2, bass.ts(blk, DB)],
                              ps_K[:, j, 0:DB * NI8].rearrange("p (d i) -> p i d", i=NI8)).then_inc(s["ev"].handle, 1)

            def powers(blk, j):
                link(v.tensor_tensor(t[:, :, :], bc(r0[:, bass.ts(blk, DB)].unsqueeze(2), [P, DB, P]),
                                     bc(iota_p[:, :].unsqueeze(1), [P, DB, P]), ALU.mult))
                link(v.tensor_scalar(t[:, :, :], t[:, :, :], cols[:, 3:4], None, ALU.add))
                link(v.tensor_scalar(m, t[:, :, :], MAGIC, MAGIC, ALU.add, ALU.subtract))
                v.tensor_tensor(t[:, :, :], t[:, :, :], m, ALU.subtract).then_inc(s["arg"].handle, 1)
                dve.wait_ge(s["exped"].handle, s["exped"].at(blk + 1))
                dve.wait_ge(s["sined"].handle, s["sined"].at(blk + 1))
                v.tensor_tensor(fine[:, j, :, :], t[:, :, :], e[:, :, :], ALU.mult).then_inc(s["fine"].handle, 1)
                dve.wait_ge(s["fine"].handle, s["fine"].at(blk + 2))

            powers(0, 0)
            powers(1, 1)
            with dve.Fori(0, NDB // 2 - 1) as i:
                link.count = i * 6 + (STEP_FINE + 6)
                for j in range(2):
                    take(i * 2 + j, j)
                    powers(i * 2 + (j + 2), j)
            for j in range(2):
                take(NDB - 2 + j, j)
            dve.wait_ge(s["ev"].handle, s["ev"].at(NDB + 1))



STEP_COARSE = 8 + 28 + 8 + 2 + 3
STEP_FINE = STEP_COARSE + 4


def check(count, expected):
    assert count == expected, (count, expected)


def L1_convolve(c, fwd, inv, UK, y):
    nc = c.nc
    s = {n: c.sig("cv_" + n) for n in "step f0 f1 i0 i1 X_mm X_ev Z V_mm V_ev prod acc".split()}
    order = [0, 4, 2, 1, 3]
    W3 = 3 * D
    with ExitStack() as st:
        F = c.sb(st, "cv_F", [P, 2, 3, 2, NF2])
        I = c.sb(st, "cv_I", [P, 2, 3, 2, NF2])
        ab = c.sb(st, "cv_ab", [P, 3, 2, W3])
        Z = c.sb(st, "cv_Z", [P, 2, 2, 2, W3])
        X = c.sb(st, "cv_X", [P, 2, 2, W3])
        Y = c.sb(st, "cv_Y", [P, 2, 2, 2 * D])
        T = c.sb(st, "cv_T", [P, 2, 2, 2 * D])
        ps_X = c.ps(st, "cv_ps_X", [P, 2, 2, 512])
        ps_V = c.ps(st, "cv_ps_V", [P, 2, 2, 512])
        block = st.enter_context(nc.Block())
        real = [f in (0, 4) for f in order]

        def u(j1):
            return UK[:, 2 * j1:2 * j1 + 2, :, :].rearrange("p q b d -> p q (b d)")

        n_V = [sum(1 if r else 2 for r in real[:i]) for i in range(NF1 + 1)]

        @block.sync
        def _(sp):
            for i, f in enumerate(order):
                if i >= 2:
                    sp.wait_ge(s["X_mm"].handle, 4 * (i - 1))
                sp.dma_start(F[:, i % 2, :, :, :], fwd[f, :, :, :].rearrange("m (q p) n -> p m q n", p=P))\
                    .then_inc(s[f"f{i % 2}"].handle, 16)
                if i >= 2:
                    sp.wait_ge(s["V_mm"].handle, n_V[i - 1])
                sp.dma_start(I[:, i % 2, :, :, :], inv[f, :, :, :].rearrange("m (q p) n -> p m q n", p=P))\
                    .then_inc(s[f"i{i % 2}"].handle, 16)

        @block.tensor
        def _(pe):
            COS, SIN, NEG = range(3)

            def forward(i):
                pe.wait_ge(s[f"f{i % 2}"].handle, 16 * (i // 2 + 1))
                pe.wait_ge(s["Z"].handle, i + 1)
                for part in range(2):
                    terms = [(COS, 0), (SIN, 1)] if part == 0 else [(NEG, 0), (COS, 1)]
                    terms = [x for x in terms if not (real[i] and x[1] == 1)]
                    for mt in range(2):
                        n = 4 * i + 2 * part + mt
                        if n >= 2:
                            pe.wait_ge(s["X_ev"].handle, n - 1)
                        for lo, hi in ((0, 512), (512, W3)):
                            for m, (plane, zp) in enumerate(terms):
                                for q in range(2):
                                    last = nc.tensor.matmul(ps_X[:, n % 2, lo // 512, 0:hi - lo],
                                                            F[:, i % 2, plane, q, mt * P:(mt + 1) * P],
                                                            Z[:, i % 2, zp, q, lo:hi], start=(m == 0 and q == 0),
                                                            stop=(m == len(terms) - 1 and q == 1))
                        last.then_inc(s["X_mm"].handle, 1)

            def backward(i):
                pe.wait_ge(s[f"i{i % 2}"].handle, 16 * (i // 2 + 1))
                pe.wait_ge(s["prod"].handle, i + 1)
                for part in range(1 if real[i] else 2):
                    terms = [(COS, 0), (NEG, 1)] if part == 0 else [(SIN, 0), (COS, 1)]
                    n = n_V[i] + part
                    if n >= 2:
                        pe.wait_ge(s["V_ev"].handle, n - 1)
                    for q in range(2):
                        for m, (plane, yp) in enumerate(terms):
                            for mt in range(2):
                                last = nc.tensor.matmul(ps_V[:, n % 2, q, :], I[:, i % 2, plane, mt, q * P:(q + 1) * P],
                                                        Y[:, yp, mt, :], start=(m == 0 and mt == 0),
                                                        stop=(m == 1 and mt == 1))
                    last.then_inc(s["V_mm"].handle, 1)

            forward(0)
            for i in range(NF1):
                if i + 1 < NF1:
                    forward(i + 1)
                backward(i)

        @block.scalar
        def _(act):
            for n in range(4 * NF1):
                i, part, mt = n // 4, n // 2 % 2, n % 2
                act.wait_ge(s["X_mm"].handle, n + 1)
                if n % 4 == 0 and i:
                    act.wait_ge(s["prod"].handle, i)
                nc.scalar.copy(X[:, part, mt, 0:512], ps_X[:, n % 2, 0, :])
                nc.scalar.copy(X[:, part, mt, 512:W3], ps_X[:, n % 2, 1, 0:D]).then_inc(s["X_ev"].handle, 1)

        @block.vector
        def _(dve):
            v = nc.vector
            link = Chain(dve, s["step"])
            add, sub = ALU.add, ALU.subtract

            def transform(i):
                f = order[i]
                zr, zi = Z[:, i % 2, 0, :, :], Z[:, i % 2, 1, :, :]
                if i >= 2:
                    dve.wait_ge(s["X_mm"].handle, 4 * (i - 1))
                if f == 0:
                    link(v.tensor_tensor(ab[:, 0, :, :], u(0), u(2), add))
                    link(v.tensor_tensor(ab[:, 1, :, :], u(1), u(3), add))
                    link(v.tensor_tensor(zr, ab[:, 0, :, :], ab[:, 1, :, :], add))
                elif f == 4:
                    link(v.tensor_tensor(zr, ab[:, 0, :, :], ab[:, 1, :, :], sub))
                elif f == 2:
                    link(v.tensor_tensor(ab[:, 2, :, :], u(3), u(1), sub))
                    link(v.tensor_copy(zi, ab[:, 2, :, :]))
                    link(v.tensor_tensor(zr, u(0), u(2), sub))
                else:
                    sign = -1.0 if f == 1 else 1.0
                    link(v.scalar_tensor_tensor(zr, ab[:, 2, :, :], sign * R2, u(0), ALU.mult, add))
                    link(v.scalar_tensor_tensor(zi, ab[:, 1, :, :], -R2, u(2), ALU.mult, sub if f == 1 else add))
                dve.sem_inc(s["Z"].handle, 1)

            def products(i):
                dve.wait_ge(s["X_ev"].handle, 4 * (i + 1))
                if i:
                    dve.wait_ge(s["V_mm"].handle, n_V[i])

                def part(n):
                    return X[:, n, :, 0:2 * D].rearrange("p m (b d) -> p m b d", b=B)

                def k(n, mt):
                    return bc(X[:, n, mt, 2 * D:W3].unsqueeze(1), [P, B, D])

                for out, ((x0, k0), (x1, k1)), op in ((0, ((0, 0), (1, 1)), sub), (1, ((0, 1), (1, 0)), add)):
                    for mt in range(2):
                        v.tensor_tensor(T[:, 0, mt, :].rearrange("p (b d) -> p b d", b=B), part(x0)[:, mt, :, :], k(k0, mt), ALU.mult)
                        link(v.tensor_tensor(T[:, 1, mt, :].rearrange("p (b d) -> p b d", b=B), part(x1)[:, mt, :, :],
                                             k(k1, mt), ALU.mult))
                    link(v.tensor_tensor(Y[:, out, :, :], T[:, 0, :, :], T[:, 1, :, :], op))
                dve.sem_inc(s["prod"].handle, 1)

            def accumulate(i):
                f = order[i]
                for part in range(1 if real[i] else 2):
                    n = n_V[i] + part
                    dve.wait_ge(s["V_mm"].handle, n + 1)
                    V = ps_V[:, n % 2, :, :].rearrange("p q (b d) -> p q b d", b=B)
                    for j1 in range(4):
                        turn = 2 * np.pi * j1 * f / 8
                        factor = float(np.cos(turn) if part == 0 else -np.sin(turn))
                        out = y[:, 2 * j1:2 * j1 + 2, :, :]
                        if i == 0:
                            link(v.tensor_copy(out, V))
                        elif abs(factor) > 1e-9:
                            link(v.scalar_tensor_tensor(out, V, factor, out, ALU.mult, add))
                    dve.sem_inc(s["V_ev"].handle, 1)

            transform(0)
            transform(1)
            for i in range(NF1):
                products(i)
                if i + 2 < NF1:
                    transform(i + 2)
                accumulate(i)


def L1_join(c, w, UK, y, film_out):
    nc = c.nc
    loaded, step = c.sig("join_loaded"), c.sig("join_step")
    with ExitStack() as st:
        skip = c.sb(st, "join_skip", [P, D])
        block = st.enter_context(nc.Block())

        @block.sync
        def _(sp):
            sp.dma_start(skip[:, :], row(w["D_skip"], P)).then_inc(loaded.handle, 16)

        @block.vector
        def _(dve):
            v = nc.vector
            link = Chain(dve, step)
            dve.wait_ge(loaded.handle, 16)
            for b in range(B):
                tiles = slice(b * TPB, (b + 1) * TPB)
                u = UK[:, :, b, :]
                link(v.tensor_tensor(u, u, bc(skip[:, :].unsqueeze(1), [P, TPB, D]), ALU.mult))
                link(v.tensor_tensor(u, u, y[:, :, b, :], ALU.add))
                link(v.tensor_tensor(u, u, film_out[:, tiles, 0:D], ALU.mult))
                link(v.tensor_tensor(u, u, film_out[:, tiles, D:2 * D], ALU.add))
                link(v.tensor_tensor(c.xn[:, tiles, :], c.xn[:, tiles, :], u, ALU.add))


def add_all(c, src):
    nc = c.nc
    added = c.sig("added")
    with nc.Block() as block:
        @block.vector
        def _(dve):
            nc.vector.tensor_tensor(c.x[:, :, :], c.x[:, :, :], src[:, :, :], ALU.add).then_inc(added.handle, 1)
            dve.wait_ge(added.handle, added.at(1))
    added.base += 1


def L1_xattn(c, w, consts, mask_tok, mask_ctx, xT):
    y = xT[:, :, :].rearrange("p k n -> p (k n)").rearrange("p (i b d) -> p i b d", i=TPB, b=B)
    xt = c.xn
    with ExitStack() as st:
        UK = c.sb(st, "l1_UK", [P, TPB, B + 1, D])
        L1_kernel(c, w, UK)
        film_out = c.sb(st, "l1_film_out", [P, NT, 2 * D])
        with ExitStack() as att:
            M = c.sb(att, "l1_M", [P, KD, B, HJ1])
            mask_row = c.sb(att, "l1_mask_row", [1, B, HJ1])
            VF = c.sb(att, "l1_VF", [JE, B, 2, 2 * D])
            tok_factor = c.sb(att, "l1_tok_factor", [P, NT])
            scores = c.sb(att, "l1_scores", [P, NT, HJ1])
            L1_fold(c, w, mask_tok, mask_ctx, M, mask_row, VF, tok_factor[:, :])
            normalise(c, c.x, xn_out=c.xn, router=(None, HJ1, scores), resident=(M, mask_row))
            ln_stats(c, c.xn)
            normalise(c, c.xn, xn_out=lambda n, b, t: UK[:, t, b, :], affine=(w["g_norm_in"], w["b_norm_in"]))
            L1_modulate(c, scores, tok_factor, VF, UK, film_out)
        L1_convolve(c, consts["dft_fwd"], consts["dft_inv"], UK, y)
        L1_join(c, w, UK, y, film_out)
    ln_stats(c, xt)
    normalise(c, xt, xT_out=xT, affine=(w["g_ffn"], w["b_ffn"]))
    one = {n: w[n].unsqueeze(0) for n in ("W1", "W2", "b1")}
    experts(c, xT, 1, 4 * D, one["W1"], None, one["W2"], one["b1"], ACT.Gelu, lambda t, e: 1.0, xt)
    add_row(c, xt, w["b2"])
    ln_stats(c, xt)
    with ExitStack() as st:
        out = c.sb(st, "l1_out", [P, NT, D])
        normalise(c, xt, xn_out=out, affine=(w["g_norm_out"], w["b_norm_out"]))
        add_all(c, out)


def store(c, out):
    nc = c.nc
    stored = c.sig("stored")
    with nc.Block() as block:
        @block.sync
        def _(sp):
            sp.dma_start(out.rearrange("b (t p) d -> p (b t) d", p=P), c.x[:, :, :]).then_inc(stored.handle, 16)
            sp.wait_ge(stored.handle, 16)


LAYERS = ("L0_xattn", "L0_ffn", "L1_xattn", "L1_ffn", "L2_xattn", "L2_ffn", "L3_xattn", "L3_ffn")


def build(nc, a, out, layers=LAYERS):
    with ExitStack() as ctx:
        c = Core(nc, ctx)
        scratch = nc.dram_tensor("scratch", (B, HJC * P, D), F32).ap()
        setup(c, a["x"], a["ctx_768"], a["mask_BxS_bf1"], a["mask_BxS2_bf1"])
        xT = c.sb(ctx, "xT", [P, KD, B * SEQ])
        for layer in layers:
            w = {n[len(layer) + 1:]: ap for n, ap in a.items() if n.startswith(layer)}
            ln_stats(c, c.x)
            if layer == "L0_xattn":
                wide_attention(c, w["Wq"], w["Wk"], w["Wv"], w["Wo"], w["bo"], scratch)
            elif layer == "L2_xattn":
                wide_attention(c, w["w_q"], w["w_k"], w["w_v"], w["w_out"], w["b_out"], scratch)
            elif layer == "L0_ffn":
                L0_ffn(c, w, xT)
            elif layer == "L2_ffn":
                L2_ffn(c, w, xT)
            elif layer == "L1_xattn":
                L1_xattn(c, w, a, a["mask_BxS_bf1"], a["mask_BxS2_bf1"], xT)
            elif layer == "L3_xattn":
                L3_xattn(c, w, scratch, xT)
            elif layer == "L1_ffn":
                L1_ffn(c, w, xT)
            elif layer == "L3_ffn":
                L3_ffn(c, w, xT)
        store(c, out)


def kernel(**inputs):
    import concourse.bacc as bacc
    from concourse.bass_utils import run_bass_kernel_spmd

    nc = bacc.Bacc("TRN2", target_bir_lowering=False, num_devices=1)
    arrays, aps = {}, {}
    for name, value in (inputs | constants()).items():
        v = np.ascontiguousarray(value)
        if v.dtype == np.bool_:
            v = v.view(np.uint8)
        if v.ndim == 0:
            v = v.reshape(1)
        arrays[f"in_{name}"] = v
        aps[name] = nc.dram_tensor(f"in_{name}", v.shape, mybir.dt.from_np(v.dtype), kind="ExternalInput").ap()
    out = nc.dram_tensor("out", (B, SEQ, D), F32, kind="ExternalOutput").ap()
    build(nc, aps, out)
    result = run_bass_kernel_spmd(nc, [arrays], core_ids=[0])
    return result.results[0]["out"]
```

```python
from contextlib import ExitStack

import numpy as np

import concourse.bass as bass
from concourse import mybir

F32 = mybir.dt.float32
U32 = mybir.dt.uint32
U8 = mybir.dt.uint8
ALU = mybir.AluOpType
ACT = mybir.ActivationFunctionType
AX = mybir.AxisListType

P = 128
B, SEQ, D = 2, 1024, 256
NT = B * SEQ // P
TPB = NT // B
KD = D // P
J, DC = 77, 192
KC = DC // 2
BJ = B * J
CH = 512
NCH = B * SEQ // CH
TPC = CH // P
LN_EPS = 1e-5
MAGIC = 1.5 * 2 ** 23


class Signal:

    def __init__(self, handle):
        self.handle, self.base = handle, 0

    def at(self, n):
        return n + self.base


class Chain:

    def __init__(self, eng, signal, start=0):
        self.eng, self.counted, self.count = eng, signal, start

    def __call__(self, instruction):
        self.count = self.count + 1
        instruction.then_inc(self.counted.handle, 1)
        self.eng.wait_ge(self.counted.handle, self.counted.at(self.count))


class Core:

    def __init__(self, nc, ctx):
        self.nc, self.ctx = nc, ctx
        self.semaphores, self.names = {}, {}

    def sig(self, name):
        if name not in self.semaphores:
            self.semaphores[name] = Signal(self.ctx.enter_context(self.nc.semaphore(name)))
        return self.semaphores[name]

    def unique(self, name):
        self.names[name] = self.names.get(name, 0) + 1
        return f"{name}_{self.names[name]}"

    def sb(self, ctx, name, shape, dt=F32):
        return ctx.enter_context(self.nc.sbuf_tensor(self.unique(name), shape, dt))

    def ps(self, ctx, name, shape, dt=F32):
        return ctx.enter_context(self.nc.psum_tensor(self.unique(name), shape, dt))


def row(v, n):
    return v.rearrange("(o n) -> o n", o=1).to_broadcast([n, v.shape[0]])


def column(v):
    return v.rearrange("(t p) -> p t", p=P)


def bc(ap, shape):
    return ap.to_broadcast(shape)


def setup(c, x, ctx_in, mask_tok, mask_ctx):
    nc = c.nc
    c.x = c.sb(c.ctx, "x", [P, NT, D])
    c.xn = c.sb(c.ctx, "xn", [P, NT, D])
    c.ident = c.sb(c.ctx, "ident", [P, P])
    c.ones = c.sb(c.ctx, "ones", [1, P])
    c.ctxT = c.sb(c.ctx, "ctxT", [KC, 2, BJ])
    c.rstd = c.sb(c.ctx, "rstd", [P, NT])
    c.nmr = c.sb(c.ctx, "nmr", [P, NT])
    loaded, ident_ready = c.sig("setup_loaded"), c.sig("ident_ready")
    transposed, copied = c.sig("setup_transposed"), c.sig("setup_copied")
    with ExitStack() as st:
        ctx_rows = c.sb(st, "ctx_rows", [J, B, DC])
        psT = c.ps(st, "setup_psT", [KC, 4 * J])
        block = st.enter_context(nc.Block())

        @block.sync
        def _(sp):
            sp.dma_start(ctx_rows[:, :, :], ctx_in.rearrange("b j d -> j b d")).then_inc(loaded.handle, 16)
            sp.dma_start(c.x[:, :, :], x.rearrange("b (t p) d -> p (b t) d", p=P)).then_inc(loaded.handle, 16)
            sp.wait_ge(loaded.handle, 32)

        @block.gpsimd
        def _(pool):
            nc.gpsimd.memset(c.ident[:, :], 0.0).then_inc(ident_ready.handle, 1)
            pool.wait_ge(ident_ready.handle, 1)
            nc.gpsimd.affine_select(out=c.ident[:, :], in_=c.ident[:, :], compare_op=ALU.not_equal, fill=1.0,
                                    base=0, pattern=[[-1, P]], channel_multiplier=1).then_inc(ident_ready.handle, 1)
            nc.gpsimd.memset(c.ones[:, :], 1.0).then_inc(ident_ready.handle, 1)

        @block.tensor
        def _(pe):
            pe.wait_ge(ident_ready.handle, 3)
            pe.wait_ge(loaded.handle, 16)
            pe.wait_ge(loaded.handle, 32)
            for b in range(B):
                for k in range(2):
                    last = nc.tensor.transpose(psT[:, (k * B + b) * J:(k * B + b + 1) * J],
                                               ctx_rows[:, b, k * KC:(k + 1) * KC], c.ident[0:J, 0:J])
            last.then_inc(transposed.handle, 1)

        @block.vector
        def _(dve):
            dve.wait_ge(transposed.handle, 1)
            nc.vector.tensor_copy(c.ctxT[:, :, :], psT[:, :].rearrange("p (k n) -> p k n", k=2)).then_inc(copied.handle, 1)
            dve.wait_ge(copied.handle, 1)


def ln_stats(c, src):
    nc = c.nc
    stats_done, var_ready, std_ready, step = c.sig("ln_stats"), c.sig("ln_var"), c.sig("ln_std"), c.sig("ln_step")
    with ExitStack() as st:
        bn = c.sb(st, "ln_bn", [P, NT, 6])
        msum = c.sb(st, "ln_msum", [P, NT])
        diff = c.sb(st, "ln_diff", [P, NT])
        var = c.sb(st, "ln_var", [P, NT])
        std = c.sb(st, "ln_std", [P, NT])
        tmp = c.sb(st, "ln_tmp", [P, NT])
        block = st.enter_context(nc.Block())

        @block.vector
        def _(dve):
            with dve.Fori(0, NT // 4) as i:
                for j in range(4):
                    nc.vector.bn_stats(bn[:, i * 4 + j, :], src[:, i * 4 + j, :]).then_inc(stats_done.handle, 1)
            dve.wait_ge(stats_done.handle, stats_done.at(NT))
            link = Chain(dve, step)
            nc.vector.tensor_tensor(msum[:, :], bn[:, :, 1], bn[:, :, 4], ALU.add).then_inc(stats_done.handle, 1)
            link(nc.vector.tensor_tensor(diff[:, :], bn[:, :, 1], bn[:, :, 4], ALU.subtract))
            nc.vector.tensor_tensor(var[:, :], bn[:, :, 2], bn[:, :, 5], ALU.add).then_inc(stats_done.handle, 1)
            link(nc.vector.tensor_tensor(diff[:, :], diff[:, :], diff[:, :], ALU.mult))
            dve.wait_ge(stats_done.handle, stats_done.at(NT + 2))
            link(nc.vector.tensor_scalar(var[:, :], var[:, :], 1.0 / D, LN_EPS, ALU.mult, ALU.add))
            nc.vector.scalar_tensor_tensor(var[:, :], diff[:, :], 0.25, var[:, :], ALU.mult, ALU.add)\
                .then_inc(var_ready.handle, 1)
            dve.wait_ge(std_ready.handle, std_ready.at(1))
            link(nc.vector.reciprocal(c.rstd[:, :], std[:, :]))
            link(nc.vector.tensor_tensor(tmp[:, :], c.rstd[:, :], c.rstd[:, :], ALU.mult))
            link(nc.vector.tensor_tensor(tmp[:, :], tmp[:, :], var[:, :], ALU.mult))
            link(nc.vector.tensor_scalar(tmp[:, :], tmp[:, :], -0.5, 1.5, ALU.mult, ALU.add))
            link(nc.vector.tensor_tensor(c.rstd[:, :], c.rstd[:, :], tmp[:, :], ALU.mult))
            link(nc.vector.scalar_tensor_tensor(c.nmr[:, :], msum[:, :], -0.5, c.rstd[:, :], ALU.mult, ALU.mult))

        @block.scalar
        def _(act):
            act.wait_ge(var_ready.handle, var_ready.at(1))
            nc.scalar.activation(std[:, :], var[:, :], ACT.Sqrt).then_inc(std_ready.handle, 1)
    stats_done.base += NT + 2
    var_ready.base += 1
    std_ready.base += 1
    step.base += 9


HEADS = 16
HJ = HEADS * J
HJC = (HJ + P - 1) // P
INNER = 1024
NI = INNER // P
SCORE_CUTS = [(0, 512), (512, 1024), (1024, HJ)]


def wide_attention(c, wq, wk, wv, wo, bo, scratch):
    nc = c.nc
    with ExitStack() as st:
        M = c.sb(st, "att_M", [P, KD, B, HJ])
        N = c.sb(st, "att_N", [P, B, HJC, D])
        wide_fold(c, wq, wk, wv, wo, scratch, M, N)
        attention(c, M, None, N, bo, None)


def wide_fold(c, wq, wk, wv, wo, scratch, M, N):
    nc = c.nc
    loaded, filled, mm, ev = c.sig("fold_loaded"), c.sig("fold_filled"), c.sig("fold_mm"), c.sig("fold_ev")
    stored = c.sig("fold_stored")
    TRIPLES = [range(g + odd, min(g + 6, HEADS), 2) for g in range(0, HEADS, 6) for odd in range(2)]
    PAIRS = [range(g + odd, g + 4, 2) for g in range(0, HEADS, 4) for odd in range(2)]
    with ExitStack() as st:
        Wq = c.sb(st, "fold_Wq", [P, KD, INNER])
        Wk = c.sb(st, "fold_Wk", [KC, 2, INNER])
        Wv = c.sb(st, "fold_Wv", [KC, 2, INNER])
        Wo = c.sb(st, "fold_Wo", [P, NI, D])
        KT = c.sb(st, "fold_KT", [P, NI, BJ])
        VT = c.sb(st, "fold_VT", [P, NI, BJ])
        WqT = c.sb(st, "fold_WqT", [P, NI, D])
        rows = c.sb(st, "fold_rows", [J, HEADS, D])
        ps = c.ps(st, "fold_ps", [P, 4, 512])
        block = st.enter_context(nc.Block())
        steps = [("K", m) for m in range(NI)] + [("V", m) for m in range(NI)] + [("Q", m) for m in range(0, NI, 2)]
        steps += [("M", (k, g)) for k in range(KD) for g in TRIPLES]
        steps += [("N", (b, g)) for b in range(B) for g in PAIRS]
        n_kvq = 2 * NI + NI // 2
        n_m = KD * len(TRIPLES)
        n_nb = HEADS // 2

        @block.sync
        def _(sp):
            sp.dma_start(Wk[:, :, :], wk.rearrange("(k p) n -> p k n", p=KC)).then_inc(loaded.handle, 16)
            sp.dma_start(Wv[:, :, :], wv.rearrange("(k p) n -> p k n", p=KC)).then_inc(loaded.handle, 16)
            sp.dma_start(Wq[:, :, :], wq.rearrange("(k p) n -> p k n", p=P)).then_inc(loaded.handle, 16)
            sp.dma_start(Wo[:, :, :], wo.rearrange("(k p) n -> p k n", p=P)).then_inc(loaded.handle, 16)
            for b in range(B):
                sp.wait_ge(ev.handle, ev.at(n_kvq + n_m + (b + 1) * n_nb))
                sp.dma_start(scratch[b, 0:HJ, :].rearrange("(h j) d -> j h d", j=J), rows[:, :, :])\
                    .then_inc(stored.handle, 16)
                sp.wait_ge(stored.handle, stored.at(16 * (3 * b + 1)))
                if b == 0:
                    sp.wait_ge(filled.handle, filled.at(1))
                full = HJ // P
                sp.dma_start(N[:, b, 0:full, :], scratch[b, 0:full * P, :].rearrange("(c p) d -> p c d", p=P))\
                    .then_inc(stored.handle, 16)
                sp.dma_start(N[0:HJ - full * P, b, full, :], scratch[b, full * P:HJ, :]).then_inc(stored.handle, 16)
                sp.wait_ge(stored.handle, stored.at(16 * (3 * b + 3)))

        @block.gpsimd
        def _(pool):
            nc.gpsimd.memset(N[:, :, HJC - 1, :], 0.0).then_inc(filled.handle, 1)

        @block.tensor
        def _(pe):
            pe.wait_ge(loaded.handle, loaded.at(64))
            for n, (kind, at) in enumerate(steps):
                bank = ps[:, n % 4, :]
                if n >= 4:
                    pe.wait_ge(ev.handle, ev.at(n - 3))
                if n == n_kvq:
                    pe.wait_ge(ev.handle, ev.at(n_kvq))
                if kind in "KV":
                    W = Wk if kind == "K" else Wv
                    for k in range(2):
                        last = nc.tensor.matmul(bank[:, 0:BJ], W[:, k, at * P:(at + 1) * P], c.ctxT[:, k, :],
                                                start=(k == 0), stop=(k == 1))
                elif kind == "Q":
                    for m in (at, at + 1):
                        for k in range(KD):
                            o = (m - at) * D + k * P
                            last = nc.tensor.transpose(bank[:, o:o + P], Wq[:, k, m * P:(m + 1) * P], c.ident[:, :])
                elif kind == "M":
                    k, g = at
                    for i, h in enumerate(g):
                        o = 64 * (h % 2)
                        last = nc.tensor.matmul(bank[:, i * BJ:(i + 1) * BJ], WqT[o:o + 64, h // 2, k * P:(k + 1) * P],
                                                KT[o:o + 64, h // 2, :], start=True, stop=True)
                else:
                    b, g = at
                    for i, h in enumerate(g):
                        o = 64 * (h % 2)
                        last = nc.tensor.matmul(bank[0:J, i * D:(i + 1) * D],
                                                VT[o:o + 64, h // 2, b * J:(b + 1) * J], Wo[o:o + 64, h // 2, :],
                                                start=True, stop=True)
                last.then_inc(mm.handle, 1)

        @block.vector
        def _(dve):
            for n, (kind, at) in enumerate(steps):
                bank = ps[:, n % 4, :]
                dve.wait_ge(mm.handle, mm.at(n + 1))
                if kind == "K":
                    last = nc.vector.tensor_scalar(KT[:, at, :], bank[:, 0:BJ], 64 ** -0.5, None, ALU.mult)
                elif kind == "V":
                    last = nc.vector.tensor_copy(VT[:, at, :], bank[:, 0:BJ])
                elif kind == "Q":
                    last = nc.vector.tensor_copy(WqT[:, at:at + 2, :], bank[:, :].rearrange("p (m d) -> p m d", m=2))
                elif kind == "M":
                    k, g = at
                    last = nc.vector.tensor_copy(
                        M[:, k, :, :].rearrange("p b (h j) -> p h b j", j=J)[:, g[0]:g[-1] + 1:2, :, :],
                        bank[:, 0:len(g) * BJ].rearrange("p (h b j) -> p h b j", h=len(g), b=B))
                else:
                    b, g = at
                    if b == 1 and g[0] == 0:
                        dve.wait_ge(stored.handle, stored.at(16))
                    last = nc.vector.tensor_copy(rows[:, g[0]:g[-1] + 1:2, :],
                                                 bank[0:J, :].rearrange("p (h d) -> p h d", h=2))
                last.then_inc(ev.handle, 1)
    loaded.base += 64
    filled.base += 1
    mm.base += len(steps)
    ev.base += len(steps)
    stored.base += 96


def attention(c, M, score_bias, N, bo, oT):
    nc = c.nc
    names = "norm xT_mm xT_ev scores shifted exped probs x_bo PT_mm PT_ev out_mm out_ev".split()
    s = {n: c.sig("att_" + n) for n in names}
    step = c.sig("att_step")
    loaded, bo_loaded = c.sig("att_padded"), c.sig("att_bo_loaded")
    with ExitStack() as st:
        xn = c.sb(st, "att_xn", [P, 2, D])
        xT = c.sb(st, "att_xT", [P, 2, KD, P])
        pr = c.sb(st, "att_probs", [P, 2, HJC * P])
        PT = c.sb(st, "att_PT", [P, 2, HJC, P])
        mx = c.sb(st, "att_mx", [P, 2, HEADS])
        rs = c.sb(st, "att_rs", [P, 2, HEADS])
        bo_row = c.sb(st, "att_bo", [P, D])
        ps_xT = c.ps(st, "att_ps_xT", [P, 512])
        ps_S = c.ps(st, "att_ps_S", [P, 3 * 512])
        ps_PT = c.ps(st, "att_ps_PT", [P, 3 * 512])
        ps_O = c.ps(st, "att_ps_O", [P, 512])
        pad = HJC * P - HJ
        block = st.enter_context(nc.Block())

        def heads(ap):
            return ap.rearrange("p (h j) -> p h j", j=J)

        if bo is not None:
            @block.sync
            def _(sp):
                sp.dma_start(bo_row[:, :], row(bo, P)).then_inc(bo_loaded.handle, 16)

        @block.tensor
        def _(pe):
            def front(n, j, b):
                pe.wait_ge(s["norm"].handle, s["norm"].at(n + 1))
                for k in range(KD):
                    last = nc.tensor.transpose(ps_xT[:, k * P:(k + 1) * P], xn[:, j, k * P:(k + 1) * P], c.ident[:, :])
                last.then_inc(s["xT_mm"].handle, 1)
                pe.wait_ge(s["xT_ev"].handle, s["xT_ev"].at(n + 1))
                pe.wait_ge(s["shifted"].handle, s["shifted"].at(n + 1))
                for lo, hi in SCORE_CUTS:
                    for k in range(KD):
                        last = nc.tensor.matmul(ps_S[:, lo:hi], xT[:, j, k, :], M[:, k, b, lo:hi], start=(k == 0),
                                                stop=(k == KD - 1 and score_bias is None))
                    if score_bias is not None:
                        last = nc.tensor.matmul(ps_S[:, lo:hi], c.ones[0:1, :], score_bias[0:1, b, lo:hi],
                                                start=False, stop=True)
                last.then_inc(s["scores"].handle, 1)

            def back(n, j, b):
                pe.wait_ge(s["probs"].handle, s["probs"].at(n + 1))
                for k in range(HJC):
                    last = nc.tensor.transpose(ps_PT[:, k * P:(k + 1) * P], pr[:, j, k * P:(k + 1) * P], c.ident[:, :])
                last.then_inc(s["PT_mm"].handle, 1)
                pe.wait_ge(s["PT_ev"].handle, s["PT_ev"].at(n + 1))
                pe.wait_ge(s["out_ev"].handle, s["out_ev"].at(n + 1))
                if oT is None:
                    for k in range(HJC):
                        last = nc.tensor.matmul(ps_O[:, 0:D], PT[:, j, k, :], N[:, b, k, :],
                                                start=(k == 0), stop=(k == HJC - 1))
                else:
                    for half in range(KD):
                        ks = range(half * HJ // 2 // P, ((half + 1) * HJ // 2 + P - 1) // P)
                        for k in ks:
                            last = nc.tensor.matmul(ps_O[:, half * P:(half + 1) * P],
                                                    N[:, b, k, half * P:(half + 1) * P], PT[:, j, k, :],
                                                    start=(k == ks[0]), stop=(k == ks[-1]))
                last.then_inc(s["out_mm"].handle, 1)

            pe.wait_ge(loaded.handle, loaded.at(1))
            front(0, 0, 0)
            for b in range(B):
                with pe.Fori(0, TPB // 2 - 1) as i:
                    for j in range(2):
                        front(i * 2 + (b * TPB + j + 1), 1 - j, b)
                        back(i * 2 + (b * TPB + j), j, b)
                front(b * TPB + TPB - 1, 1, b)
                back(b * TPB + TPB - 2, 0, b)
                if b + 1 < B:
                    front(b * TPB + TPB, 0, b + 1)
                back(b * TPB + TPB - 1, 1, b)

        @block.vector
        def _(dve):
            link = Chain(dve, step)

            def norm(n, j):
                nc.vector.tensor_scalar(xn[:, j, :], c.x[:, n, :], c.rstd[:, bass.ts(n, 1)], c.nmr[:, bass.ts(n, 1)],
                                        ALU.mult, ALU.add).then_inc(s["norm"].handle, 1)

            def softmax(n, j, ahead):
                dve.wait_ge(s["scores"].handle, s["scores"].at(n + 1))
                link(nc.vector.tensor_reduce(mx[:, j, :], heads(ps_S[:, 0:HJ]), AX.X, ALU.max))
                nc.vector.tensor_tensor(heads(pr[:, j, 0:HJ]), heads(ps_S[:, 0:HJ]),
                                        bc(mx[:, j, :].unsqueeze(2), [P, HEADS, J]), ALU.subtract)\
                    .then_inc(s["shifted"].handle, 1)
                if ahead:
                    norm(n + 2, j)
                dve.wait_ge(s["exped"].handle, s["exped"].at(n + 1))
                link(nc.vector.tensor_reduce(rs[:, j, :], heads(pr[:, j, 0:HJ]), AX.X, ALU.add))
                link(nc.vector.reciprocal(rs[:, j, :], rs[:, j, :]))
                nc.vector.tensor_tensor(heads(pr[:, j, 0:HJ]), heads(pr[:, j, 0:HJ]),
                                        bc(rs[:, j, :].unsqueeze(2), [P, HEADS, J]), ALU.mult)\
                    .then_inc(s["probs"].handle, 1)

            def take(n):
                dve.wait_ge(s["out_mm"].handle, s["out_mm"].at(n + 1))
                if oT is None:
                    dve.wait_ge(s["x_bo"].handle, s["x_bo"].at(n + 1))
                    nc.vector.tensor_tensor(c.x[:, n, :], c.x[:, n, :], ps_O[:, 0:D], ALU.add)\
                        .then_inc(s["out_ev"].handle, 1)
                else:
                    nc.vector.tensor_copy(oT[:, :, bass.ts(n, P)], ps_O[:, 0:D].rearrange("p (k n) -> p k n", k=KD))\
                        .then_inc(s["out_ev"].handle, 1)

            dve.sem_inc(s["shifted"].handle, 1)
            dve.sem_inc(s["out_ev"].handle, 1)
            norm(0, 0)
            norm(1, 1)
            softmax(0, 0, True)
            last_rolled = NT - 4
            with dve.Fori(0, last_rolled // 2) as i:
                link.count = i * 6 + 3
                for j in (1, 0):
                    n = i * 2 + (2 - j)
                    softmax(n, j, True)
                    take(n - 1)
            link.count = 3 + 3 * last_rolled
            for n in range(last_rolled + 1, NT):
                softmax(n, n % 2, n + 2 < NT)
                take(n - 1)
            take(NT - 1)
            dve.wait_ge(s["out_ev"].handle, s["out_ev"].at(NT + 1))

        if bo is not None:
            @block.gpsimd
            def _(pool):
                nc.gpsimd.memset(pr[:, :, HJ:], 0.0).then_inc(loaded.handle, 1)
                pool.wait_ge(bo_loaded.handle, bo_loaded.at(16))
                with pool.Fori(0, NT) as n:
                    pool.wait_ge(s["norm"].handle, s["norm"].at(n + 1))
                    nc.gpsimd.tensor_tensor(c.x[:, n, :], c.x[:, n, :], bo_row[:, :], ALU.add)\
                        .then_inc(s["x_bo"].handle, 1)
        else:
            @block.gpsimd
            def _(pool):
                nc.gpsimd.memset(pr[:, :, HJ:], 0.0).then_inc(loaded.handle, 1)

        @block.scalar
        def _(act):
            def copy_xT(n, j):
                act.wait_ge(s["xT_mm"].handle, s["xT_mm"].at(n + 1))
                nc.scalar.copy(xT[:, j, :, :], ps_xT[:, 0:D].rearrange("p (k n) -> p k n", k=KD))\
                    .then_inc(s["xT_ev"].handle, 1)

            def exp_and_copy(n, j, ahead):
                act.wait_ge(s["shifted"].handle, s["shifted"].at(n + 2))
                nc.scalar.activation(pr[:, j, 0:HJ], pr[:, j, 0:HJ], ACT.Exp).then_inc(s["exped"].handle, 1)
                if ahead:
                    copy_xT(n + 1, 1 - j)
                act.wait_ge(s["PT_mm"].handle, s["PT_mm"].at(n + 1))
                nc.scalar.copy(PT[:, j, :, :], ps_PT[:, 0:HJC * P].rearrange("p (k n) -> p k n", k=HJC))\
                    .then_inc(s["PT_ev"].handle, 1)

            copy_xT(0, 0)
            with act.Fori(0, NT // 2 - 1) as i:
                for j in range(2):
                    exp_and_copy(i * 2 + j, j, True)
            exp_and_copy(NT - 2, 0, True)
            exp_and_copy(NT - 1, 1, False)
    for name, one in s.items():
        one.base += NT
    if bo is None:
        s["x_bo"].base -= NT
    s["shifted"].base += 1
    s["out_ev"].base += 1
    step.base += 3 * NT
    loaded.base += 1
    bo_loaded.base += 16 if bo is not None else 0


def ring(eng, signal, n):
    eng.sem_inc(signal.handle, n)


def normalise(c, src, xn_out=None, xT_out=None, affine=None, router=None, resident=None):
    nc = c.nc
    names = "loaded rows T_mm T_ev L_mm L_ev step".split()
    s = {n: c.sig("norm_" + n) for n in names}
    with ExitStack() as st:
        xb = c.sb(st, "norm_xb", [P, 2, D])
        xTb = c.sb(st, "norm_xTb", [P, 2, KD, P])
        gb = c.sb(st, "norm_gb", [P, 2, D])
        ps_T = c.ps(st, "norm_ps_T", [P, 2, 512])
        ps_L = c.ps(st, "norm_ps_L", [P, 2, 512])
        n_loads = 0
        if router is not None:
            w, n_r, logits = router
            wr = c.sb(st, "norm_wr", [P, KD, n_r]) if resident is None else None
        block = st.enter_context(nc.Block())
        transposing = xT_out is not None or router is not None
        per_pair = 4 if affine is not None else 0
        if affine is not None:
            n_loads += 2
        if router is not None and resident is None:
            n_loads += KD

        @block.sync
        def _(sp):
            if affine is not None:
                for i in range(2):
                    sp.dma_start(gb[:, i, :], row(affine[i], P)).then_inc(s["loaded"].handle, 16)
            if router is not None and resident is None:
                for k in range(KD):
                    sp.dma_start(wr[:, k, :], w[k * P:(k + 1) * P, :], allow_slow_non_contiguous=True)\
                        .then_inc(s["loaded"].handle, 16)
            if n_loads:
                sp.wait_ge(s["loaded"].handle, s["loaded"].at(16 * n_loads))

        @block.vector
        def _(dve):
            link = Chain(dve, s["step"])
            if affine is not None:
                dve.wait_ge(s["loaded"].handle, s["loaded"].at(16 * n_loads))

            def tile_pair(i, b):
                link.count = i * per_pair + b * (TPB // 2) * per_pair
                for j in range(2):
                    n = i * 2 + (b * TPB + j)
                    kept = None
                    if xn_out is not None:
                        kept = xn_out(n, b, i * 2 + j) if callable(xn_out) else xn_out[:, n, :]
                    rows = xb[:, j, :]
                    if transposing:
                        dve.wait_ge(s["T_mm"].handle, s["T_mm"].at(n + 1))
                    if affine is not None:
                        link(nc.vector.tensor_scalar(rows, src[:, n, :], c.rstd[:, bass.ts(n, 1)],
                                                     c.nmr[:, bass.ts(n, 1)], ALU.mult, ALU.add))
                        link(nc.vector.tensor_tensor(rows, rows, gb[:, 0, :], ALU.mult))
                        if kept is not None:
                            nc.vector.tensor_tensor(kept, rows, gb[:, 1, :], ALU.add)\
                                .then_inc(s["rows"].handle, 1)
                        if transposing:
                            nc.vector.tensor_tensor(rows, rows, gb[:, 1, :], ALU.add).then_inc(s["rows"].handle, 1)
                    else:
                        for out in ([kept] if kept is not None else []) + ([rows] if transposing else []):
                            nc.vector.tensor_scalar(out, src[:, n, :], c.rstd[:, bass.ts(n, 1)],
                                                    c.nmr[:, bass.ts(n, 1)], ALU.mult, ALU.add)\
                                .then_inc(s["rows"].handle, 1)

            for b in range(B):
                with dve.Fori(0, TPB // 2) as i:
                    tile_pair(i, b)
        per_tile = (1 if xn_out is not None else 0) + (1 if transposing else 0)

        if transposing:
            @block.tensor
            def _(pe):
                ring(pe, s["T_mm"], 2)
                ring(pe, s["L_mm"], 2)
                if router is not None and n_loads:
                    pe.wait_ge(s["loaded"].handle, s["loaded"].at(16 * n_loads))

                def route(n, j, b):
                    pe.wait_ge(s["T_ev"].handle, s["T_ev"].at(n + 3))
                    pe.wait_ge(s["L_ev"].handle, s["L_ev"].at(n + 1))
                    for k in range(KD):
                        right = wr[:, k, :] if resident is None else resident[0][:, k, b, :]
                        last = nc.tensor.matmul(ps_L[:, j, 0:n_r], xTb[:, j, k, :], right,
                                                start=(k == 0), stop=(k == KD - 1 and resident is None))
                    if resident is not None:
                        last = nc.tensor.matmul(ps_L[:, j, 0:n_r], c.ones[0:1, :], resident[1][0:1, b, :],
                                                start=False, stop=True)
                    last.then_inc(s["L_mm"].handle, 1)

                def tile_pair(i, b):
                    for j in range(2):
                        n = i * 2 + (b * TPB + j)
                        pe.wait_ge(s["rows"].handle, s["rows"].at((n + 1) * per_tile))
                        pe.wait_ge(s["T_ev"].handle, s["T_ev"].at(n + 1))
                        for k in range(KD):
                            last = nc.tensor.transpose(ps_T[:, j, k * P:(k + 1) * P], xb[:, j, k * P:(k + 1) * P],
                                                       c.ident[:, :])
                        last.then_inc(s["T_mm"].handle, 1)
                    if router is not None:
                        for j in range(2):
                            route(i * 2 + (b * TPB + j), j, b)

                for b in range(B):
                    with pe.Fori(0, TPB // 2) as i:
                        tile_pair(i, b)

            @block.scalar
            def _(act):
                ring(act, s["T_ev"], 2)
                ring(act, s["L_ev"], 2)
                with act.Fori(0, NT // 2) as i:
                    for j in range(2):
                        n = i * 2 + j
                        act.wait_ge(s["T_mm"].handle, s["T_mm"].at(n + 3))
                        tile = ps_T[:, j, 0:D].rearrange("p (k n) -> p k n", k=KD)
                        if xT_out is not None:
                            one = nc.scalar.copy(xT_out[:, :, bass.ts(n, P)], tile)
                        if router is not None:
                            act.wait_ge(s["L_mm"].handle, s["L_mm"].at(n + 1))
                            one = nc.scalar.copy(xTb[:, j, :, :], tile)
                        one.then_inc(s["T_ev"].handle, 1)
                    if router is not None:
                        for j in range(2):
                            n = i * 2 + j
                            act.wait_ge(s["L_mm"].handle, s["L_mm"].at(n + 3))
                            nc.scalar.copy(logits[:, n, :], ps_L[:, j, 0:n_r]).then_inc(s["L_ev"].handle, 1)
    s["loaded"].base += 16 * n_loads
    s["rows"].base += per_tile * NT
    if transposing:
        for n in ("T_mm", "T_ev"):
            s[n].base += NT + 2
        for n in ("L_mm", "L_ev"):
            s[n].base += 2 + (NT if router is not None else 0)
    if affine is not None:
        s["step"].base += 2 * NT


def each_expert(eng, n_exp, body):
    if n_exp <= 2:
        for e in range(n_exp):
            body(e, e, 1)
        return
    with eng.Fori(0, n_exp // 2) as i:
        for s in range(2):
            body(i * 2 + s, s, i + 1)


def experts(c, xT, n_exp, F, w1, w3, w2, b1, func, gate, acc, chunks=range(NCH), resident=None,
            meanwhile=None):
    nc = c.nc
    FT = F // P
    swiglu = w3 is not None
    names = "exp_H_mm exp_sil exp_H_ev exp_O_mm exp_O_ev exp_slot0 exp_slot1".split()
    H_mm, sil_done, H_ev, O_mm, O_ev, *slot = [c.sig(n) for n in names]
    n_w = 0 if resident else 2 + (w3 is not None) + (b1 is not None)
    n_ch = len(chunks)
    per_expert = n_ch * TPC
    n_slots = min(n_exp, 2)
    with ExitStack() as st:
        if resident:
            W1, W2, b1c = resident
        else:
            W1 = c.sb(st, "exp_W1", [P, n_slots, KD, F])
            W2 = c.sb(st, "exp_W2", [P, n_slots, FT, D])
            b1c = c.sb(st, "exp_b1c", [P, n_slots, FT]) if b1 is not None else None
        W3 = c.sb(st, "exp_W3", [P, n_slots, KD, F]) if swiglu else None
        hT = c.sb(st, "exp_hT", [P, 2, FT, CH])
        sil = c.sb(st, "exp_sil", [P, 2, CH]) if swiglu else None
        ps_H = c.ps(st, "exp_ps_H", [P, 2, 2 if swiglu else 1, CH])
        ps_O = c.ps(st, "exp_ps_O", [P, 2, 512])
        block = st.enter_context(nc.Block())

        if not resident:
            @block.sync
            def _(sp):
                def load(e, s, use):
                    if n_exp > 1:
                        sp.wait_ge(O_mm.handle, O_mm.at((e + 1) * per_expert))
                    sp.dma_start(W1[:, s, :, :], w1[e, :, :].rearrange("(k p) f -> p k f", p=P)).then_inc(slot[s].handle, 16)
                    if swiglu:
                        sp.dma_start(W3[:, s, :, :], w3[e, :, :].rearrange("(k p) f -> p k f", p=P))\
                            .then_inc(slot[s].handle, 16)
                    sp.dma_start(W2[:, s, :, :], w2[e, :, :].rearrange("(k p) f -> p k f", p=P)).then_inc(slot[s].handle, 16)
                    if b1 is not None:
                        sp.dma_start(b1c[:, s, :], b1[e, :].rearrange("(f p) -> p f", p=P),
                                     allow_slow_non_contiguous=True).then_inc(slot[s].handle, 16)

                each_expert(sp, n_exp, load)
                for s in range(n_slots):
                    sp.wait_ge(slot[s].handle, slot[s].at(16 * n_w * n_exp // n_slots))

        @block.tensor
        def _(pe):
            ring(pe, O_mm, 2 * per_expert)

            def up(e, s, i):
                g = e * n_ch + i
                at = chunks[i] * CH
                for f in range(FT):
                    pe.wait_ge(H_ev.handle, H_ev.at(g * FT + (f + 1)))
                    for m, W in enumerate([W1, W3] if swiglu else [W1]):
                        for k in range(KD):
                            last = nc.tensor.matmul(ps_H[:, f % 2, m, :], W[:, s, k, f * P:(f + 1) * P],
                                                    xT[:, k, at:at + CH], start=(k == 0), stop=(k == KD - 1))
                    last.then_inc(H_mm.handle, 1)

            def down(e, s, i):
                g = e * n_ch + i
                pe.wait_ge(H_ev.handle, H_ev.at((g + 1) * FT + 2))
                for j in range(TPC):
                    pe.wait_ge(O_ev.handle, O_ev.at(g * TPC + (j + 1)))
                    for f in range(FT):
                        last = nc.tensor.matmul(ps_O[:, j % 2, 0:D], hT[:, i % 2, f, j * P:(j + 1) * P], W2[:, s, f, :],
                                                start=(f == 0), stop=(f == FT - 1))
                    last.then_inc(O_mm.handle, 1)

            def one(e, s, use):
                if n_w:
                    pe.wait_ge(slot[s].handle, slot[s].at(use * (16 * n_w)))
                up(e, s, 0)
                for i in range(1, n_ch):
                    up(e, s, i)
                    down(e, s, i - 1)
                down(e, s, n_ch - 1)

            each_expert(pe, n_exp, one)

        @block.scalar
        def _(act):
            if not swiglu:
                ring(act, H_ev, 2)

            def one(e, s, use):
                if b1 is not None and n_w:
                    act.wait_ge(slot[s].handle, slot[s].at(use * (16 * n_w)))
                for i in range(n_ch):
                    for f in range(FT):
                        act.wait_ge(H_mm.handle, H_mm.at((e * n_ch + i) * FT + (f + 1)))
                        if swiglu:
                            nc.scalar.activation(sil[:, f % 2, :], ps_H[:, f % 2, 0, :], func).then_inc(sil_done.handle, 1)
                        else:
                            nc.scalar.activation(hT[:, i % 2, f, :], ps_H[:, f % 2, 0, :], func, bias=b1c[:, s, f:f + 1])\
                                .then_inc(H_ev.handle, 1)

            each_expert(act, n_exp, one)

        @block.vector
        def _(dve):
            if swiglu:
                ring(dve, H_ev, 2)
            ring(dve, O_ev, 2)

            def product(e, i):
                for f in range(FT):
                    dve.wait_ge(sil_done.handle, sil_done.at((e * n_ch + i) * FT + (f + 1)))
                    nc.vector.tensor_tensor(hT[:, i % 2, f, :], sil[:, f % 2, :], ps_H[:, f % 2, 1, :], ALU.mult)\
                        .then_inc(H_ev.handle, 1)
                    if meanwhile:
                        meanwhile(dve, (e * n_ch + i) * FT + f, True)

            def take(e, i):
                for j in range(TPC):
                    t = chunks[i] * TPC + j
                    dve.wait_ge(O_mm.handle, O_mm.at((e * n_ch + i) * TPC + (2 * per_expert + j + 1)))
                    nc.vector.scalar_tensor_tensor(acc[:, t, :], ps_O[:, j % 2, 0:D], gate(t, e), acc[:, t, :],
                                                   ALU.mult, ALU.add).then_inc(O_ev.handle, 1)
                    if meanwhile:
                        meanwhile(dve, (e * n_ch + i) * TPC + j, False)

            def one(e, s, use):
                if swiglu:
                    product(e, 0)
                for i in range(n_ch):
                    if swiglu and i + 1 < n_ch:
                        product(e, i + 1)
                    take(e, i)

            each_expert(dve, n_exp, one)
            dve.wait_ge(O_ev.handle, O_ev.at(n_exp * n_ch * TPC + 2))
    for one, n in ((H_mm, FT), (H_ev, FT), (O_mm, TPC), (O_ev, TPC)):
        one.base += n * n_exp * n_ch
    sil_done.base += FT * n_exp * n_ch if swiglu else 0
    H_ev.base += 2
    O_ev.base += 2
    O_mm.base += 2 * per_expert
    for one in slot[:n_slots]:
        one.base += 16 * n_w * n_exp // n_slots


class Router:

    def __init__(self, c, st, n_exp, dve_signal):
        self.c, self.nc, self.E = c, c.nc, n_exp
        self.iota = c.sb(st, "rt_iota", [P, NT, n_exp])
        self.cand = c.sb(st, "rt_cand", [P, NT, n_exp])

    def wide(self, small):
        return bc(small.unsqueeze(2), [P, NT, self.E])

    def first_max(self, link, scores, value, onehot, index):
        v = self.nc.vector
        link(v.tensor_reduce(value, scores, AX.X, ALU.max))
        link(v.tensor_tensor(self.cand[:, :, :], scores, self.wide(value), ALU.is_equal))
        link(v.scalar_tensor_tensor(self.cand[:, :, :], self.cand[:, :, :], -64.0, self.iota[:, :, :], ALU.mult, ALU.add))
        link(v.tensor_reduce(index, self.cand[:, :, :], AX.X, ALU.min))
        link(v.tensor_tensor(onehot, self.cand[:, :, :], self.wide(index), ALU.is_equal))

    def softmax_divide(self, link, scores, value):
        v = self.nc.vector
        link(v.tensor_reduce(value, scores, AX.X, ALU.add))
        link(v.reciprocal(value, value))
        link(v.tensor_tensor(scores, scores, self.wide(value), ALU.mult))


def slots_of(E, mode):
    if mode == "top1":
        return B * SEQ // E, E
    if mode == "capacity":
        return -(-(B * SEQ * 2 * 5) // (E * 4)), E
    unit = 2 * P
    return unit, E + (2 * B * SEQ - E) // unit


ROOM = 29 * 256
NO_ROW = float(1 << 20)


def route(c, logits, E, mode, bias, extra, plan, meanwhile=None):
    nc = c.nc
    to, back_from, gate, unit_expert = plan
    unit, n_units = slots_of(E, mode)
    n_k = 1 if mode == "top1" else 2
    FAR, TAKEN = -1.0e30, -3.0e38
    loaded, iota, ready, exped, step = [c.sig("rt_" + n) for n in ("loaded", "iota", "ready", "exped", "step")]
    mm, asked = c.sig("rt_mm"), c.sig("rt_asked")
    steps, taken_out = [], [0]
    with ExitStack() as st:
        r = Router(c, st, E, step)
        probs = c.sb(st, "rt_probs", [P, NT, E])
        oh = c.sb(st, "rt_oh", [P, 2, NT, E])
        mask = c.sb(st, "rt_mask", [P, NT, E])
        pos = c.sb(st, "rt_pos", [P, NT, E])
        v = c.sb(st, "rt_v", [P, 2, NT])
        idx = c.sb(st, "rt_idx", [P, NT])
        some = c.sb(st, "rt_some", [P, NT])
        base = c.sb(st, "rt_base", [P, E])
        small = c.sb(st, "rt_small", [P, 2, E])
        before = c.sb(st, "rt_before", [P, E, E])
        units = c.sb(st, "rt_units", [P, 2, n_units])
        cmp = c.sb(st, "rt_cmp", [P, n_units, E])
        bias_row = c.sb(st, "rt_bias", [P, E])
        tri = c.sb(st, "rt_tri", [P, 2, P])
        eight = c.sb(st, "rt_eight", [E, 8])
        wT = c.sb(st, "rt_wT", [E, B * SEQ]) if mode == "capacity" else None
        choosing = ExitStack()
        ps_w = c.ps(choosing, "rt_ps_w", [P, 4, 512]) if mode == "capacity" else None
        block = choosing.enter_context(nc.Block())

        @block.sync
        def _(sp):
            if bias is not None:
                sp.dma_start(bias_row[:, :], row(bias, P)).then_inc(loaded.handle, 16)

        @block.gpsimd
        def _(pool):
            g = nc.gpsimd
            g.iota(r.iota[:, :, :], pattern=[[0, NT], [1, E]], base=0, channel_multiplier=0,
                   allow_small_or_imprecise_dtypes=True).then_inc(iota.handle, 1)
            pool.wait_ge(iota.handle, iota.at(1))
            g.memset(tri[:, :, :], 1.0).then_inc(iota.handle, 1)
            pool.wait_ge(iota.handle, iota.at(2))
            g.affine_select(out=tri[:, 0, :], in_=tri[:, 0, :], compare_op=ALU.is_ge, fill=0.0,
                            base=0, pattern=[[1, P]], channel_multiplier=-1).then_inc(iota.handle, 1)
            g.memset(before[:, :, :], 1.0).then_inc(iota.handle, 1)
            pool.wait_ge(iota.handle, iota.at(4))
            g.affine_select(out=before[:, :, :], in_=before[:, :, :], compare_op=ALU.is_gt, fill=0.0,
                            base=0, pattern=[[1, E], [-1, E]], channel_multiplier=0).then_inc(iota.handle, 1)
            g.iota(units[:, 0, :], pattern=[[1, n_units]], base=0, channel_multiplier=0,
                   allow_small_or_imprecise_dtypes=True).then_inc(iota.handle, 1)

        @block.scalar
        def _(act):
            act.wait_ge(ready.handle, ready.at(1))
            nc.scalar.activation(probs[:, :, :], probs[:, :, :], ACT.Exp).then_inc(exped.handle, 1)

        if mode == "capacity":
            @block.tensor
            def _(pe):
                pe.wait_ge(asked.handle, asked.at(1))
                for t in range(NT):
                    last = nc.tensor.transpose(ps_w[0:E, t // 4, (t % 4) * P:(t % 4 + 1) * P], probs[:, t, :], c.ident[:, :])
                last.then_inc(mm.handle, 1)

        @block.vector
        def _(dve):
            link = Chain(dve, step)
            V = nc.vector
            bias_wide = bc(bias_row[:, :].unsqueeze(1), [P, NT, E])
            tt, ts, stt = V.tensor_tensor, V.tensor_scalar, V.scalar_tensor_tensor
            dve.wait_ge(iota.handle, iota.at(6))
            if bias is not None:
                dve.wait_ge(loaded.handle, loaded.at(16))
            if mode == "top1":
                link(tt(logits[:, :, :], logits[:, :, :], bias_wide, ALU.add))
            link(V.tensor_reduce(v[:, 0, :], logits[:, :, :], AX.X, ALU.max))
            tt(probs[:, :, :], logits[:, :, :], r.wide(v[:, 0, :]), ALU.subtract).then_inc(ready.handle, 1)
            dve.wait_ge(exped.handle, exped.at(1))
            r.softmax_divide(link, probs[:, :, :], v[:, 0, :])
            if mode == "capacity":
                link(tt(probs[:, :, :], probs[:, :, :], bias_wide, ALU.add))
            r.first_max(link, probs[:, :, :], v[:, 0, :], oh[:, 0, :, :], idx[:, :])
            if mode == "top1":
                link(V.tensor_copy(mask[:, :, :], oh[:, 0, :, :]))
                link(V.tensor_copy(extra, v[:, 0, :]))
                link(V.tensor_copy(gate[:, 0, :], v[:, 0, :]))
            else:
                link(stt(probs[:, :, :], oh[:, 0, :, :], FAR, probs[:, :, :], ALU.mult, ALU.add))
                r.first_max(link, probs[:, :, :], v[:, 1, :], oh[:, 1, :, :], idx[:, :])
                link(tt(mask[:, :, :], oh[:, 0, :, :], oh[:, 1, :, :], ALU.add))
            if mode == "top2":
                link(tt(some[:, :], v[:, 0, :], v[:, 1, :], ALU.add))
                link(ts(some[:, :], some[:, :], 1e-10, None, ALU.max))
                link(V.reciprocal(some[:, :], some[:, :]))
                for k in range(2):
                    link(tt(gate[:, k, :], v[:, k, :], some[:, :], ALU.mult))
            if mode == "capacity":
                link(tt(probs[:, :, :], logits[:, :, :], mask[:, :, :], ALU.mult))
                link(ts(pos[:, :, :], mask[:, :, :], 1.0, -FAR, ALU.subtract, ALU.mult))
                tt(probs[:, :, :], probs[:, :, :], pos[:, :, :], ALU.add).then_inc(asked.handle, 1)
                dve.wait_ge(mm.handle, mm.at(1))
                link(V.tensor_copy(wT[:, :], ps_w[0:E, :, :].rearrange("e a n -> e (a n)")))
            steps.append(link.count)

        choosing.close()
        if mode == "capacity":
            halves = 2 * (unit // 8)

            def take_out(dve, n, hidden):
                link = Chain(dve, step, steps[0] + taken_out[0])
                share = (1 + n % 2) if hidden else 1
                for _ in range(min(share, halves - taken_out[0])):
                    if taken_out[0] % 2 == 0:
                        link(nc.vector.max(eight[:, :], wT[:, :]))
                    else:
                        link(nc.vector.match_replace(wT[:, :], eight[:, :], wT[:, :], TAKEN))
                    taken_out[0] += 1

            meanwhile(take_out)
            assert taken_out[0] == halves, taken_out
            steps[0] += halves
        ps = c.ps(st, "rt_ps", [P, 512])
        ps_g = c.ps(st, "rt_ps_g", [P, 512])
        ps_n = c.ps(st, "rt_ps_n", [P, 512])
        block = st.enter_context(nc.Block())

        @block.tensor
        def _(pe):
            n_asked = 0
            if mode == "capacity":
                n_asked = 2
                pe.wait_ge(asked.handle, asked.at(2))
                for t in range(NT):
                    last = nc.tensor.transpose(ps_g[:, t * E:(t + 1) * E], wT[:, t * P:(t + 1) * P], c.ident[0:E, 0:E])
                last.then_inc(mm.handle, 1)
            pe.wait_ge(asked.handle, asked.at(n_asked + 1))
            nc.tensor.matmul(ps[:, 0:NT * E], tri[:, 0, :], mask[:, :, :], start=True, stop=False)
            for t in range(1, NT):
                nc.tensor.matmul(ps[:, t * E:NT * E], tri[:, 1, :], mask[:, 0:NT - t, :],
                                 start=False, stop=(t == NT - 1))
            for t in range(NT):
                last = nc.tensor.matmul(ps_n[:, 0:E], tri[:, 1, :], mask[:, t, :], start=(t == 0), stop=(t == NT - 1))
            last.then_inc(mm.handle, 1)

        @block.vector
        def _(dve):
            link = Chain(dve, step, steps[0])
            V = nc.vector
            tt, ts, stt = V.tensor_tensor, V.tensor_scalar, V.scalar_tensor_tensor
            if mode == "capacity":
                ts(wT[:, :], wT[:, :], 2 * FAR, None, ALU.is_lt).then_inc(asked.handle, 1)
                dve.wait_ge(mm.handle, mm.at(2))
                taken = ps_g[:, 0:NT * E].rearrange("p (t e) -> p t e", e=E)
                for k in range(2):
                    link(tt(oh[:, k, :, :], oh[:, k, :, :], taken, ALU.mult))
                    link(tt(pos[:, :, :], oh[:, k, :, :], logits[:, :, :], ALU.mult))
                    link(V.tensor_reduce(gate[:, k, :], pos[:, :, :], AX.X, ALU.add))
                link(tt(mask[:, :, :], oh[:, 0, :, :], oh[:, 1, :, :], ALU.add))
            dve.sem_inc(asked.handle, 1)
            if mode != "top2":
                link(ts(base[:, :], r.iota[:, 0, :], float(unit), None, ALU.mult))
            dve.wait_ge(mm.handle, mm.at(3 if mode == "capacity" else 1))
            link(V.tensor_copy(pos[:, :, :], ps[:, 0:NT * E].rearrange("p (t e) -> p t e", e=E)))
            if mode == "top1":
                link(ts(mask[:, :, :], pos[:, :, :], float(unit), None, ALU.is_lt))
                link(tt(oh[:, 0, :, :], oh[:, 0, :, :], mask[:, :, :], ALU.mult))
            if mode == "top2":
                link(ts(small[:, 0, :], ps_n[:, 0:E], 1.0 / unit, (unit / 2 - 0.5) / unit, ALU.mult, ALU.add))
                link(ts(small[:, 0, :], small[:, 0, :], MAGIC, MAGIC, ALU.add, ALU.subtract))
                link(tt(before[:, :, :], before[:, :, :], bc(small[:, 0, :].unsqueeze(1), [P, E, E]), ALU.mult))
                link(V.tensor_reduce(small[:, 1, :], before[:, :, :], AX.X, ALU.add))
                link(ts(base[:, :], small[:, 1, :], float(unit), None, ALU.mult))
                link(tt(small[:, 0, :], small[:, 0, :], small[:, 1, :], ALU.add))
                link(tt(cmp[:, :, :], bc(units[:, 0, :].unsqueeze(2), [P, n_units, E]),
                        bc(small[:, 0, :].unsqueeze(1), [P, n_units, E]), ALU.is_ge))
                link(V.tensor_reduce(units[:, 1, :], cmp[:, :, :], AX.X, ALU.add))
                link(ts(unit_expert, units[0:1, 1, :], float(E - 1), None, ALU.min))
            link(tt(pos[:, :, :], pos[:, :, :], bc(base[:, :].unsqueeze(1), [P, NT, E]), ALU.add))
            for k in range(n_k):
                link(tt(probs[:, :, :], oh[:, k, :, :], pos[:, :, :], ALU.mult))
                link(V.tensor_reduce(idx[:, :], probs[:, :, :], AX.X, ALU.add))
                link(V.tensor_reduce(some[:, :], oh[:, k, :, :], AX.X, ALU.add))
                link(stt(v[:, 0, :], some[:, :], -1.0 - NO_ROW, idx[:, :], ALU.mult, ALU.add))
                link(ts(to[:, k, :], v[:, 0, :], NO_ROW, None, ALU.add))
                link(V.tensor_copy(back_from[:, k, :], idx[:, :]))
            steps.append(link.count)
    loaded.base += 16 if bias is not None else 0
    iota.base += 6
    ready.base += 1
    exped.base += 1
    step.base += steps[-1]
    mm.base += 3 if mode == "capacity" else 1
    asked.base += 3 if mode == "capacity" else 1


def scatter(c, rows, to, n_k, n_rows, Xg):
    nc = c.nc
    sent = c.sig("scattered")
    with nc.Block() as block:
        @block.gpsimd
        def _(pool):
            pool.wait_ge(c.sig("zeros_sent").handle, c.zeros_sent)
            for k in range(n_k):
                for t in range(NT):
                    nc.gpsimd.indirect_dma_start(
                        out=Xg[0:n_rows, :], out_offset=bass.IndirectOffsetOnAxis(ap=to[:, k, t:t + 1], axis=0),
                        in_=rows[:, t, :], in_offset=None, bounds_check=n_rows - 1, oob_is_err=False)\
                        .then_inc(sent.handle, 16)
            pool.wait_ge(sent.handle, sent.at(16 * n_k * NT))
    sent.base += 16 * n_k * NT


def gather(c, back_from, gate, n_k, n_rows, Yg, acc):
    nc = c.nc
    got, added = c.sig("gathered"), c.sig("gather_added")
    RING = 8
    with ExitStack() as st:
        G = c.sb(st, "gather_rows", [P, RING, D])
        arrived = [c.sig(f"gather_{i}") for i in range(RING)]
        block = st.enter_context(nc.Block())
        order = [(t, k) for t in range(NT) for k in range(n_k)]
        uses = len(order) // RING

        @block.gpsimd
        def _(pool):
            for n, (t, k) in enumerate(order):
                if n >= RING:
                    pool.wait_ge(added.handle, added.at(n - RING + 1))
                nc.gpsimd.indirect_dma_start(
                    out=G[:, n % RING, :], out_offset=None, in_=Yg[0:n_rows + 1, :],
                    in_offset=bass.IndirectOffsetOnAxis(ap=back_from[:, k, t:t + 1], axis=0))\
                    .then_inc(arrived[n % RING].handle, 16)

        @block.vector
        def _(dve):
            for n, (t, k) in enumerate(order):
                one = arrived[n % RING]
                dve.wait_ge(one.handle, one.at(16 * (n // RING + 1)))
                if k:
                    dve.wait_ge(added.handle, added.at(n))
                nc.vector.scalar_tensor_tensor(acc[:, t, :], G[:, n % RING, :], gate[:, k, t:t + 1], acc[:, t, :],
                                               ALU.mult, ALU.add).then_inc(added.handle, 1)
            dve.wait_ge(added.handle, added.at(len(order)))
    added.base += len(order)
    for one in arrived:
        one.base += 16 * uses


def slot_experts(c, n_units, unit, F, w1, w3, w2, b1, b2, func, unit_expert, Xg, Yg, beside=None):
    nc = c.nc
    FT = F // P
    swiglu = w3 is not None
    n_w = 2 + swiglu + (0 if b1 is None else 2)
    names = "T_mm T_ev H_mm sil H_ev O_mm O_ev".split()
    s_ = {n: c.sig("se_" + n) for n in names}
    T_mm, T_ev, H_mm, sil_done, H_ev, O_mm, O_ev = [s_[n] for n in names]
    rows_in = [c.sig(f"se_rows{i}") for i in range(2)]
    w_in = [c.sig(f"se_w{i}") for i in range(2)]
    out_sent = [c.sig(f"se_out{i}") for i in range(2)]
    tiles = [(lo, min(P, unit - lo)) for lo in range(0, unit, P)]
    nt = len(tiles)
    full = unit // P
    n_rows = nt - full + 1
    with ExitStack() as st:
        W1 = c.sb(st, "se_W1", [P, 2, KD, F])
        W3 = c.sb(st, "se_W3", [P, 2, KD, F]) if swiglu else None
        W2 = c.sb(st, "se_W2", [P, 2, FT, D])
        b1c = c.sb(st, "se_b1", [P, 2, FT]) if b1 is not None else None
        b2r = c.sb(st, "se_b2", [P, 2, D]) if b1 is not None else None
        X = c.sb(st, "se_X", [P, 2, nt, D])
        XT = c.sb(st, "se_XT", [P, 2, KD, unit])
        hT = c.sb(st, "se_hT", [P, 2, FT, unit])
        sil = c.sb(st, "se_sil", [P, 2, unit]) if swiglu else None
        Y = c.sb(st, "se_Y", [P, 2, nt, D])
        ps_T = c.ps(st, "se_ps_T", [P, KD, 512])
        ps_H = c.ps(st, "se_ps_H", [P, 2, 2 if swiglu else 1, 512])
        ps_O = c.ps(st, "se_ps_O", [P, 2, 512])
        ps_beside = c.ps(st, "se_ps_beside", [P, 512]) if beside else None
        block = st.enter_context(nc.Block())

        def row_views(dram, sbuf, u, s, start=0):
            at = u * unit + start
            yield dram[bass.ds(at, full * P), :].rearrange("(t p) d -> p t d", p=P), sbuf[:, s, 0:full, :]
            if nt > full:
                yield dram[bass.ds(at + full * P, unit - full * P), :], sbuf[0:unit - full * P, s, full, :]

        @block.sync
        def _(sp):
            def load(u, s, first=False):
                if not first:
                    sp.wait_ge(T_mm.handle, T_mm.at(u - 1))
                for dram, sbuf in row_views(Xg, X, u, s):
                    sp.dma_start(sbuf, dram).then_inc(rows_in[s].handle, 16)
                if not first:
                    sp.wait_ge(O_ev.handle, O_ev.at((u - 1) * nt + 2))
                e = u if unit_expert is None else sp.value_load(unit_expert[0:1, bass.ds(u, 1)], min_val=0,
                                                                max_val=w1.shape[0] - 1)
                sp.dma_start(W1[:, s, :, :], w1[e, :, :].rearrange("(k p) f -> p k f", p=P)).then_inc(w_in[s].handle, 16)
                if swiglu:
                    sp.dma_start(W3[:, s, :, :], w3[e, :, :].rearrange("(k p) f -> p k f", p=P)).then_inc(w_in[s].handle, 16)
                sp.dma_start(W2[:, s, :, :], w2[e, :, :].rearrange("(k p) f -> p k f", p=P)).then_inc(w_in[s].handle, 16)
                if b1 is not None:
                    sp.dma_start(b1c[:, s, :], b1[e, :].rearrange("(f p) -> p f", p=P),
                                 allow_slow_non_contiguous=True).then_inc(w_in[s].handle, 16)
                    sp.dma_start(b2r[:, s, :], row(b2[e, :], P)).then_inc(w_in[s].handle, 16)

            def send(u, s):
                sp.wait_ge(O_ev.handle, O_ev.at((u + 1) * nt + 2))
                for dram, sbuf in row_views(Yg, Y, u, s, 1):
                    sp.dma_start(dram, sbuf).then_inc(out_sent[s].handle, 16)

            for s in range(2):
                ring(sp, out_sent[s], 16 * n_rows)
                load(s, s, first=True)
            units = n_units - 2
            with sp.Fori(0, units // 2) as i:
                for s in range(2):
                    load(i * 2 + (s + 2), s)
                    send(i * 2 + s, s)
            for u in range(units // 2 * 2, n_units):
                if u < units:
                    load(u + 2, u % 2)
                send(u, u % 2)
            for s in range(2):
                uses = (n_units + 1 - s) // 2
                sp.wait_ge(w_in[s].handle, w_in[s].at(16 * n_w * uses))
                sp.wait_ge(rows_in[s].handle, rows_in[s].at(16 * n_rows * uses))
                sp.wait_ge(out_sent[s].handle, out_sent[s].at(16 * n_rows * (uses + 1)))

        if beside:
            @block.gpsimd
            def _(pool):
                with pool.Fori(0, (n_units - 1) // 2) as i:
                    beside.beside_gpsimd(pool, i)

        @block.tensor
        def _(pe):
            def transpose(u, s, use):
                pe.wait_ge(rows_in[s].handle, rows_in[s].at(use * (16 * n_rows)))
                pe.wait_ge(T_ev.handle, T_ev.at(u + 1))
                for k in range(KD):
                    for n, (lo, size) in enumerate(tiles):
                        last = nc.tensor.transpose(ps_T[:, k, lo:lo + size], X[0:size, s, n, k * P:(k + 1) * P],
                                                   c.ident[0:size, 0:size])
                last.then_inc(T_mm.handle, 1)

            def body(u, s, use, more):
                pe.wait_ge(w_in[s].handle, w_in[s].at(use * (16 * n_w)))
                pe.wait_ge(T_ev.handle, T_ev.at(u + 2))
                for f in range(FT):
                    pe.wait_ge(H_ev.handle, H_ev.at(u * FT + (f + 1)))
                    for m, W in enumerate([W1, W3] if swiglu else [W1]):
                        for k in range(KD):
                            last = nc.tensor.matmul(ps_H[:, f % 2, m, 0:unit], W[:, s, k, f * P:(f + 1) * P],
                                                    XT[:, s, k, :], start=(k == 0), stop=(k == KD - 1))
                    last.then_inc(H_mm.handle, 1)
                if more:
                    transpose(u + 1, 1 - s, use + s)
                pe.wait_ge(H_ev.handle, H_ev.at((u + 1) * FT + 2))
                for n, (lo, size) in enumerate(tiles):
                    pe.wait_ge(O_ev.handle, O_ev.at(u * nt + (n + 1)))
                    for f in range(FT):
                        last = nc.tensor.matmul(ps_O[0:size, (s * nt + n) % 2, 0:D], hT[:, s, f, lo:lo + size],
                                                W2[:, s, f, :], start=(f == 0), stop=(f == FT - 1))
                    last.then_inc(O_mm.handle, 1)

            transpose(0, 0, 1)
            pairs = (n_units - 1) // 2
            with pe.Fori(0, pairs) as i:
                for s in range(2):
                    body(i * 2 + s, s, i + 1, True)
                if beside:
                    beside.multiply(pe, ps_beside, i)
            for u in range(2 * pairs, n_units):
                body(u, u % 2, u // 2 + 1, u + 1 < n_units)

        def copy_T(eng, u, s):
            eng.wait_ge(T_mm.handle, T_mm.at(u + 1))
            nc.scalar.copy(XT[:, s, :, :], ps_T[:, :, 0:unit]).then_inc(T_ev.handle, 1)

        @block.scalar
        def _(act):
            ring(act, T_ev, 1)
            if not swiglu:
                ring(act, H_ev, 2)
            copy_T(act, 0, 0)

            def body(u, s, use, more):
                if b1 is not None:
                    act.wait_ge(w_in[s].handle, w_in[s].at(use * (16 * n_w)))
                for f in range(FT):
                    act.wait_ge(H_mm.handle, H_mm.at(u * FT + (f + 1)))
                    if swiglu:
                        nc.scalar.activation(sil[:, f % 2, :], ps_H[:, f % 2, 0, 0:unit], func).then_inc(sil_done.handle, 1)
                    else:
                        nc.scalar.activation(hT[:, s, f, :], ps_H[:, f % 2, 0, 0:unit], func, bias=b1c[:, s, f:f + 1])\
                            .then_inc(H_ev.handle, 1)
                if more:
                    copy_T(act, u + 1, 1 - s)

            pairs = (n_units - 1) // 2
            with act.Fori(0, pairs) as i:
                for s in range(2):
                    body(i * 2 + s, s, i + 1, True)
                    if beside:
                        beside.beside_scalar(act, i, s)
            for u in range(2 * pairs, n_units):
                body(u, u % 2, u // 2 + 1, u + 1 < n_units)

        @block.vector
        def _(dve):
            if swiglu:
                ring(dve, H_ev, 2)
            ring(dve, O_ev, 2)

            def body(u, s, use, more):
                if swiglu:
                    for f in range(FT):
                        dve.wait_ge(sil_done.handle, sil_done.at(u * FT + (f + 1)))
                        nc.vector.tensor_tensor(hT[:, s, f, :], sil[:, f % 2, :], ps_H[:, f % 2, 1, 0:unit], ALU.mult)\
                            .then_inc(H_ev.handle, 1)
                dve.wait_ge(out_sent[s].handle, out_sent[s].at(use * (16 * n_rows)))
                if b2 is not None:
                    dve.wait_ge(w_in[s].handle, w_in[s].at(use * (16 * n_w)))
                for n, (lo, size) in enumerate(tiles):
                    dve.wait_ge(O_mm.handle, O_mm.at(u * nt + (n + 1)))
                    got = ps_O[0:size, (s * nt + n) % 2, 0:D]
                    if b2 is not None:
                        one = nc.vector.tensor_tensor(Y[0:size, s, n, :], got, b2r[0:size, s, :], ALU.add)
                    else:
                        one = nc.vector.tensor_copy(Y[0:size, s, n, :], got)
                    one.then_inc(O_ev.handle, 1)

            pairs = (n_units - 1) // 2
            with dve.Fori(0, pairs) as i:
                for s in range(2):
                    body(i * 2 + s, s, i + 1, True)
                    if beside:
                        beside.beside_vector(dve, ps_beside, i, s)
            for u in range(2 * pairs, n_units):
                body(u, u % 2, u // 2 + 1, u + 1 < n_units)
    T_mm.base += n_units
    T_ev.base += n_units + 1
    H_mm.base += n_units * FT
    sil_done.base += n_units * FT if swiglu else 0
    H_ev.base += n_units * FT + 2
    O_mm.base += n_units * nt
    O_ev.base += n_units * nt + 2
    for s in range(2):
        uses = (n_units + 1 - s) // 2
        w_in[s].base += 16 * n_w * uses
        rows_in[s].base += 16 * n_rows * uses
        out_sent[s].base += 16 * n_rows * (uses + 1)


def exchange_buffers(c):
    nc = c.nc
    c.Xg = nc.dram_tensor("slot_rows", (ROOM, D), F32).ap()
    c.Yg = nc.dram_tensor("slot_outputs", (ROOM + 1, D), F32).ap()
    made, sent = c.sig("zeros_made"), c.sig("zeros_sent")
    zeros = c.sb(c.ctx, "zeros", [P, D * 2])
    with ExitStack() as st:
        block = st.enter_context(nc.Block())

        @block.gpsimd
        def _(pool):
            nc.gpsimd.memset(zeros[:, :], 0.0).then_inc(made.handle, 1)

        @block.sync
        def _(sp):
            sp.wait_ge(made.handle, 1)
            n = 0
            for lo in range(0, ROOM // P, 2):
                sp.dma_start(c.Xg[lo * P:(lo + 2) * P, :].rearrange("(p t) d -> p (t d)", p=P), zeros[:, :])\
                    .then_inc(sent.handle, 16)
                n += 1
            sp.dma_start(c.Yg[0:1, :], zeros[0:1, 0:D]).then_inc(sent.handle, 16)
            c.zeros_sent = 16 * (n + 1)


def make_plan(c, st, n_units):
    to = c.sb(st, "plan_to", [P, 2, NT], U32)
    back_from = c.sb(st, "plan_from", [P, 2, NT], U32)
    gate = c.sb(st, "plan_gate", [P, 2, NT])
    unit_expert = c.sb(st, "plan_expert", [1, n_units], U32)
    return to, back_from, gate, unit_expert[:, :]


def clip_add(c):
    nc = c.nc
    clipped = c.sig("clipped")
    with nc.Block() as block:
        @block.vector
        def _(dve):
            nc.vector.tensor_scalar(c.xn[:, :, :], c.xn[:, :, :], -100.0, 100.0, ALU.max, ALU.min)\
                .then_inc(clipped.handle, 1)
            dve.wait_ge(clipped.handle, clipped.at(1))
            nc.vector.tensor_tensor(c.x[:, :, :], c.x[:, :, :], c.xn[:, :, :], ALU.add).then_inc(clipped.handle, 1)
            dve.wait_ge(clipped.handle, clipped.at(2))
    clipped.base += 2


def L0_ffn(c, w, kernel_l1):
    E = 14
    unit, n_units = slots_of(E, "top2")
    with ExitStack() as st:
        logits = c.sb(st, "L0_logits", [P, NT, E])
        plan = make_plan(c, st, n_units)
        to, back_from, gate, unit_expert = plan
        normalise(c, c.x, xn_out=c.xn, router=(w["gate_w"].rearrange("e d -> d e"), E, logits))
        route(c, logits, E, "top2", None, None, plan)
        scatter(c, c.xn, to, 2, n_units * unit, c.Xg)
        slot_experts(c, n_units, unit, 512, w["w1"], None, w["w2"], w["b1"], w["b2"], ACT.Gelu, unit_expert, c.Xg, c.Yg,
                     beside=kernel_l1)
        kernel_l1.finish((n_units - 1) // 2)
        gather(c, back_from, gate, 2, n_units * unit, c.Yg, c.xn)
        clip_add(c)


def L2_ffn(c, w):
    E = 8
    unit, n_units = slots_of(E, "top1")
    nc = c.nc
    with ExitStack() as st:
        logits = c.sb(st, "L2_logits", [P, NT, E])
        top = c.sb(st, "L2_top", [P, NT])
        plan = make_plan(c, st, n_units)
        to, back_from, gate, _ = plan
        normalise(c, c.x, router=(w["Wr"], E, logits))
        route(c, logits, E, "top1", w["br"], top[:, :], plan)
        scaled = c.sig("L2_scaled")
        with nc.Block() as block:
            @block.vector
            def _(dve):
                nc.vector.tensor_tensor(c.rstd[:, :], c.rstd[:, :], top[:, :], ALU.mult).then_inc(scaled.handle, 1)
                nc.vector.tensor_tensor(c.nmr[:, :], c.nmr[:, :], top[:, :], ALU.mult).then_inc(scaled.handle, 1)
                dve.wait_ge(scaled.handle, scaled.at(2))
        scaled.base += 2
        normalise(c, c.x, xn_out=c.xn)
        scatter(c, c.xn, to, 1, n_units * unit, c.Xg)
        slot_experts(c, n_units, unit, 256, w["W1"], None, w["W2"], w["b1"], w["b2"], ACT.Relu, None, c.Xg, c.Yg)
        gather(c, back_from, gate, 1, n_units * unit, c.Yg, c.x)


def L3_ffn(c, w, xT):
    E = 16
    unit, n_units = slots_of(E, "capacity")
    with ExitStack() as st:
        logits = c.sb(st, "L3_logits", [P, NT, E])
        plan = make_plan(c, st, n_units)
        to, back_from, gate, _ = plan
        normalise(c, c.x, xn_out=c.xn, xT_out=xT, router=(w["gate_w"], E, logits))
        route(c, logits, E, "capacity", w["gate_b"], None, plan, meanwhile=lambda take_out: experts(
            c, xT, 2, 512, w["sw1"], w["sw3"], w["sw2"], None, ACT.Silu, lambda t, e: 0.5, c.x, meanwhile=take_out))
        scatter(c, c.xn, to, 2, n_units * unit, c.Xg)
        slot_experts(c, n_units, unit, 512, w["ew1"], w["ew3"], w["ew2"], None, None, ACT.Silu, None, c.Xg, c.Yg)
        gather(c, back_from, gate, 2, n_units * unit, c.Yg, c.x)


def add_row(c, acc, v, tiles=range(NT)):
    nc = c.nc
    loaded, added = c.sig("row_loaded"), c.sig("row_added")
    with ExitStack() as st:
        r = c.sb(st, "row", [P, D])
        block = st.enter_context(nc.Block())

        @block.sync
        def _(sp):
            sp.dma_start(r[:, :], row(v, P)).then_inc(loaded.handle, 16)

        @block.vector
        def _(dve):
            dve.wait_ge(loaded.handle, loaded.at(16))
            nc.vector.tensor_tensor(acc[:, :, :], acc[:, :, :], bc(r[:, :].unsqueeze(1), [P, NT, D]), ALU.add)\
                .then_inc(added.handle, 1)
            dve.wait_ge(added.handle, added.at(1))
    loaded.base += 16
    added.base += 1


DH3 = D // HEADS
HPT = P // DH3
HPTJ = HPT * J


def narrow_fold(c, w, scratch, M, bias, N):
    nc = c.nc
    loaded, made, mm, ev, stored = [c.sig("nf_" + n) for n in ("loaded", "made", "mm", "ev", "stored")]
    with ExitStack() as st:
        Wq = c.sb(st, "nf_Wq", [P, KD, D])
        Wk = c.sb(st, "nf_Wk", [KC, 2, D])
        Wv = c.sb(st, "nf_Wv", [KC, 2, D])
        bq = c.sb(st, "nf_bq", [P, KD])
        bk = c.sb(st, "nf_bk", [P, KD])
        bv = c.sb(st, "nf_bv", [J, D])
        WqT = c.sb(st, "nf_WqT", [P, KD, D])
        KT = c.sb(st, "nf_KT", [P, KD, BJ])
        Kd = c.sb(st, "nf_Kd", [P, KD, B, HPTJ])
        V = c.sb(st, "nf_V", [J, B, D])
        own = c.sb(st, "nf_own", [P, HPT])
        zeros = c.sb(st, "nf_zeros", [P, HJC * D])
        ps = c.ps(st, "nf_ps", [P, 4, 512])
        block = st.enter_context(nc.Block())
        half = HPTJ // 2
        first = [("K", m) for m in range(KD)] + [("V", b) for b in range(B)] + [("Q", m) for m in range(KD)]
        halves = [(m, b, q) for m in range(KD) for b in range(B) for q in range(2)]
        steps = first + [("M", (k, *x)) for k in range(KD) for x in halves] + [("B", x) for x in halves]
        n_kd = KD * B

        @block.sync
        def _(sp):
            for out, a in ((Wk[:, :, :], w["Wk"].rearrange("(k p) n -> p k n", p=KC)),
                           (Wv[:, :, :], w["Wv"].rearrange("(k p) n -> p k n", p=KC)),
                           (Wq[:, :, :], w["Wq"].rearrange("(k p) n -> p k n", p=P)),
                           (bq[:, :], column(w["bq"])), (bk[:, :], column(w["bk"])), (bv[:, :], row(w["bv"], J))):
                sp.dma_start(out, a, allow_slow_non_contiguous=True).then_inc(loaded.handle, 16)
            sp.wait_ge(made.handle, made.at(4))
            for b in range(B):
                sp.dma_start(scratch[b, :, :].rearrange("(c p) d -> p c d", p=P),
                             zeros[:, :].rearrange("p (c d) -> p c d", d=D)).then_inc(stored.handle, 16)
            sp.wait_ge(stored.handle, stored.at(16 * B))
            sp.wait_ge(ev.handle, ev.at(KD + B))
            with sp.Fori(0, HEADS) as h:
                sp.dma_start(scratch[:, bass.ts(h, J), bass.ts(h, DH3)].rearrange("b j c -> j b c"),
                             V[:, :, bass.ts(h, DH3)]).then_inc(stored.handle, 16)
            sp.wait_ge(stored.handle, stored.at(16 * (B + HEADS)))
            for b in range(B):
                sp.dma_start(N[:, b, :, :], scratch[b, :, :].rearrange("(c p) d -> p c d", p=P)).then_inc(stored.handle, 16)
            sp.wait_ge(stored.handle, stored.at(16 * (2 * B + HEADS)))

        @block.gpsimd
        def _(pool):
            nc.gpsimd.memset(own[:, :], 1.0).then_inc(made.handle, 1)
            pool.wait_ge(made.handle, made.at(1))
            nc.gpsimd.affine_select(out=own[:, :], in_=own[:, :], compare_op=ALU.is_ge, fill=0.0, base=0,
                                    pattern=[[-DH3, HPT]], channel_multiplier=1).then_inc(made.handle, 1)
            pool.wait_ge(made.handle, made.at(2))
            nc.gpsimd.affine_select(out=own[:, :], in_=own[:, :], compare_op=ALU.is_ge, fill=0.0, base=DH3 - 1,
                                    pattern=[[DH3, HPT]], channel_multiplier=-1).then_inc(made.handle, 1)
            nc.gpsimd.memset(zeros[:, :], 0.0).then_inc(made.handle, 1)

        @block.tensor
        def _(pe):
            pe.wait_ge(loaded.handle, loaded.at(96))
            for n, (kind, at) in enumerate(steps):
                bank = ps[:, n % 4, :]
                if n == len(first):
                    pe.wait_ge(ev.handle, ev.at(len(first) + n_kd))
                elif n >= 4:
                    pe.wait_ge(ev.handle, ev.at(n - 3 + (n_kd if n > len(first) else 0)))
                if kind == "K":
                    for k in range(2):
                        last = nc.tensor.matmul(bank[:, 0:BJ], Wk[:, k, at * P:(at + 1) * P], c.ctxT[:, k, :],
                                                start=(k == 0), stop=(k == 1))
                elif kind == "V":
                    for k in range(2):
                        last = nc.tensor.matmul(bank[0:J, 0:D], c.ctxT[:, k, at * J:(at + 1) * J], Wv[:, k, :],
                                                start=(k == 0), stop=(k == 1))
                elif kind == "Q":
                    for k in range(KD):
                        last = nc.tensor.transpose(bank[:, k * P:(k + 1) * P], Wq[:, k, at * P:(at + 1) * P], c.ident[:, :])
                elif kind == "M":
                    k, m, b, q = at
                    last = nc.tensor.matmul(bank[:, 0:half], WqT[:, m, k * P:(k + 1) * P],
                                            Kd[:, m, b, q * half:(q + 1) * half], start=True, stop=True)
                else:
                    m, b, q = at
                    last = nc.tensor.matmul(bank[0:1, 0:half], bq[:, m:m + 1], Kd[:, m, b, q * half:(q + 1) * half],
                                            start=True, stop=True)
                last.then_inc(mm.handle, 1)

        @block.vector
        def _(dve):
            dve.wait_ge(loaded.handle, loaded.at(96))
            for n, (kind, at) in enumerate(steps):
                bank = ps[:, n % 4, :]
                if n == len(first):
                    dve.wait_ge(made.handle, made.at(3))
                    dve.wait_ge(ev.handle, ev.at(len(first)))
                    for m in range(KD):
                        for b in range(B):
                            nc.vector.tensor_tensor(Kd[:, m, b, :].rearrange("p (h j) -> p h j", j=J),
                                                    bc(KT[:, m, b * J:(b + 1) * J].unsqueeze(1), [P, HPT, J]),
                                                    bc(own[:, :].unsqueeze(2), [P, HPT, J]), ALU.mult).then_inc(ev.handle, 1)
                dve.wait_ge(mm.handle, mm.at(n + 1))
                if kind == "K":
                    last = nc.vector.tensor_scalar(KT[:, at, :], bank[:, 0:BJ], bk[:, at:at + 1], DH3 ** -0.5,
                                                   ALU.add, ALU.mult)
                elif kind == "V":
                    last = nc.vector.tensor_tensor(V[:, at, :], bank[0:J, 0:D], bv[:, :], ALU.add)
                elif kind == "Q":
                    last = nc.vector.tensor_copy(WqT[:, at, :], bank[:, 0:D])
                else:
                    m, b, q = at[-3:]
                    lo = m * HPTJ + q * half
                    if kind == "M":
                        last = nc.vector.tensor_copy(M[:, at[0], b, lo:lo + half], bank[:, 0:half])
                    else:
                        last = nc.vector.tensor_copy(bias[0:1, b, lo:lo + half], bank[0:1, 0:half])
                last.then_inc(ev.handle, 1)
            dve.wait_ge(ev.handle, ev.at(len(steps) + n_kd))
    loaded.base += 96
    made.base += 4
    mm.base += len(steps)
    ev.base += len(steps) + n_kd
    stored.base += 16 * (2 * B + HEADS)


def L3_xattn(c, w, scratch, xT):
    with ExitStack() as st:
        M = c.sb(st, "l3_M", [P, KD, B, HJ])
        N = c.sb(st, "l3_N", [P, B, HJC, D])
        bias = c.sb(st, "l3_bias", [1, B, HJ])
        narrow_fold(c, w, scratch, M, bias, N)
        attention(c, M, bias, N, None, xT)
    one = {n: w[n].unsqueeze(0) for n in ("W1", "W2", "b1")}
    experts(c, xT, 1, 512, one["W1"], None, one["W2"], one["b1"], ACT.Relu, lambda t, e: 1.0, c.x)
    add_row(c, c.x, w["b2"])


def L1_ffn(c, w, xT):
    nc = c.nc
    E, F = 8, 512
    FT = F // P
    names = "loaded mm act top weights T_ev step".split()
    s = {n: c.sig("l1f_" + n) for n in names}
    normalise(c, c.x, xn_out=c.xn, xT_out=xT)
    with ExitStack() as st:
        W1 = c.sb(st, "l1f_W1", [P, B, KD, F])
        W2o = c.sb(st, "l1f_W2o", [P, B, FT, D])
        b1 = c.sb(st, "l1f_b1", [P, B, FT])
        with ExitStack() as pre:
            Wp1 = c.sb(pre, "l1f_Wp1", [P, KD, P])
            bp1 = c.sb(pre, "l1f_bp1", [P, 1])
            Wp2 = c.sb(pre, "l1f_Wp2", [P, E])
            bp2 = c.sb(pre, "l1f_bp2", [1, E])
            Wo = c.sb(pre, "l1f_Wo", [P, KD, D])
            bo = c.sb(pre, "l1f_bo", [P, D])
            W2 = c.sb(pre, "l1f_W2", [P, B, FT, D])
            W2T = c.sb(pre, "l1f_W2T", [P, B, KD, F])
            b2 = c.sb(pre, "l1f_b2", [P, B, KD])
            b2w = c.sb(pre, "l1f_b2w", [P, B, KD, P])
            ends = c.sb(pre, "l1f_ends", [P, KD, B])
            nav = c.sb(pre, "l1f_nav", [P, B])
            lg = c.sb(pre, "l1f_lg", [1, B, E])
            v1 = c.sb(pre, "l1f_v1", [1, B])
            eight = c.sb(pre, "l1f_eight", [1, B, 8])
            idx = c.sb(pre, "l1f_idx", [1, B, 8], U32)
            rowb = c.sb(pre, "l1f_rowb", [P, B, D])
            ps = c.ps(pre, "l1f_ps", [P, 4, 512])
            block = pre.enter_context(nc.Block())

            @block.sync
            def _(sp):
                for out, a in ((Wp1[:, :, :], w["Wp1"].rearrange("(k p) n -> p k n", p=P)), (bp1[:, :], column(w["bp1"])),
                               (Wp2[:, :], w["Wp2"]), (bp2[:, :], row(w["bp2"], 1)),
                               (Wo[:, :, :], w["Wo"].rearrange("(k p) n -> p k n", p=P)), (bo[:, :], row(w["bo"], P))):
                    sp.dma_start(out, a, allow_slow_non_contiguous=True).then_inc(s["loaded"].handle, 16)
                sp.wait_ge(s["top"].handle, s["top"].at(1))
                for b in range(B):
                    e = sp.value_load(idx[0:1, b, 0:1], min_val=0, max_val=E - 1)
                    sp.dma_start(W2[:, b, :, :], w["W2"][e, :, :].rearrange("(k p) f -> p k f", p=P))\
                        .then_inc(s["weights"].handle, 16)
                    sp.dma_start(W1[:, b, :, :], w["W1"][e, :, :].rearrange("(k p) f -> p k f", p=P))\
                        .then_inc(s["weights"].handle, 16)
                    sp.dma_start(b1[:, b, :], w["b1"][e, :].rearrange("(f p) -> p f", p=P), allow_slow_non_contiguous=True)\
                        .then_inc(s["weights"].handle, 16)
                    sp.dma_start(b2[:, b, :], w["b2"][e, :].rearrange("(f p) -> p f", p=P), allow_slow_non_contiguous=True)\
                        .then_inc(s["weights"].handle, 16)
                sp.wait_ge(s["weights"].handle, s["weights"].at(128))

            @block.tensor
            def _(pe):
                pe.wait_ge(s["loaded"].handle, s["loaded"].at(96))
                pe.wait_ge(s["act"].handle, s["act"].at(1))
                for k in range(KD):
                    last = nc.tensor.matmul(ps[:, 0, 0:B], Wp1[:, k, :], ends[:, k, :], start=(k == 0), stop=(k == KD - 1))
                last.then_inc(s["mm"].handle, 1)
                pe.wait_ge(s["act"].handle, s["act"].at(2))
                for b in range(B):
                    last = nc.tensor.matmul(ps[0:1, 1, b * E:(b + 1) * E], nav[:, b:b + 1], Wp2[:, :], start=True, stop=True)
                last.then_inc(s["mm"].handle, 1)
                pe.wait_ge(s["weights"].handle, s["weights"].at(128))
                for b in range(B):
                    for k in range(KD):
                        if b:
                            pe.wait_ge(s["T_ev"].handle, s["T_ev"].at((b - 1) * KD + k + 1))
                        for f in range(FT):
                            last = nc.tensor.transpose(ps[:, 2 + k, f * P:(f + 1) * P], W2[:, b, f, k * P:(k + 1) * P],
                                                       c.ident[:, :])
                        last.then_inc(s["mm"].handle, 1)
                pe.wait_ge(s["T_ev"].handle, s["T_ev"].at(B * KD))
                pe.wait_ge(s["step"].handle, s["step"].at(8))
                for b in range(B):
                    for f in range(0, FT, 2):
                        n = b * FT // 2 + f // 2
                        if n:
                            pe.wait_ge(s["T_ev"].handle, s["T_ev"].at(B * KD + n))
                        for q in range(2):
                            for k in range(KD):
                                last = nc.tensor.matmul(ps[:, 0, q * D:(q + 1) * D],
                                                        W2T[:, b, k, (f + q) * P:(f + q + 1) * P], Wo[:, k, :],
                                                        start=(k == 0), stop=(k == KD - 1))
                        last.then_inc(s["mm"].handle, 1)
                for b in range(B):
                    for k in range(KD):
                        last = nc.tensor.matmul(ps[:, 1, b * D:(b + 1) * D], b2w[:, b, k, :], Wo[:, k, :],
                                                start=(k == 0), stop=(k == KD - 1))
                last.then_inc(s["mm"].handle, 1)

            @block.scalar
            def _(act):
                for b in range(B):
                    last = nc.scalar.copy(ends[:, :, b], xT[:, :, (b + 1) * SEQ - 1])
                last.then_inc(s["act"].handle, 1)
                act.wait_ge(s["mm"].handle, s["mm"].at(1))
                nc.scalar.activation(nav[:, :], ps[:, 0, 0:B], ACT.Gelu, bias=bp1[:, 0:1]).then_inc(s["act"].handle, 1)
                act.wait_ge(s["step"].handle, s["step"].at(3))
                nc.scalar.activation(lg[:, :, :], lg[:, :, :], ACT.Exp).then_inc(s["act"].handle, 1)

            @block.vector
            def _(dve):
                v = nc.vector
                link = Chain(dve, s["step"])
                wide = bc(v1[:, :].unsqueeze(2), [1, B, E])
                dve.wait_ge(s["mm"].handle, s["mm"].at(2))
                link(v.tensor_tensor(lg[:, :, :], ps[0:1, 1, 0:B * E].rearrange("p (b e) -> p b e", e=E),
                                     bc(bp2[:, :].unsqueeze(1), [1, B, E]), ALU.add))
                link(v.tensor_reduce(v1[:, :], lg[:, :, :], AX.X, ALU.max))
                link(v.tensor_tensor(lg[:, :, :], lg[:, :, :], wide, ALU.subtract))
                dve.wait_ge(s["act"].handle, s["act"].at(3))
                link(v.tensor_reduce(v1[:, :], lg[:, :, :], AX.X, ALU.add))
                link(v.reciprocal(v1[:, :], v1[:, :]))
                link(v.tensor_tensor(lg[:, :, :], lg[:, :, :], wide, ALU.mult))
                v.max(eight[:, 0, :], lg[:, 0, :])
                link(v.max(eight[:, 1, :], lg[:, 1, :]))
                v.max_index(idx[:, 0, :], eight[:, 0, :], lg[:, 0, :])
                v.max_index(idx[:, 1, :], eight[:, 1, :], lg[:, 1, :]).then_inc(s["top"].handle, 1)
                dve.wait_ge(s["weights"].handle, s["weights"].at(128))
                for b in range(B):
                    for k in range(KD):
                        dve.wait_ge(s["mm"].handle, s["mm"].at(3 + b * KD + k))
                        v.tensor_copy(W2T[:, b, k, :], ps[:, 2 + k, :]).then_inc(s["T_ev"].handle, 1)
                link(v.tensor_copy(b2w[:, :, :, :], bc(b2[:, :, :].unsqueeze(3), [P, B, KD, P])))
                for b in range(B):
                    for f in range(0, FT, 2):
                        dve.wait_ge(s["mm"].handle, s["mm"].at(7 + b * FT // 2 + f // 2))
                        v.tensor_copy(W2o[:, b, f:f + 2, :], ps[:, 0, :].rearrange("p (f d) -> p f d", d=D))\
                            .then_inc(s["T_ev"].handle, 1)
                dve.wait_ge(s["mm"].handle, s["mm"].at(7 + B * FT // 2))
                link(v.tensor_tensor(rowb[:, :, :], ps[:, 1, :].rearrange("p (b d) -> p b d", d=D),
                                     bc(bo[:, :].unsqueeze(1), [P, B, D]), ALU.add))
                for b in range(B):
                    tiles = slice(b * TPB, (b + 1) * TPB)
                    link(v.scalar_tensor_tensor(c.x[:, tiles, :], bc(rowb[:, b, :].unsqueeze(1), [P, TPB, D]), 0.3,
                                                c.x[:, tiles, :], ALU.mult, ALU.add))
                link(v.tensor_tensor(c.x[:, :, :], c.x[:, :, :], c.xn[:, :, :], ALU.add))
        s["loaded"].base += 96
        for n, k in (("mm", 12), ("act", 3), ("top", 1), ("weights", 128), ("T_ev", 8), ("step", 12)):
            s[n].base += k
        for b in range(B):
            experts(c, xT, 1, F, None, None, None, True, ACT.Gelu, lambda t, e: 0.3, c.x,
                    chunks=range(b * NCH // B, (b + 1) * NCH // B),
                    resident=(W1[:, b:b + 1, :, :], W2o[:, b:b + 1, :, :], b1[:, b:b + 1, :]))


H1, DH1 = 4, 32
HJ1 = H1 * J
JE = J + 1
TOP = 32
NS = 64
MASKED, TAKEN1 = -1.0e30, -3.0e38
NF1, NF2 = 5, 256
TWO_PI = 6.2831845
R2 = 0.5 ** 0.5


def constants():
    n = 2 * SEQ
    f1, j2, f2 = np.arange(NF1)[:, None, None], np.arange(NF2)[None, :, None], np.arange(NF2)[None, None, :]
    turn = 2 * np.pi * ((j2 * (f1 + 8 * f2)) % n) / n
    fwd = np.stack([np.cos(turn), np.sin(turn), -np.sin(turn)], axis=1)
    scale = np.array([1, 2, 2, 2, 1]).reshape(NF1, 1, 1, 1) / n
    inv = np.swapaxes(fwd, 2, 3) * scale
    return {"dft_fwd": fwd.astype(np.float32), "dft_inv": inv.astype(np.float32)}


def L1_fold(c, w, mask_tok, mask_ctx, M, mask_row, VF, tok_factor):
    nc = c.nc
    s = {n: c.sig("l1_" + n) for n in "loaded mm ev step bias".split()}
    with ExitStack() as st:
        Wq = c.sb(st, "l1_Wq", [P, KD, P])
        Wk = c.sb(st, "l1_Wk", [KC, 2, P])
        Wv = c.sb(st, "l1_Wv", [KC, 2, D])
        Wf = c.sb(st, "l1_Wf", [P, 2, KD, 2 * D])
        bf = c.sb(st, "l1_bf", [1, 2, 2 * D])
        KT = c.sb(st, "l1_KT", [P, BJ])
        VT = c.sb(st, "l1_VT", [P, KD, BJ])
        WqT = c.sb(st, "l1_WqT", [P, D])
        gate = c.sb(st, "l1_gate", [P, 1])
        mt8 = c.sb(st, "l1_mt8", [P, NT], U8)
        mc8 = c.sb(st, "l1_mc8", [1, B, J], U8)
        mcf = c.sb(st, "l1_mcf", [1, B, J])
        ps = c.ps(st, "l1_ps", [P, 4, 512])
        block = st.enter_context(nc.Block())
        steps = [("K", 0), ("V", 0), ("V", 1), ("Q", 0)] + [("M", h) for h in range(H1)]
        steps += [("F", (b, o)) for b in range(B) for o in range(2)]
        loads = 10

        @block.sync
        def _(sp):
            for out, a in ((Wk[:, :, :], w["Wk"].rearrange("(k p) n -> p k n", p=KC)),
                           (Wv[:, :, :], w["Wv"].rearrange("(k p) n -> p k n", p=KC)),
                           (Wq[:, :, :], w["Wq"].rearrange("(k p) n -> p k n", p=P)),
                           (Wf[:, 0, :, :], w["W_film_in"].rearrange("(k p) n -> p k n", p=P)),
                           (Wf[:, 1, :, :], w["W_film_out"].rearrange("(k p) n -> p k n", p=P)),
                           (bf[:, 0, :], row(w["b_film_in"], 1)), (bf[:, 1, :], row(w["b_film_out"], 1)),
                           (gate[:, :], row(w["mod_gate"], P)),
                           (mt8[:, :], mask_tok.rearrange("b (t p) -> p (b t)", p=P)),
                           (mc8[:, :, :], mask_ctx.unsqueeze(0))):
                sp.dma_start(out, a, allow_slow_non_contiguous=True).then_inc(s["loaded"].handle, 16)
            sp.wait_ge(s["step"].handle, s["step"].at(2))
            for b in range(B):
                sp.dma_start(VF[J:JE, b, :, :], bf[:, :, :]).then_inc(s["bias"].handle, 16)
            sp.wait_ge(s["bias"].handle, s["bias"].at(32))

        @block.tensor
        def _(pe):
            pe.wait_ge(s["loaded"].handle, s["loaded"].at(16 * loads))
            for n, (kind, at) in enumerate(steps):
                bank = ps[:, n % 4, :]
                if n >= 4:
                    pe.wait_ge(s["ev"].handle, s["ev"].at(max(n - 3, 4)))
                if kind == "K":
                    for k in range(2):
                        last = nc.tensor.matmul(bank[:, 0:BJ], Wk[:, k, :], c.ctxT[:, k, :], start=(k == 0), stop=(k == 1))
                elif kind == "V":
                    for k in range(2):
                        last = nc.tensor.matmul(bank[:, 0:BJ], Wv[:, k, at * P:(at + 1) * P], c.ctxT[:, k, :],
                                                start=(k == 0), stop=(k == 1))
                elif kind == "Q":
                    for k in range(KD):
                        last = nc.tensor.transpose(bank[:, k * P:(k + 1) * P], Wq[:, k, :], c.ident[:, :])
                elif kind == "M":
                    lo = at * DH1
                    for k in range(KD):
                        last = nc.tensor.matmul(bank[:, k * BJ:(k + 1) * BJ], WqT[lo:lo + DH1, k * P:(k + 1) * P],
                                                KT[lo:lo + DH1, :], start=True, stop=True)
                else:
                    b, o = at
                    for k in range(KD):
                        last = nc.tensor.matmul(bank[0:J, :], VT[:, k, b * J:(b + 1) * J], Wf[:, o, k, :],
                                                start=(k == 0), stop=(k == KD - 1))
                last.then_inc(s["mm"].handle, 1)

        @block.vector
        def _(dve):
            v = nc.vector
            link = Chain(dve, s["step"])
            dve.wait_ge(s["loaded"].handle, s["loaded"].at(16 * loads))
            link(v.tensor_scalar(bf[:, :, :], bf[:, :, :], gate[0:1, 0:1], None, ALU.mult))
            link(v.tensor_scalar(bf[:, :, 0:D], bf[:, :, 0:D], 1.0, None, ALU.add))
            link(v.tensor_copy(tok_factor, mt8[:, :]))
            link(v.tensor_scalar(tok_factor, tok_factor, 1.0 / H1, None, ALU.mult))
            link(v.tensor_copy(mcf[:, :, :], mc8[:, :, :]))
            link(v.tensor_scalar(mcf[:, :, :], mcf[:, :, :], 1.0, -MASKED, ALU.subtract, ALU.mult))
            for h in range(H1):
                link(v.tensor_copy(mask_row[:, :, h * J:(h + 1) * J], mcf[:, :, :]))
            for n, (kind, at) in enumerate(steps):
                bank = ps[:, n % 4, :]
                dve.wait_ge(s["mm"].handle, s["mm"].at(n + 1))
                if kind == "K":
                    last = v.tensor_scalar(KT[:, :], bank[:, 0:BJ], DH1 ** -0.5, None, ALU.mult)
                elif kind == "V":
                    last = v.tensor_copy(VT[:, at, :], bank[:, 0:BJ])
                elif kind == "Q":
                    last = v.tensor_copy(WqT[:, :], bank[:, 0:D])
                elif kind == "M":
                    last = v.tensor_copy(M[:, :, :, at * J:(at + 1) * J],
                                         bank[:, 0:KD * BJ].rearrange("p (k b j) -> p k b j", k=KD, b=B))
                else:
                    b, o = at
                    last = v.tensor_scalar(VF[0:J, b, o, :], bank[0:J, :], gate[0:J, 0:1], None, ALU.mult)
                last.then_inc(s["ev"].handle, 1)
            dve.wait_ge(s["ev"].handle, s["ev"].at(len(steps)))
    s["loaded"].base += 16 * loads
    s["mm"].base += len(steps)
    s["ev"].base += len(steps)
    s["step"].base += 6 + H1
    s["bias"].base += 32


def L1_modulate(c, scores, tok_factor, VF, UK, film_out):
    nc = c.nc
    s = {n: c.sig("l1m_" + n) for n in "step fence shifted exped mean T_mm T_ev F_mm F_ev kept".split()}
    rounds = TOP // 8
    with ExitStack() as st:
        sc = c.sb(st, "l1m_sc", [P, 2, H1, J])
        work = c.sb(st, "l1m_work", [P, 2, H1, J])
        eight = c.sb(st, "l1m_eight", [P, 2, H1, 8])
        rs = c.sb(st, "l1m_rs", [P, 2, H1])
        am = c.sb(st, "l1m_am", [P, 2, JE])
        amT = c.sb(st, "l1m_amT", [JE, 2, P])
        ps_T = c.ps(st, "l1m_ps_T", [JE, 2, 512])
        ps_F = c.ps(st, "l1m_ps_F", [P, 2, 2, 512])
        block = st.enter_context(nc.Block())

        @block.vector
        def _(dve):
            v = nc.vector
            link = Chain(dve, s["step"])
            ring(dve, s["F_ev"], 2)
            link(v.memset(am[:, :, :], 1.0))

            def fence():
                dve.sem_inc(s["fence"].handle, 1)

            def heads(n):
                return scores[:, bass.ds(n, 2), :].rearrange("p t (h j) -> p t h j", j=J)

            def select(n):
                link(v.tensor_copy(work[:, :, :, :], heads(n)))
                fence()
                for r in range(rounds):
                    for j in range(2):
                        for h in range(H1):
                            last = v.max(eight[:, j, h, :], work[:, j, h, :])
                    link(last)
                    fence()
                    if r == 0:
                        v.tensor_tensor(sc[:, :, :, :], heads(n), bc(eight[:, :, :, 0:1], [P, 2, H1, J]), ALU.subtract)\
                            .then_inc(s["shifted"].handle, 1)
                    for j in range(2):
                        for h in range(H1):
                            last = v.match_replace(work[:, j, h, :], eight[:, j, h, :], work[:, j, h, :], TAKEN1)
                    link(last)
                    fence()

            def average(pair, n):
                dve.wait_ge(s["exped"].handle, s["exped"].at(pair + 1))
                link(v.scalar_tensor_tensor(sc[:, :, :, :], work[:, :, :, :], 10 * MASKED, sc[:, :, :, :],
                                            ALU.is_lt, ALU.mult))
                link(v.tensor_reduce(rs[:, :, :], sc[:, :, :, :], AX.X, ALU.add))
                link(v.reciprocal(rs[:, :, :], rs[:, :, :]))
                link(v.tensor_tensor(rs[:, :, :], rs[:, :, :], bc(tok_factor[:, bass.ds(n, 2)].unsqueeze(2), [P, 2, H1]),
                                     ALU.mult))
                link(v.tensor_tensor(sc[:, :, :, :], sc[:, :, :, :], bc(rs[:, :, :].unsqueeze(3), [P, 2, H1, J]), ALU.mult))
                dve.wait_ge(s["T_mm"].handle, s["T_mm"].at(n + 2))
                v.tensor_reduce(am[:, :, 0:J], sc[:, :, :, :].rearrange("p t h j -> p t j h"), AX.X, ALU.add)\
                    .then_inc(s["mean"].handle, 1)

            def apply(n, t, b):
                dve.wait_ge(s["F_mm"].handle, s["F_mm"].at(n + 2))
                u = UK[:, bass.ds(t, 2), b, :]
                link(v.tensor_tensor(u, u, ps_F[:, 0, :, 0:D], ALU.mult))
                link(v.tensor_tensor(u, u, ps_F[:, 0, :, D:2 * D], ALU.add))
                dve.wait_ge(s["kept"].handle, s["kept"].at(n + 2))
                dve.sem_inc(s["F_ev"].handle, 2)

            per_pair = 2 * rounds + 1 + 5
            pairs = TPB // 2
            select(0)
            average(0, 0)
            for b in range(B):
                first, count = b * pairs + 1, pairs - 1
                link_base = link.count
                with dve.Fori(0, count) as i:
                    link.count = i * (per_pair + 2) + link_base
                    select(i * 2 + first * 2)
                    apply(i * 2 + (first - 1) * 2, i * 2, b)
                    average(i + first, i * 2 + first * 2)
                link.count = link_base + count * (per_pair + 2)
                if b + 1 < B:
                    select((first + count) * 2)
                apply((first + count - 1) * 2, count * 2, b)
                if b + 1 < B:
                    average(first + count, (first + count) * 2)

        @block.scalar
        def _(act):
            ring(act, s["T_ev"], 2)
            with act.Fori(0, NT // 2) as i:
                act.wait_ge(s["shifted"].handle, s["shifted"].at(i + 1))
                nc.scalar.activation(sc[:, :, :, :], sc[:, :, :, :], ACT.Exp).then_inc(s["exped"].handle, 1)
                for j in range(2):
                    n = i * 2 + j
                    act.wait_ge(s["T_mm"].handle, s["T_mm"].at(n + 3))
                    nc.scalar.copy(amT[:, j, :], ps_T[:, j, 0:P]).then_inc(s["T_ev"].handle, 1)
                for j in range(2):
                    n = i * 2 + j
                    act.wait_ge(s["F_mm"].handle, s["F_mm"].at(n + 1))
                    nc.scalar.copy(film_out[:, n, :], ps_F[:, 1, j, :]).then_inc(s["kept"].handle, 1)

        @block.tensor
        def _(pe):
            ring(pe, s["T_mm"], 2)
            for b in range(B):
                with pe.Fori(0, TPB // 2) as i:
                    for j in range(2):
                        n = i * 2 + (b * TPB + j)
                        pe.wait_ge(s["mean"].handle, s["mean"].at(i + (b * TPB // 2 + 1)))
                        pe.wait_ge(s["T_ev"].handle, s["T_ev"].at(n + 1))
                        nc.tensor.transpose(ps_T[:, j, 0:P], am[:, j, :], c.ident[:, :]).then_inc(s["T_mm"].handle, 1)
                    for j in range(2):
                        n = i * 2 + (b * TPB + j)
                        pe.wait_ge(s["T_ev"].handle, s["T_ev"].at(n + 3))
                        pe.wait_ge(s["F_ev"].handle, s["F_ev"].at(n + 1))
                        for o in range(2):
                            last = nc.tensor.matmul(ps_F[:, o, j, :], amT[:, j, :], VF[:, b, o, :], start=True, stop=True)
                        last.then_inc(s["F_mm"].handle, 1)
    s["step"].base += 1 + NT // 2 * (2 * rounds + 1 + 5 + 2)
    s["fence"].base += NT // 2 * (2 * rounds + 1)
    for n in ("shifted", "exped", "mean"):
        s[n].base += NT // 2
    for n in ("F_mm", "kept"):
        s[n].base += NT
    for n in ("T_mm", "T_ev", "F_ev"):
        s[n].base += NT + 2


DB = 16
NDB = D // DB
NI8 = SEQ // P


class L1Kernel:

    def __init__(self, c, st, UK):
        self.c, self.nc, self.UK = c, c.nc, UK
        self.s = {n: c.sig("ker_" + n) for n in
                  "loaded made T_mm step act arg turned earg sined exped fine mm ev".split()}
        self.a = c.sb(st, "ker_a", [P, D])
        self.r0 = c.sb(st, "ker_r0", [P, D])
        self.cols = c.sb(st, "ker_cols", [P, 5])
        self.iota_p = c.sb(st, "ker_iota", [P, P])
        self.coarse = c.sb(st, "ker_coarse", [P, SEQ // P, D])
        self.fine = c.sb(st, "ker_fine", [P, DB, P])
        self.t = c.sb(st, "ker_t", [P, DB, P])
        self.e = c.sb(st, "ker_e", [P, DB, P])
        self.m = c.sb(st, "ker_m", [P, DB, P])
        self.coarse_b = c.sb(st, "ker_coarse_b", [P, DB, NI8])


    def turns_and_exponents(self, pool, b):
        s, g = self.s, self.nc.gpsimd
        for out, of, done in ((self.e, self.a, "earg"), (self.t, self.r0, "turned")):
            g.tensor_tensor(out[:, :, :], bc(of[:, bass.ts(b, DB)].unsqueeze(2), [P, DB, P]),
                            bc(self.iota_p[:, :].unsqueeze(1), [P, DB, P]), ALU.mult).then_inc(s[done].handle, 1)

    def fractions(self, dve, b, count):
        s, v = self.s, self.nc.vector
        link = Chain(dve, s["step"], count)
        dve.wait_ge(s["turned"].handle, s["turned"].at(b + 1))
        link(v.tensor_scalar(self.t[:, :, :], self.t[:, :, :], self.cols[:, 3:4], None, ALU.add))
        link(v.tensor_scalar(self.m[:, :, :], self.t[:, :, :], MAGIC, MAGIC, ALU.add, ALU.subtract))
        v.tensor_tensor(self.t[:, :, :], self.t[:, :, :], self.m[:, :, :], ALU.subtract).then_inc(s["arg"].handle, 1)

    def exponentials(self, act, b):
        s = self.s
        act.wait_ge(s["earg"].handle, s["earg"].at(b + 1))
        self.nc.scalar.activation(self.e[:, :, :], self.e[:, :, :], ACT.Exp).then_inc(s["exped"].handle, 1)


    def sines(self, act, b):
        s = self.s
        act.wait_ge(s["arg"].handle, s["arg"].at(b + 1))
        self.nc.scalar.activation(self.t[:, :, :], self.t[:, :, :], ACT.Sin, scale=TWO_PI).then_inc(s["sined"].handle, 1)

    def powers(self, dve, b):
        s = self.s
        dve.wait_ge(s["exped"].handle, s["exped"].at(b + 1))
        dve.wait_ge(s["sined"].handle, s["sined"].at(b + 1))
        dve.wait_ge(s["mm"].handle, s["mm"].at(b + 1))
        self.nc.vector.tensor_copy(self.coarse_b[:, :, :], self.coarse[:, :, bass.ts(b, DB)].rearrange("p i d -> p d i"))\
            .then_inc(s["fine"].handle, 1)
        self.nc.vector.tensor_tensor(self.fine[:, :, :], self.t[:, :, :], self.e[:, :, :], ALU.mult)\
            .then_inc(s["fine"].handle, 1)

    def multiply(self, pe, ps_K, b):
        s = self.s
        pe.wait_ge(s["fine"].handle, s["fine"].at(b * 2 + 2))
        pe.wait_ge(s["ev"].handle, s["ev"].at(b + 1))
        for d in range(DB):
            last = self.nc.tensor.matmul(ps_K[:, d * NI8:(d + 1) * NI8], self.fine[:, d, :],
                                         self.coarse_b[:, d, :], start=True, stop=True)
        last.then_inc(s["mm"].handle, 1)

    def take(self, dve, ps_K, b):
        s = self.s
        dve.wait_ge(s["mm"].handle, s["mm"].at(b + 2))
        self.nc.vector.tensor_copy(self.UK[:, :, 2, bass.ts(b, DB)],
                                   ps_K[:, 0:DB * NI8].rearrange("p (d i) -> p i d", i=NI8)).then_inc(s["ev"].handle, 1)


    def beside_gpsimd(self, pool, b):
        pool.wait_ge(self.s["fine"].handle, self.s["fine"].at(b * 2 + 2))
        self.turns_and_exponents(pool, b + 1)

    def beside_scalar(self, act, b, half):
        if half == 0:
            self.sines(act, b)
        else:
            self.exponentials(act, b + 1)

    def beside_vector(self, dve, ps_K, b, half):
        if half == 0:
            self.powers(dve, b)
        else:
            self.fractions(dve, b + 1, (b + 1) * 2 + STEP_FINE)
            self.take(dve, ps_K, b)

    def begin(self, w):
        c, nc, s = self.c, self.nc, self.s
        a, r0, cols, iota_p, coarse = self.a, self.r0, self.cols, self.iota_p, self.coarse
        ARE, AIM, CRE, CIM = range(4)
        with ExitStack() as st:
            raw = c.sb(st, "ker_raw", [P, 4, KD, 2, NS])
            par = c.sb(st, "ker_par", [P, 4, D])
            dt = c.sb(st, "ker_dt", [P, D])
            arg = c.sb(st, "ker_arg", [P, 3, D])
            ea = c.sb(st, "ker_ea", [P, 2, D])
            tmp = c.sb(st, "ker_tmp", [P, 8, D])
            P12 = c.sb(st, "ker_P12", [P, 2, D])
            big = c.sb(st, "ker_big", [P, 3, SEQ // P, D])
            ps_T = c.ps(st, "ker_ps_T", [P, 2, 512])
            block = st.enter_context(nc.Block())

            @block.sync
            def _(sp):
                for q, name in enumerate(("A_re", "A_im", "C_re", "C_im")):
                    for twice in range(2):
                        sp.dma_start(raw[:, q, :, twice, :], w[name].rearrange("(t p) n -> p t n", p=P))\
                            .then_inc(s["loaded"].handle, 16)
                sp.dma_start(dt[:, :], row(w["log_dt"], P)).then_inc(s["loaded"].handle, 16)

            @block.gpsimd
            def _(pool):
                g = nc.gpsimd
                for q, (upper, lower) in enumerate(((2.0, 0.0), (0.0, -2.0), (-2.0, 0.0), (0.25, 0.0), (0.25 * TWO_PI, 0.0))):
                    g.memset(cols[0:NS, q:q + 1], upper).then_inc(s["made"].handle, 1)
                    pool.wait_ge(s["made"].handle, 2 * q + 1)
                    g.memset(cols[NS:P, q:q + 1], lower).then_inc(s["made"].handle, 1)
                    pool.wait_ge(s["made"].handle, 2 * q + 2)
                g.iota(iota_p[:, :], pattern=[[1, P]], base=0, channel_multiplier=0,
                       allow_small_or_imprecise_dtypes=True).then_inc(s["made"].handle, 1)
                pool.wait_ge(s["made"].handle, s["made"].at(11))
                pool.wait_ge(s["step"].handle, s["step"].at(5))
                self.turns_and_exponents(pool, 0)

            @block.tensor
            def _(pe):
                pe.wait_ge(s["loaded"].handle, s["loaded"].at(16 * 9))
                for q in range(4):
                    for k in range(KD):
                        o = (q % 2) * D + k * P
                        last = nc.tensor.transpose(ps_T[:, q // 2, o:o + P], raw[:, q, k, :, :].rearrange("p a n -> p (a n)"),
                                                   c.ident[:, :])
                last.then_inc(s["T_mm"].handle, 1)

            @block.scalar
            def _(act):
                A = s["act"]
                act.wait_ge(s["loaded"].handle, s["loaded"].at(16 * 9))
                nc.scalar.activation(dt[:, :], dt[:, :], ACT.Exp).then_inc(A.handle, 1)
                act.wait_ge(s["step"].handle, s["step"].at(8))
                nc.scalar.activation(ea[:, 0, :], a[:, :], ACT.Exp).then_inc(A.handle, 1)
                nc.scalar.activation(ea[:, 1, :], a[:, :], ACT.Tanh, scale=0.5).then_inc(A.handle, 1)
                nc.scalar.activation(arg[:, :, :], arg[:, :, :], ACT.Sin, scale=TWO_PI).then_inc(A.handle, 1)
                act.wait_ge(s["step"].handle, s["step"].at(STEP_COARSE))
                for q in range(2):
                    nc.scalar.activation(big[:, q, :, :], big[:, q, :, :], ACT.Sin, scale=TWO_PI).then_inc(A.handle, 1)
                nc.scalar.activation(big[:, 2, :, :], big[:, 2, :, :], ACT.Exp).then_inc(A.handle, 1)
                self.exponentials(act, 0)

            @block.vector
            def _(dve):
                v = nc.vector
                link = Chain(dve, s["step"])
                x = tmp
                dve.wait_ge(s["T_mm"].handle, s["T_mm"].at(1))
                dve.wait_ge(s["act"].handle, s["act"].at(1))
                v.tensor_copy(par[:, :, :].rearrange("p (a q) d -> p a (q d)", a=2), ps_T[:, :, :]).then_inc(s["ev"].handle, 1)
                dve.wait_ge(s["ev"].handle, s["ev"].at(1))
                dve.wait_ge(s["made"].handle, s["made"].at(11))
                link(v.tensor_tensor(a[:, :], par[:, ARE, :], dt[:, :], ALU.mult))

                def turns(out, cycles, work, more=0.0):
                    link(v.tensor_scalar(out, cycles, more, None, ALU.add))
                    link(v.tensor_scalar(work, out, MAGIC, MAGIC, ALU.add, ALU.subtract))
                    link(v.tensor_tensor(out, out, work, ALU.subtract))

                link(v.tensor_tensor(r0[:, :], par[:, AIM, :], dt[:, :], ALU.mult))
                link(v.tensor_scalar(r0[:, :], r0[:, :], 0.5 / np.pi, None, ALU.mult))
                link(v.tensor_scalar(x[:, 0, :], r0[:, :], MAGIC, MAGIC, ALU.add, ALU.subtract))
                link(v.tensor_tensor(r0[:, :], r0[:, :], x[:, 0, :], ALU.subtract))
                v.tensor_copy(arg[:, 0, :], r0[:, :])
                v.tensor_scalar(arg[:, 2, :], r0[:, :], 0.5, None, ALU.mult)
                turns(arg[:, 1, :], r0[:, :], x[:, 0, :], 0.25)
                dve.wait_ge(s["act"].handle, s["act"].at(4))
                sn, cs, sh, e1, th = arg[:, 0, :], arg[:, 1, :], arg[:, 2, :], ea[:, 0, :], ea[:, 1, :]
                are, aim, cre, cim = [par[:, q, :] for q in range(4)]

                def mul(out, p, q):
                    link(v.tensor_tensor(out, p, q, ALU.mult))

                er, ei, tr, ti, q, u1, u2 = [x[:, n, :] for n in range(7)]
                link(v.tensor_scalar(u1, e1, 1.0, None, ALU.add))
                mul(er, th, u1)
                mul(er, er, cs)
                mul(u2, sh, sh)
                link(v.scalar_tensor_tensor(er, u2, -2.0, er, ALU.mult, ALU.add))
                mul(ei, e1, sn)
                mul(u1, er, are)
                mul(u2, ei, aim)
                link(v.tensor_tensor(tr, u1, u2, ALU.add))
                mul(u1, ei, are)
                mul(u2, er, aim)
                link(v.tensor_tensor(ti, u1, u2, ALU.subtract))
                mul(u1, are, are)
                mul(u2, aim, aim)
                link(v.tensor_tensor(q, u1, u2, ALU.add))
                link(v.reciprocal(q, q))
                mul(tr, tr, q)
                mul(ti, ti, q)
                mul(u1, cre, tr)
                mul(u2, cim, ti)
                link(v.tensor_tensor(er, u1, u2, ALU.subtract))
                mul(u1, cre, ti)
                mul(u2, cim, tr)
                link(v.tensor_tensor(ei, u1, u2, ALU.add))
                link(v.tensor_scalar(u1, ei, cols[:, 1:2], None, ALU.mult))
                link(v.scalar_tensor_tensor(P12[:, 0, :], er, cols[:, 0:1], u1, ALU.mult, ALU.add))
                link(v.tensor_scalar(u1, ei, cols[:, 2:3], None, ALU.mult))
                link(v.scalar_tensor_tensor(P12[:, 1, :], er, cols[:, 1:2], u1, ALU.mult, ALU.add))
                for i in range(NI8):
                    v.tensor_scalar(big[:, 0, i, :], r0[:, :], float(i * P), None, ALU.mult)
                    link(v.tensor_scalar(big[:, 2, i, :], a[:, :], float(i * P), None, ALU.mult))
                link(v.tensor_scalar(coarse[:, :, :], big[:, 0, :, :], MAGIC, MAGIC, ALU.add, ALU.subtract))
                link(v.tensor_tensor(big[:, 0, :, :], big[:, 0, :, :], coarse[:, :, :], ALU.subtract))
                turns(big[:, 1, :, :], big[:, 0, :, :], coarse[:, :, :], 0.25)
                check(link.count, STEP_COARSE)
                dve.wait_ge(s["act"].handle, s["act"].at(7))
                for q in range(2):
                    mul(big[:, 1 - q, :, :], big[:, 1 - q, :, :], bc(P12[:, q, :].unsqueeze(1), [P, NI8, D]))
                link(v.tensor_tensor(big[:, 0, :, :], big[:, 0, :, :], big[:, 1, :, :], ALU.add))
                mul(coarse[:, :, :], big[:, 0, :, :], big[:, 2, :, :])
                check(link.count, STEP_FINE)
                ring(dve, s["mm"], 1)
                self.fractions(dve, 0, STEP_FINE)
                dve.wait_ge(s["arg"].handle, s["arg"].at(1))

    def finish(self, first):
        c, nc, s = self.c, self.nc, self.s
        with ExitStack() as st:
            ps_K = c.ps(st, "ker_ps_K", [P, 512])
            block = st.enter_context(nc.Block())

            @block.gpsimd
            def _(pool):
                for b in range(first, NDB - 1):
                    self.beside_gpsimd(pool, b)

            @block.scalar
            def _(act):
                for b in range(first, NDB):
                    self.sines(act, b)
                    if b + 1 < NDB:
                        self.exponentials(act, b + 1)

            @block.vector
            def _(dve):
                for b in range(first, NDB):
                    self.powers(dve, b)
                    if b + 1 < NDB:
                        self.fractions(dve, b + 1, (b + 1) * 2 + STEP_FINE)
                    self.take(dve, ps_K, b)
                dve.wait_ge(s["ev"].handle, s["ev"].at(NDB + 1))

            @block.tensor
            def _(pe):
                for b in range(first, NDB):
                    self.multiply(pe, ps_K, b)


STEP_COARSE = 8 + 28 + 8 + 2 + 3
STEP_FINE = STEP_COARSE + 4


def check(count, expected):
    assert count == expected, (count, expected)


def L1_convolve(c, fwd, inv, UK, y):
    nc = c.nc
    s = {n: c.sig("cv_" + n) for n in "step f0 f1 i0 i1 X_mm X_ev Z V_mm V_ev prod acc".split()}
    order = [0, 4, 2, 1, 3]
    W3 = 3 * D
    with ExitStack() as st:
        F = c.sb(st, "cv_F", [P, 2, 3, 2, NF2])
        I = c.sb(st, "cv_I", [P, 2, 3, 2, NF2])
        ab = c.sb(st, "cv_ab", [P, 3, 2, W3])
        Z = c.sb(st, "cv_Z", [P, 2, 2, 2, W3])
        X = c.sb(st, "cv_X", [P, 2, 2, W3])
        Y = c.sb(st, "cv_Y", [P, 2, 2, 2 * D])
        T = c.sb(st, "cv_T", [P, 2, 2, 2 * D])
        ps_X = c.ps(st, "cv_ps_X", [P, 2, 2, 512])
        ps_V = c.ps(st, "cv_ps_V", [P, 2, 2, 512])
        block = st.enter_context(nc.Block())
        real = [f in (0, 4) for f in order]

        def u(j1):
            return UK[:, 2 * j1:2 * j1 + 2, :, :].rearrange("p q b d -> p q (b d)")

        n_V = [sum(1 if r else 2 for r in real[:i]) for i in range(NF1 + 1)]

        @block.sync
        def _(sp):
            for i, f in enumerate(order):
                if i >= 2:
                    sp.wait_ge(s["X_mm"].handle, 4 * (i - 1))
                sp.dma_start(F[:, i % 2, :, :, :], fwd[f, :, :, :].rearrange("m (q p) n -> p m q n", p=P))\
                    .then_inc(s[f"f{i % 2}"].handle, 16)
                if i >= 2:
                    sp.wait_ge(s["V_mm"].handle, n_V[i - 1])
                sp.dma_start(I[:, i % 2, :, :, :], inv[f, :, :, :].rearrange("m (q p) n -> p m q n", p=P))\
                    .then_inc(s[f"i{i % 2}"].handle, 16)

        @block.tensor
        def _(pe):
            COS, SIN, NEG = range(3)

            def forward(i):
                pe.wait_ge(s[f"f{i % 2}"].handle, 16 * (i // 2 + 1))
                pe.wait_ge(s["Z"].handle, i + 1)
                for part in range(2):
                    terms = [(COS, 0), (SIN, 1)] if part == 0 else [(NEG, 0), (COS, 1)]
                    terms = [x for x in terms if not (real[i] and x[1] == 1)]
                    for mt in range(2):
                        n = 4 * i + 2 * part + mt
                        if n >= 2:
                            pe.wait_ge(s["X_ev"].handle, n - 1)
                        for lo, hi in ((0, 512), (512, W3)):
                            for m, (plane, zp) in enumerate(terms):
                                for q in range(2):
                                    last = nc.tensor.matmul(ps_X[:, n % 2, lo // 512, 0:hi - lo],
                                                            F[:, i % 2, plane, q, mt * P:(mt + 1) * P],
                                                            Z[:, i % 2, zp, q, lo:hi], start=(m == 0 and q == 0),
                                                            stop=(m == len(terms) - 1 and q == 1))
                        last.then_inc(s["X_mm"].handle, 1)

            def backward(i):
                pe.wait_ge(s[f"i{i % 2}"].handle, 16 * (i // 2 + 1))
                pe.wait_ge(s["prod"].handle, i + 1)
                for part in range(1 if real[i] else 2):
                    terms = [(COS, 0), (NEG, 1)] if part == 0 else [(SIN, 0), (COS, 1)]
                    n = n_V[i] + part
                    if n >= 2:
                        pe.wait_ge(s["V_ev"].handle, n - 1)
                    for q in range(2):
                        for m, (plane, yp) in enumerate(terms):
                            for mt in range(2):
                                last = nc.tensor.matmul(ps_V[:, n % 2, q, :], I[:, i % 2, plane, mt, q * P:(q + 1) * P],
                                                        Y[:, yp, mt, :], start=(m == 0 and mt == 0),
                                                        stop=(m == 1 and mt == 1))
                    last.then_inc(s["V_mm"].handle, 1)

            forward(0)
            for i in range(NF1):
                if i + 1 < NF1:
                    forward(i + 1)
                backward(i)

        @block.scalar
        def _(act):
            for n in range(4 * NF1):
                i, part, mt = n // 4, n // 2 % 2, n % 2
                act.wait_ge(s["X_mm"].handle, n + 1)
                if n % 4 == 0 and i:
                    act.wait_ge(s["prod"].handle, i)
                nc.scalar.copy(X[:, part, mt, 0:512], ps_X[:, n % 2, 0, :])
                nc.scalar.copy(X[:, part, mt, 512:W3], ps_X[:, n % 2, 1, 0:D]).then_inc(s["X_ev"].handle, 1)

        @block.vector
        def _(dve):
            v = nc.vector
            link = Chain(dve, s["step"])
            add, sub = ALU.add, ALU.subtract

            def transform(i):
                f = order[i]
                zr, zi = Z[:, i % 2, 0, :, :], Z[:, i % 2, 1, :, :]
                if i >= 2:
                    dve.wait_ge(s["X_mm"].handle, 4 * (i - 1))
                if f == 0:
                    link(v.tensor_tensor(ab[:, 0, :, :], u(0), u(2), add))
                    link(v.tensor_tensor(ab[:, 1, :, :], u(1), u(3), add))
                    link(v.tensor_tensor(zr, ab[:, 0, :, :], ab[:, 1, :, :], add))
                elif f == 4:
                    link(v.tensor_tensor(zr, ab[:, 0, :, :], ab[:, 1, :, :], sub))
                elif f == 2:
                    link(v.tensor_tensor(ab[:, 2, :, :], u(3), u(1), sub))
                    link(v.tensor_copy(zi, ab[:, 2, :, :]))
                    link(v.tensor_tensor(zr, u(0), u(2), sub))
                else:
                    sign = -1.0 if f == 1 else 1.0
                    link(v.scalar_tensor_tensor(zr, ab[:, 2, :, :], sign * R2, u(0), ALU.mult, add))
                    link(v.scalar_tensor_tensor(zi, ab[:, 1, :, :], -R2, u(2), ALU.mult, sub if f == 1 else add))
                dve.sem_inc(s["Z"].handle, 1)

            def products(i):
                dve.wait_ge(s["X_ev"].handle, 4 * (i + 1))
                if i:
                    dve.wait_ge(s["V_mm"].handle, n_V[i])

                def part(n):
                    return X[:, n, :, 0:2 * D].rearrange("p m (b d) -> p m b d", b=B)

                def k(n, mt):
                    return bc(X[:, n, mt, 2 * D:W3].unsqueeze(1), [P, B, D])

                for out, ((x0, k0), (x1, k1)), op in ((0, ((0, 0), (1, 1)), sub), (1, ((0, 1), (1, 0)), add)):
                    for mt in range(2):
                        v.tensor_tensor(T[:, 0, mt, :].rearrange("p (b d) -> p b d", b=B), part(x0)[:, mt, :, :], k(k0, mt), ALU.mult)
                        link(v.tensor_tensor(T[:, 1, mt, :].rearrange("p (b d) -> p b d", b=B), part(x1)[:, mt, :, :],
                                             k(k1, mt), ALU.mult))
                    link(v.tensor_tensor(Y[:, out, :, :], T[:, 0, :, :], T[:, 1, :, :], op))
                dve.sem_inc(s["prod"].handle, 1)

            def accumulate(i):
                f = order[i]
                for part in range(1 if real[i] else 2):
                    n = n_V[i] + part
                    dve.wait_ge(s["V_mm"].handle, n + 1)
                    V = ps_V[:, n % 2, :, :].rearrange("p q (b d) -> p q b d", b=B)
                    for j1 in range(4):
                        turn = 2 * np.pi * j1 * f / 8
                        factor = float(np.cos(turn) if part == 0 else -np.sin(turn))
                        out = y[:, 2 * j1:2 * j1 + 2, :, :]
                        if i == 0:
                            link(v.tensor_copy(out, V))
                        elif abs(factor) > 1e-9:
                            link(v.scalar_tensor_tensor(out, V, factor, out, ALU.mult, add))
                    dve.sem_inc(s["V_ev"].handle, 1)

            transform(0)
            transform(1)
            for i in range(NF1):
                products(i)
                if i + 2 < NF1:
                    transform(i + 2)
                accumulate(i)


def L1_join(c, w, UK, y, film_out):
    nc = c.nc
    loaded, step = c.sig("join_loaded"), c.sig("join_step")
    with ExitStack() as st:
        skip = c.sb(st, "join_skip", [P, D])
        block = st.enter_context(nc.Block())

        @block.sync
        def _(sp):
            sp.dma_start(skip[:, :], row(w["D_skip"], P)).then_inc(loaded.handle, 16)

        @block.vector
        def _(dve):
            v = nc.vector
            link = Chain(dve, step)
            dve.wait_ge(loaded.handle, 16)
            for b in range(B):
                tiles = slice(b * TPB, (b + 1) * TPB)
                u = UK[:, :, b, :]
                link(v.tensor_tensor(u, u, bc(skip[:, :].unsqueeze(1), [P, TPB, D]), ALU.mult))
                link(v.tensor_tensor(u, u, y[:, :, b, :], ALU.add))
                link(v.tensor_tensor(u, u, film_out[:, tiles, 0:D], ALU.mult))
                link(v.tensor_tensor(u, u, film_out[:, tiles, D:2 * D], ALU.add))
                link(v.tensor_tensor(c.xn[:, tiles, :], c.xn[:, tiles, :], u, ALU.add))


def add_all(c, src):
    nc = c.nc
    added = c.sig("added")
    with nc.Block() as block:
        @block.vector
        def _(dve):
            nc.vector.tensor_tensor(c.x[:, :, :], c.x[:, :, :], src[:, :, :], ALU.add).then_inc(added.handle, 1)
            dve.wait_ge(added.handle, added.at(1))
    added.base += 1


def L1_xattn(c, w, consts, mask_tok, mask_ctx, xT, UK):
    y = xT[:, :, :].rearrange("p k n -> p (k n)").rearrange("p (i b d) -> p i b d", i=TPB, b=B)
    xt = c.xn
    with ExitStack() as st:
        film_out = c.sb(st, "l1_film_out", [P, NT, 2 * D])
        with ExitStack() as att:
            M = c.sb(att, "l1_M", [P, KD, B, HJ1])
            mask_row = c.sb(att, "l1_mask_row", [1, B, HJ1])
            VF = c.sb(att, "l1_VF", [JE, B, 2, 2 * D])
            tok_factor = c.sb(att, "l1_tok_factor", [P, NT])
            scores = c.sb(att, "l1_scores", [P, NT, HJ1])
            L1_fold(c, w, mask_tok, mask_ctx, M, mask_row, VF, tok_factor[:, :])
            normalise(c, c.x, xn_out=c.xn, router=(None, HJ1, scores), resident=(M, mask_row))
            ln_stats(c, c.xn)
            normalise(c, c.xn, xn_out=lambda n, b, t: UK[:, t, b, :], affine=(w["g_norm_in"], w["b_norm_in"]))
            L1_modulate(c, scores, tok_factor, VF, UK, film_out)
        L1_convolve(c, consts["dft_fwd"], consts["dft_inv"], UK, y)
        L1_join(c, w, UK, y, film_out)
    ln_stats(c, xt)
    normalise(c, xt, xT_out=xT, affine=(w["g_ffn"], w["b_ffn"]))
    one = {n: w[n].unsqueeze(0) for n in ("W1", "W2", "b1")}
    experts(c, xT, 1, 4 * D, one["W1"], None, one["W2"], one["b1"], ACT.Gelu, lambda t, e: 1.0, xt)
    add_row(c, xt, w["b2"])
    ln_stats(c, xt)
    with ExitStack() as st:
        out = c.sb(st, "l1_out", [P, NT, D])
        normalise(c, xt, xn_out=out, affine=(w["g_norm_out"], w["b_norm_out"]))
        add_all(c, out)


def store(c, out):
    nc = c.nc
    stored = c.sig("stored")
    with nc.Block() as block:
        @block.sync
        def _(sp):
            sp.dma_start(out.rearrange("b (t p) d -> p (b t) d", p=P), c.x[:, :, :]).then_inc(stored.handle, 16)
            sp.wait_ge(stored.handle, 16)


LAYERS = ("L0_xattn", "L0_ffn", "L1_xattn", "L1_ffn", "L2_xattn", "L2_ffn", "L3_xattn", "L3_ffn")


def build(nc, a, out, layers=LAYERS):
    with ExitStack() as ctx:
        c = Core(nc, ctx)
        scratch = nc.dram_tensor("scratch", (B, HJC * P, D), F32).ap()
        setup(c, a["x"], a["ctx_768"], a["mask_BxS_bf1"], a["mask_BxS2_bf1"])
        exchange_buffers(c)
        xT = c.sb(ctx, "xT", [P, KD, B * SEQ])
        for layer in layers:
            w = {n[len(layer) + 1:]: ap for n, ap in a.items() if n.startswith(layer)}
            ln_stats(c, c.x)
            if layer == "L0_xattn":
                wide_attention(c, w["Wq"], w["Wk"], w["Wv"], w["Wo"], w["bo"], scratch)
            elif layer == "L2_xattn":
                wide_attention(c, w["w_q"], w["w_k"], w["w_v"], w["w_out"], w["b_out"], scratch)
            elif layer == "L0_ffn":
                made_of_l1 = ctx.enter_context(ExitStack())
                UK = c.sb(made_of_l1, "l1_UK", [P, TPB, B + 1, D])
                with ExitStack() as st:
                    kernel_l1 = L1Kernel(c, st, UK)
                    kernel_l1.begin({n: a["L1_xattn_" + n] for n in ("log_dt", "A_re", "A_im", "C_re", "C_im")})
                    L0_ffn(c, w, kernel_l1)
            elif layer == "L2_ffn":
                L2_ffn(c, w)
            elif layer == "L1_xattn":
                L1_xattn(c, w, a, a["mask_BxS_bf1"], a["mask_BxS2_bf1"], xT, UK)
                made_of_l1.close()
            elif layer == "L3_xattn":
                L3_xattn(c, w, scratch, xT)
            elif layer == "L1_ffn":
                L1_ffn(c, w, xT)
            elif layer == "L3_ffn":
                L3_ffn(c, w, xT)
        store(c, out)


def kernel(**inputs):
    import concourse.bacc as bacc
    from concourse.bass_utils import run_bass_kernel_spmd

    nc = bacc.Bacc("TRN2", target_bir_lowering=False, num_devices=1)
    arrays, aps = {}, {}
    for name, value in (inputs | constants()).items():
        v = np.ascontiguousarray(value)
        if v.dtype == np.bool_:
            v = v.view(np.uint8)
        if v.ndim == 0:
            v = v.reshape(1)
        arrays[f"in_{name}"] = v
        aps[name] = nc.dram_tensor(f"in_{name}", v.shape, mybir.dt.from_np(v.dtype), kind="ExternalInput").ap()
    out = nc.dram_tensor("out", (B, SEQ, D), F32, kind="ExternalOutput").ap()
    build(nc, aps, out)
    result = run_bass_kernel_spmd(nc, [arrays], core_ids=[0])
    return result.results[0]["out"]
```

```python
from contextlib import ExitStack

import numpy as np

import concourse.bass as bass
from concourse import mybir

F32 = mybir.dt.float32
U32 = mybir.dt.uint32
U8 = mybir.dt.uint8
ALU = mybir.AluOpType
ACT = mybir.ActivationFunctionType
AX = mybir.AxisListType

P = 128
B, SEQ, D = 2, 1024, 256
NT = B * SEQ // P
TPB = NT // B
KD = D // P
J, DC = 77, 192
KC = DC // 2
BJ = B * J
CH = 512
NCH = B * SEQ // CH
TPC = CH // P
LN_EPS = 1e-5
MAGIC = 1.5 * 2 ** 23


class Signal:

    def __init__(self, handle):
        self.handle, self.base = handle, 0

    def at(self, n):
        return n + self.base


class Chain:

    def __init__(self, eng, signal, start=0):
        self.eng, self.counted, self.count = eng, signal, start

    def __call__(self, instruction):
        self.count = self.count + 1
        instruction.then_inc(self.counted.handle, 1)
        self.eng.wait_ge(self.counted.handle, self.counted.at(self.count))


class Core:

    def __init__(self, nc, ctx):
        self.nc, self.ctx = nc, ctx
        self.semaphores, self.names = {}, {}

    def sig(self, name):
        if name not in self.semaphores:
            self.semaphores[name] = Signal(self.ctx.enter_context(self.nc.semaphore(name)))
        return self.semaphores[name]

    def unique(self, name):
        self.names[name] = self.names.get(name, 0) + 1
        return f"{name}_{self.names[name]}"

    def sb(self, ctx, name, shape, dt=F32):
        return ctx.enter_context(self.nc.sbuf_tensor(self.unique(name), shape, dt))

    def ps(self, ctx, name, shape, dt=F32):
        return ctx.enter_context(self.nc.psum_tensor(self.unique(name), shape, dt))


def row(v, n):
    return v.rearrange("(o n) -> o n", o=1).to_broadcast([n, v.shape[0]])


def column(v):
    return v.rearrange("(t p) -> p t", p=P)


def bc(ap, shape):
    return ap.to_broadcast(shape)


def setup(c, x, ctx_in, mask_tok, mask_ctx):
    nc = c.nc
    c.x = c.sb(c.ctx, "x", [P, NT, D])
    c.xn = c.sb(c.ctx, "xn", [P, NT, D])
    c.ident = c.sb(c.ctx, "ident", [P, P])
    c.ones = c.sb(c.ctx, "ones", [1, P])
    c.zeros = c.sb(c.ctx, "zeros", [P, D * 2])
    c.ctxT = c.sb(c.ctx, "ctxT", [KC, 2, BJ])
    c.rstd = c.sb(c.ctx, "rstd", [P, NT])
    c.nmr = c.sb(c.ctx, "nmr", [P, NT])
    loaded, ident_ready = c.sig("setup_loaded"), c.sig("ident_ready")
    transposed, copied = c.sig("setup_transposed"), c.sig("setup_copied")
    with ExitStack() as st:
        ctx_rows = c.sb(st, "ctx_rows", [J, B, DC])
        psT = c.ps(st, "setup_psT", [KC, 4 * J])
        block = st.enter_context(nc.Block())

        @block.sync
        def _(sp):
            sp.dma_start(ctx_rows[:, :, :], ctx_in.rearrange("b j d -> j b d")).then_inc(loaded.handle, 16)
            sp.dma_start(c.x[:, :, :], x.rearrange("b (t p) d -> p (b t) d", p=P)).then_inc(loaded.handle, 16)
            sp.wait_ge(loaded.handle, 32)

        @block.gpsimd
        def _(pool):
            nc.gpsimd.memset(c.ident[:, :], 0.0).then_inc(ident_ready.handle, 1)
            pool.wait_ge(ident_ready.handle, 1)
            nc.gpsimd.affine_select(out=c.ident[:, :], in_=c.ident[:, :], compare_op=ALU.not_equal, fill=1.0,
                                    base=0, pattern=[[-1, P]], channel_multiplier=1).then_inc(ident_ready.handle, 1)
            nc.gpsimd.memset(c.ones[:, :], 1.0).then_inc(ident_ready.handle, 1)
            nc.gpsimd.memset(c.zeros[:, :], 0.0).then_inc(ident_ready.handle, 1)
            pool.wait_ge(ident_ready.handle, 4)

        @block.tensor
        def _(pe):
            pe.wait_ge(ident_ready.handle, 3)
            pe.wait_ge(loaded.handle, 16)
            pe.wait_ge(loaded.handle, 32)
            for b in range(B):
                for k in range(2):
                    last = nc.tensor.transpose(psT[:, (k * B + b) * J:(k * B + b + 1) * J],
                                               ctx_rows[:, b, k * KC:(k + 1) * KC], c.ident[0:J, 0:J])
            last.then_inc(transposed.handle, 1)

        @block.vector
        def _(dve):
            dve.wait_ge(transposed.handle, 1)
            nc.vector.tensor_copy(c.ctxT[:, :, :], psT[:, :].rearrange("p (k n) -> p k n", k=2)).then_inc(copied.handle, 1)
            dve.wait_ge(copied.handle, 1)


class TokenStats:

    def __init__(self, c, st, src):
        self.c, self.nc, self.src = c, c.nc, src
        self.stats_done, self.var_ready, self.std_ready, self.step = \
            c.sig("ln_stats"), c.sig("ln_var"), c.sig("ln_std"), c.sig("ln_step")
        self.bn = c.sb(st, "ln_bn", [P, NT, 6])
        self.msum = c.sb(st, "ln_msum", [P, NT])
        self.diff = c.sb(st, "ln_diff", [P, NT])
        self.var = c.sb(st, "ln_var", [P, NT])
        self.std = c.sb(st, "ln_std", [P, NT])
        self.tmp = c.sb(st, "ln_tmp", [P, NT])

    def tile(self, t):
        self.nc.vector.bn_stats(self.bn[:, t, :], self.src[:, t, :]).then_inc(self.stats_done.handle, 1)

    def all_tiles(self, dve):
        with dve.Fori(0, NT // 4) as i:
            for j in range(4):
                self.tile(i * 4 + j)

    def finish(self, dve):
        c, nc, stats_done = self.c, self.nc, self.stats_done
        bn, msum, diff, var, tmp = self.bn, self.msum, self.diff, self.var, self.tmp
        dve.wait_ge(stats_done.handle, stats_done.at(NT))
        link = Chain(dve, self.step)
        nc.vector.tensor_tensor(msum[:, :], bn[:, :, 1], bn[:, :, 4], ALU.add).then_inc(stats_done.handle, 1)
        link(nc.vector.tensor_tensor(diff[:, :], bn[:, :, 1], bn[:, :, 4], ALU.subtract))
        nc.vector.tensor_tensor(var[:, :], bn[:, :, 2], bn[:, :, 5], ALU.add).then_inc(stats_done.handle, 1)
        link(nc.vector.tensor_tensor(diff[:, :], diff[:, :], diff[:, :], ALU.mult))
        dve.wait_ge(stats_done.handle, stats_done.at(NT + 2))
        link(nc.vector.tensor_scalar(var[:, :], var[:, :], 1.0 / D, LN_EPS, ALU.mult, ALU.add))
        nc.vector.scalar_tensor_tensor(var[:, :], diff[:, :], 0.25, var[:, :], ALU.mult, ALU.add)\
            .then_inc(self.var_ready.handle, 1)
        dve.wait_ge(self.std_ready.handle, self.std_ready.at(1))
        link(nc.vector.reciprocal(c.rstd[:, :], self.std[:, :]))
        link(nc.vector.tensor_tensor(tmp[:, :], c.rstd[:, :], c.rstd[:, :], ALU.mult))
        link(nc.vector.tensor_tensor(tmp[:, :], tmp[:, :], var[:, :], ALU.mult))
        link(nc.vector.tensor_scalar(tmp[:, :], tmp[:, :], -0.5, 1.5, ALU.mult, ALU.add))
        link(nc.vector.tensor_tensor(c.rstd[:, :], c.rstd[:, :], tmp[:, :], ALU.mult))
        link(nc.vector.scalar_tensor_tensor(c.nmr[:, :], msum[:, :], -0.5, c.rstd[:, :], ALU.mult, ALU.mult))

    def finish_alone(self):
        with self.nc.Block() as block:
            @block.vector
            def _(dve):
                self.finish(dve)

            @block.scalar
            def _(act):
                self.square_roots(act)
        self.done()

    def square_roots(self, act):
        act.wait_ge(self.var_ready.handle, self.var_ready.at(1))
        self.nc.scalar.activation(self.std[:, :], self.var[:, :], ACT.Sqrt).then_inc(self.std_ready.handle, 1)

    def done(self):
        self.stats_done.base += NT + 2
        self.var_ready.base += 1
        self.std_ready.base += 1
        self.step.base += 9


def ln_stats(c, src):
    with ExitStack() as st:
        stats = TokenStats(c, st, src)
        block = st.enter_context(c.nc.Block())

        @block.vector
        def _(dve):
            stats.all_tiles(dve)
            stats.finish(dve)

        @block.scalar
        def _(act):
            stats.square_roots(act)
        stats.done()


HEADS = 16
HJ = HEADS * J
HJC = (HJ + P - 1) // P
PT_CUT = 512 // P
INNER = 1024
NI = INNER // P
SCORE_CUTS = [(0, 512), (512, 1024), (1024, HJ)]


def wide_attention(c, wq, wk, wv, wo, bo, scratch, beside=None):
    nc = c.nc
    with ExitStack() as st:
        M = c.sb(st, "att_M", [P, KD, B, HJ])
        N = c.sb(st, "att_N", [P, B, HJC, D])
        wide_fold(c, wq, wk, wv, wo, scratch, M, N)
        attention(c, M, None, N, bo, None, beside)


def wide_fold(c, wq, wk, wv, wo, scratch, M, N):
    nc = c.nc
    loaded, filled, mm, ev = c.sig("fold_loaded"), c.sig("fold_filled"), c.sig("fold_mm"), c.sig("fold_ev")
    stored = c.sig("fold_stored")
    TRIPLES = [range(g + odd, min(g + 6, HEADS), 2) for g in range(0, HEADS, 6) for odd in range(2)]
    PAIRS = [range(g + odd, g + 4, 2) for g in range(0, HEADS, 4) for odd in range(2)]
    with ExitStack() as st:
        Wq = c.sb(st, "fold_Wq", [P, KD, INNER])
        Wk = c.sb(st, "fold_Wk", [KC, 2, INNER])
        Wv = c.sb(st, "fold_Wv", [KC, 2, INNER])
        Wo = c.sb(st, "fold_Wo", [P, NI, D])
        KT = c.sb(st, "fold_KT", [P, NI, BJ])
        VT = c.sb(st, "fold_VT", [P, NI, BJ])
        WqT = c.sb(st, "fold_WqT", [P, NI, D])
        rows = c.sb(st, "fold_rows", [J, HEADS, D])
        ps = c.ps(st, "fold_ps", [P, 4, 512])
        stats = TokenStats(c, st, c.x)
        block = st.enter_context(nc.Block())
        steps = [("K", m) for m in range(NI)] + [("V", m) for m in range(NI)] + [("Q", m) for m in range(0, NI, 2)]
        steps += [("M", (k, g)) for k in range(KD) for g in TRIPLES]
        steps += [("N", (b, g)) for b in range(B) for g in PAIRS]
        n_kvq = 2 * NI + NI // 2
        n_m = KD * len(TRIPLES)
        n_nb = HEADS // 2

        @block.sync
        def _(sp):
            sp.dma_start(Wk[:, :, :], wk.rearrange("(k p) n -> p k n", p=KC)).then_inc(loaded.handle, 16)
            sp.dma_start(Wv[:, :, :], wv.rearrange("(k p) n -> p k n", p=KC)).then_inc(loaded.handle, 16)
            sp.dma_start(Wq[:, :, :], wq.rearrange("(k p) n -> p k n", p=P)).then_inc(loaded.handle, 16)
            sp.dma_start(Wo[:, :, :], wo.rearrange("(k p) n -> p k n", p=P)).then_inc(loaded.handle, 16)
            for b in range(B):
                sp.wait_ge(ev.handle, ev.at(n_kvq + n_m + (b + 1) * n_nb))
                sp.dma_start(scratch[b, 0:HJ, :].rearrange("(h j) d -> j h d", j=J), rows[:, :, :])\
                    .then_inc(stored.handle, 16)
                sp.wait_ge(stored.handle, stored.at(16 * (3 * b + 1)))
                if b == 0:
                    sp.wait_ge(filled.handle, filled.at(1))
                full = HJ // P
                sp.dma_start(N[:, b, 0:full, :], scratch[b, 0:full * P, :].rearrange("(c p) d -> p c d", p=P))\
                    .then_inc(stored.handle, 16)
                sp.dma_start(N[0:HJ - full * P, b, full, :], scratch[b, full * P:HJ, :]).then_inc(stored.handle, 16)
                sp.wait_ge(stored.handle, stored.at(16 * (3 * b + 3)))

        @block.gpsimd
        def _(pool):
            nc.gpsimd.memset(N[:, :, HJC - 1, :], 0.0).then_inc(filled.handle, 1)

        @block.tensor
        def _(pe):
            pe.wait_ge(loaded.handle, loaded.at(64))
            for n, (kind, at) in enumerate(steps):
                bank = ps[:, n % 4, :]
                if n >= 4:
                    pe.wait_ge(ev.handle, ev.at(n - 3))
                if n == n_kvq:
                    pe.wait_ge(ev.handle, ev.at(n_kvq))
                if kind in "KV":
                    W = Wk if kind == "K" else Wv
                    for k in range(2):
                        last = nc.tensor.matmul(bank[:, 0:BJ], W[:, k, at * P:(at + 1) * P], c.ctxT[:, k, :],
                                                start=(k == 0), stop=(k == 1))
                elif kind == "Q":
                    for m in (at, at + 1):
                        for k in range(KD):
                            o = (m - at) * D + k * P
                            last = nc.tensor.transpose(bank[:, o:o + P], Wq[:, k, m * P:(m + 1) * P], c.ident[:, :])
                elif kind == "M":
                    k, g = at
                    for i, h in enumerate(g):
                        o = 64 * (h % 2)
                        last = nc.tensor.matmul(bank[:, i * BJ:(i + 1) * BJ], WqT[o:o + 64, h // 2, k * P:(k + 1) * P],
                                                KT[o:o + 64, h // 2, :], start=True, stop=True)
                else:
                    b, g = at
                    for i, h in enumerate(g):
                        o = 64 * (h % 2)
                        last = nc.tensor.matmul(bank[0:J, i * D:(i + 1) * D],
                                                VT[o:o + 64, h // 2, b * J:(b + 1) * J], Wo[o:o + 64, h // 2, :],
                                                start=True, stop=True)
                last.then_inc(mm.handle, 1)

        @block.scalar
        def _(act):
            stats.square_roots(act)

        @block.vector
        def _(dve):
            stats.all_tiles(dve)
            stats.finish(dve)
            for n, (kind, at) in enumerate(steps):
                bank = ps[:, n % 4, :]
                dve.wait_ge(mm.handle, mm.at(n + 1))
                if kind == "K":
                    last = nc.vector.tensor_scalar(KT[:, at, :], bank[:, 0:BJ], 64 ** -0.5, None, ALU.mult)
                elif kind == "V":
                    last = nc.vector.tensor_copy(VT[:, at, :], bank[:, 0:BJ])
                elif kind == "Q":
                    last = nc.vector.tensor_copy(WqT[:, at:at + 2, :], bank[:, :].rearrange("p (m d) -> p m d", m=2))
                elif kind == "M":
                    k, g = at
                    last = nc.vector.tensor_copy(
                        M[:, k, :, :].rearrange("p b (h j) -> p h b j", j=J)[:, g[0]:g[-1] + 1:2, :, :],
                        bank[:, 0:len(g) * BJ].rearrange("p (h b j) -> p h b j", h=len(g), b=B))
                else:
                    b, g = at
                    if b == 1 and g[0] == 0:
                        dve.wait_ge(stored.handle, stored.at(16))
                    last = nc.vector.tensor_copy(rows[:, g[0]:g[-1] + 1:2, :],
                                                 bank[0:J, :].rearrange("p (h d) -> p h d", h=2))
                last.then_inc(ev.handle, 1)
    stats.done()
    loaded.base += 64
    filled.base += 1
    mm.base += len(steps)
    ev.base += len(steps)
    stored.base += 96


def attention(c, M, score_bias, N, bo, oT, beside=None):
    nc = c.nc
    names = "norm xT_mm xT_ev scores shifted exped probs x_bo PT_mm PT_ev out_mm out_ev".split()
    s = {n: c.sig("att_" + n) for n in names}
    step = c.sig("att_step")
    loaded, bo_loaded = c.sig("att_padded"), c.sig("att_bo_loaded")
    with ExitStack() as st:
        xn = c.sb(st, "att_xn", [P, 2, D])
        xT = c.sb(st, "att_xT", [P, 2, KD, P])
        pr = c.sb(st, "att_probs", [P, 2, HJC * P])
        PT = c.sb(st, "att_PT", [P, 2, HJC, P])
        mx = c.sb(st, "att_mx", [P, 2, HEADS])
        rs = c.sb(st, "att_rs", [P, 2, HEADS])
        bo_row = c.sb(st, "att_bo", [P, D])
        ps_xT = c.ps(st, "att_ps_xT", [P, 512])
        ps_S = c.ps(st, "att_ps_S", [P, 3 * 512])
        ps_PT = c.ps(st, "att_ps_PT", [P, 3 * 512])
        ps_O = c.ps(st, "att_ps_O", [P, 512])
        pad = HJC * P - HJ
        block = st.enter_context(nc.Block())

        def heads(ap):
            return ap.rearrange("p (h j) -> p h j", j=J)

        if bo is not None:
            @block.sync
            def _(sp):
                sp.dma_start(bo_row[:, :], row(bo, P)).then_inc(bo_loaded.handle, 16)
                if beside:
                    beside(sp)

        @block.tensor
        def _(pe):
            def turn(n, j):
                pe.wait_ge(s["norm"].handle, s["norm"].at(n + 1))
                for k in range(KD):
                    last = nc.tensor.transpose(ps_xT[:, k * P:(k + 1) * P], xn[:, j, k * P:(k + 1) * P], c.ident[:, :])
                last.then_inc(s["xT_mm"].handle, 1)

            def score(n, j, b):
                pe.wait_ge(s["xT_ev"].handle, s["xT_ev"].at(n + 1))
                pe.wait_ge(s["shifted"].handle, s["shifted"].at(n + 1))
                for lo, hi in SCORE_CUTS:
                    for k in range(KD):
                        last = nc.tensor.matmul(ps_S[:, lo:hi], xT[:, j, k, :], M[:, k, b, lo:hi], start=(k == 0),
                                                stop=(k == KD - 1 and score_bias is None))
                    if score_bias is not None:
                        last = nc.tensor.matmul(ps_S[:, lo:hi], c.ones[0:1, :], score_bias[0:1, b, lo:hi],
                                                start=False, stop=True)
                last.then_inc(s["scores"].handle, 1)

            def turn_probs(n, j):
                pe.wait_ge(s["probs"].handle, s["probs"].at(n + 1))
                for k in range(HJC):
                    last = nc.tensor.transpose(ps_PT[:, k * P:(k + 1) * P], pr[:, j, k * P:(k + 1) * P], c.ident[:, :])
                    if k in (PT_CUT - 1, HJC - 1):
                        last.then_inc(s["PT_mm"].handle, 1)

            def values(n, j, b):
                pe.wait_ge(s["out_ev"].handle, s["out_ev"].at(n + 1))
                pe.wait_ge(s["PT_ev"].handle, s["PT_ev"].at(n * 2 + 1))
                if oT is None:
                    for k in range(HJC):
                        if k == PT_CUT:
                            pe.wait_ge(s["PT_ev"].handle, s["PT_ev"].at(n * 2 + 2))
                        last = nc.tensor.matmul(ps_O[:, 0:D], PT[:, j, k, :], N[:, b, k, :],
                                                start=(k == 0), stop=(k == HJC - 1))
                else:
                    for half in range(KD):
                        ks = range(half * HJ // 2 // P, ((half + 1) * HJ // 2 + P - 1) // P)
                        for k in ks:
                            if half == 0 and k == PT_CUT:
                                pe.wait_ge(s["PT_ev"].handle, s["PT_ev"].at(n * 2 + 2))
                            last = nc.tensor.matmul(ps_O[:, half * P:(half + 1) * P],
                                                    N[:, b, k, half * P:(half + 1) * P], PT[:, j, k, :],
                                                    start=(k == ks[0]), stop=(k == ks[-1]))
                last.then_inc(s["out_mm"].handle, 1)

            pe.wait_ge(loaded.handle, loaded.at(1))
            turn(0, 0)
            score(0, 0, 0)
            turn(1, 1)
            for b in range(B):
                with pe.Fori(0, TPB // 2 - 1) as i:
                    for j in range(2):
                        n = i * 2 + (b * TPB + j)
                        score(i * 2 + (b * TPB + j + 1), 1 - j, b)
                        turn_probs(n, j)
                        turn(i * 2 + (b * TPB + j + 2), j)
                        values(n, j, b)
                for n in (b * TPB + TPB - 2, b * TPB + TPB - 1):
                    if n + 1 < NT:
                        score(n + 1, 1 - n % 2, (n + 1) // TPB)
                    turn_probs(n, n % 2)
                    if n + 2 < NT:
                        turn(n + 2, n % 2)
                    values(n, n % 2, b)

        @block.vector
        def _(dve):
            link = Chain(dve, step)

            def norm(n, j):
                nc.vector.tensor_scalar(xn[:, j, :], c.x[:, n, :], c.rstd[:, bass.ts(n, 1)], c.nmr[:, bass.ts(n, 1)],
                                        ALU.mult, ALU.add).then_inc(s["norm"].handle, 1)

            def softmax(n, j, ahead):
                dve.wait_ge(s["scores"].handle, s["scores"].at(n + 1))
                link(nc.vector.tensor_reduce(mx[:, j, :], heads(ps_S[:, 0:HJ]), AX.X, ALU.max))
                nc.vector.tensor_tensor(heads(pr[:, j, 0:HJ]), heads(ps_S[:, 0:HJ]),
                                        bc(mx[:, j, :].unsqueeze(2), [P, HEADS, J]), ALU.subtract)\
                    .then_inc(s["shifted"].handle, 1)
                if ahead:
                    norm(n + 2, j)
                dve.wait_ge(s["exped"].handle, s["exped"].at(n + 1))
                link(nc.vector.tensor_reduce(rs[:, j, :], heads(pr[:, j, 0:HJ]), AX.X, ALU.add))
                link(nc.vector.reciprocal(rs[:, j, :], rs[:, j, :]))
                nc.vector.tensor_tensor(heads(pr[:, j, 0:HJ]), heads(pr[:, j, 0:HJ]),
                                        bc(rs[:, j, :].unsqueeze(2), [P, HEADS, J]), ALU.mult)\
                    .then_inc(s["probs"].handle, 1)

            def take(n):
                dve.wait_ge(s["out_mm"].handle, s["out_mm"].at(n + 1))
                if oT is None:
                    dve.wait_ge(s["x_bo"].handle, s["x_bo"].at(n + 1))
                    nc.vector.tensor_tensor(c.x[:, n, :], c.x[:, n, :], ps_O[:, 0:D], ALU.add)\
                        .then_inc(s["out_ev"].handle, 1)
                else:
                    nc.vector.tensor_copy(oT[:, :, bass.ts(n, P)], ps_O[:, 0:D].rearrange("p (k n) -> p k n", k=KD))\
                        .then_inc(s["out_ev"].handle, 1)

            dve.sem_inc(s["shifted"].handle, 1)
            dve.sem_inc(s["out_ev"].handle, 1)
            norm(0, 0)
            norm(1, 1)
            softmax(0, 0, True)
            last_rolled = NT - 4
            with dve.Fori(0, last_rolled // 2) as i:
                link.count = i * 6 + 3
                for j in (1, 0):
                    n = i * 2 + (2 - j)
                    softmax(n, j, True)
                    take(n - 1)
            link.count = 3 + 3 * last_rolled
            for n in range(last_rolled + 1, NT):
                softmax(n, n % 2, n + 2 < NT)
                take(n - 1)
            take(NT - 1)
            dve.wait_ge(s["out_ev"].handle, s["out_ev"].at(NT + 1))

        if bo is not None:
            @block.gpsimd
            def _(pool):
                nc.gpsimd.memset(pr[:, :, HJ:], 0.0).then_inc(loaded.handle, 1)
                pool.wait_ge(bo_loaded.handle, bo_loaded.at(16))
                with pool.Fori(0, NT) as n:
                    pool.wait_ge(s["norm"].handle, s["norm"].at(n + 1))
                    nc.gpsimd.tensor_tensor(c.x[:, n, :], c.x[:, n, :], bo_row[:, :], ALU.add)\
                        .then_inc(s["x_bo"].handle, 1)
        else:
            @block.gpsimd
            def _(pool):
                nc.gpsimd.memset(pr[:, :, HJ:], 0.0).then_inc(loaded.handle, 1)

        @block.scalar
        def _(act):
            def copy_xT(n, j):
                act.wait_ge(s["xT_mm"].handle, s["xT_mm"].at(n + 1))
                nc.scalar.copy(xT[:, j, :, :], ps_xT[:, 0:D].rearrange("p (k n) -> p k n", k=KD))\
                    .then_inc(s["xT_ev"].handle, 1)

            def exponentials(n, j):
                act.wait_ge(s["shifted"].handle, s["shifted"].at(n + 2))
                nc.scalar.activation(pr[:, j, 0:HJ], pr[:, j, 0:HJ], ACT.Exp).then_inc(s["exped"].handle, 1)

            def copy_PT(n, j):
                for part, (lo, hi) in enumerate(((0, PT_CUT), (PT_CUT, HJC))):
                    act.wait_ge(s["PT_mm"].handle, s["PT_mm"].at(n * 2 + (part + 1)))
                    nc.scalar.copy(PT[:, j, lo:hi, :], ps_PT[:, lo * P:hi * P].rearrange("p (k n) -> p k n", n=P))\
                        .then_inc(s["PT_ev"].handle, 1)

            copy_xT(0, 0)
            copy_xT(1, 1)
            exponentials(0, 0)
            with act.Fori(0, NT // 2 - 1) as i:
                for j in range(2):
                    copy_PT(i * 2 + j, j)
                    copy_xT(i * 2 + (j + 2), j)
                    exponentials(i * 2 + (j + 1), 1 - j)
            copy_PT(NT - 2, 0)
            exponentials(NT - 1, 1)
            copy_PT(NT - 1, 1)
    for name, one in s.items():
        one.base += NT
    s["PT_mm"].base += NT
    s["PT_ev"].base += NT
    if bo is None:
        s["x_bo"].base -= NT
    s["shifted"].base += 1
    s["out_ev"].base += 1
    step.base += 3 * NT
    loaded.base += 1
    bo_loaded.base += 16 if bo is not None else 0


def ring(eng, signal, n):
    eng.sem_inc(signal.handle, n)


G = 4


def normalise(c, src, xn_out=None, xT_out=None, affine=None, router=None, resident=None, stats=None,
              added_to=None):
    nc = c.nc
    names = "loaded rows T_mm T_ev L_mm L_ev step".split()
    s = {n: c.sig("norm_" + n) for n in names}
    with ExitStack() as st:
        xb = c.sb(st, "norm_xb", [P, G, D])
        xTb = c.sb(st, "norm_xTb", [P, G, KD, P])
        gb = c.sb(st, "norm_gb", [P, 2, D])
        ps_T = c.ps(st, "norm_ps_T", [P, G, 512])
        ps_L = c.ps(st, "norm_ps_L", [P, G, 512])
        n_loads = 0
        if router is not None:
            w, n_r, logits = router
            wr = c.sb(st, "norm_wr", [P, KD, n_r]) if resident is None else None
        block = st.enter_context(nc.Block())
        transposing = xT_out is not None or router is not None
        outputs = (1 if xn_out is not None else 0) + (1 if transposing else 0)
        per_turn = outputs * (G if affine is None else 1)
        if affine is not None:
            n_loads += 2
        if router is not None and resident is None:
            n_loads += KD

        @block.sync
        def _(sp):
            if affine is not None:
                for i in range(2):
                    sp.dma_start(gb[:, i, :], row(affine[i], P)).then_inc(s["loaded"].handle, 16)
            if router is not None and resident is None:
                for k in range(KD):
                    sp.dma_start(wr[:, k, :], w[k * P:(k + 1) * P, :], allow_slow_non_contiguous=True)\
                        .then_inc(s["loaded"].handle, 16)
            if n_loads:
                sp.wait_ge(s["loaded"].handle, s["loaded"].at(16 * n_loads))

        @block.vector
        def _(dve):
            v = nc.vector

            def scale(out, n):
                return v.tensor_scalar(out, src[:, n, :], c.rstd[:, bass.ts(n, 1)], c.nmr[:, bass.ts(n, 1)],
                                       ALU.mult, ALU.add)

            def turn(i, b):
                first = i * G + b * TPB
                if affine is None:
                    for j in range(G):
                        n = i * G + (b * TPB + j)
                        if xn_out is not None:
                            scale(xn_out[:, n, :], n).then_inc(s["rows"].handle, 1)
                        if transposing:
                            dve.wait_ge(s["T_mm"].handle, s["T_mm"].at(n + 1))
                            scale(xb[:, j, :], n).then_inc(s["rows"].handle, 1)
                    if stats is not None:
                        dve.wait_ge(s["rows"].handle, s["rows"].at((i + (b * (TPB // G) + 1)) * per_turn))
                        for j in range(G):
                            stats.tile(i * G + (b * TPB + j))
                    return
                if transposing:
                    dve.wait_ge(s["T_mm"].handle, s["T_mm"].at(first + G))
                for j in range(G):
                    last = scale(xb[:, j, :], i * G + (b * TPB + j))
                link = Chain(dve, s["step"], (i + b * (TPB // G)) * (2 if added_to is None else 3))
                link(last)
                link(v.tensor_tensor(xb[:, :, :], xb[:, :, :], bc(gb[:, 0:1, :], [P, G, D]), ALU.mult))
                out = xb[:, :, :]
                if xn_out is not None:
                    out = xn_out(first, b, i * G) if callable(xn_out) else xn_out[:, bass.ds(first, G), :]
                v.tensor_tensor(out, xb[:, :, :], bc(gb[:, 1:2, :], [P, G, D]), ALU.add).then_inc(s["rows"].handle, 1)
                if not transposing:
                    dve.wait_ge(s["rows"].handle, s["rows"].at(i + (b * (TPB // G) + 1)))
                if added_to is not None:
                    total = added_to[:, bass.ds(first, G), :]
                    link(v.tensor_tensor(total, total, out, ALU.add))
                    for j in range(G):
                        stats.tile(i * G + (b * TPB + j))

            if affine is not None:
                assert outputs == 1
                dve.wait_ge(s["loaded"].handle, s["loaded"].at(16 * n_loads))
            for b in range(B):
                with dve.Fori(0, TPB // G) as i:
                    turn(i, b)

        if transposing:
            @block.tensor
            def _(pe):
                ring(pe, s["T_mm"], G)
                ring(pe, s["L_mm"], G)
                if router is not None and n_loads:
                    pe.wait_ge(s["loaded"].handle, s["loaded"].at(16 * n_loads))

                def route(n, j, b):
                    pe.wait_ge(s["T_ev"].handle, s["T_ev"].at(n + (G + 1)))
                    pe.wait_ge(s["L_ev"].handle, s["L_ev"].at(n + 1))
                    for k in range(KD):
                        right = wr[:, k, :] if resident is None else resident[0][:, k, b, :]
                        last = nc.tensor.matmul(ps_L[:, j, 0:n_r], xTb[:, j, k, :], right,
                                                start=(k == 0), stop=(k == KD - 1 and resident is None))
                    if resident is not None:
                        last = nc.tensor.matmul(ps_L[:, j, 0:n_r], c.ones[0:1, :], resident[1][0:1, b, :],
                                                start=False, stop=True)
                    last.then_inc(s["L_mm"].handle, 1)

                def turn(i, b):
                    for j in range(G):
                        n = i * G + (b * TPB + j)
                        rows = (i + (b * (TPB // G))) * per_turn + (outputs * (j + 1) if affine is None else 1)
                        pe.wait_ge(s["rows"].handle, s["rows"].at(rows))
                        pe.wait_ge(s["T_ev"].handle, s["T_ev"].at(n + 1))
                        for k in range(KD):
                            last = nc.tensor.transpose(ps_T[:, j, k * P:(k + 1) * P], xb[:, j, k * P:(k + 1) * P],
                                                       c.ident[:, :])
                        last.then_inc(s["T_mm"].handle, 1)
                    if router is not None:
                        for j in range(G):
                            route(i * G + (b * TPB + j), j, b)

                for b in range(B):
                    with pe.Fori(0, TPB // G) as i:
                        turn(i, b)

            @block.scalar
            def _(act):
                ring(act, s["T_ev"], G)
                ring(act, s["L_ev"], G)
                with act.Fori(0, NT // G) as i:
                    for j in range(G):
                        n = i * G + j
                        act.wait_ge(s["T_mm"].handle, s["T_mm"].at(n + (G + 1)))
                        tile = ps_T[:, j, 0:D].rearrange("p (k n) -> p k n", k=KD)
                        if xT_out is not None:
                            one = nc.scalar.copy(xT_out[:, :, bass.ts(n, P)], tile)
                        if router is not None:
                            act.wait_ge(s["L_mm"].handle, s["L_mm"].at(n + 1))
                            one = nc.scalar.copy(xTb[:, j, :, :], tile)
                        one.then_inc(s["T_ev"].handle, 1)
                    if router is not None:
                        for j in range(G):
                            n = i * G + j
                            act.wait_ge(s["L_mm"].handle, s["L_mm"].at(n + (G + 1)))
                            nc.scalar.copy(logits[:, n, :], ps_L[:, j, 0:n_r]).then_inc(s["L_ev"].handle, 1)
    s["loaded"].base += 16 * n_loads
    s["rows"].base += per_turn * (NT // G)
    if transposing:
        for n in ("T_mm", "T_ev"):
            s[n].base += NT + G
        for n in ("L_mm", "L_ev"):
            s[n].base += G + (NT if router is not None else 0)
    if affine is not None:
        s["step"].base += (2 if added_to is None else 3) * (NT // G)


def each_expert(eng, n_exp, body):
    if n_exp <= 2:
        for e in range(n_exp):
            body(e, e, 1)
        return
    with eng.Fori(0, n_exp // 2) as i:
        for s in range(2):
            body(i * 2 + s, s, i + 1)


def experts(c, xT, n_exp, F, w1, w3, w2, b1, func, gate, acc, resident=None, meanwhile=None, plus=None):
    nc = c.nc
    FT = F // P
    swiglu = w3 is not None
    names = "exp_H_mm exp_sil exp_H_ev exp_O_mm exp_O_ev exp_slot0 exp_slot1".split()
    H_mm, sil_done, H_ev, O_mm, O_ev, *slot = [c.sig(n) for n in names]
    plus_in, plus_added = c.sig("exp_plus_in"), c.sig("exp_plus_added")
    n_w = 0 if resident else 2 + (w3 is not None) + (b1 is not None)
    n_ch = NCH
    per_expert = n_ch * TPC
    n_slots = min(n_exp, 2)
    with ExitStack() as st:
        if resident:
            W1, W2, b1c = resident
        else:
            W1 = c.sb(st, "exp_W1", [P, n_slots, KD, F])
            W2 = c.sb(st, "exp_W2", [P, n_slots, FT, D])
            b1c = c.sb(st, "exp_b1c", [P, n_slots, FT]) if b1 is not None else None
        W3 = c.sb(st, "exp_W3", [P, n_slots, KD, F]) if swiglu else None
        hT = c.sb(st, "exp_hT", [P, 2, FT, CH])
        sil = c.sb(st, "exp_sil", [P, 2, CH]) if swiglu else None
        ps_H = c.ps(st, "exp_ps_H", [P, 2, 2 if swiglu else 1, CH])
        ps_O = c.ps(st, "exp_ps_O", [P, 2, 512])

        def entry(s, i):
            return i * B // NCH if resident else s

        plus_row = c.sb(st, "exp_plus", [P, D]) if plus is not None else None
        block = st.enter_context(nc.Block())

        if plus is not None:
            @block.gpsimd
            def _(pool):
                pool.wait_ge(plus_in.handle, plus_in.at(16))
                for i in range(NCH):
                    tiles = acc[:, i * TPC:(i + 1) * TPC, :]
                    nc.gpsimd.tensor_tensor(tiles, tiles, bc(plus_row[:, :].unsqueeze(1), [P, TPC, D]), ALU.add)\
                        .then_inc(plus_added.handle, 1)

        if not resident:
            @block.sync
            def _(sp):
                if plus is not None:
                    sp.dma_start(plus_row[:, :], row(plus, P)).then_inc(plus_in.handle, 16)

                def load(e, s, use):
                    if n_exp > 1:
                        sp.wait_ge(O_mm.handle, O_mm.at((e + 1) * per_expert))
                    sp.dma_start(W1[:, s, :, :], w1[e, :, :].rearrange("(k p) f -> p k f", p=P)).then_inc(slot[s].handle, 16)
                    if swiglu:
                        sp.dma_start(W3[:, s, :, :], w3[e, :, :].rearrange("(k p) f -> p k f", p=P))\
                            .then_inc(slot[s].handle, 16)
                    sp.dma_start(W2[:, s, :, :], w2[e, :, :].rearrange("(k p) f -> p k f", p=P)).then_inc(slot[s].handle, 16)
                    if b1 is not None:
                        sp.dma_start(b1c[:, s, :], b1[e, :].rearrange("(f p) -> p f", p=P),
                                     allow_slow_non_contiguous=True).then_inc(slot[s].handle, 16)

                each_expert(sp, n_exp, load)
                for s in range(n_slots):
                    sp.wait_ge(slot[s].handle, slot[s].at(16 * n_w * n_exp // n_slots))

        @block.tensor
        def _(pe):
            ring(pe, O_mm, 2 * per_expert)

            def up(e, s, i):
                g = e * n_ch + i
                at = i * CH
                s = entry(s, i)
                for f in range(FT):
                    pe.wait_ge(H_ev.handle, H_ev.at(g * FT + (f + 1)))
                    for m, W in enumerate([W1, W3] if swiglu else [W1]):
                        for k in range(KD):
                            last = nc.tensor.matmul(ps_H[:, f % 2, m, :], W[:, s, k, f * P:(f + 1) * P],
                                                    xT[:, k, at:at + CH], start=(k == 0), stop=(k == KD - 1))
                    last.then_inc(H_mm.handle, 1)

            def down(e, s, i):
                g = e * n_ch + i
                s = entry(s, i)
                pe.wait_ge(H_ev.handle, H_ev.at((g + 1) * FT + 2))
                for j in range(TPC):
                    pe.wait_ge(O_ev.handle, O_ev.at(g * TPC + (j + 1)))
                    for f in range(FT):
                        last = nc.tensor.matmul(ps_O[:, j % 2, 0:D], hT[:, i % 2, f, j * P:(j + 1) * P], W2[:, s, f, :],
                                                start=(f == 0), stop=(f == FT - 1))
                    last.then_inc(O_mm.handle, 1)

            def one(e, s, use):
                if n_w:
                    pe.wait_ge(slot[s].handle, slot[s].at(use * (16 * n_w)))
                up(e, s, 0)
                for i in range(1, n_ch):
                    up(e, s, i)
                    down(e, s, i - 1)
                down(e, s, n_ch - 1)

            each_expert(pe, n_exp, one)

        @block.scalar
        def _(act):
            if not swiglu:
                ring(act, H_ev, 2)

            def one(e, s, use):
                if b1 is not None and n_w:
                    act.wait_ge(slot[s].handle, slot[s].at(use * (16 * n_w)))
                for i in range(n_ch):
                    for f in range(FT):
                        act.wait_ge(H_mm.handle, H_mm.at((e * n_ch + i) * FT + (f + 1)))
                        if swiglu:
                            nc.scalar.activation(sil[:, f % 2, :], ps_H[:, f % 2, 0, :], func).then_inc(sil_done.handle, 1)
                        else:
                            nc.scalar.activation(hT[:, i % 2, f, :], ps_H[:, f % 2, 0, :], func,
                                                 bias=b1c[:, entry(s, i), f:f + 1]).then_inc(H_ev.handle, 1)

            each_expert(act, n_exp, one)

        @block.vector
        def _(dve):
            if swiglu:
                ring(dve, H_ev, 2)
            ring(dve, O_ev, 2)

            def product(e, i):
                for f in range(FT):
                    dve.wait_ge(sil_done.handle, sil_done.at((e * n_ch + i) * FT + (f + 1)))
                    nc.vector.tensor_tensor(hT[:, i % 2, f, :], sil[:, f % 2, :], ps_H[:, f % 2, 1, :], ALU.mult)\
                        .then_inc(H_ev.handle, 1)
                    if meanwhile:
                        meanwhile(dve, (e * n_ch + i) * FT + f, True)

            def take(e, i):
                if plus is not None:
                    dve.wait_ge(plus_added.handle, plus_added.at(i + 1))
                for j in range(TPC):
                    t = i * TPC + j
                    dve.wait_ge(O_mm.handle, O_mm.at((e * n_ch + i) * TPC + (2 * per_expert + j + 1)))
                    nc.vector.scalar_tensor_tensor(acc[:, t, :], ps_O[:, j % 2, 0:D], gate(t, e), acc[:, t, :],
                                                   ALU.mult, ALU.add).then_inc(O_ev.handle, 1)
                    if meanwhile:
                        meanwhile(dve, (e * n_ch + i) * TPC + j, False)

            def one(e, s, use):
                if swiglu:
                    product(e, 0)
                for i in range(n_ch):
                    if swiglu and i + 1 < n_ch:
                        product(e, i + 1)
                    take(e, i)

            each_expert(dve, n_exp, one)
            dve.wait_ge(O_ev.handle, O_ev.at(n_exp * n_ch * TPC + 2))
    for one, n in ((H_mm, FT), (H_ev, FT), (O_mm, TPC), (O_ev, TPC)):
        one.base += n * n_exp * n_ch
    sil_done.base += FT * n_exp * n_ch if swiglu else 0
    if plus is not None:
        plus_in.base += 16
        plus_added.base += n_ch
    H_ev.base += 2
    O_ev.base += 2
    O_mm.base += 2 * per_expert
    for one in slot[:n_slots]:
        one.base += 16 * n_w * n_exp // n_slots


class Router:

    def __init__(self, c, st, n_exp, dve_signal):
        self.c, self.nc, self.E = c, c.nc, n_exp
        self.iota = c.sb(st, "rt_iota", [P, NT, n_exp])
        self.cand = c.sb(st, "rt_cand", [P, NT, n_exp])

    def wide(self, small):
        return bc(small.unsqueeze(2), [P, NT, self.E])

    def first_max(self, link, scores, value, onehot, index):
        v = self.nc.vector
        link(v.tensor_reduce(value, scores, AX.X, ALU.max))
        link(v.tensor_tensor(self.cand[:, :, :], scores, self.wide(value), ALU.is_equal))
        link(v.scalar_tensor_tensor(self.cand[:, :, :], self.cand[:, :, :], -64.0, self.iota[:, :, :], ALU.mult, ALU.add))
        link(v.tensor_reduce(index, self.cand[:, :, :], AX.X, ALU.min))
        link(v.tensor_tensor(onehot, self.cand[:, :, :], self.wide(index), ALU.is_equal))

    def softmax_divide(self, link, scores, value):
        v = self.nc.vector
        link(v.tensor_reduce(value, scores, AX.X, ALU.add))
        link(v.reciprocal(value, value))
        link(v.tensor_tensor(scores, scores, self.wide(value), ALU.mult))


def slots_of(E, mode):
    if mode == "top1":
        return B * SEQ // E, E
    if mode == "capacity":
        return -(-(B * SEQ * 2 * 5) // (E * 4)), E
    unit = 2 * P
    return unit, E + (2 * B * SEQ - E) // unit


ROOM = 29 * 256
NO_ROW = float(1 << 20)


def route(c, logits, E, mode, bias, extra, plan, meanwhile=None):
    nc = c.nc
    to, back_from, gate, unit_expert = plan
    unit, n_units = slots_of(E, mode)
    n_k = 1 if mode == "top1" else 2
    FAR, TAKEN = -1.0e30, -3.0e38
    loaded, iota, ready, exped, step = [c.sig("rt_" + n) for n in ("loaded", "iota", "ready", "exped", "step")]
    mm, asked = c.sig("rt_mm"), c.sig("rt_asked")
    steps, taken_out = [], [0]
    with ExitStack() as st:
        r = Router(c, st, E, step)
        probs = c.sb(st, "rt_probs", [P, NT, E])
        oh = c.sb(st, "rt_oh", [P, 2, NT, E])
        mask = c.sb(st, "rt_mask", [P, NT, E])
        pos = c.sb(st, "rt_pos", [P, NT, E])
        v = c.sb(st, "rt_v", [P, 2, NT])
        idx = c.sb(st, "rt_idx", [P, NT])
        some = c.sb(st, "rt_some", [P, NT])
        base = c.sb(st, "rt_base", [P, E])
        small = c.sb(st, "rt_small", [P, 2, E])
        before = c.sb(st, "rt_before", [P, E, E])
        units = c.sb(st, "rt_units", [P, 2, n_units])
        cmp = c.sb(st, "rt_cmp", [P, n_units, E])
        bias_row = c.sb(st, "rt_bias", [P, E])
        tri = c.sb(st, "rt_tri", [P, 2, P])
        eight = c.sb(st, "rt_eight", [E, 8])
        wT = c.sb(st, "rt_wT", [E, B * SEQ]) if mode == "capacity" else None
        choosing = ExitStack()
        ps_w = c.ps(choosing, "rt_ps_w", [P, 4, 512]) if mode == "capacity" else None
        block = choosing.enter_context(nc.Block())

        @block.sync
        def _(sp):
            if bias is not None:
                sp.dma_start(bias_row[:, :], row(bias, P)).then_inc(loaded.handle, 16)

        @block.gpsimd
        def _(pool):
            g = nc.gpsimd
            g.iota(r.iota[:, :, :], pattern=[[0, NT], [1, E]], base=0, channel_multiplier=0,
                   allow_small_or_imprecise_dtypes=True).then_inc(iota.handle, 1)
            pool.wait_ge(iota.handle, iota.at(1))
            g.memset(tri[:, :, :], 1.0).then_inc(iota.handle, 1)
            pool.wait_ge(iota.handle, iota.at(2))
            g.affine_select(out=tri[:, 0, :], in_=tri[:, 0, :], compare_op=ALU.is_ge, fill=0.0,
                            base=0, pattern=[[1, P]], channel_multiplier=-1).then_inc(iota.handle, 1)
            g.memset(before[:, :, :], 1.0).then_inc(iota.handle, 1)
            pool.wait_ge(iota.handle, iota.at(4))
            g.affine_select(out=before[:, :, :], in_=before[:, :, :], compare_op=ALU.is_gt, fill=0.0,
                            base=0, pattern=[[1, E], [-1, E]], channel_multiplier=0).then_inc(iota.handle, 1)
            g.iota(units[:, 0, :], pattern=[[1, n_units]], base=0, channel_multiplier=0,
                   allow_small_or_imprecise_dtypes=True).then_inc(iota.handle, 1)

        @block.scalar
        def _(act):
            act.wait_ge(ready.handle, ready.at(1))
            nc.scalar.activation(probs[:, :, :], probs[:, :, :], ACT.Exp).then_inc(exped.handle, 1)

        if mode == "capacity":
            @block.tensor
            def _(pe):
                pe.wait_ge(asked.handle, asked.at(1))
                for t in range(NT):
                    last = nc.tensor.transpose(ps_w[0:E, t // 4, (t % 4) * P:(t % 4 + 1) * P], probs[:, t, :], c.ident[:, :])
                last.then_inc(mm.handle, 1)

        @block.vector
        def _(dve):
            link = Chain(dve, step)
            V = nc.vector
            bias_wide = bc(bias_row[:, :].unsqueeze(1), [P, NT, E])
            tt, ts, stt = V.tensor_tensor, V.tensor_scalar, V.scalar_tensor_tensor
            if bias is not None:
                dve.wait_ge(loaded.handle, loaded.at(16))
            if mode == "top1":
                link(tt(logits[:, :, :], logits[:, :, :], bias_wide, ALU.add))
            link(V.tensor_reduce(v[:, 0, :], logits[:, :, :], AX.X, ALU.max))
            tt(probs[:, :, :], logits[:, :, :], r.wide(v[:, 0, :]), ALU.subtract).then_inc(ready.handle, 1)
            dve.wait_ge(exped.handle, exped.at(1))
            r.softmax_divide(link, probs[:, :, :], v[:, 0, :])
            if mode == "capacity":
                link(tt(probs[:, :, :], probs[:, :, :], bias_wide, ALU.add))
            dve.wait_ge(iota.handle, iota.at(6))
            r.first_max(link, probs[:, :, :], v[:, 0, :], oh[:, 0, :, :], idx[:, :])
            if mode == "top1":
                link(V.tensor_copy(mask[:, :, :], oh[:, 0, :, :]))
                link(V.tensor_copy(extra, v[:, 0, :]))
                link(V.tensor_copy(gate[:, 0, :], v[:, 0, :]))
            else:
                link(stt(probs[:, :, :], oh[:, 0, :, :], FAR, probs[:, :, :], ALU.mult, ALU.add))
                r.first_max(link, probs[:, :, :], v[:, 1, :], oh[:, 1, :, :], idx[:, :])
                link(tt(mask[:, :, :], oh[:, 0, :, :], oh[:, 1, :, :], ALU.add))
            if mode == "top2":
                link(tt(some[:, :], v[:, 0, :], v[:, 1, :], ALU.add))
                link(ts(some[:, :], some[:, :], 1e-10, None, ALU.max))
                link(V.reciprocal(some[:, :], some[:, :]))
                for k in range(2):
                    link(tt(gate[:, k, :], v[:, k, :], some[:, :], ALU.mult))
            if mode == "capacity":
                link(tt(probs[:, :, :], logits[:, :, :], mask[:, :, :], ALU.mult))
                link(ts(pos[:, :, :], mask[:, :, :], 1.0, -FAR, ALU.subtract, ALU.mult))
                tt(probs[:, :, :], probs[:, :, :], pos[:, :, :], ALU.add).then_inc(asked.handle, 1)
                dve.wait_ge(mm.handle, mm.at(1))
                link(V.tensor_copy(wT[:, :], ps_w[0:E, :, :].rearrange("e a n -> e (a n)")))
            steps.append(link.count)

        choosing.close()
        if mode == "capacity":
            halves = 2 * (unit // 8)

            def take_out(dve, n, hidden):
                link = Chain(dve, step, steps[0] + taken_out[0])
                share = (1 + n % 2) if hidden else 1
                for _ in range(min(share, halves - taken_out[0])):
                    if taken_out[0] % 2 == 0:
                        link(nc.vector.max(eight[:, :], wT[:, :]))
                    else:
                        link(nc.vector.match_replace(wT[:, :], eight[:, :], wT[:, :], TAKEN))
                    taken_out[0] += 1

            meanwhile(take_out)
            assert taken_out[0] == halves, taken_out
            steps[0] += halves
        ps = c.ps(st, "rt_ps", [P, 512])
        ps_g = c.ps(st, "rt_ps_g", [P, 512])
        ps_n = c.ps(st, "rt_ps_n", [P, 512])
        block = st.enter_context(nc.Block())

        @block.tensor
        def _(pe):
            n_asked = 0
            if mode == "capacity":
                n_asked = 2
                pe.wait_ge(asked.handle, asked.at(2))
                for t in range(NT):
                    last = nc.tensor.transpose(ps_g[:, t * E:(t + 1) * E], wT[:, t * P:(t + 1) * P], c.ident[0:E, 0:E])
                last.then_inc(mm.handle, 1)
            pe.wait_ge(asked.handle, asked.at(n_asked + 1))
            nc.tensor.matmul(ps[:, 0:NT * E], tri[:, 0, :], mask[:, :, :], start=True, stop=False)
            for t in range(1, NT):
                nc.tensor.matmul(ps[:, t * E:NT * E], tri[:, 1, :], mask[:, 0:NT - t, :],
                                 start=False, stop=(t == NT - 1))
            for t in range(NT):
                last = nc.tensor.matmul(ps_n[:, 0:E], tri[:, 1, :], mask[:, t, :], start=(t == 0), stop=(t == NT - 1))
            last.then_inc(mm.handle, 1)

        @block.vector
        def _(dve):
            link = Chain(dve, step, steps[0])
            V = nc.vector
            tt, ts, stt = V.tensor_tensor, V.tensor_scalar, V.scalar_tensor_tensor
            if mode == "capacity":
                ts(wT[:, :], wT[:, :], 2 * FAR, None, ALU.is_lt).then_inc(asked.handle, 1)
                dve.wait_ge(mm.handle, mm.at(2))
                taken = ps_g[:, 0:NT * E].rearrange("p (t e) -> p t e", e=E)
                for k in range(2):
                    link(tt(oh[:, k, :, :], oh[:, k, :, :], taken, ALU.mult))
                    link(tt(pos[:, :, :], oh[:, k, :, :], logits[:, :, :], ALU.mult))
                    link(V.tensor_reduce(gate[:, k, :], pos[:, :, :], AX.X, ALU.add))
                link(tt(mask[:, :, :], oh[:, 0, :, :], oh[:, 1, :, :], ALU.add))
            dve.sem_inc(asked.handle, 1)
            if mode != "top2":
                link(ts(base[:, :], r.iota[:, 0, :], float(unit), None, ALU.mult))
            dve.wait_ge(mm.handle, mm.at(3 if mode == "capacity" else 1))
            link(V.tensor_copy(pos[:, :, :], ps[:, 0:NT * E].rearrange("p (t e) -> p t e", e=E)))
            if mode == "top1":
                link(ts(mask[:, :, :], pos[:, :, :], float(unit), None, ALU.is_lt))
                link(tt(oh[:, 0, :, :], oh[:, 0, :, :], mask[:, :, :], ALU.mult))
            if mode == "top2":
                link(ts(small[:, 0, :], ps_n[:, 0:E], 1.0 / unit, (unit / 2 - 0.5) / unit, ALU.mult, ALU.add))
                link(ts(small[:, 0, :], small[:, 0, :], MAGIC, MAGIC, ALU.add, ALU.subtract))
                link(tt(before[:, :, :], before[:, :, :], bc(small[:, 0, :].unsqueeze(1), [P, E, E]), ALU.mult))
                link(V.tensor_reduce(small[:, 1, :], before[:, :, :], AX.X, ALU.add))
                link(ts(base[:, :], small[:, 1, :], float(unit), None, ALU.mult))
                link(tt(small[:, 0, :], small[:, 0, :], small[:, 1, :], ALU.add))
                link(tt(cmp[:, :, :], bc(units[:, 0, :].unsqueeze(2), [P, n_units, E]),
                        bc(small[:, 0, :].unsqueeze(1), [P, n_units, E]), ALU.is_ge))
                link(V.tensor_reduce(units[:, 1, :], cmp[:, :, :], AX.X, ALU.add))
                link(ts(unit_expert, units[0:1, 1, :], float(E - 1), None, ALU.min))
            link(tt(pos[:, :, :], pos[:, :, :], bc(base[:, :].unsqueeze(1), [P, NT, E]), ALU.add))
            for k in range(n_k):
                link(tt(probs[:, :, :], oh[:, k, :, :], pos[:, :, :], ALU.mult))
                link(V.tensor_reduce(idx[:, :], probs[:, :, :], AX.X, ALU.add))
                link(V.tensor_reduce(some[:, :], oh[:, k, :, :], AX.X, ALU.add))
                link(stt(v[:, 0, :], some[:, :], -1.0 - NO_ROW, idx[:, :], ALU.mult, ALU.add))
                link(ts(to[:, k, :], v[:, 0, :], NO_ROW, None, ALU.add))
                link(V.tensor_copy(back_from[:, k, :], idx[:, :]))
            steps.append(link.count)
    loaded.base += 16 if bias is not None else 0
    iota.base += 6
    ready.base += 1
    exped.base += 1
    step.base += steps[-1]
    mm.base += 3 if mode == "capacity" else 1
    asked.base += 3 if mode == "capacity" else 1


def scatter(c, rows, to, n_k, n_rows, Xg):
    nc = c.nc
    sent = c.sig("scattered")
    sent.base += 16 * n_k * NT

    def program(pool):
        pool.wait_ge(c.sig("zeros_sent").handle, c.zeros_sent)
        for k in range(n_k):
            for t in range(NT):
                nc.gpsimd.indirect_dma_start(
                    out=Xg[0:n_rows, :], out_offset=bass.IndirectOffsetOnAxis(ap=to[:, k, t:t + 1], axis=0),
                    in_=rows[:, t, :], in_offset=None, bounds_check=n_rows - 1, oob_is_err=False)\
                    .then_inc(sent.handle, 16)
        pool.wait_ge(sent.handle, sent.at(0))

    return program, sent.at(0)


def gather(c, back_from, gate, n_k, n_rows, Yg, acc, clipped=None, stored_to=None, beside=None):
    nc = c.nc
    added, step = c.sig("gather_added"), c.sig("gather_step")
    RING = 8
    with ExitStack() as st:
        rows = c.sb(st, "gather_rows", [P, RING, D])
        arrived = [c.sig(f"gather_{i}") for i in range(RING)]
        ps_beside = c.ps(st, "gather_ps_beside", [P, 512]) if beside else None
        block = st.enter_context(nc.Block())
        order = [(t, k) for t in range(NT) for k in range(n_k)]
        uses = len(order) // RING

        @block.gpsimd
        def _(pool):
            for n, (t, k) in enumerate(order):
                if n >= RING:
                    pool.wait_ge(added.handle, added.at(n - RING + 1))
                nc.gpsimd.indirect_dma_start(
                    out=rows[:, n % RING, :], out_offset=None, in_=Yg[0:n_rows + 1, :],
                    in_offset=bass.IndirectOffsetOnAxis(ap=back_from[:, k, t:t + 1], axis=0))\
                    .then_inc(arrived[n % RING].handle, 16)
                if beside:
                    beside.rest_gpsimd(pool, n)

        if beside:
            @block.scalar
            def _(act):
                beside.rest_scalar(act)

            @block.tensor
            def _(pe):
                beside.rest_tensor(pe, ps_beside)

        if stored_to is not None:
            @block.sync
            def _(sp):
                stored = c.sig("stored")
                for t in range(0, NT, 2):
                    sp.wait_ge(added.handle, added.at((t + 2) * n_k))
                    sp.dma_start(stored_to[:, t:t + 2, :], acc[:, t:t + 2, :]).then_inc(stored.handle, 16)
                sp.wait_ge(stored.handle, 16 * (NT // 2))

        @block.vector
        def _(dve):
            v = nc.vector
            link = Chain(dve, step)
            for n, (t, k) in enumerate(order):
                one = arrived[n % RING]
                dve.wait_ge(one.handle, one.at(16 * (n // RING + 1)))
                if k:
                    dve.wait_ge(added.handle, added.at(n))
                v.scalar_tensor_tensor(acc[:, t, :], rows[:, n % RING, :], gate[:, k, t:t + 1], acc[:, t, :],
                                       ALU.mult, ALU.add).then_inc(added.handle, 1)
                if k + 1 == n_k and clipped is not None:
                    dve.wait_ge(added.handle, added.at(n + 1))
                    link(v.tensor_scalar(acc[:, t, :], acc[:, t, :], -100.0, 100.0, ALU.max, ALU.min))
                    link(v.tensor_tensor(clipped[:, t, :], clipped[:, t, :], acc[:, t, :], ALU.add))
                if beside:
                    beside.rest_vector(dve, ps_beside, n)
            dve.wait_ge(added.handle, added.at(len(order)))
    added.base += len(order)
    if clipped is not None:
        step.base += 2 * NT
    for one in arrived:
        one.base += 16 * uses


def slot_experts(c, n_units, unit, F, w1, w3, w2, b1, b2, func, unit_expert, Xg, Yg, beside=None,
                 scatter=None):
    nc = c.nc
    FT = F // P
    swiglu = w3 is not None
    n_w = 2 + swiglu + (0 if b1 is None else 2)
    names = "T_mm T_ev H_mm sil H_ev O_mm O_ev".split()
    s_ = {n: c.sig("se_" + n) for n in names}
    T_mm, T_ev, H_mm, sil_done, H_ev, O_mm, O_ev = [s_[n] for n in names]
    rows_in = [c.sig(f"se_rows{i}") for i in range(2)]
    w_in = [c.sig(f"se_w{i}") for i in range(2)]
    out_sent = [c.sig(f"se_out{i}") for i in range(2)]
    tiles = [(lo, min(P, unit - lo)) for lo in range(0, unit, P)]
    nt = len(tiles)
    full = unit // P
    n_rows = nt - full + 1
    with ExitStack() as st:
        W1 = c.sb(st, "se_W1", [P, 2, KD, F])
        W3 = c.sb(st, "se_W3", [P, 2, KD, F]) if swiglu else None
        W2 = c.sb(st, "se_W2", [P, 2, FT, D])
        b1c = c.sb(st, "se_b1", [P, 2, FT]) if b1 is not None else None
        b2r = c.sb(st, "se_b2", [P, 2, D]) if b1 is not None else None
        X = c.sb(st, "se_X", [P, 2, nt, D])
        XT = c.sb(st, "se_XT", [P, 2, KD, unit])
        hT = c.sb(st, "se_hT", [P, 2, FT, unit])
        sil = c.sb(st, "se_sil", [P, 2, unit]) if swiglu else None
        Y = c.sb(st, "se_Y", [P, 2, nt, D])
        ps_T = c.ps(st, "se_ps_T", [P, KD, 512])
        ps_H = c.ps(st, "se_ps_H", [P, 2, 2 if swiglu else 1, 512])
        ps_O = c.ps(st, "se_ps_O", [P, 2, 512])
        ps_beside = c.ps(st, "se_ps_beside", [P, 512]) if beside else None
        block = st.enter_context(nc.Block())

        def row_views(dram, sbuf, u, s, start=0):
            at = u * unit + start
            yield dram[bass.ds(at, full * P), :].rearrange("(t p) d -> p t d", p=P), sbuf[:, s, 0:full, :]
            if nt > full:
                yield dram[bass.ds(at + full * P, unit - full * P), :], sbuf[0:unit - full * P, s, full, :]

        @block.sync
        def _(sp):
            def load_rows(u, s):
                for dram, sbuf in row_views(Xg, X, u, s):
                    sp.dma_start(sbuf, dram).then_inc(rows_in[s].handle, 16)

            def load_weights(u, s):
                e = u if unit_expert is None else sp.value_load(unit_expert[0:1, bass.ds(u, 1)], min_val=0,
                                                                max_val=w1.shape[0] - 1)
                sp.dma_start(W1[:, s, :, :], w1[e, :, :].rearrange("(k p) f -> p k f", p=P)).then_inc(w_in[s].handle, 16)
                if swiglu:
                    sp.dma_start(W3[:, s, :, :], w3[e, :, :].rearrange("(k p) f -> p k f", p=P)).then_inc(w_in[s].handle, 16)
                sp.dma_start(W2[:, s, :, :], w2[e, :, :].rearrange("(k p) f -> p k f", p=P)).then_inc(w_in[s].handle, 16)
                if b1 is not None:
                    sp.dma_start(b1c[:, s, :], b1[e, :].rearrange("(f p) -> p f", p=P),
                                 allow_slow_non_contiguous=True).then_inc(w_in[s].handle, 16)
                    sp.dma_start(b2r[:, s, :], row(b2[e, :], P)).then_inc(w_in[s].handle, 16)

            def load(u, s):
                sp.wait_ge(T_mm.handle, T_mm.at(u - 1))
                load_rows(u, s)
                sp.wait_ge(O_ev.handle, O_ev.at((u - 1) * nt + 2))
                load_weights(u, s)

            def send(u, s):
                sp.wait_ge(O_ev.handle, O_ev.at((u + 1) * nt + 2))
                for dram, sbuf in row_views(Yg, Y, u, s, 1):
                    sp.dma_start(dram, sbuf).then_inc(out_sent[s].handle, 16)

            for s in range(2):
                ring(sp, out_sent[s], 16 * n_rows)
                load_weights(s, s)
            if scatter:
                sp.wait_ge(c.sig("scattered").handle, scatter[1])
            for s in range(2):
                load_rows(s, s)
            units = n_units - 2
            with sp.Fori(0, units // 2) as i:
                for s in range(2):
                    load(i * 2 + (s + 2), s)
                    send(i * 2 + s, s)
            for u in range(units // 2 * 2, n_units):
                if u < units:
                    load(u + 2, u % 2)
                send(u, u % 2)
            for s in range(2):
                uses = (n_units + 1 - s) // 2
                sp.wait_ge(w_in[s].handle, w_in[s].at(16 * n_w * uses))
                sp.wait_ge(rows_in[s].handle, rows_in[s].at(16 * n_rows * uses))
                sp.wait_ge(out_sent[s].handle, out_sent[s].at(16 * n_rows * (uses + 1)))

        if scatter:
            @block.gpsimd
            def _(pool):
                scatter[0](pool)

        if beside:
            @block.gpsimd
            def _(pool):
                with pool.Fori(0, (n_units - 1) // 2) as i:
                    beside.beside_gpsimd(pool, i)

        @block.tensor
        def _(pe):
            def transpose(u, s, use):
                pe.wait_ge(rows_in[s].handle, rows_in[s].at(use * (16 * n_rows)))
                pe.wait_ge(T_ev.handle, T_ev.at(u + 1))
                for k in range(KD):
                    for n, (lo, size) in enumerate(tiles):
                        last = nc.tensor.transpose(ps_T[:, k, lo:lo + size], X[0:size, s, n, k * P:(k + 1) * P],
                                                   c.ident[0:size, 0:size])
                last.then_inc(T_mm.handle, 1)

            def body(u, s, use, more):
                pe.wait_ge(w_in[s].handle, w_in[s].at(use * (16 * n_w)))
                pe.wait_ge(T_ev.handle, T_ev.at(u + 2))
                for f in range(FT):
                    pe.wait_ge(H_ev.handle, H_ev.at(u * FT + (f + 1)))
                    for m, W in enumerate([W1, W3] if swiglu else [W1]):
                        for k in range(KD):
                            last = nc.tensor.matmul(ps_H[:, f % 2, m, 0:unit], W[:, s, k, f * P:(f + 1) * P],
                                                    XT[:, s, k, :], start=(k == 0), stop=(k == KD - 1))
                    last.then_inc(H_mm.handle, 1)
                if more:
                    transpose(u + 1, 1 - s, use + s)
                pe.wait_ge(H_ev.handle, H_ev.at((u + 1) * FT + 2))
                for n, (lo, size) in enumerate(tiles):
                    pe.wait_ge(O_ev.handle, O_ev.at(u * nt + (n + 1)))
                    for f in range(FT):
                        last = nc.tensor.matmul(ps_O[0:size, (s * nt + n) % 2, 0:D], hT[:, s, f, lo:lo + size],
                                                W2[:, s, f, :], start=(f == 0), stop=(f == FT - 1))
                    last.then_inc(O_mm.handle, 1)

            transpose(0, 0, 1)
            pairs = (n_units - 1) // 2
            with pe.Fori(0, pairs) as i:
                for s in range(2):
                    body(i * 2 + s, s, i + 1, True)
                if beside:
                    beside.multiply(pe, ps_beside, i)
            for u in range(2 * pairs, n_units):
                body(u, u % 2, u // 2 + 1, u + 1 < n_units)

        def copy_T(eng, u, s):
            eng.wait_ge(T_mm.handle, T_mm.at(u + 1))
            nc.scalar.copy(XT[:, s, :, :], ps_T[:, :, 0:unit]).then_inc(T_ev.handle, 1)

        @block.scalar
        def _(act):
            ring(act, T_ev, 1)
            if not swiglu:
                ring(act, H_ev, 2)
            copy_T(act, 0, 0)

            def body(u, s, use, more):
                if b1 is not None:
                    act.wait_ge(w_in[s].handle, w_in[s].at(use * (16 * n_w)))
                for f in range(FT):
                    act.wait_ge(H_mm.handle, H_mm.at(u * FT + (f + 1)))
                    if swiglu:
                        nc.scalar.activation(sil[:, f % 2, :], ps_H[:, f % 2, 0, 0:unit], func).then_inc(sil_done.handle, 1)
                    else:
                        nc.scalar.activation(hT[:, s, f, :], ps_H[:, f % 2, 0, 0:unit], func, bias=b1c[:, s, f:f + 1])\
                            .then_inc(H_ev.handle, 1)
                if more:
                    copy_T(act, u + 1, 1 - s)

            pairs = (n_units - 1) // 2
            with act.Fori(0, pairs) as i:
                for s in range(2):
                    body(i * 2 + s, s, i + 1, True)
                    if beside:
                        beside.beside_scalar(act, i, s)
            for u in range(2 * pairs, n_units):
                body(u, u % 2, u // 2 + 1, u + 1 < n_units)

        @block.vector
        def _(dve):
            if swiglu:
                ring(dve, H_ev, 2)
            ring(dve, O_ev, 2)

            def body(u, s, use, more):
                if swiglu:
                    for f in range(FT):
                        dve.wait_ge(sil_done.handle, sil_done.at(u * FT + (f + 1)))
                        nc.vector.tensor_tensor(hT[:, s, f, :], sil[:, f % 2, :], ps_H[:, f % 2, 1, 0:unit], ALU.mult)\
                            .then_inc(H_ev.handle, 1)
                dve.wait_ge(out_sent[s].handle, out_sent[s].at(use * (16 * n_rows)))
                if b2 is not None:
                    dve.wait_ge(w_in[s].handle, w_in[s].at(use * (16 * n_w)))
                for n, (lo, size) in enumerate(tiles):
                    dve.wait_ge(O_mm.handle, O_mm.at(u * nt + (n + 1)))
                    got = ps_O[0:size, (s * nt + n) % 2, 0:D]
                    if b2 is not None:
                        one = nc.vector.tensor_tensor(Y[0:size, s, n, :], got, b2r[0:size, s, :], ALU.add)
                    else:
                        one = nc.vector.tensor_copy(Y[0:size, s, n, :], got)
                    one.then_inc(O_ev.handle, 1)

            pairs = (n_units - 1) // 2
            with dve.Fori(0, pairs) as i:
                for s in range(2):
                    body(i * 2 + s, s, i + 1, True)
                    if beside:
                        beside.beside_vector(dve, ps_beside, i, s)
            for u in range(2 * pairs, n_units):
                body(u, u % 2, u // 2 + 1, u + 1 < n_units)
    T_mm.base += n_units
    T_ev.base += n_units + 1
    H_mm.base += n_units * FT
    sil_done.base += n_units * FT if swiglu else 0
    H_ev.base += n_units * FT + 2
    O_mm.base += n_units * nt
    O_ev.base += n_units * nt + 2
    for s in range(2):
        uses = (n_units + 1 - s) // 2
        w_in[s].base += 16 * n_w * uses
        rows_in[s].base += 16 * n_rows * uses
        out_sent[s].base += 16 * n_rows * (uses + 1)


def split_slot_experts(c, n_units, unit, F, w1, w3, w2, func, Xg, Yg, scatter):
    nc = c.nc
    FT = F // P
    names = "T_mm T_hi T_lo H_mm sil prod h_hi h_lo W_hi W_lo O_mm O_ev".split()
    T_mm, T_hi, T_lo, H_mm, sil_done, prod, h_hi, h_lo, W_hi, W_lo, O_mm, O_ev = [c.sig("sp_" + n) for n in names]
    rows_in = [c.sig(f"se_rows{i}") for i in range(2)]
    w_in = [c.sig(f"se_w{i}") for i in range(2)]
    out_sent = [c.sig(f"se_out{i}") for i in range(2)]
    tiles = [(lo, min(P, unit - lo)) for lo in range(0, unit, P)]
    nt = len(tiles)
    full = unit // P
    n_rows = nt - full + 1
    n_w = 3
    F32R = mybir.dt.float32r
    with ExitStack() as st:
        shapes = ([P, 2, KD, F], [P, 2, KD, F], [P, 2, FT, D])
        W = [c.sb(st, f"sp_W{n}", shape) for n, shape in enumerate(shapes)]
        Wh = [c.sb(st, f"sp_Wh{n}", shape, F32R) for n, shape in enumerate(shapes)]
        Wl = [c.sb(st, f"sp_Wl{n}", shape, F32R) for n, shape in enumerate(shapes)]
        X = c.sb(st, "sp_X", [P, 2, nt, D])
        XTh = c.sb(st, "sp_XTh", [P, 2, KD, unit], F32R)
        XTl = c.sb(st, "sp_XTl", [P, 2, KD, unit], F32R)
        sil = c.sb(st, "sp_sil", [P, 2, unit])
        h = c.sb(st, "sp_h", [P, 2, unit])
        hh = c.sb(st, "sp_hh", [P, 2, FT, unit], F32R)
        hl = c.sb(st, "sp_hl", [P, 2, FT, unit], F32R)
        Y = c.sb(st, "sp_Y", [P, 2, nt, D])
        ps_T = c.ps(st, "sp_ps_T", [P, KD, 512])
        ps_H = c.ps(st, "sp_ps_H", [P, 2, 2, 512])
        ps_O = c.ps(st, "sp_ps_O", [P, 2, 512])
        block = st.enter_context(nc.Block())

        def for_units(eng, body):
            pairs = (n_units - 1) // 2
            with eng.Fori(0, pairs) as i:
                for s in range(2):
                    body(i * 2 + s, s, i + 1, True)
            for u in range(2 * pairs, n_units):
                body(u, u % 2, u // 2 + 1, u + 1 < n_units)

        def row_views(dram, sbuf, u, s, start=0):
            at = u * unit + start
            yield dram[bass.ds(at, full * P), :].rearrange("(t p) d -> p t d", p=P), sbuf[:, s, 0:full, :]
            if nt > full:
                yield dram[bass.ds(at + full * P, unit - full * P), :], sbuf[0:unit - full * P, s, full, :]

        @block.sync
        def _(sp):
            def load_rows(u, s):
                for dram, sbuf in row_views(Xg, X, u, s):
                    sp.dma_start(sbuf, dram).then_inc(rows_in[s].handle, 16)

            def load_weights(u, s):
                for out, w in zip(W, (w1, w3, w2)):
                    sp.dma_start(out[:, s, :, :], w[u, :, :].rearrange("(k p) f -> p k f", p=P))\
                        .then_inc(w_in[s].handle, 16)

            def load(u, s):
                sp.wait_ge(T_mm.handle, T_mm.at(u - 1))
                load_rows(u, s)
                sp.wait_ge(W_lo.handle, W_lo.at((u - 1) * n_w))
                load_weights(u, s)

            def send(u, s):
                sp.wait_ge(O_ev.handle, O_ev.at((u + 1) * nt + 2))
                for dram, sbuf in row_views(Yg, Y, u, s, 1):
                    sp.dma_start(dram, sbuf).then_inc(out_sent[s].handle, 16)

            for s in range(2):
                ring(sp, out_sent[s], 16 * n_rows)
                load_weights(s, s)
            sp.wait_ge(c.sig("scattered").handle, scatter[1])
            for s in range(2):
                load_rows(s, s)
            units = n_units - 2
            with sp.Fori(0, units // 2) as i:
                for s in range(2):
                    load(i * 2 + (s + 2), s)
                    send(i * 2 + s, s)
            for u in range(units // 2 * 2, n_units):
                if u < units:
                    load(u + 2, u % 2)
                send(u, u % 2)
            for s in range(2):
                uses = (n_units + 1 - s) // 2
                sp.wait_ge(w_in[s].handle, w_in[s].at(16 * n_w * uses))
                sp.wait_ge(rows_in[s].handle, rows_in[s].at(16 * n_rows * uses))
                sp.wait_ge(out_sent[s].handle, out_sent[s].at(16 * n_rows * (uses + 1)))

        @block.gpsimd
        def _(pool):
            scatter[0](pool)

        @block.tensor
        def _(pe):
            def transpose(u, s, use):
                pe.wait_ge(rows_in[s].handle, rows_in[s].at(use * (16 * n_rows)))
                pe.wait_ge(T_lo.handle, T_lo.at(u + 1))
                for k in range(KD):
                    for n, (lo, size) in enumerate(tiles):
                        last = nc.tensor.transpose(ps_T[:, k, lo:lo + size], X[0:size, s, n, k * P:(k + 1) * P],
                                                   c.ident[0:size, 0:size])
                last.then_inc(T_mm.handle, 1)

            def product(out, left, right, first, final):
                for n, (a, b) in enumerate(((0, 0), (0, 1), (1, 0))):
                    last = nc.tensor.matmul(out, left[a], right[b], start=(first and n == 0), stop=(final and n == 2))
                return last

            def body(u, s, use, more):
                pe.wait_ge(W_lo.handle, W_lo.at(u * n_w + 2))
                pe.wait_ge(T_lo.handle, T_lo.at(u + 2))
                for f in range(FT):
                    pe.wait_ge(prod.handle, prod.at(u * FT + (f + 1)))
                    for m in range(2):
                        for k in range(KD):
                            last = product(ps_H[:, f % 2, m, 0:unit],
                                           [w[m][:, s, k, f * P:(f + 1) * P] for w in (Wh, Wl)],
                                           (XTh[:, s, k, :], XTl[:, s, k, :]), k == 0, k == KD - 1)
                    last.then_inc(H_mm.handle, 1)
                if more:
                    transpose(u + 1, 1 - s, use + s)
                pe.wait_ge(W_lo.handle, W_lo.at(u * n_w + 3))
                for n, (lo, size) in enumerate(tiles):
                    pe.wait_ge(O_ev.handle, O_ev.at(u * nt + (n + 1)))
                    for f in range(FT):
                        if n == 0:
                            pe.wait_ge(h_lo.handle, h_lo.at(u * FT + (f + 3)))
                        last = product(ps_O[0:size, (s * nt + n) % 2, 0:D],
                                       (hh[:, s, f, lo:lo + size], hl[:, s, f, lo:lo + size]),
                                       [w[2][:, s, f, :] for w in (Wh, Wl)], f == 0, f == FT - 1)
                    last.then_inc(O_mm.handle, 1)

            ring(pe, T_lo, 1)
            transpose(0, 0, 1)
            for_units(pe, body)

        @block.scalar
        def _(act):
            def round_rows(u, s):
                act.wait_ge(T_mm.handle, T_mm.at(u + 1))
                nc.scalar.copy(XTh[:, s, :, :], ps_T[:, :, 0:unit]).then_inc(T_hi.handle, 1)

            def round_weights(s, n):
                nc.scalar.copy(Wh[n][:, s, :, :], W[n][:, s, :, :]).then_inc(W_hi.handle, 1)

            def body(u, s, use, more):
                def round_hidden(f):
                    act.wait_ge(prod.handle, prod.at(u * FT + (f + 3)))
                    nc.scalar.copy(hh[:, s, f, :], h[:, f % 2, :]).then_inc(h_hi.handle, 1)

                for f in range(FT):
                    act.wait_ge(H_mm.handle, H_mm.at(u * FT + (f + 1)))
                    nc.scalar.activation(sil[:, f % 2, :], ps_H[:, f % 2, 0, 0:unit], func).then_inc(sil_done.handle, 1)
                    if f:
                        round_hidden(f - 1)
                        if f == 1:
                            round_weights(s, 2)
                round_hidden(FT - 1)
                if more:
                    round_rows(u + 1, 1 - s)
                    act.wait_ge(w_in[1 - s].handle, w_in[1 - s].at((use + s) * (16 * n_w)))
                    for n in range(2):
                        round_weights(1 - s, n)

            act.wait_ge(w_in[0].handle, w_in[0].at(16 * n_w))
            for n in range(2):
                round_weights(0, n)
            round_rows(0, 0)
            for_units(act, body)

        @block.vector
        def _(dve):
            v = nc.vector

            def rest_of_rows(u, s):
                dve.wait_ge(T_hi.handle, T_hi.at(u + 1))
                v.tensor_tensor(XTl[:, s, :, :], ps_T[:, :, 0:unit], XTh[:, s, :, :], ALU.subtract).then_inc(T_lo.handle, 1)

            def rest_of_weights(u, s, n):
                dve.wait_ge(W_hi.handle, W_hi.at(u * n_w + (n + 1)))
                v.tensor_tensor(Wl[n][:, s, :, :], W[n][:, s, :, :], Wh[n][:, s, :, :], ALU.subtract)\
                    .then_inc(W_lo.handle, 1)

            def body(u, s, use, more):
                def rest_of_hidden(f):
                    dve.wait_ge(h_hi.handle, h_hi.at(u * FT + (f + 1)))
                    v.tensor_tensor(hl[:, s, f, :], h[:, f % 2, :], hh[:, s, f, :], ALU.subtract).then_inc(h_lo.handle, 1)

                for f in range(FT):
                    dve.wait_ge(h_lo.handle, h_lo.at(u * FT + (f + 1)))
                    dve.wait_ge(sil_done.handle, sil_done.at(u * FT + (f + 1)))
                    v.tensor_tensor(h[:, f % 2, :], sil[:, f % 2, :], ps_H[:, f % 2, 1, 0:unit], ALU.mult)\
                        .then_inc(prod.handle, 1)
                    if f:
                        rest_of_hidden(f - 1)
                        if f == 1:
                            rest_of_weights(u, s, 2)
                rest_of_hidden(FT - 1)
                if more:
                    rest_of_rows(u + 1, 1 - s)
                dve.wait_ge(out_sent[s].handle, out_sent[s].at(use * (16 * n_rows)))
                for n, (lo, size) in enumerate(tiles):
                    dve.wait_ge(O_mm.handle, O_mm.at(u * nt + (n + 1)))
                    v.tensor_copy(Y[0:size, s, n, :], ps_O[0:size, (s * nt + n) % 2, 0:D]).then_inc(O_ev.handle, 1)
                    if more and n < 2:
                        rest_of_weights(u + 1, 1 - s, n)

            ring(dve, prod, 2)
            ring(dve, h_lo, 2)
            ring(dve, O_ev, 2)
            for n in range(2):
                rest_of_weights(0, 0, n)
            rest_of_rows(0, 0)
            for_units(dve, body)
    for s in range(2):
        uses = (n_units + 1 - s) // 2
        w_in[s].base += 16 * n_w * uses
        rows_in[s].base += 16 * n_rows * uses
        out_sent[s].base += 16 * n_rows * (uses + 1)


def exchange_buffers(c):
    c.Xg = c.nc.dram_tensor("slot_rows", (ROOM, D), F32).ap()
    c.Yg = c.nc.dram_tensor("slot_outputs", (ROOM + 1, D), F32).ap()
    sent = c.sig("zeros_sent")
    tiles = 2
    c.zeros_sent = 16 * (ROOM // (P * tiles) + 1)

    def fill(sp):
        for lo in range(0, ROOM, P * tiles):
            sp.dma_start(c.Xg[lo:lo + P * tiles, :].rearrange("(p t) d -> p (t d)", p=P), c.zeros[:, :])\
                .then_inc(sent.handle, 16)
        sp.dma_start(c.Yg[0:1, :], c.zeros[0:1, 0:D]).then_inc(sent.handle, 16)

    return fill


def make_plan(c, st, n_units):
    to = c.sb(st, "plan_to", [P, 2, NT], U32)
    back_from = c.sb(st, "plan_from", [P, 2, NT], U32)
    gate = c.sb(st, "plan_gate", [P, 2, NT])
    unit_expert = c.sb(st, "plan_expert", [1, n_units], U32)
    return to, back_from, gate, unit_expert[:, :]


def L0_ffn(c, w, kernel_l1, kernel_w):
    E = 14
    unit, n_units = slots_of(E, "top2")
    with ExitStack() as st:
        logits = c.sb(st, "L0_logits", [P, NT, E])
        plan = make_plan(c, st, n_units)
        to, back_from, gate, unit_expert = plan
        normalise(c, c.x, xn_out=c.xn, router=(w["gate_w"].rearrange("e d -> d e"), E, logits))
        route(c, logits, E, "top2", None, None, plan)
        kernel_l1.begin(kernel_w, scatter(c, c.xn, to, 2, n_units * unit, c.Xg)[0])
        slot_experts(c, n_units, unit, 512, w["w1"], None, w["w2"], w["b1"], w["b2"], ACT.Gelu, unit_expert, c.Xg, c.Yg,
                     beside=kernel_l1)
        gather(c, back_from, gate, 2, n_units * unit, c.Yg, c.xn, clipped=c.x, beside=kernel_l1)


def L2_ffn(c, w):
    E = 8
    unit, n_units = slots_of(E, "top1")
    nc = c.nc
    with ExitStack() as st:
        logits = c.sb(st, "L2_logits", [P, NT, E])
        top = c.sb(st, "L2_top", [P, NT])
        plan = make_plan(c, st, n_units)
        to, back_from, gate, _ = plan
        normalise(c, c.x, router=(w["Wr"], E, logits))
        route(c, logits, E, "top1", w["br"], top[:, :], plan)
        scaled = c.sig("L2_scaled")
        with nc.Block() as block:
            @block.vector
            def _(dve):
                nc.vector.tensor_tensor(c.rstd[:, :], c.rstd[:, :], top[:, :], ALU.mult).then_inc(scaled.handle, 1)
                nc.vector.tensor_tensor(c.nmr[:, :], c.nmr[:, :], top[:, :], ALU.mult).then_inc(scaled.handle, 1)
                dve.wait_ge(scaled.handle, scaled.at(2))
        scaled.base += 2
        normalise(c, c.x, xn_out=c.xn)
        slot_experts(c, n_units, unit, 256, w["W1"], None, w["W2"], w["b1"], w["b2"], ACT.Relu, None, c.Xg, c.Yg,
                     scatter=scatter(c, c.xn, to, 1, n_units * unit, c.Xg))
        gather(c, back_from, gate, 1, n_units * unit, c.Yg, c.x)


def L3_ffn(c, w, xT, out):
    E = 16
    unit, n_units = slots_of(E, "capacity")
    with ExitStack() as st:
        logits = c.sb(st, "L3_logits", [P, NT, E])
        plan = make_plan(c, st, n_units)
        to, back_from, gate, _ = plan
        normalise(c, c.x, xn_out=c.xn, xT_out=xT, router=(w["gate_w"], E, logits))
        route(c, logits, E, "capacity", w["gate_b"], None, plan, meanwhile=lambda take_out: experts(
            c, xT, 2, 512, w["sw1"], w["sw3"], w["sw2"], None, ACT.Silu, lambda t, e: 0.5, c.x, meanwhile=take_out))
        split_slot_experts(c, n_units, unit, 512, w["ew1"], w["ew3"], w["ew2"], ACT.Silu, c.Xg, c.Yg,
                           scatter(c, c.xn, to, 2, n_units * unit, c.Xg))
        gather(c, back_from, gate, 2, n_units * unit, c.Yg, c.x, stored_to=out)


DH3 = D // HEADS
HPT = P // DH3
HPTJ = HPT * J


def narrow_fold(c, w, scratch, M, bias, N):
    nc = c.nc
    loaded, made, mm, ev, stored = [c.sig("nf_" + n) for n in ("loaded", "made", "mm", "ev", "stored")]
    with ExitStack() as st:
        Wq = c.sb(st, "nf_Wq", [P, KD, D])
        Wk = c.sb(st, "nf_Wk", [KC, 2, D])
        Wv = c.sb(st, "nf_Wv", [KC, 2, D])
        bq = c.sb(st, "nf_bq", [P, KD])
        bk = c.sb(st, "nf_bk", [P, KD])
        bv = c.sb(st, "nf_bv", [J, D])
        WqT = c.sb(st, "nf_WqT", [P, KD, D])
        KT = c.sb(st, "nf_KT", [P, KD, BJ])
        Kd = c.sb(st, "nf_Kd", [P, KD, B, HPTJ])
        V = c.sb(st, "nf_V", [J, B, D])
        own = c.sb(st, "nf_own", [P, HPT])
        zeros = c.sb(st, "nf_zeros", [P, HJC * D])
        ps = c.ps(st, "nf_ps", [P, 4, 512])
        stats = TokenStats(c, st, c.x)
        block = st.enter_context(nc.Block())
        half = HPTJ // 2
        first = [("K", m) for m in range(KD)] + [("V", b) for b in range(B)] + [("Q", m) for m in range(KD)]
        halves = [(m, b, q) for m in range(KD) for b in range(B) for q in range(2)]
        steps = first + [("M", (k, *x)) for k in range(KD) for x in halves] + [("B", x) for x in halves]
        n_kd = KD * B

        @block.sync
        def _(sp):
            for out, a in ((Wk[:, :, :], w["Wk"].rearrange("(k p) n -> p k n", p=KC)),
                           (Wv[:, :, :], w["Wv"].rearrange("(k p) n -> p k n", p=KC)),
                           (Wq[:, :, :], w["Wq"].rearrange("(k p) n -> p k n", p=P)),
                           (bq[:, :], column(w["bq"])), (bk[:, :], column(w["bk"])), (bv[:, :], row(w["bv"], J))):
                sp.dma_start(out, a, allow_slow_non_contiguous=True).then_inc(loaded.handle, 16)
            sp.wait_ge(made.handle, made.at(4))
            for b in range(B):
                sp.dma_start(scratch[b, :, :].rearrange("(c p) d -> p c d", p=P),
                             zeros[:, :].rearrange("p (c d) -> p c d", d=D)).then_inc(stored.handle, 16)
            sp.wait_ge(stored.handle, stored.at(16 * B))
            sp.wait_ge(ev.handle, ev.at(KD + B))
            with sp.Fori(0, HEADS) as h:
                sp.dma_start(scratch[:, bass.ts(h, J), bass.ts(h, DH3)].rearrange("b j c -> j b c"),
                             V[:, :, bass.ts(h, DH3)]).then_inc(stored.handle, 16)
            sp.wait_ge(stored.handle, stored.at(16 * (B + HEADS)))
            for b in range(B):
                sp.dma_start(N[:, b, :, :], scratch[b, :, :].rearrange("(c p) d -> p c d", p=P)).then_inc(stored.handle, 16)
            sp.wait_ge(stored.handle, stored.at(16 * (2 * B + HEADS)))

        @block.gpsimd
        def _(pool):
            nc.gpsimd.memset(own[:, :], 1.0).then_inc(made.handle, 1)
            pool.wait_ge(made.handle, made.at(1))
            nc.gpsimd.affine_select(out=own[:, :], in_=own[:, :], compare_op=ALU.is_ge, fill=0.0, base=0,
                                    pattern=[[-DH3, HPT]], channel_multiplier=1).then_inc(made.handle, 1)
            pool.wait_ge(made.handle, made.at(2))
            nc.gpsimd.affine_select(out=own[:, :], in_=own[:, :], compare_op=ALU.is_ge, fill=0.0, base=DH3 - 1,
                                    pattern=[[DH3, HPT]], channel_multiplier=-1).then_inc(made.handle, 1)
            nc.gpsimd.memset(zeros[:, :], 0.0).then_inc(made.handle, 1)

        @block.tensor
        def _(pe):
            pe.wait_ge(loaded.handle, loaded.at(96))
            for n, (kind, at) in enumerate(steps):
                bank = ps[:, n % 4, :]
                if n == len(first):
                    pe.wait_ge(ev.handle, ev.at(len(first) + n_kd))
                elif n >= 4:
                    pe.wait_ge(ev.handle, ev.at(n - 3 + (n_kd if n > len(first) else 0)))
                if kind == "K":
                    for k in range(2):
                        last = nc.tensor.matmul(bank[:, 0:BJ], Wk[:, k, at * P:(at + 1) * P], c.ctxT[:, k, :],
                                                start=(k == 0), stop=(k == 1))
                elif kind == "V":
                    for k in range(2):
                        last = nc.tensor.matmul(bank[0:J, 0:D], c.ctxT[:, k, at * J:(at + 1) * J], Wv[:, k, :],
                                                start=(k == 0), stop=(k == 1))
                elif kind == "Q":
                    for k in range(KD):
                        last = nc.tensor.transpose(bank[:, k * P:(k + 1) * P], Wq[:, k, at * P:(at + 1) * P], c.ident[:, :])
                elif kind == "M":
                    k, m, b, q = at
                    last = nc.tensor.matmul(bank[:, 0:half], WqT[:, m, k * P:(k + 1) * P],
                                            Kd[:, m, b, q * half:(q + 1) * half], start=True, stop=True)
                else:
                    m, b, q = at
                    last = nc.tensor.matmul(bank[0:1, 0:half], bq[:, m:m + 1], Kd[:, m, b, q * half:(q + 1) * half],
                                            start=True, stop=True)
                last.then_inc(mm.handle, 1)

        @block.scalar
        def _(act):
            stats.square_roots(act)

        @block.vector
        def _(dve):
            stats.all_tiles(dve)
            stats.finish(dve)
            dve.wait_ge(loaded.handle, loaded.at(96))
            for n, (kind, at) in enumerate(steps):
                bank = ps[:, n % 4, :]
                if n == len(first):
                    dve.wait_ge(made.handle, made.at(3))
                    dve.wait_ge(ev.handle, ev.at(len(first)))
                    for m in range(KD):
                        for b in range(B):
                            nc.vector.tensor_tensor(Kd[:, m, b, :].rearrange("p (h j) -> p h j", j=J),
                                                    bc(KT[:, m, b * J:(b + 1) * J].unsqueeze(1), [P, HPT, J]),
                                                    bc(own[:, :].unsqueeze(2), [P, HPT, J]), ALU.mult).then_inc(ev.handle, 1)
                dve.wait_ge(mm.handle, mm.at(n + 1))
                if kind == "K":
                    last = nc.vector.tensor_scalar(KT[:, at, :], bank[:, 0:BJ], bk[:, at:at + 1], DH3 ** -0.5,
                                                   ALU.add, ALU.mult)
                elif kind == "V":
                    last = nc.vector.tensor_tensor(V[:, at, :], bank[0:J, 0:D], bv[:, :], ALU.add)
                elif kind == "Q":
                    last = nc.vector.tensor_copy(WqT[:, at, :], bank[:, 0:D])
                else:
                    m, b, q = at[-3:]
                    lo = m * HPTJ + q * half
                    if kind == "M":
                        last = nc.vector.tensor_copy(M[:, at[0], b, lo:lo + half], bank[:, 0:half])
                    else:
                        last = nc.vector.tensor_copy(bias[0:1, b, lo:lo + half], bank[0:1, 0:half])
                last.then_inc(ev.handle, 1)
            dve.wait_ge(ev.handle, ev.at(len(steps) + n_kd))
    stats.done()
    loaded.base += 96
    made.base += 4
    mm.base += len(steps)
    ev.base += len(steps) + n_kd
    stored.base += 16 * (2 * B + HEADS)


def L3_xattn(c, w, scratch, xT):
    with ExitStack() as st:
        M = c.sb(st, "l3_M", [P, KD, B, HJ])
        N = c.sb(st, "l3_N", [P, B, HJC, D])
        bias = c.sb(st, "l3_bias", [1, B, HJ])
        narrow_fold(c, w, scratch, M, bias, N)
        attention(c, M, bias, N, None, xT)
    one = {n: w[n].unsqueeze(0) for n in ("W1", "W2", "b1")}
    experts(c, xT, 1, 512, one["W1"], None, one["W2"], one["b1"], ACT.Relu, lambda t, e: 1.0, c.x, plus=w["b2"])


def L1_ffn(c, w, xT):
    nc = c.nc
    E, F = 8, 512
    FT = F // P
    names = "loaded mm act top weights T_ev step".split()
    s = {n: c.sig("l1f_" + n) for n in names}
    normalise(c, c.x, xn_out=c.xn, xT_out=xT)
    with ExitStack() as st:
        W1 = c.sb(st, "l1f_W1", [P, B, KD, F])
        W2o = c.sb(st, "l1f_W2o", [P, B, FT, D])
        b1 = c.sb(st, "l1f_b1", [P, B, FT])
        with ExitStack() as pre:
            Wp1 = c.sb(pre, "l1f_Wp1", [P, KD, P])
            bp1 = c.sb(pre, "l1f_bp1", [P, 1])
            Wp2 = c.sb(pre, "l1f_Wp2", [P, E])
            bp2 = c.sb(pre, "l1f_bp2", [1, E])
            Wo = c.sb(pre, "l1f_Wo", [P, KD, D])
            bo = c.sb(pre, "l1f_bo", [P, D])
            W2 = c.sb(pre, "l1f_W2", [P, B, FT, D])
            W2T = c.sb(pre, "l1f_W2T", [P, B, KD, F])
            b2 = c.sb(pre, "l1f_b2", [P, B, KD])
            b2w = c.sb(pre, "l1f_b2w", [P, B, KD, P])
            ends = c.sb(pre, "l1f_ends", [P, KD, B])
            nav = c.sb(pre, "l1f_nav", [P, B])
            lg = c.sb(pre, "l1f_lg", [1, B, E])
            v1 = c.sb(pre, "l1f_v1", [1, B])
            eight = c.sb(pre, "l1f_eight", [1, B, 8])
            idx = c.sb(pre, "l1f_idx", [1, B, 8], U32)
            rowb = c.sb(pre, "l1f_rowb", [P, B, D])
            ps = c.ps(pre, "l1f_ps", [P, 4, 512])
            block = pre.enter_context(nc.Block())

            @block.sync
            def _(sp):
                for out, a in ((Wp1[:, :, :], w["Wp1"].rearrange("(k p) n -> p k n", p=P)), (bp1[:, :], column(w["bp1"])),
                               (Wp2[:, :], w["Wp2"]), (bp2[:, :], row(w["bp2"], 1)),
                               (Wo[:, :, :], w["Wo"].rearrange("(k p) n -> p k n", p=P)), (bo[:, :], row(w["bo"], P))):
                    sp.dma_start(out, a, allow_slow_non_contiguous=True).then_inc(s["loaded"].handle, 16)
                sp.wait_ge(s["top"].handle, s["top"].at(1))
                for b in range(B):
                    e = sp.value_load(idx[0:1, b, 0:1], min_val=0, max_val=E - 1)
                    sp.dma_start(W2[:, b, :, :], w["W2"][e, :, :].rearrange("(k p) f -> p k f", p=P))\
                        .then_inc(s["weights"].handle, 16)
                    sp.dma_start(W1[:, b, :, :], w["W1"][e, :, :].rearrange("(k p) f -> p k f", p=P))\
                        .then_inc(s["weights"].handle, 16)
                    sp.dma_start(b1[:, b, :], w["b1"][e, :].rearrange("(f p) -> p f", p=P), allow_slow_non_contiguous=True)\
                        .then_inc(s["weights"].handle, 16)
                    sp.dma_start(b2[:, b, :], w["b2"][e, :].rearrange("(f p) -> p f", p=P), allow_slow_non_contiguous=True)\
                        .then_inc(s["weights"].handle, 16)
                sp.wait_ge(s["weights"].handle, s["weights"].at(128))

            @block.tensor
            def _(pe):
                pe.wait_ge(s["loaded"].handle, s["loaded"].at(96))
                pe.wait_ge(s["act"].handle, s["act"].at(1))
                for k in range(KD):
                    last = nc.tensor.matmul(ps[:, 0, 0:B], Wp1[:, k, :], ends[:, k, :], start=(k == 0), stop=(k == KD - 1))
                last.then_inc(s["mm"].handle, 1)
                pe.wait_ge(s["act"].handle, s["act"].at(2))
                for b in range(B):
                    last = nc.tensor.matmul(ps[0:1, 1, b * E:(b + 1) * E], nav[:, b:b + 1], Wp2[:, :], start=True, stop=True)
                last.then_inc(s["mm"].handle, 1)
                pe.wait_ge(s["weights"].handle, s["weights"].at(128))
                for b in range(B):
                    for k in range(KD):
                        if b:
                            pe.wait_ge(s["T_ev"].handle, s["T_ev"].at((b - 1) * KD + k + 1))
                        for f in range(FT):
                            last = nc.tensor.transpose(ps[:, 2 + k, f * P:(f + 1) * P], W2[:, b, f, k * P:(k + 1) * P],
                                                       c.ident[:, :])
                        last.then_inc(s["mm"].handle, 1)
                pe.wait_ge(s["T_ev"].handle, s["T_ev"].at(B * KD))
                pe.wait_ge(s["step"].handle, s["step"].at(8))
                for b in range(B):
                    for f in range(0, FT, 2):
                        n = b * FT // 2 + f // 2
                        if n:
                            pe.wait_ge(s["T_ev"].handle, s["T_ev"].at(B * KD + n))
                        for q in range(2):
                            for k in range(KD):
                                last = nc.tensor.matmul(ps[:, 0, q * D:(q + 1) * D],
                                                        W2T[:, b, k, (f + q) * P:(f + q + 1) * P], Wo[:, k, :],
                                                        start=(k == 0), stop=(k == KD - 1))
                        last.then_inc(s["mm"].handle, 1)
                for b in range(B):
                    for k in range(KD):
                        last = nc.tensor.matmul(ps[:, 1, b * D:(b + 1) * D], b2w[:, b, k, :], Wo[:, k, :],
                                                start=(k == 0), stop=(k == KD - 1))
                last.then_inc(s["mm"].handle, 1)

            @block.scalar
            def _(act):
                for b in range(B):
                    last = nc.scalar.copy(ends[:, :, b], xT[:, :, (b + 1) * SEQ - 1])
                last.then_inc(s["act"].handle, 1)
                act.wait_ge(s["mm"].handle, s["mm"].at(1))
                nc.scalar.activation(nav[:, :], ps[:, 0, 0:B], ACT.Gelu, bias=bp1[:, 0:1]).then_inc(s["act"].handle, 1)
                act.wait_ge(s["step"].handle, s["step"].at(3))
                nc.scalar.activation(lg[:, :, :], lg[:, :, :], ACT.Exp).then_inc(s["act"].handle, 1)

            @block.vector
            def _(dve):
                v = nc.vector
                link = Chain(dve, s["step"])
                wide = bc(v1[:, :].unsqueeze(2), [1, B, E])
                dve.wait_ge(s["mm"].handle, s["mm"].at(2))
                link(v.tensor_tensor(lg[:, :, :], ps[0:1, 1, 0:B * E].rearrange("p (b e) -> p b e", e=E),
                                     bc(bp2[:, :].unsqueeze(1), [1, B, E]), ALU.add))
                link(v.tensor_reduce(v1[:, :], lg[:, :, :], AX.X, ALU.max))
                link(v.tensor_tensor(lg[:, :, :], lg[:, :, :], wide, ALU.subtract))
                dve.wait_ge(s["act"].handle, s["act"].at(3))
                link(v.tensor_reduce(v1[:, :], lg[:, :, :], AX.X, ALU.add))
                link(v.reciprocal(v1[:, :], v1[:, :]))
                link(v.tensor_tensor(lg[:, :, :], lg[:, :, :], wide, ALU.mult))
                v.max(eight[:, 0, :], lg[:, 0, :])
                link(v.max(eight[:, 1, :], lg[:, 1, :]))
                v.max_index(idx[:, 0, :], eight[:, 0, :], lg[:, 0, :])
                v.max_index(idx[:, 1, :], eight[:, 1, :], lg[:, 1, :]).then_inc(s["top"].handle, 1)
                dve.wait_ge(s["weights"].handle, s["weights"].at(128))
                for b in range(B):
                    for k in range(KD):
                        dve.wait_ge(s["mm"].handle, s["mm"].at(3 + b * KD + k))
                        v.tensor_copy(W2T[:, b, k, :], ps[:, 2 + k, :]).then_inc(s["T_ev"].handle, 1)
                link(v.tensor_copy(b2w[:, :, :, :], bc(b2[:, :, :].unsqueeze(3), [P, B, KD, P])))
                for b in range(B):
                    for f in range(0, FT, 2):
                        dve.wait_ge(s["mm"].handle, s["mm"].at(7 + b * FT // 2 + f // 2))
                        v.tensor_copy(W2o[:, b, f:f + 2, :], ps[:, 0, :].rearrange("p (f d) -> p f d", d=D))\
                            .then_inc(s["T_ev"].handle, 1)
                dve.wait_ge(s["mm"].handle, s["mm"].at(7 + B * FT // 2))
                link(v.tensor_tensor(rowb[:, :, :], ps[:, 1, :].rearrange("p (b d) -> p b d", d=D),
                                     bc(bo[:, :].unsqueeze(1), [P, B, D]), ALU.add))
                for b in range(B):
                    tiles = slice(b * TPB, (b + 1) * TPB)
                    link(v.scalar_tensor_tensor(c.x[:, tiles, :], bc(rowb[:, b, :].unsqueeze(1), [P, TPB, D]), 0.3,
                                                c.x[:, tiles, :], ALU.mult, ALU.add))
                link(v.tensor_tensor(c.x[:, :, :], c.x[:, :, :], c.xn[:, :, :], ALU.add))
        s["loaded"].base += 96
        for n, k in (("mm", 12), ("act", 3), ("top", 1), ("weights", 128), ("T_ev", 8), ("step", 12)):
            s[n].base += k
        experts(c, xT, 1, F, None, None, None, True, ACT.Gelu, lambda t, e: 0.3, c.x, resident=(W1, W2o, b1))


H1, DH1 = 4, 32
HJ1 = H1 * J
JE = J + 1
TOP = 32
NS = 64
MASKED, TAKEN1 = -1.0e30, -3.0e38
NF1, NF2 = 5, 256
TWO_PI = 6.2831845
R2 = 0.5 ** 0.5


def constants():
    n = 2 * SEQ
    f1, j2, f2 = np.arange(NF1)[:, None, None], np.arange(NF2)[None, :, None], np.arange(NF2)[None, None, :]
    turn = 2 * np.pi * ((j2 * (f1 + 8 * f2)) % n) / n
    fwd = np.stack([np.cos(turn), np.sin(turn), -np.sin(turn)], axis=1)
    scale = np.array([1, 2, 2, 2, 1]).reshape(NF1, 1, 1, 1) / n
    inv = np.swapaxes(fwd, 2, 3) * scale
    return {"dft_fwd": fwd.astype(np.float32), "dft_inv": inv.astype(np.float32)}


def L1_fold(c, w, mask_tok, mask_ctx, M, mask_row, VF, tok_factor):
    nc = c.nc
    s = {n: c.sig("l1_" + n) for n in "loaded mm ev step bias".split()}
    with ExitStack() as st:
        Wq = c.sb(st, "l1_Wq", [P, KD, P])
        Wk = c.sb(st, "l1_Wk", [KC, 2, P])
        Wv = c.sb(st, "l1_Wv", [KC, 2, D])
        Wf = c.sb(st, "l1_Wf", [P, 2, KD, 2 * D])
        bf = c.sb(st, "l1_bf", [1, 2, 2 * D])
        KT = c.sb(st, "l1_KT", [P, BJ])
        VT = c.sb(st, "l1_VT", [P, KD, BJ])
        WqT = c.sb(st, "l1_WqT", [P, D])
        gate = c.sb(st, "l1_gate", [P, 1])
        mt8 = c.sb(st, "l1_mt8", [P, NT], U8)
        mc8 = c.sb(st, "l1_mc8", [1, B, J], U8)
        mcf = c.sb(st, "l1_mcf", [1, B, J])
        ps = c.ps(st, "l1_ps", [P, 4, 512])
        stats = TokenStats(c, st, c.x)
        block = st.enter_context(nc.Block())
        steps = [("K", 0), ("V", 0), ("V", 1), ("Q", 0)] + [("M", h) for h in range(H1)]
        steps += [("F", (b, o)) for b in range(B) for o in range(2)]
        loads = 10

        @block.sync
        def _(sp):
            for out, a in ((Wk[:, :, :], w["Wk"].rearrange("(k p) n -> p k n", p=KC)),
                           (Wv[:, :, :], w["Wv"].rearrange("(k p) n -> p k n", p=KC)),
                           (Wq[:, :, :], w["Wq"].rearrange("(k p) n -> p k n", p=P)),
                           (Wf[:, 0, :, :], w["W_film_in"].rearrange("(k p) n -> p k n", p=P)),
                           (Wf[:, 1, :, :], w["W_film_out"].rearrange("(k p) n -> p k n", p=P)),
                           (bf[:, 0, :], row(w["b_film_in"], 1)), (bf[:, 1, :], row(w["b_film_out"], 1)),
                           (gate[:, :], row(w["mod_gate"], P)),
                           (mt8[:, :], mask_tok.rearrange("b (t p) -> p (b t)", p=P)),
                           (mc8[:, :, :], mask_ctx.unsqueeze(0))):
                sp.dma_start(out, a, allow_slow_non_contiguous=True).then_inc(s["loaded"].handle, 16)
            sp.wait_ge(s["step"].handle, s["step"].at(2))
            for b in range(B):
                sp.dma_start(VF[J:JE, b, :, :], bf[:, :, :]).then_inc(s["bias"].handle, 16)
            sp.wait_ge(s["bias"].handle, s["bias"].at(32))

        @block.tensor
        def _(pe):
            pe.wait_ge(s["loaded"].handle, s["loaded"].at(16 * loads))
            for n, (kind, at) in enumerate(steps):
                bank = ps[:, n % 4, :]
                if n >= 4:
                    pe.wait_ge(s["ev"].handle, s["ev"].at(max(n - 3, 4)))
                if kind == "K":
                    for k in range(2):
                        last = nc.tensor.matmul(bank[:, 0:BJ], Wk[:, k, :], c.ctxT[:, k, :], start=(k == 0), stop=(k == 1))
                elif kind == "V":
                    for k in range(2):
                        last = nc.tensor.matmul(bank[:, 0:BJ], Wv[:, k, at * P:(at + 1) * P], c.ctxT[:, k, :],
                                                start=(k == 0), stop=(k == 1))
                elif kind == "Q":
                    for k in range(KD):
                        last = nc.tensor.transpose(bank[:, k * P:(k + 1) * P], Wq[:, k, :], c.ident[:, :])
                elif kind == "M":
                    lo = at * DH1
                    for k in range(KD):
                        last = nc.tensor.matmul(bank[:, k * BJ:(k + 1) * BJ], WqT[lo:lo + DH1, k * P:(k + 1) * P],
                                                KT[lo:lo + DH1, :], start=True, stop=True)
                else:
                    b, o = at
                    for k in range(KD):
                        last = nc.tensor.matmul(bank[0:J, :], VT[:, k, b * J:(b + 1) * J], Wf[:, o, k, :],
                                                start=(k == 0), stop=(k == KD - 1))
                last.then_inc(s["mm"].handle, 1)

        @block.scalar
        def _(act):
            stats.square_roots(act)

        @block.vector
        def _(dve):
            stats.all_tiles(dve)
            stats.finish(dve)
            v = nc.vector
            link = Chain(dve, s["step"])
            dve.wait_ge(s["loaded"].handle, s["loaded"].at(16 * loads))
            link(v.tensor_scalar(bf[:, :, :], bf[:, :, :], gate[0:1, 0:1], None, ALU.mult))
            link(v.tensor_scalar(bf[:, :, 0:D], bf[:, :, 0:D], 1.0, None, ALU.add))
            link(v.tensor_copy(tok_factor, mt8[:, :]))
            link(v.tensor_scalar(tok_factor, tok_factor, 1.0 / H1, None, ALU.mult))
            link(v.tensor_copy(mcf[:, :, :], mc8[:, :, :]))
            link(v.tensor_scalar(mcf[:, :, :], mcf[:, :, :], 1.0, -MASKED, ALU.subtract, ALU.mult))
            for h in range(H1):
                link(v.tensor_copy(mask_row[:, :, h * J:(h + 1) * J], mcf[:, :, :]))
            for n, (kind, at) in enumerate(steps):
                bank = ps[:, n % 4, :]
                dve.wait_ge(s["mm"].handle, s["mm"].at(n + 1))
                if kind == "K":
                    last = v.tensor_scalar(KT[:, :], bank[:, 0:BJ], DH1 ** -0.5, None, ALU.mult)
                elif kind == "V":
                    last = v.tensor_copy(VT[:, at, :], bank[:, 0:BJ])
                elif kind == "Q":
                    last = v.tensor_copy(WqT[:, :], bank[:, 0:D])
                elif kind == "M":
                    last = v.tensor_copy(M[:, :, :, at * J:(at + 1) * J],
                                         bank[:, 0:KD * BJ].rearrange("p (k b j) -> p k b j", k=KD, b=B))
                else:
                    b, o = at
                    last = v.tensor_scalar(VF[0:J, b, o, :], bank[0:J, :], gate[0:J, 0:1], None, ALU.mult)
                last.then_inc(s["ev"].handle, 1)
            dve.wait_ge(s["ev"].handle, s["ev"].at(len(steps)))
    stats.done()
    s["loaded"].base += 16 * loads
    s["mm"].base += len(steps)
    s["ev"].base += len(steps)
    s["step"].base += 6 + H1
    s["bias"].base += 32


def L1_modulate(c, scores, tok_factor, VF, UK, film_out):
    nc = c.nc
    s = {n: c.sig("l1m_" + n) for n in "step fence shifted exped mean T_mm T_ev F_mm F_ev kept applied pool_fence".split()}
    rounds = TOP // 8
    with ExitStack() as st:
        sc = c.sb(st, "l1m_sc", [P, 2, H1, J])
        work = c.sb(st, "l1m_work", [P, 2, H1, J])
        eight = c.sb(st, "l1m_eight", [P, 2, H1, 8])
        rs = c.sb(st, "l1m_rs", [P, 2, H1])
        am = c.sb(st, "l1m_am", [P, 2, JE])
        amT = c.sb(st, "l1m_amT", [JE, 2, P])
        film_in = c.sb(st, "l1m_film_in", [P, 2, 2 * D])
        ps_T = c.ps(st, "l1m_ps_T", [JE, 2, 512])
        ps_F = c.ps(st, "l1m_ps_F", [P, 2, 2, 512])
        block = st.enter_context(nc.Block())

        @block.vector
        def _(dve):
            v = nc.vector
            link = Chain(dve, s["step"])
            link(v.memset(am[:, :, :], 1.0))

            def fence():
                dve.sem_inc(s["fence"].handle, 1)

            def heads(n):
                return scores[:, bass.ds(n, 2), :].rearrange("p t (h j) -> p t h j", j=J)

            def select(n):
                link(v.tensor_copy(work[:, :, :, :], heads(n)))
                fence()
                for r in range(rounds):
                    for j in range(2):
                        for h in range(H1):
                            last = v.max(eight[:, j, h, :], work[:, j, h, :])
                    link(last)
                    fence()
                    if r == 0:
                        v.tensor_tensor(sc[:, :, :, :], heads(n), bc(eight[:, :, :, 0:1], [P, 2, H1, J]), ALU.subtract)\
                            .then_inc(s["shifted"].handle, 1)
                    for j in range(2):
                        for h in range(H1):
                            last = v.match_replace(work[:, j, h, :], eight[:, j, h, :], work[:, j, h, :], TAKEN1)
                    link(last)
                    fence()

            def average(pair, n):
                dve.wait_ge(s["exped"].handle, s["exped"].at(pair + 1))
                link(v.scalar_tensor_tensor(sc[:, :, :, :], work[:, :, :, :], 10 * MASKED, sc[:, :, :, :],
                                            ALU.is_lt, ALU.mult))
                link(v.tensor_reduce(rs[:, :, :], sc[:, :, :, :], AX.X, ALU.add))
                link(v.reciprocal(rs[:, :, :], rs[:, :, :]))
                link(v.tensor_tensor(rs[:, :, :], rs[:, :, :], bc(tok_factor[:, bass.ds(n, 2)].unsqueeze(2), [P, 2, H1]),
                                     ALU.mult))
                link(v.tensor_tensor(sc[:, :, :, :], sc[:, :, :, :], bc(rs[:, :, :].unsqueeze(3), [P, 2, H1, J]), ALU.mult))
                dve.wait_ge(s["T_mm"].handle, s["T_mm"].at(n + 2))
                v.tensor_reduce(am[:, :, 0:J], sc[:, :, :, :].rearrange("p t h j -> p t j h"), AX.X, ALU.add)\
                    .then_inc(s["mean"].handle, 1)

            per_pair = 2 * rounds + 1 + 5
            with dve.Fori(0, NT // 2) as i:
                link.count = i * per_pair + 1
                select(i * 2)
                average(i, i * 2)

        @block.gpsimd
        def _(pool):
            for b in range(B):
                with pool.Fori(0, TPB // 2) as i:
                    n = i * 2 + b * TPB
                    pool.wait_ge(s["kept"].handle, s["kept"].at((n + 2) * 2))
                    pool.sem_inc(s["pool_fence"].handle, 1)
                    u = UK[:, bass.ds(i * 2, 2), b, :]
                    nc.gpsimd.tensor_tensor(u, u, film_in[:, :, 0:D], ALU.mult).then_inc(s["applied"].handle, 1)
                    pool.wait_ge(s["applied"].handle, s["applied"].at(n + 3))
                    pool.sem_inc(s["pool_fence"].handle, 1)
                    nc.gpsimd.tensor_tensor(u, u, film_in[:, :, D:2 * D], ALU.add).then_inc(s["applied"].handle, 1)
                    pool.wait_ge(s["applied"].handle, s["applied"].at(n + 4))

        @block.scalar
        def _(act):
            ring(act, s["T_ev"], 2)
            ring(act, s["F_ev"], 2)
            ring(act, s["applied"], 2)
            with act.Fori(0, NT // 2) as i:
                act.wait_ge(s["shifted"].handle, s["shifted"].at(i + 1))
                nc.scalar.activation(sc[:, :, :, :], sc[:, :, :, :], ACT.Exp).then_inc(s["exped"].handle, 1)
                for j in range(2):
                    n = i * 2 + j
                    act.wait_ge(s["T_mm"].handle, s["T_mm"].at(n + 3))
                    nc.scalar.copy(amT[:, j, :], ps_T[:, j, 0:P]).then_inc(s["T_ev"].handle, 1)
                for j in range(2):
                    n = i * 2 + j
                    act.wait_ge(s["F_mm"].handle, s["F_mm"].at(n + 1))
                    nc.scalar.copy(film_out[:, n, :], ps_F[:, 1, j, :]).then_inc(s["kept"].handle, 1)
                act.wait_ge(s["applied"].handle, s["applied"].at(i * 2 + 2))
                for j in range(2):
                    nc.scalar.copy(film_in[:, j, :], ps_F[:, 0, j, :]).then_inc(s["kept"].handle, 1)
                act.wait_ge(s["kept"].handle, s["kept"].at(i * 4 + 4))
                act.sem_inc(s["F_ev"].handle, 2)

        @block.tensor
        def _(pe):
            ring(pe, s["T_mm"], 2)
            for b in range(B):
                with pe.Fori(0, TPB // 2) as i:
                    for j in range(2):
                        n = i * 2 + (b * TPB + j)
                        pe.wait_ge(s["mean"].handle, s["mean"].at(i + (b * TPB // 2 + 1)))
                        pe.wait_ge(s["T_ev"].handle, s["T_ev"].at(n + 1))
                        nc.tensor.transpose(ps_T[:, j, 0:P], am[:, j, :], c.ident[:, :]).then_inc(s["T_mm"].handle, 1)
                    for j in range(2):
                        n = i * 2 + (b * TPB + j)
                        pe.wait_ge(s["T_ev"].handle, s["T_ev"].at(n + 3))
                        pe.wait_ge(s["F_ev"].handle, s["F_ev"].at(n + 1))
                        for o in range(2):
                            last = nc.tensor.matmul(ps_F[:, o, j, :], amT[:, j, :], VF[:, b, o, :], start=True, stop=True)
                        last.then_inc(s["F_mm"].handle, 1)
    s["step"].base += 1 + NT // 2 * (2 * rounds + 1 + 5)
    s["fence"].base += NT // 2 * (2 * rounds + 1)
    for n in ("shifted", "exped", "mean"):
        s[n].base += NT // 2
    s["F_mm"].base += NT
    s["kept"].base += 2 * NT
    s["applied"].base += NT + 2
    for n in ("T_mm", "T_ev", "F_ev"):
        s[n].base += NT + 2


DB = 16
NDB = D // DB
NI8 = SEQ // P


class L1Kernel:

    def __init__(self, c, st, UK):
        self.c, self.nc, self.UK = c, c.nc, UK
        self.s = {n: c.sig("ker_" + n) for n in
                  "loaded made T_mm step act arg turned earg sined exped fine mm ev".split()}
        self.a = c.sb(st, "ker_a", [P, D])
        self.r0 = c.sb(st, "ker_r0", [P, D])
        self.cols = c.sb(st, "ker_cols", [P, 5])
        self.iota_p = c.sb(st, "ker_iota", [P, P])
        self.coarse = c.sb(st, "ker_coarse", [P, SEQ // P, D])
        self.fine = c.sb(st, "ker_fine", [P, DB, P])
        self.t = c.sb(st, "ker_t", [P, DB, P])
        self.e = c.sb(st, "ker_e", [P, DB, P])
        self.m = c.sb(st, "ker_m", [P, DB, P])
        self.coarse_b = c.sb(st, "ker_coarse_b", [P, DB, NI8])


    def turns_and_exponents(self, pool, b):
        s, g = self.s, self.nc.gpsimd
        for out, of, done in ((self.e, self.a, "earg"), (self.t, self.r0, "turned")):
            g.tensor_tensor(out[:, :, :], bc(of[:, bass.ts(b, DB)].unsqueeze(2), [P, DB, P]),
                            bc(self.iota_p[:, :].unsqueeze(1), [P, DB, P]), ALU.mult).then_inc(s[done].handle, 1)

    def fractions(self, dve, b, count):
        s, v = self.s, self.nc.vector
        link = Chain(dve, s["step"], count)
        dve.wait_ge(s["turned"].handle, s["turned"].at(b + 1))
        link(v.tensor_scalar(self.t[:, :, :], self.t[:, :, :], self.cols[:, 3:4], None, ALU.add))
        link(v.tensor_scalar(self.m[:, :, :], self.t[:, :, :], MAGIC, MAGIC, ALU.add, ALU.subtract))
        v.tensor_tensor(self.t[:, :, :], self.t[:, :, :], self.m[:, :, :], ALU.subtract).then_inc(s["arg"].handle, 1)

    def exponentials(self, act, b):
        s = self.s
        act.wait_ge(s["earg"].handle, s["earg"].at(b + 1))
        self.nc.scalar.activation(self.e[:, :, :], self.e[:, :, :], ACT.Exp).then_inc(s["exped"].handle, 1)


    def sines(self, act, b):
        s = self.s
        act.wait_ge(s["arg"].handle, s["arg"].at(b + 1))
        self.nc.scalar.activation(self.t[:, :, :], self.t[:, :, :], ACT.Sin, scale=TWO_PI).then_inc(s["sined"].handle, 1)

    def powers(self, dve, b):
        s = self.s
        dve.wait_ge(s["exped"].handle, s["exped"].at(b + 1))
        dve.wait_ge(s["sined"].handle, s["sined"].at(b + 1))
        dve.wait_ge(s["mm"].handle, s["mm"].at(b + 1))
        self.nc.vector.tensor_copy(self.coarse_b[:, :, :], self.coarse[:, :, bass.ts(b, DB)].rearrange("p i d -> p d i"))\
            .then_inc(s["fine"].handle, 1)
        self.nc.vector.tensor_tensor(self.fine[:, :, :], self.t[:, :, :], self.e[:, :, :], ALU.mult)\
            .then_inc(s["fine"].handle, 1)

    def multiply(self, pe, ps_K, b):
        s = self.s
        pe.wait_ge(s["fine"].handle, s["fine"].at(b * 2 + 2))
        pe.wait_ge(s["ev"].handle, s["ev"].at(b + 1))
        for d in range(DB):
            last = self.nc.tensor.matmul(ps_K[:, d * NI8:(d + 1) * NI8], self.fine[:, d, :],
                                         self.coarse_b[:, d, :], start=True, stop=True)
        last.then_inc(s["mm"].handle, 1)

    def take(self, dve, ps_K, b):
        s = self.s
        dve.wait_ge(s["mm"].handle, s["mm"].at(b + 2))
        self.nc.vector.tensor_copy(self.UK[:, :, 2, bass.ts(b, DB)],
                                   ps_K[:, 0:DB * NI8].rearrange("p (d i) -> p i d", i=NI8)).then_inc(s["ev"].handle, 1)


    def beside_gpsimd(self, pool, b):
        pool.wait_ge(self.s["fine"].handle, self.s["fine"].at(b * 2 + 2))
        self.turns_and_exponents(pool, b + 1)

    def beside_scalar(self, act, b, half):
        if half == 0:
            self.sines(act, b)
        else:
            self.exponentials(act, b + 1)

    def beside_vector(self, dve, ps_K, b, half):
        if half == 0:
            self.powers(dve, b)
        else:
            self.fractions(dve, b + 1, (b + 1) * 2 + STEP_FINE)
            self.take(dve, ps_K, b)

    def begin(self, w, scatter):
        c, nc, s = self.c, self.nc, self.s
        a, r0, cols, iota_p, coarse = self.a, self.r0, self.cols, self.iota_p, self.coarse
        ARE, AIM, CRE, CIM = range(4)
        with ExitStack() as st:
            raw = c.sb(st, "ker_raw", [P, 4, KD, 2, NS])
            par = c.sb(st, "ker_par", [P, 4, D])
            dt = c.sb(st, "ker_dt", [P, D])
            arg = c.sb(st, "ker_arg", [P, 3, D])
            ea = c.sb(st, "ker_ea", [P, 2, D])
            tmp = c.sb(st, "ker_tmp", [P, 8, D])
            P12 = c.sb(st, "ker_P12", [P, 2, D])
            big = c.sb(st, "ker_big", [P, 3, SEQ // P, D])
            ps_T = c.ps(st, "ker_ps_T", [P, 2, 512])
            block = st.enter_context(nc.Block())

            @block.sync
            def _(sp):
                for q, name in enumerate(("A_re", "A_im", "C_re", "C_im")):
                    for twice in range(2):
                        sp.dma_start(raw[:, q, :, twice, :], w[name].rearrange("(t p) n -> p t n", p=P))\
                            .then_inc(s["loaded"].handle, 16)
                sp.dma_start(dt[:, :], row(w["log_dt"], P)).then_inc(s["loaded"].handle, 16)

            @block.gpsimd
            def _(pool):
                g = nc.gpsimd
                for q, (upper, lower) in enumerate(((2.0, 0.0), (0.0, -2.0), (-2.0, 0.0), (0.25, 0.0), (0.25 * TWO_PI, 0.0))):
                    g.memset(cols[0:NS, q:q + 1], upper).then_inc(s["made"].handle, 1)
                    pool.wait_ge(s["made"].handle, 2 * q + 1)
                    g.memset(cols[NS:P, q:q + 1], lower).then_inc(s["made"].handle, 1)
                    pool.wait_ge(s["made"].handle, 2 * q + 2)
                g.iota(iota_p[:, :], pattern=[[1, P]], base=0, channel_multiplier=0,
                       allow_small_or_imprecise_dtypes=True).then_inc(s["made"].handle, 1)
                pool.wait_ge(s["made"].handle, s["made"].at(11))
                pool.wait_ge(s["step"].handle, s["step"].at(5))
                self.turns_and_exponents(pool, 0)
                scatter(pool)

            @block.tensor
            def _(pe):
                pe.wait_ge(s["loaded"].handle, s["loaded"].at(16 * 9))
                for q in range(4):
                    for k in range(KD):
                        o = (q % 2) * D + k * P
                        last = nc.tensor.transpose(ps_T[:, q // 2, o:o + P], raw[:, q, k, :, :].rearrange("p a n -> p (a n)"),
                                                   c.ident[:, :])
                last.then_inc(s["T_mm"].handle, 1)

            @block.scalar
            def _(act):
                A = s["act"]
                act.wait_ge(s["loaded"].handle, s["loaded"].at(16 * 9))
                nc.scalar.activation(dt[:, :], dt[:, :], ACT.Exp).then_inc(A.handle, 1)
                act.wait_ge(s["step"].handle, s["step"].at(8))
                nc.scalar.activation(ea[:, 0, :], a[:, :], ACT.Exp).then_inc(A.handle, 1)
                nc.scalar.activation(ea[:, 1, :], a[:, :], ACT.Tanh, scale=0.5).then_inc(A.handle, 1)
                nc.scalar.activation(arg[:, :, :], arg[:, :, :], ACT.Sin, scale=TWO_PI).then_inc(A.handle, 1)
                act.wait_ge(s["step"].handle, s["step"].at(STEP_COARSE))
                for q in range(2):
                    nc.scalar.activation(big[:, q, :, :], big[:, q, :, :], ACT.Sin, scale=TWO_PI).then_inc(A.handle, 1)
                nc.scalar.activation(big[:, 2, :, :], big[:, 2, :, :], ACT.Exp).then_inc(A.handle, 1)
                self.exponentials(act, 0)

            @block.vector
            def _(dve):
                v = nc.vector
                link = Chain(dve, s["step"])
                x = tmp
                dve.wait_ge(s["T_mm"].handle, s["T_mm"].at(1))
                dve.wait_ge(s["act"].handle, s["act"].at(1))
                v.tensor_copy(par[:, :, :].rearrange("p (a q) d -> p a (q d)", a=2), ps_T[:, :, :]).then_inc(s["ev"].handle, 1)
                dve.wait_ge(s["ev"].handle, s["ev"].at(1))
                dve.wait_ge(s["made"].handle, s["made"].at(11))
                link(v.tensor_tensor(a[:, :], par[:, ARE, :], dt[:, :], ALU.mult))

                def turns(out, cycles, work, more=0.0):
                    link(v.tensor_scalar(out, cycles, more, None, ALU.add))
                    link(v.tensor_scalar(work, out, MAGIC, MAGIC, ALU.add, ALU.subtract))
                    link(v.tensor_tensor(out, out, work, ALU.subtract))

                link(v.tensor_tensor(r0[:, :], par[:, AIM, :], dt[:, :], ALU.mult))
                link(v.tensor_scalar(r0[:, :], r0[:, :], 0.5 / np.pi, None, ALU.mult))
                link(v.tensor_scalar(x[:, 0, :], r0[:, :], MAGIC, MAGIC, ALU.add, ALU.subtract))
                link(v.tensor_tensor(r0[:, :], r0[:, :], x[:, 0, :], ALU.subtract))
                v.tensor_copy(arg[:, 0, :], r0[:, :])
                v.tensor_scalar(arg[:, 2, :], r0[:, :], 0.5, None, ALU.mult)
                turns(arg[:, 1, :], r0[:, :], x[:, 0, :], 0.25)
                dve.wait_ge(s["act"].handle, s["act"].at(4))
                sn, cs, sh, e1, th = arg[:, 0, :], arg[:, 1, :], arg[:, 2, :], ea[:, 0, :], ea[:, 1, :]
                are, aim, cre, cim = [par[:, q, :] for q in range(4)]

                def mul(out, p, q):
                    link(v.tensor_tensor(out, p, q, ALU.mult))

                er, ei, tr, ti, q, u1, u2 = [x[:, n, :] for n in range(7)]
                link(v.tensor_scalar(u1, e1, 1.0, None, ALU.add))
                mul(er, th, u1)
                mul(er, er, cs)
                mul(u2, sh, sh)
                link(v.scalar_tensor_tensor(er, u2, -2.0, er, ALU.mult, ALU.add))
                mul(ei, e1, sn)
                mul(u1, er, are)
                mul(u2, ei, aim)
                link(v.tensor_tensor(tr, u1, u2, ALU.add))
                mul(u1, ei, are)
                mul(u2, er, aim)
                link(v.tensor_tensor(ti, u1, u2, ALU.subtract))
                mul(u1, are, are)
                mul(u2, aim, aim)
                link(v.tensor_tensor(q, u1, u2, ALU.add))
                link(v.reciprocal(q, q))
                mul(tr, tr, q)
                mul(ti, ti, q)
                mul(u1, cre, tr)
                mul(u2, cim, ti)
                link(v.tensor_tensor(er, u1, u2, ALU.subtract))
                mul(u1, cre, ti)
                mul(u2, cim, tr)
                link(v.tensor_tensor(ei, u1, u2, ALU.add))
                link(v.tensor_scalar(u1, ei, cols[:, 1:2], None, ALU.mult))
                link(v.scalar_tensor_tensor(P12[:, 0, :], er, cols[:, 0:1], u1, ALU.mult, ALU.add))
                link(v.tensor_scalar(u1, ei, cols[:, 2:3], None, ALU.mult))
                link(v.scalar_tensor_tensor(P12[:, 1, :], er, cols[:, 1:2], u1, ALU.mult, ALU.add))
                for i in range(NI8):
                    v.tensor_scalar(big[:, 0, i, :], r0[:, :], float(i * P), None, ALU.mult)
                    link(v.tensor_scalar(big[:, 2, i, :], a[:, :], float(i * P), None, ALU.mult))
                link(v.tensor_scalar(coarse[:, :, :], big[:, 0, :, :], MAGIC, MAGIC, ALU.add, ALU.subtract))
                link(v.tensor_tensor(big[:, 0, :, :], big[:, 0, :, :], coarse[:, :, :], ALU.subtract))
                turns(big[:, 1, :, :], big[:, 0, :, :], coarse[:, :, :], 0.25)
                check(link.count, STEP_COARSE)
                dve.wait_ge(s["act"].handle, s["act"].at(7))
                for q in range(2):
                    mul(big[:, 1 - q, :, :], big[:, 1 - q, :, :], bc(P12[:, q, :].unsqueeze(1), [P, NI8, D]))
                link(v.tensor_tensor(big[:, 0, :, :], big[:, 0, :, :], big[:, 1, :, :], ALU.add))
                mul(coarse[:, :, :], big[:, 0, :, :], big[:, 2, :, :])
                check(link.count, STEP_FINE)
                ring(dve, s["mm"], 1)
                self.fractions(dve, 0, STEP_FINE)
                dve.wait_ge(s["arg"].handle, s["arg"].at(1))


    def rest_gpsimd(self, pool, n):
        if n == 2:
            self.beside_gpsimd(pool, NDB - 2)

    def rest_scalar(self, act):
        for b in (NDB - 2, NDB - 1):
            self.sines(act, b)
            if b + 1 < NDB:
                self.exponentials(act, b + 1)

    def rest_vector(self, dve, ps_K, n):
        if n == 0:
            self.powers(dve, NDB - 2)
        elif n == 10:
            self.fractions(dve, NDB - 1, (NDB - 1) * 2 + STEP_FINE)
            self.take(dve, ps_K, NDB - 2)
        elif n == 18:
            self.powers(dve, NDB - 1)
        elif n == 22:
            self.take(dve, ps_K, NDB - 1)
            dve.wait_ge(self.s["ev"].handle, self.s["ev"].at(NDB + 1))

    def rest_tensor(self, pe, ps_K):
        for b in (NDB - 2, NDB - 1):
            self.multiply(pe, ps_K, b)


STEP_COARSE = 8 + 28 + 8 + 2 + 3
STEP_FINE = STEP_COARSE + 4


def check(count, expected):
    assert count == expected, (count, expected)


def L1_convolve(c, fwd, inv, UK, y):
    nc = c.nc
    s = {n: c.sig("cv_" + n) for n in "step f0 f1 i0 i1 X_mm X_ev Z V_mm V_ev prod acc".split()}
    order = [0, 4, 2, 1, 3]
    W3 = 3 * D
    with ExitStack() as st:
        F = c.sb(st, "cv_F", [P, 2, 3, 2, NF2])
        I = c.sb(st, "cv_I", [P, 2, 3, 2, NF2])
        ab = c.sb(st, "cv_ab", [P, 3, 2, W3])
        Z = c.sb(st, "cv_Z", [P, 2, 2, 2, W3])
        X = c.sb(st, "cv_X", [P, 2, 2, W3])
        Y = c.sb(st, "cv_Y", [P, 2, 2, 2 * D])
        T = c.sb(st, "cv_T", [P, 2, 2, 2 * D])
        ps_X = c.ps(st, "cv_ps_X", [P, 2, 2, 512])
        ps_V = c.ps(st, "cv_ps_V", [P, 2, 2, 512])
        block = st.enter_context(nc.Block())
        real = [f in (0, 4) for f in order]

        def u(j1):
            return UK[:, 2 * j1:2 * j1 + 2, :, :].rearrange("p q b d -> p q (b d)")

        n_loads = [16 * sum(2 if real[j] else 1 for j in range(i % 2, i + 1, 2)) for i in range(NF1)]
        n_V = [sum(1 if r else 2 for r in real[:i]) for i in range(NF1 + 1)]

        @block.sync
        def _(sp):
            def load(out, a, i, signal):
                for lo, hi in ((0, 1), (2, 3)) if real[i] else ((0, 3),):
                    sp.dma_start(out[:, i % 2, lo:hi, :, :], a[order[i], lo:hi, :, :].rearrange("m (q p) n -> p m q n", p=P))\
                        .then_inc(signal.handle, 16)

            for i in range(NF1):
                if i >= 2:
                    sp.wait_ge(s["X_mm"].handle, 4 * (i - 1))
                load(F, fwd, i, s[f"f{i % 2}"])
                if i >= 1:
                    j = i - 1
                    if j >= 2:
                        sp.wait_ge(s["V_mm"].handle, n_V[j - 1])
                    load(I, inv, j, s[f"i{j % 2}"])
            sp.wait_ge(s["V_mm"].handle, n_V[NF1 - 2])
            load(I, inv, NF1 - 1, s[f"i{(NF1 - 1) % 2}"])

        @block.tensor
        def _(pe):
            COS, SIN, NEG = range(3)

            def forward(i):
                pe.wait_ge(s[f"f{i % 2}"].handle, n_loads[i])
                pe.wait_ge(s["Z"].handle, i + 1)
                for part in range(2):
                    terms = [(COS, 0), (SIN, 1)] if part == 0 else [(NEG, 0), (COS, 1)]
                    terms = [x for x in terms if not (real[i] and x[1] == 1)]
                    for mt in range(2):
                        n = 4 * i + 2 * part + mt
                        if n >= 2:
                            pe.wait_ge(s["X_ev"].handle, n - 1)
                        for lo, hi in ((0, 512), (512, W3)):
                            for m, (plane, zp) in enumerate(terms):
                                for q in range(2):
                                    last = nc.tensor.matmul(ps_X[:, n % 2, lo // 512, 0:hi - lo],
                                                            F[:, i % 2, plane, q, mt * P:(mt + 1) * P],
                                                            Z[:, i % 2, zp, q, lo:hi], start=(m == 0 and q == 0),
                                                            stop=(m == len(terms) - 1 and q == 1))
                        last.then_inc(s["X_mm"].handle, 1)

            def backward(i):
                pe.wait_ge(s[f"i{i % 2}"].handle, n_loads[i])
                pe.wait_ge(s["prod"].handle, i + 1)
                for part in range(1 if real[i] else 2):
                    terms = [(COS, 0), (NEG, 1)] if part == 0 else [(SIN, 0), (COS, 1)]
                    n = n_V[i] + part
                    if n >= 2:
                        pe.wait_ge(s["V_ev"].handle, n - 1)
                    for q in range(2):
                        for m, (plane, yp) in enumerate(terms):
                            for mt in range(2):
                                last = nc.tensor.matmul(ps_V[:, n % 2, q, :], I[:, i % 2, plane, mt, q * P:(q + 1) * P],
                                                        Y[:, yp, mt, :], start=(m == 0 and mt == 0),
                                                        stop=(m == 1 and mt == 1))
                    last.then_inc(s["V_mm"].handle, 1)

            forward(0)
            for i in range(NF1):
                if i + 1 < NF1:
                    forward(i + 1)
                backward(i)

        @block.scalar
        def _(act):
            for n in range(4 * NF1):
                i, part, mt = n // 4, n // 2 % 2, n % 2
                act.wait_ge(s["X_mm"].handle, n + 1)
                if n % 4 == 0 and i:
                    act.wait_ge(s["prod"].handle, i)
                nc.scalar.copy(X[:, part, mt, 0:512], ps_X[:, n % 2, 0, :])
                nc.scalar.copy(X[:, part, mt, 512:W3], ps_X[:, n % 2, 1, 0:D]).then_inc(s["X_ev"].handle, 1)

        @block.vector
        def _(dve):
            v = nc.vector
            link = Chain(dve, s["step"])
            add, sub = ALU.add, ALU.subtract

            def transform(i):
                f = order[i]
                zr, zi = Z[:, i % 2, 0, :, :], Z[:, i % 2, 1, :, :]
                if i >= 2:
                    dve.wait_ge(s["X_mm"].handle, 4 * (i - 1))
                if f == 0:
                    link(v.tensor_tensor(ab[:, 0, :, :], u(0), u(2), add))
                    link(v.tensor_tensor(ab[:, 1, :, :], u(1), u(3), add))
                    link(v.tensor_tensor(zr, ab[:, 0, :, :], ab[:, 1, :, :], add))
                elif f == 4:
                    link(v.tensor_tensor(zr, ab[:, 0, :, :], ab[:, 1, :, :], sub))
                elif f == 2:
                    link(v.tensor_tensor(ab[:, 2, :, :], u(3), u(1), sub))
                    link(v.tensor_copy(zi, ab[:, 2, :, :]))
                    link(v.tensor_tensor(zr, u(0), u(2), sub))
                else:
                    sign = -1.0 if f == 1 else 1.0
                    link(v.scalar_tensor_tensor(zr, ab[:, 2, :, :], sign * R2, u(0), ALU.mult, add))
                    link(v.scalar_tensor_tensor(zi, ab[:, 1, :, :], -R2, u(2), ALU.mult, sub if f == 1 else add))
                dve.sem_inc(s["Z"].handle, 1)

            def products(i):
                dve.wait_ge(s["X_ev"].handle, 4 * (i + 1))
                if i:
                    dve.wait_ge(s["V_mm"].handle, n_V[i])

                def part(n):
                    return X[:, n, :, 0:2 * D].rearrange("p m (b d) -> p m b d", b=B)

                def k(n, mt):
                    return bc(X[:, n, mt, 2 * D:W3].unsqueeze(1), [P, B, D])

                for out, ((x0, k0), (x1, k1)), op in ((0, ((0, 0), (1, 1)), sub), (1, ((0, 1), (1, 0)), add)):
                    for mt in range(2):
                        v.tensor_tensor(T[:, 0, mt, :].rearrange("p (b d) -> p b d", b=B), part(x0)[:, mt, :, :], k(k0, mt), ALU.mult)
                        link(v.tensor_tensor(T[:, 1, mt, :].rearrange("p (b d) -> p b d", b=B), part(x1)[:, mt, :, :],
                                             k(k1, mt), ALU.mult))
                    link(v.tensor_tensor(Y[:, out, :, :], T[:, 0, :, :], T[:, 1, :, :], op))
                dve.sem_inc(s["prod"].handle, 1)

            def accumulate(i):
                f = order[i]
                for part in range(1 if real[i] else 2):
                    n = n_V[i] + part
                    dve.wait_ge(s["V_mm"].handle, n + 1)
                    V = ps_V[:, n % 2, :, :].rearrange("p q (b d) -> p q b d", b=B)
                    for j1 in range(4):
                        turn = 2 * np.pi * j1 * f / 8
                        factor = float(np.cos(turn) if part == 0 else -np.sin(turn))
                        out = y[:, 2 * j1:2 * j1 + 2, :, :]
                        if i == 0:
                            link(v.tensor_copy(out, V))
                        elif abs(factor) > 1e-9:
                            link(v.scalar_tensor_tensor(out, V, factor, out, ALU.mult, add))
                    dve.sem_inc(s["V_ev"].handle, 1)

            transform(0)
            transform(1)
            for i in range(NF1):
                products(i)
                if i + 2 < NF1:
                    transform(i + 2)
                accumulate(i)


def L1_join(c, w, UK, y, film_out):
    nc = c.nc
    loaded, step = c.sig("join_loaded"), c.sig("join_step")
    with ExitStack() as st:
        skip = c.sb(st, "join_skip", [P, D])
        block = st.enter_context(nc.Block())

        @block.sync
        def _(sp):
            sp.dma_start(skip[:, :], row(w["D_skip"], P)).then_inc(loaded.handle, 16)

        @block.vector
        def _(dve):
            v = nc.vector
            link = Chain(dve, step)
            dve.wait_ge(loaded.handle, 16)
            for b in range(B):
                tiles = slice(b * TPB, (b + 1) * TPB)
                u = UK[:, :, b, :]
                link(v.tensor_tensor(u, u, bc(skip[:, :].unsqueeze(1), [P, TPB, D]), ALU.mult))
                link(v.tensor_tensor(u, u, y[:, :, b, :], ALU.add))
                link(v.tensor_tensor(u, u, film_out[:, tiles, 0:D], ALU.mult))
                link(v.tensor_tensor(u, u, film_out[:, tiles, D:2 * D], ALU.add))
                link(v.tensor_tensor(c.xn[:, tiles, :], c.xn[:, tiles, :], u, ALU.add))


def L1_xattn(c, w, consts, mask_tok, mask_ctx, xT, UK):
    y = xT[:, :, :].rearrange("p k n -> p (k n)").rearrange("p (i b d) -> p i b d", i=TPB, b=B)
    xt = c.xn
    with ExitStack() as st:
        film_out = c.sb(st, "l1_film_out", [P, NT, 2 * D])
        with ExitStack() as att:
            M = c.sb(att, "l1_M", [P, KD, B, HJ1])
            mask_row = c.sb(att, "l1_mask_row", [1, B, HJ1])
            VF = c.sb(att, "l1_VF", [JE, B, 2, 2 * D])
            tok_factor = c.sb(att, "l1_tok_factor", [P, NT])
            scores = c.sb(att, "l1_scores", [P, NT, HJ1])
            L1_fold(c, w, mask_tok, mask_ctx, M, mask_row, VF, tok_factor[:, :])
            with ExitStack() as lns:
                stats = TokenStats(c, lns, c.xn)
                normalise(c, c.x, xn_out=c.xn, router=(None, HJ1, scores), resident=(M, mask_row), stats=stats)
                stats.finish_alone()
            normalise(c, c.xn, xn_out=lambda n, b, t: UK[:, bass.ds(t, G), b, :], affine=(w["g_norm_in"], w["b_norm_in"]))
            L1_modulate(c, scores, tok_factor, VF, UK, film_out)
        L1_convolve(c, consts["dft_fwd"], consts["dft_inv"], UK, y)
        L1_join(c, w, UK, y, film_out)
    ln_stats(c, xt)
    normalise(c, xt, xT_out=xT, affine=(w["g_ffn"], w["b_ffn"]))
    one = {n: w[n].unsqueeze(0) for n in ("W1", "W2", "b1")}
    experts(c, xT, 1, 4 * D, one["W1"], None, one["W2"], one["b1"], ACT.Gelu, lambda t, e: 1.0, xt,
            plus=w["b2"])
    ln_stats(c, xt)
    with ExitStack() as st:
        out = c.sb(st, "l1_out", [P, NT, D])
        stats = TokenStats(c, st, c.x)
        normalise(c, xt, xn_out=out, affine=(w["g_norm_out"], w["b_norm_out"]), added_to=c.x, stats=stats)
        stats.finish_alone()


LAYERS = ("L0_xattn", "L0_ffn", "L1_xattn", "L1_ffn", "L2_xattn", "L2_ffn", "L3_xattn", "L3_ffn")


def build(nc, a, out, layers=LAYERS):
    with ExitStack() as ctx:
        c = Core(nc, ctx)
        scratch = nc.dram_tensor("scratch", (B, HJC * P, D), F32).ap()
        setup(c, a["x"], a["ctx_768"], a["mask_BxS_bf1"], a["mask_BxS2_bf1"])
        fill_exchange = exchange_buffers(c)
        xT = c.sb(ctx, "xT", [P, KD, B * SEQ])
        for layer in layers:
            w = {n[len(layer) + 1:]: ap for n, ap in a.items() if n.startswith(layer)}
            if layer in ("L0_ffn", "L2_ffn", "L3_ffn"):
                ln_stats(c, c.x)
            if layer == "L0_xattn":
                wide_attention(c, w["Wq"], w["Wk"], w["Wv"], w["Wo"], w["bo"], scratch,
                               beside=fill_exchange)
            elif layer == "L2_xattn":
                wide_attention(c, w["w_q"], w["w_k"], w["w_v"], w["w_out"], w["b_out"], scratch)
            elif layer == "L0_ffn":
                made_of_l1 = ctx.enter_context(ExitStack())
                UK = c.sb(made_of_l1, "l1_UK", [P, TPB, B + 1, D])
                with ExitStack() as st:
                    kernel_l1 = L1Kernel(c, st, UK)
                    L0_ffn(c, w, kernel_l1, {n: a["L1_xattn_" + n] for n in ("log_dt", "A_re", "A_im", "C_re", "C_im")})
            elif layer == "L2_ffn":
                L2_ffn(c, w)
            elif layer == "L1_xattn":
                L1_xattn(c, w, a, a["mask_BxS_bf1"], a["mask_BxS2_bf1"], xT, UK)
                made_of_l1.close()
            elif layer == "L3_xattn":
                L3_xattn(c, w, scratch, xT)
            elif layer == "L1_ffn":
                L1_ffn(c, w, xT)
            elif layer == "L3_ffn":
                L3_ffn(c, w, xT, out.rearrange("b (t p) d -> p (b t) d", p=P))


def kernel(**inputs):
    import concourse.bacc as bacc
    from concourse.bass_utils import run_bass_kernel_spmd

    nc = bacc.Bacc("TRN2", target_bir_lowering=False, num_devices=1)
    arrays, aps = {}, {}
    for name, value in (inputs | constants()).items():
        v = np.ascontiguousarray(value)
        if v.dtype == np.bool_:
            v = v.view(np.uint8)
        if v.ndim == 0:
            v = v.reshape(1)
        arrays[f"in_{name}"] = v
        aps[name] = nc.dram_tensor(f"in_{name}", v.shape, mybir.dt.from_np(v.dtype), kind="ExternalInput").ap()
    out = nc.dram_tensor("out", (B, SEQ, D), F32, kind="ExternalOutput").ap()
    build(nc, aps, out)
    result = run_bass_kernel_spmd(nc, [arrays], core_ids=[0])
    return result.results[0]["out"]
```
